# Optimizing a Trainium2 kernel written in Bass

```python
import numpy as np
import jax
import jax.numpy as jnp

def _softmax(x, axis=-1):
    return jax.nn.softmax(x, axis=axis)

def _gelu(x):
    return jax.nn.gelu(x, approximate=True)

def _silu(x):
    return jax.nn.silu(x)

def _sigmoid(x):
    return jax.nn.sigmoid(x)

def _layernorm(x, axis=-1, eps=1e-05):
    m = jnp.mean(x, axis=axis, keepdims=True)
    v = jnp.var(x, axis=axis, keepdims=True)
    return (x - m) / jnp.sqrt(v + eps)

def _scatter_add(tgt, idx, src, axis=0):
    return tgt.at[idx].add(src)

def _segment_sum(src, seg, n):
    return jax.ops.segment_sum(src, seg, n)
kernel_name = 'mk_flamingo_gated_d4_seqx_r8_41e615'

def setup_inputs(seed: int=0):
    np.random.seed(seed)
    _w = jnp.asarray

    def _rec_inputs():
        import jax
        import jax.numpy as jnp
        _rk = jax.random.key(seed)
        x = 4.136e-05 + 0.9999 * jax.random.normal(jax.random.fold_in(_rk, 1), (4, 256, 256), jnp.float32)
        _lenS = 256 - jax.random.randint(jax.random.fold_in(_rk, 7), (4,), 0, max(1, 256 // 4) + 1, jnp.int32)
        _lenS2 = 256 - jax.random.randint(jax.random.fold_in(_rk, 8), (4,), 0, max(1, 256 // 4) + 1, jnp.int32)
        _ctx_1024P = jax.random.normal(jax.random.fold_in(_rk, 11), (4, 16, 128), jnp.float32)
        _ctx_1024c = jax.random.dirichlet(jax.random.fold_in(_rk, 511), 0.3 * jnp.ones((16,), jnp.float32), (4, 256))
        _ctx_1024t = jnp.einsum('bsk,bkd->bsd', _ctx_1024c, _ctx_1024P)
        _ctx_1024t = _ctx_1024t * jax.lax.rsqrt(jnp.mean(jnp.square(_ctx_1024t)) + 1e-12) * 0.953939
        ctx_1024 = -0.000292821 + 1.00034 * (_ctx_1024t + 0.3 * jax.random.normal(jax.random.fold_in(_rk, 611), (4, 256, 128), jnp.float32))
        fside_BxSx2_0 = jax.random.uniform(jax.random.fold_in(_rk, 12), (4, 256, 2), jnp.float32, 0.0, 0.999707)
        fside_BxS2xS2_0 = -3.05549e-07 + 0.0199987 * jax.random.normal(jax.random.fold_in(_rk, 13), (4, 256, 256), jnp.float32)
        _g = jax.random.normal(jax.random.fold_in(_rk, 9001), (2, 4), jnp.float32)
        _g = jnp.sign(_g) * jnp.maximum(jnp.abs(_g), 1.0) + (_g == 0) * 1.0
        g_xattn = _g[0]
        g_ffn = _g[1]
        return (x, ctx_1024, fside_BxSx2_0, fside_BxS2xS2_0, g_xattn, g_ffn)
    x, ctx_1024, fside_BxSx2_0, fside_BxS2xS2_0, g_xattn, g_ffn = _rec_inputs()

    def _L0_xattn_setup():
        import jax, jax.numpy as jnp
        import numpy as np
        import math
        B, L, DM = (2, 256, 128)
        DS, DC, EXP = (16, 4, 2)
        DI = EXP * DM
        DR = math.ceil(DM / 16)
        DT_MIN, DT_MAX, DT_FLOOR = (0.001, 0.1, 0.0001)

        def _ssm_forward(hidden_states, z, in_proj_w, conv_w, conv_b, x_proj_w, dt_proj_w, dt_proj_b, A_log, D):
            b = hidden_states.shape[0]
            x = jnp.einsum('ed,bld->bel', in_proj_w, hidden_states)
            xp = jnp.pad(x, ((0, 0), (0, 0), (DC - 1, 0)))
            xc = jax.lax.conv_general_dilated(xp, conv_w[:, None, :], window_strides=(1,), padding='VALID', dimension_numbers=('NCH', 'OIH', 'NCH'), feature_group_count=DI)
            u = jax.nn.silu(xc + conv_b[None, :, None])
            x_dbl = jnp.einsum('ke,bel->bkl', x_proj_w, u)
            dt_lo = x_dbl[:, :DR]
            Bm = x_dbl[:, DR:DR + DS]
            Cm = x_dbl[:, DR + DS:]
            delta = jax.nn.softplus(jnp.einsum('er,brl->bel', dt_proj_w, dt_lo) + dt_proj_b[None, :, None])
            A = -jnp.exp(A_log)

            def step(state, xs):
                d_t, B_t, C_t, u_t = xs
                dA = jnp.exp(d_t[..., None] * A)
                state = state * dA + (d_t * u_t)[..., None] * B_t[:, None, :]
                y_t = jnp.einsum('ben,bn->be', state, C_t)
                return (state, y_t)
            xs = (jnp.moveaxis(delta, -1, 0), jnp.moveaxis(Bm, -1, 0), jnp.moveaxis(Cm, -1, 0), jnp.moveaxis(u, -1, 0))
            state0 = jnp.zeros((b, DI, DS), delta.dtype)
            _, ys = jax.lax.scan(step, state0, xs)
            y = jnp.moveaxis(ys, 0, -1)
            y = y + D[None, :, None] * u
            y = y * jax.nn.silu(z)
            return jnp.swapaxes(y, 1, 2)
        key = jax.random.key(seed)
        ks = jax.random.split(key, 8)
        hidden_states = jax.random.normal(ks[0], (B, L, DM), jnp.float32)
        z = jax.random.normal(ks[1], (B, DI, L), jnp.float32)
        in_proj_w = jax.random.normal(ks[2], (DI, DM), jnp.float32) * DM ** (-0.5)
        conv_w = jax.random.normal(ks[3], (DI, DC), jnp.float32) * DC ** (-0.5)
        conv_b = jnp.zeros((DI,), jnp.float32)
        x_proj_w = jax.random.normal(ks[4], (DR + 2 * DS, DI), jnp.float32) * DI ** (-0.5)
        dt_std = DR ** (-0.5)
        dt_proj_w = jax.random.uniform(ks[5], (DI, DR), jnp.float32, -dt_std, dt_std)
        dt = jnp.exp(jax.random.uniform(ks[6], (DI,), jnp.float32) * (math.log(DT_MAX) - math.log(DT_MIN)) + math.log(DT_MIN))
        dt = jnp.clip(dt, DT_FLOOR)
        dt_proj_b = dt + jnp.log(-jnp.expm1(-dt))
        A_log = jnp.log(jnp.broadcast_to(jnp.arange(1, DS + 1, dtype=jnp.float32), (DI, DS)))
        D = jnp.ones((DI,), jnp.float32)
        return dict(hidden_states=hidden_states, z=z, in_proj_w=in_proj_w, conv_w=conv_w, conv_b=conv_b, x_proj_w=x_proj_w, dt_proj_w=dt_proj_w, dt_proj_b=dt_proj_b, A_log=A_log, D=D)
    _L0_xattn_all = _L0_xattn_setup()
    _L0_xattn_in = {k: v for k, v in _L0_xattn_all.items() if k in ('in_proj_w', 'conv_w', 'conv_b', 'x_proj_w', 'dt_proj_w', 'dt_proj_b', 'A_log', 'D')}
    del _L0_xattn_all

    def _L0_ffn_setup():
        import jax, jax.numpy as jnp
        import numpy as np
        RANK = 64
        SCALING = 1.0 / RANK
        TEMPERATURE = 1.0
        key = jax.random.key(seed)
        k_x, k_a, k_b, k_w = jax.random.split(key, 4)
        B_, S, D = (4, 256, 256)
        E, R, O = (8, RANK, 256)
        x = jax.random.normal(k_x, (B_, S, D), dtype=jnp.float32)
        A = jax.random.normal(k_a, (E, R, D), dtype=jnp.float32) * (1.0 / np.sqrt(D))
        Bw = jax.random.normal(k_b, (E, O, R), dtype=jnp.float32) * 0.02
        Wr = jax.random.normal(k_w, (E, D), dtype=jnp.float32) * (1.0 / np.sqrt(D))
        br = jnp.zeros((E,), dtype=jnp.float32)
        return {'x': x, 'A': A, 'B': Bw, 'Wr': Wr, 'br': br}
    _L0_ffn_all = _L0_ffn_setup()
    _L0_ffn_in = {k: v for k, v in _L0_ffn_all.items() if k in ('A', 'B', 'Wr', 'br')}
    del _L0_ffn_all

    def _L1_xattn_setup():
        import jax, jax.numpy as jnp
        import numpy as np
        EPS = 1e-05

        def rmsnorm(x, g, eps=EPS):
            var = jnp.mean(jnp.square(x), axis=-1, keepdims=True)
            return x * jax.lax.rsqrt(var + eps) * g
        key = jax.random.key(seed)
        ks = jax.random.split(key, 8)
        B, Sq, Skv = (2, 512, 64)
        dim, cdim, H, D = (256, 128, 16, 128)
        inner = H * D
        s = lambda f: 1.0 / np.sqrt(f)
        return {'hidden_states': jax.random.normal(ks[0], (B, Sq, dim), jnp.float32), 'encoder_hidden_states': jax.random.normal(ks[1], (B, Skv, cdim), jnp.float32), 'Wq': jax.random.normal(ks[2], (dim, inner), jnp.float32) * s(dim), 'Wk': jax.random.normal(ks[3], (cdim, inner), jnp.float32) * s(cdim), 'Wv': jax.random.normal(ks[4], (cdim, inner), jnp.float32) * s(cdim), 'Wo': jax.random.normal(ks[5], (inner, dim), jnp.float32) * s(inner), 'gq': jnp.ones((D,), jnp.float32), 'gk': jnp.ones((D,), jnp.float32)}
    _L1_xattn_all = _L1_xattn_setup()
    _L1_xattn_in = {k: v for k, v in _L1_xattn_all.items() if k in ('Wq', 'Wk', 'Wv', 'Wo', 'gq', 'gk')}
    del _L1_xattn_all

    def _L1_ffn_setup():
        import jax, jax.numpy as jnp
        import numpy as np
        ACT_BITS = 8
        EPS = 1e-05

        def act_quant(x, bits=ACT_BITS):
            qb = float(2 ** (bits - 1))
            scale = qb / jnp.clip(jnp.max(jnp.abs(x), axis=-1, keepdims=True), EPS)
            xq = jnp.clip(jnp.round(x * scale), -qb, qb - 1) / scale
            return x + jax.lax.stop_gradient(xq - x)

        def weight_quant(w):
            scale = 1.0 / jnp.clip(jnp.mean(jnp.abs(w)), EPS)
            wq = jnp.clip(jnp.round(w * scale), -1.0, 1.0) / scale
            return w + jax.lax.stop_gradient(wq - w)

        def fwht(x):
            shape = x.shape
            n = shape[-1]
            x = x.reshape(-1, n)
            h = 1
            while h < n:
                x = x.reshape(-1, n // (2 * h), 2, h)
                a, b = (x[..., 0, :], x[..., 1, :])
                x = jnp.stack([a + b, a - b], axis=-2).reshape(-1, n)
                h *= 2
            return (x * (1.0 / np.sqrt(n)).astype(np.float32)).reshape(shape)

        def bitlinear(x, w):
            return jnp.einsum('bsh,oh->bso', act_quant(x), weight_quant(w))

        def h_bitlinear(x, w):
            return jnp.einsum('bsh,oh->bso', act_quant(fwht(x)), weight_quant(w))
        key = jax.random.key(seed)
        k1, k2, k3, k4 = jax.random.split(key, 4)
        H, I = (256, 1024)
        B, S = (4, 256)
        std_in = 1.0 / np.sqrt(H)
        std_mid = 1.0 / np.sqrt(I)
        return {'x': jax.random.normal(k1, (B, S, H), dtype=jnp.float32), 'w_gate': jax.random.normal(k2, (I, H), dtype=jnp.float32) * std_in, 'w_up': jax.random.normal(k3, (I, H), dtype=jnp.float32) * std_in, 'w_down': jax.random.normal(k4, (H, I), dtype=jnp.float32) * std_mid}
    _L1_ffn_all = _L1_ffn_setup()
    _L1_ffn_in = {k: v for k, v in _L1_ffn_all.items() if k in ('w_gate', 'w_up', 'w_down')}
    del _L1_ffn_all

    def _L2_xattn_setup():
        import jax, jax.numpy as jnp
        import numpy as np
        DIM = 256
        CTX_DIM = 128
        N_HEADS = 32
        HEAD_DIM = DIM // N_HEADS
        POS_DIM = 2
        B, N, CTXN = (2, 256, 256)
        ROPE_BASE = 10000.0

        def apply_axial_rope(x, pos):
            b, n, h, d = x.shape
            p = pos.shape[-1]
            dpa = d // p
            half = dpa // 2
            freqs = ROPE_BASE ** (-jnp.arange(half, dtype=x.dtype) / half)
            ang = pos[..., :, None] * freqs
            cos = jnp.cos(ang)[:, :, None, :, :]
            sin = jnp.sin(ang)[:, :, None, :, :]
            xr = x.reshape(b, n, h, p, half, 2)
            x1, x2 = (xr[..., 0], xr[..., 1])
            out = jnp.stack([x1 * cos - x2 * sin, x1 * sin + x2 * cos], axis=-1)
            return out.reshape(b, n, h, d)
        key = jax.random.key(seed)
        ks = jax.random.split(key, 8)
        x = jax.random.normal(ks[0], (B, N, DIM), jnp.float32)
        ctx = jax.random.normal(ks[1], (B, CTXN, CTX_DIM), jnp.float32)
        pos_map = jax.random.uniform(ks[2], (B, N, POS_DIM), jnp.float32)
        ctx_pos_map = jax.random.uniform(ks[3], (B, CTXN, POS_DIM), jnp.float32)
        Wq = jax.random.normal(ks[4], (DIM, DIM), jnp.float32) / np.sqrt(DIM)
        Wkv = jax.random.normal(ks[5], (CTX_DIM, 2 * DIM), jnp.float32) / np.sqrt(CTX_DIM)
        Wout = jax.random.normal(ks[6], (DIM, DIM), jnp.float32) / np.sqrt(DIM)
        bout = jnp.zeros((DIM,), jnp.float32)
        return {'x': x, 'ctx': ctx, 'pos_map': pos_map, 'ctx_pos_map': ctx_pos_map, 'Wq': Wq, 'Wkv': Wkv, 'Wout': Wout, 'bout': bout}
    _L2_xattn_all = _L2_xattn_setup()
    _L2_xattn_in = {k: v for k, v in _L2_xattn_all.items() if k in ('Wq', 'Wkv', 'Wout', 'bout')}
    del _L2_xattn_all

    def _L2_ffn_setup():
        import jax, jax.numpy as jnp
        import numpy as np
        D_MODEL = 256
        FFN_DIM = 1024
        HALF_FFN = FFN_DIM // 2
        NUM_EXPERTS = 8
        TOP_K = 2

        def _moe_forward(x_flat, gate_w, w_up, w_down):
            T = x_flat.shape[0]
            logits = x_flat @ gate_w.T
            probs = jax.nn.softmax(logits, axis=-1)
            vals, idx = jax.lax.top_k(probs, TOP_K)
            weights = vals / jnp.sum(vals, axis=-1, keepdims=True)
            c = jnp.zeros((T, NUM_EXPERTS), dtype=x_flat.dtype)
            c = c.at[jnp.arange(T)[:, None], idx].add(weights)

            def body(acc, ew):
                wu, wd, ce = ew
                h = x_flat @ wu.T
                g, u = (h[:, :HALF_FFN], h[:, HALF_FFN:])
                a = jax.nn.silu(g) * u
                out_e = a @ wd.T
                return (acc + ce[:, None] * out_e, None)
            init = jnp.zeros_like(x_flat)
            out, _ = jax.lax.scan(body, init, (w_up, w_down, c.T))
            return out
        key = jax.random.key(seed)
        k_x, k_g, k_u, k_d = jax.random.split(key, 4)
        x = jax.random.normal(k_x, (4, 256, D_MODEL), dtype=jnp.float32)
        gate_w = jax.random.normal(k_g, (NUM_EXPERTS, D_MODEL), dtype=jnp.float32) * 0.01
        s_u = 1.0 / np.sqrt(D_MODEL)
        s_d = 1.0 / np.sqrt(HALF_FFN)
        w_up = jax.random.uniform(k_u, (NUM_EXPERTS, FFN_DIM, D_MODEL), jnp.float32, -s_u, s_u)
        w_down = jax.random.uniform(k_d, (NUM_EXPERTS, D_MODEL, HALF_FFN), jnp.float32, -s_d, s_d)
        return {'x': x, 'gate_w': gate_w, 'w_up': w_up, 'w_down': w_down}
    _L2_ffn_all = _L2_ffn_setup()
    _L2_ffn_in = {k: v for k, v in _L2_ffn_all.items() if k in ('gate_w', 'w_up', 'w_down')}
    del _L2_ffn_all

    def _L3_xattn_setup():
        import jax, jax.numpy as jnp
        import numpy as np
        EPS = 1e-06
        QMAX = 127.0

        def _smooth_quant_linear(x, w):
            amax_x = jnp.max(jnp.abs(x), axis=0)
            amax_w = jnp.max(jnp.abs(w), axis=0)
            s = jnp.sqrt(jnp.maximum(amax_x, EPS) / jnp.maximum(amax_w, EPS))
            s = jnp.maximum(s, EPS)
            xs = x / s
            ws = w * s
            x_scale = jnp.maximum(jnp.max(jnp.abs(xs), axis=-1, keepdims=True), EPS) / QMAX
            w_scale = jnp.maximum(jnp.max(jnp.abs(ws), axis=-1, keepdims=True), EPS) / QMAX
            x_q = jnp.clip(jnp.round(xs / x_scale), -QMAX, QMAX)
            w_q = jnp.clip(jnp.round(ws / w_scale), -QMAX, QMAX)
            return x_q @ w_q.T * x_scale * w_scale.T

        def _expert_forward(xe, guw, dw):
            h = _smooth_quant_linear(xe, guw)
            gate, up = jnp.split(h, 2, axis=-1)
            a = jax.nn.silu(gate) * up
            return _smooth_quant_linear(a, dw)
        key = jax.random.key(seed)
        k1, k2, k3 = jax.random.split(key, 3)
        E, T, D, I = (8, 256, 256, 128)
        x = jax.random.normal(k1, (E, T, D), dtype=jnp.float32)
        gate_up_weight = jax.random.normal(k2, (E, 2 * I, D), dtype=jnp.float32) * 0.02
        down_weight = jax.random.normal(k3, (E, D, I), dtype=jnp.float32) * 0.02
        return {'x': x, 'gate_up_weight': gate_up_weight, 'down_weight': down_weight}
    _L3_xattn_all = _L3_xattn_setup()
    _L3_xattn_in = {k: v for k, v in _L3_xattn_all.items() if k in ()}
    del _L3_xattn_all

    def _L3_ffn_setup():
        import jax, jax.numpy as jnp
        import numpy as np
        B, S, H, I = (1, 64, 256, 768)

        def _quantized_matmul(x, w, scale):
            wq = w.astype(jnp.float8_e4m3fn).astype(x.dtype)
            y = jnp.einsum('bsi,io->bso', x, wq)
            return y * scale
        key = jax.random.key(seed)
        ks = jax.random.split(key, 7)
        return {'x': jax.random.normal(ks[0], (B, S, H), dtype=jnp.float32), 'gate_w': jax.random.normal(ks[1], (H, I), dtype=jnp.float32) * 0.02, 'up_w': jax.random.normal(ks[2], (H, I), dtype=jnp.float32) * 0.02, 'down_w': jax.random.normal(ks[3], (I, H), dtype=jnp.float32) * 0.02, 'gate_scale': jax.random.uniform(ks[4], (I,), dtype=jnp.float32, minval=0.5, maxval=1.5), 'up_scale': jax.random.uniform(ks[5], (I,), dtype=jnp.float32, minval=0.5, maxval=1.5), 'down_scale': jax.random.uniform(ks[6], (H,), dtype=jnp.float32, minval=0.5, maxval=1.5)}
    _L3_ffn_all = _L3_ffn_setup()
    _L3_ffn_in = {k: v for k, v in _L3_ffn_all.items() if k in ('gate_w', 'up_w', 'down_w', 'gate_scale', 'up_scale', 'down_scale')}
    del _L3_ffn_all
    return {'x': x, 'ctx_1024': ctx_1024, 'fside_BxSx2_0': fside_BxSx2_0, 'fside_BxS2xS2_0': fside_BxS2xS2_0, 'g_xattn': g_xattn, 'g_ffn': g_ffn, 'L0_xattn_in_proj_w': _L0_xattn_in['in_proj_w'], 'L0_xattn_conv_w': _L0_xattn_in['conv_w'], 'L0_xattn_conv_b': _L0_xattn_in['conv_b'], 'L0_xattn_x_proj_w': _L0_xattn_in['x_proj_w'], 'L0_xattn_dt_proj_w': _L0_xattn_in['dt_proj_w'], 'L0_xattn_dt_proj_b': _L0_xattn_in['dt_proj_b'], 'L0_xattn_A_log': _L0_xattn_in['A_log'], 'L0_xattn_D': _L0_xattn_in['D'], 'L0_ffn_A': _L0_ffn_in['A'], 'L0_ffn_B': _L0_ffn_in['B'], 'L0_ffn_Wr': _L0_ffn_in['Wr'], 'L0_ffn_br': _L0_ffn_in['br'], 'L1_xattn_Wq': _L1_xattn_in['Wq'], 'L1_xattn_Wk': _L1_xattn_in['Wk'], 'L1_xattn_Wv': _L1_xattn_in['Wv'], 'L1_xattn_Wo': _L1_xattn_in['Wo'], 'L1_xattn_gq': _L1_xattn_in['gq'], 'L1_xattn_gk': _L1_xattn_in['gk'], 'L1_ffn_w_gate': _L1_ffn_in['w_gate'], 'L1_ffn_w_up': _L1_ffn_in['w_up'], 'L1_ffn_w_down': _L1_ffn_in['w_down'], 'L2_xattn_Wq': _L2_xattn_in['Wq'], 'L2_xattn_Wkv': _L2_xattn_in['Wkv'], 'L2_xattn_Wout': _L2_xattn_in['Wout'], 'L2_xattn_bout': _L2_xattn_in['bout'], 'L2_ffn_gate_w': _L2_ffn_in['gate_w'], 'L2_ffn_w_up': _L2_ffn_in['w_up'], 'L2_ffn_w_down': _L2_ffn_in['w_down'], 'L3_ffn_gate_w': _L3_ffn_in['gate_w'], 'L3_ffn_up_w': _L3_ffn_in['up_w'], 'L3_ffn_down_w': _L3_ffn_in['down_w'], 'L3_ffn_gate_scale': _L3_ffn_in['gate_scale'], 'L3_ffn_up_scale': _L3_ffn_in['up_scale'], 'L3_ffn_down_scale': _L3_ffn_in['down_scale']}

def reference(x, ctx_1024, fside_BxSx2_0, fside_BxS2xS2_0, g_xattn, g_ffn, L0_xattn_in_proj_w, L0_xattn_conv_w, L0_xattn_conv_b, L0_xattn_x_proj_w, L0_xattn_dt_proj_w, L0_xattn_dt_proj_b, L0_xattn_A_log, L0_xattn_D, L0_ffn_A, L0_ffn_B, L0_ffn_Wr, L0_ffn_br, L1_xattn_Wq, L1_xattn_Wk, L1_xattn_Wv, L1_xattn_Wo, L1_xattn_gq, L1_xattn_gk, L1_ffn_w_gate, L1_ffn_w_up, L1_ffn_w_down, L2_xattn_Wq, L2_xattn_Wkv, L2_xattn_Wout, L2_xattn_bout, L2_ffn_gate_w, L2_ffn_w_up, L2_ffn_w_down, L3_ffn_gate_w, L3_ffn_up_w, L3_ffn_down_w, L3_ffn_gate_scale, L3_ffn_up_scale, L3_ffn_down_scale):
    import jax
    import jax.numpy as jnp

    def _L0_xattn_ref(hidden_states, z, in_proj_w, conv_w, conv_b, x_proj_w, dt_proj_w, dt_proj_b, A_log, D):
        import jax, jax.numpy as jnp
        import numpy as np
        import math
        B, L, DM = (2, 256, 128)
        DS, DC, EXP = (16, 4, 2)
        DI = EXP * DM
        DR = math.ceil(DM / 16)
        DT_MIN, DT_MAX, DT_FLOOR = (0.001, 0.1, 0.0001)

        def _ssm_forward(hidden_states, z, in_proj_w, conv_w, conv_b, x_proj_w, dt_proj_w, dt_proj_b, A_log, D):
            b = hidden_states.shape[0]
            x = jnp.einsum('ed,bld->bel', in_proj_w, hidden_states)
            xp = jnp.pad(x, ((0, 0), (0, 0), (DC - 1, 0)))
            xc = jax.lax.conv_general_dilated(xp, conv_w[:, None, :], window_strides=(1,), padding='VALID', dimension_numbers=('NCH', 'OIH', 'NCH'), feature_group_count=DI)
            u = jax.nn.silu(xc + conv_b[None, :, None])
            x_dbl = jnp.einsum('ke,bel->bkl', x_proj_w, u)
            dt_lo = x_dbl[:, :DR]
            Bm = x_dbl[:, DR:DR + DS]
            Cm = x_dbl[:, DR + DS:]
            delta = jax.nn.softplus(jnp.einsum('er,brl->bel', dt_proj_w, dt_lo) + dt_proj_b[None, :, None])
            A = -jnp.exp(A_log)

            def step(state, xs):
                d_t, B_t, C_t, u_t = xs
                dA = jnp.exp(d_t[..., None] * A)
                state = state * dA + (d_t * u_t)[..., None] * B_t[:, None, :]
                y_t = jnp.einsum('ben,bn->be', state, C_t)
                return (state, y_t)
            xs = (jnp.moveaxis(delta, -1, 0), jnp.moveaxis(Bm, -1, 0), jnp.moveaxis(Cm, -1, 0), jnp.moveaxis(u, -1, 0))
            state0 = jnp.zeros((b, DI, DS), delta.dtype)
            _, ys = jax.lax.scan(step, state0, xs)
            y = jnp.moveaxis(ys, 0, -1)
            y = y + D[None, :, None] * u
            y = y * jax.nn.silu(z)
            return jnp.swapaxes(y, 1, 2)
        return _ssm_forward(hidden_states, z, in_proj_w, conv_w, conv_b, x_proj_w, dt_proj_w, dt_proj_b, A_log, D)

    def _L0_ffn_ref(x, A, B, Wr, br):
        import jax, jax.numpy as jnp
        import numpy as np
        RANK = 64
        SCALING = 1.0 / RANK
        TEMPERATURE = 1.0
        batch, seq, d = x.shape
        E, out_dim = (B.shape[0], B.shape[1])
        x_flat = x.reshape(-1, d)
        logits = (x_flat @ Wr.T + br) / TEMPERATURE
        probs = jax.nn.softmax(logits, axis=-1)
        expert_idx = jnp.argmax(probs, axis=-1)
        expert_weight = jnp.max(probs, axis=-1)
        h = jnp.einsum('nd,erd->ner', x_flat, A)
        y = jnp.einsum('ner,eor->neo', h, B) * SCALING
        sel = jnp.take_along_axis(y, expert_idx[:, None, None], axis=1)[:, 0, :]
        out_flat = sel * expert_weight[:, None]
        return out_flat.reshape(batch, seq, out_dim)

    def _L1_xattn_ref(hidden_states, encoder_hidden_states, Wq, Wk, Wv, Wo, gq, gk):
        import jax, jax.numpy as jnp
        import numpy as np
        EPS = 1e-05

        def rmsnorm(x, g, eps=EPS):
            var = jnp.mean(jnp.square(x), axis=-1, keepdims=True)
            return x * jax.lax.rsqrt(var + eps) * g
        B, Sq, _ = hidden_states.shape
        Skv = encoder_hidden_states.shape[1]
        D = gq.shape[0]
        H = Wq.shape[1] // D
        scale = 1.0 / np.sqrt(D)
        q = (hidden_states @ Wq).reshape(B, Sq, H, D)
        k = (encoder_hidden_states @ Wk).reshape(B, Skv, H, D)
        v = (encoder_hidden_states @ Wv).reshape(B, Skv, H, D)
        q = rmsnorm(q, gq)
        k = rmsnorm(k, gk)
        scores = jnp.einsum('bqhd,bkhd->bhqk', q, k) * scale
        attn = jax.nn.softmax(scores, axis=-1)
        out = jnp.einsum('bhqk,bkhd->bqhd', attn, v)
        out = out.reshape(B, Sq, H * D)
        return out @ Wo

    def _L1_ffn_ref(x, w_gate, w_up, w_down):
        import jax, jax.numpy as jnp
        import numpy as np
        ACT_BITS = 8
        EPS = 1e-05

        def act_quant(x, bits=ACT_BITS):
            qb = float(2 ** (bits - 1))
            scale = qb / jnp.clip(jnp.max(jnp.abs(x), axis=-1, keepdims=True), EPS)
            xq = jnp.clip(jnp.round(x * scale), -qb, qb - 1) / scale
            return x + jax.lax.stop_gradient(xq - x)

        def weight_quant(w):
            scale = 1.0 / jnp.clip(jnp.mean(jnp.abs(w)), EPS)
            wq = jnp.clip(jnp.round(w * scale), -1.0, 1.0) / scale
            return w + jax.lax.stop_gradient(wq - w)

        def fwht(x):
            shape = x.shape
            n = shape[-1]
            x = x.reshape(-1, n)
            h = 1
            while h < n:
                x = x.reshape(-1, n // (2 * h), 2, h)
                a, b = (x[..., 0, :], x[..., 1, :])
                x = jnp.stack([a + b, a - b], axis=-2).reshape(-1, n)
                h *= 2
            return (x * (1.0 / np.sqrt(n)).astype(np.float32)).reshape(shape)

        def bitlinear(x, w):
            return jnp.einsum('bsh,oh->bso', act_quant(x), weight_quant(w))

        def h_bitlinear(x, w):
            return jnp.einsum('bsh,oh->bso', act_quant(fwht(x)), weight_quant(w))
        gate = bitlinear(x, w_gate)
        up = bitlinear(x, w_up)
        intermediate = jax.nn.silu(gate) * up
        return h_bitlinear(intermediate, w_down)

    def _L2_xattn_ref(x, ctx, pos_map, ctx_pos_map, Wq, Wkv, Wout, bout):
        import jax, jax.numpy as jnp
        import numpy as np
        DIM = 256
        CTX_DIM = 128
        N_HEADS = 32
        HEAD_DIM = DIM // N_HEADS
        POS_DIM = 2
        B, N, CTXN = (2, 256, 256)
        ROPE_BASE = 10000.0

        def apply_axial_rope(x, pos):
            b, n, h, d = x.shape
            p = pos.shape[-1]
            dpa = d // p
            half = dpa // 2
            freqs = ROPE_BASE ** (-jnp.arange(half, dtype=x.dtype) / half)
            ang = pos[..., :, None] * freqs
            cos = jnp.cos(ang)[:, :, None, :, :]
            sin = jnp.sin(ang)[:, :, None, :, :]
            xr = x.reshape(b, n, h, p, half, 2)
            x1, x2 = (xr[..., 0], xr[..., 1])
            out = jnp.stack([x1 * cos - x2 * sin, x1 * sin + x2 * cos], axis=-1)
            return out.reshape(b, n, h, d)
        b, n, _ = x.shape
        ctx_n = ctx.shape[1]
        q = (x @ Wq).reshape(b, n, N_HEADS, HEAD_DIM)
        k, v = jnp.split(ctx @ Wkv, 2, axis=-1)
        k = k.reshape(b, ctx_n, N_HEADS, HEAD_DIM)
        v = v.reshape(b, ctx_n, N_HEADS, HEAD_DIM)
        q = apply_axial_rope(q, pos_map)
        k = apply_axial_rope(k, ctx_pos_map)
        scale = 1.0 / np.sqrt(HEAD_DIM).astype(np.float32)
        logits = jnp.einsum('bqhd,bkhd->bhqk', q, k) * scale
        w = jax.nn.softmax(logits, axis=-1)
        attn = jnp.einsum('bhqk,bkhd->bqhd', w, v)
        attn = attn.reshape(b, n, N_HEADS * HEAD_DIM)
        return attn @ Wout + bout

    def _L2_ffn_ref(x, gate_w, w_up, w_down):
        import jax, jax.numpy as jnp
        import numpy as np
        D_MODEL = 256
        FFN_DIM = 1024
        HALF_FFN = FFN_DIM // 2
        NUM_EXPERTS = 8
        TOP_K = 2

        def _moe_forward(x_flat, gate_w, w_up, w_down):
            T = x_flat.shape[0]
            logits = x_flat @ gate_w.T
            probs = jax.nn.softmax(logits, axis=-1)
            vals, idx = jax.lax.top_k(probs, TOP_K)
            weights = vals / jnp.sum(vals, axis=-1, keepdims=True)
            c = jnp.zeros((T, NUM_EXPERTS), dtype=x_flat.dtype)
            c = c.at[jnp.arange(T)[:, None], idx].add(weights)

            def body(acc, ew):
                wu, wd, ce = ew
                h = x_flat @ wu.T
                g, u = (h[:, :HALF_FFN], h[:, HALF_FFN:])
                a = jax.nn.silu(g) * u
                out_e = a @ wd.T
                return (acc + ce[:, None] * out_e, None)
            init = jnp.zeros_like(x_flat)
            out, _ = jax.lax.scan(body, init, (w_up, w_down, c.T))
            return out
        leading = x.shape[:-1]
        x_flat = x.reshape(-1, x.shape[-1])
        out = _moe_forward(x_flat, gate_w, w_up, w_down)
        return out.reshape(*leading, x.shape[-1])

    def _L3_xattn_ref(x, gate_up_weight, down_weight):
        import jax, jax.numpy as jnp
        import numpy as np
        EPS = 1e-06
        QMAX = 127.0

        def _smooth_quant_linear(x, w):
            amax_x = jnp.max(jnp.abs(x), axis=0)
            amax_w = jnp.max(jnp.abs(w), axis=0)
            s = jnp.sqrt(jnp.maximum(amax_x, EPS) / jnp.maximum(amax_w, EPS))
            s = jnp.maximum(s, EPS)
            xs = x / s
            ws = w * s
            x_scale = jnp.maximum(jnp.max(jnp.abs(xs), axis=-1, keepdims=True), EPS) / QMAX
            w_scale = jnp.maximum(jnp.max(jnp.abs(ws), axis=-1, keepdims=True), EPS) / QMAX
            x_q = jnp.clip(jnp.round(xs / x_scale), -QMAX, QMAX)
            w_q = jnp.clip(jnp.round(ws / w_scale), -QMAX, QMAX)
            return x_q @ w_q.T * x_scale * w_scale.T

        def _expert_forward(xe, guw, dw):
            h = _smooth_quant_linear(xe, guw)
            gate, up = jnp.split(h, 2, axis=-1)
            a = jax.nn.silu(gate) * up
            return _smooth_quant_linear(a, dw)
        return jax.vmap(_expert_forward)(x, gate_up_weight, down_weight)

    def _L3_ffn_ref(x, gate_w, up_w, down_w, gate_scale, up_scale, down_scale):
        import jax, jax.numpy as jnp
        import numpy as np
        B, S, H, I = (1, 64, 256, 768)

        def _quantized_matmul(x, w, scale):
            wq = w.astype(jnp.float8_e4m3fn).astype(x.dtype)
            y = jnp.einsum('bsi,io->bso', x, wq)
            return y * scale
        gate = jax.nn.silu(_quantized_matmul(x, gate_w, gate_scale))
        up = _quantized_matmul(x, up_w, up_scale)
        fuse = gate * up
        return _quantized_matmul(fuse, down_w, down_scale)
    x = x + jnp.tanh(g_xattn[0]) * _L0_xattn_ref(ctx_1024, _layernorm(x, axis=-1), L0_xattn_in_proj_w, L0_xattn_conv_w, L0_xattn_conv_b, L0_xattn_x_proj_w, L0_xattn_dt_proj_w, L0_xattn_dt_proj_b, L0_xattn_A_log, L0_xattn_D)
    x = x + jnp.tanh(g_ffn[0]) * _L0_ffn_ref(_layernorm(x, axis=-1), L0_ffn_A, L0_ffn_B, L0_ffn_Wr, L0_ffn_br)
    x = x + jnp.tanh(g_xattn[1]) * _L1_xattn_ref(_layernorm(x, axis=-1), ctx_1024, L1_xattn_Wq, L1_xattn_Wk, L1_xattn_Wv, L1_xattn_Wo, L1_xattn_gq, L1_xattn_gk)
    x = x + jnp.tanh(g_ffn[1]) * _L1_ffn_ref(_layernorm(x, axis=-1), L1_ffn_w_gate, L1_ffn_w_up, L1_ffn_w_down)
    x = x + jnp.tanh(g_xattn[2]) * _L2_xattn_ref(_layernorm(x, axis=-1), ctx_1024, fside_BxSx2_0, fside_BxSx2_0, L2_xattn_Wq, L2_xattn_Wkv, L2_xattn_Wout, L2_xattn_bout)
    x = x + jnp.tanh(g_ffn[2]) * _L2_ffn_ref(_layernorm(x, axis=-1), L2_ffn_gate_w, L2_ffn_w_up, L2_ffn_w_down)
    x = x + jnp.tanh(g_xattn[3]) * _L3_xattn_ref(_layernorm(x, axis=-1), fside_BxS2xS2_0, ctx_1024)
    x = x + jnp.tanh(g_ffn[3]) * _L3_ffn_ref(_layernorm(x, axis=-1), L3_ffn_gate_w, L3_ffn_up_w, L3_ffn_down_w, L3_ffn_gate_scale, L3_ffn_up_scale, L3_ffn_down_scale)
    return x

_drawn_inputs = setup_inputs


def setup_inputs(seed=0):
    import zlib

    import numpy as np

    out = dict(_drawn_inputs(seed))
    spreads = {'L0_xattn_conv_b': (0.0, 0.1),
     'L0_xattn_D': (1.0, 0.565),
     'L0_ffn_br': (0.0, 0.8),
     'L1_xattn_gq': (1.0, 0.6),
     'L1_xattn_gk': (1.0, 0.6),
     'L2_xattn_bout': (0.0, 0.1)}
    factors = {'g_ffn': 6.428,
     'L0_xattn_dt_proj_w': 19.587,
     'L0_xattn_dt_proj_b': 10.296,
     'L0_xattn_A_log': 9.61,
     'L0_ffn_A': 8.0,
     'L0_ffn_B': 8.0,
     'L0_ffn_Wr': 8.0,
     'L3_ffn_gate_scale': 8.0,
     'L3_ffn_up_scale': 8.0,
     'L3_ffn_down_scale': 8.0,
     'L0_xattn_x_proj_w': 2.779,
     'fside_BxSx2_0': 2.722}
    for name, (base, spread) in spreads.items():
        noise = np.random.default_rng([zlib.crc32(name.encode()), seed]).standard_normal(out[name].shape)
        drawn = base * np.exp(spread * noise) if base else spread * noise
        out[name] = jnp.asarray(drawn.astype(out[name].dtype))
    for name, factor in factors.items():
        out[name] = (out[name] * factor).astype(out[name].dtype)
    return out
```

```python
from contextlib import ExitStack

import numpy as np
import concourse.bass as bass
from concourse import mybir

ALU = mybir.AluOpType
ACT = mybir.ActivationFunctionType
AX = mybir.AxisListType
F32 = mybir.dt.float32
BF16 = mybir.dt.bfloat16
F16 = mybir.dt.float16

P = 128
NB, SEQ, DM = 4, 256, 256
NT = NB * SEQ // P
NTOK = NB * SEQ
DC = DM // P
CTX = 128
HALF = 512
LN_EPS = 1e-5
ROUND = 1.5 * 2.0 ** 23

STAGES = (0, 1, 2, 3, 4, 5, 6, 7)


def await_count(engine, semaphore, value):
    if isinstance(value, int) and value <= 0:
        return
    engine.wait_ge(semaphore, value)


class Core:

    def __init__(self, nc, ctx, dram):
        self.nc, self.dram = nc, dram
        sb = lambda name, shape, dt=F32: ctx.enter_context(nc.sbuf_tensor(name, shape, dt))
        self.X = sb("X", [P, NT, DM])
        self.xn = sb("xn", [P, NT, DM])
        self.xnT = sb("xnT", [P, DC, NTOK])
        self.stats = sb("stats", [P, NT, 6])
        self.meanvar = sb("meanvar", [P, NT, 2])
        self.rstd = sb("rstd", [P, NT])
        self.ident = sb("ident", [P, P])
        self.identh = sb("identh", [P, P], BF16)
        self.ones = sb("ones", [P, P])
        self.eps = sb("eps", [P, 1])
        self.gates = sb("gates", [P, 8])
        self.bank = ctx.enter_context(nc.psum_tensor("bank", [P, 8, HALF], F32))
        self.semaphores = []

    def stage(self, name):
        return Stage(self, name)

    def clear_semaphores(self):
        self.nc.all_engine_barrier()
        self.nc.clear_and_free_semaphores(self.semaphores)
        self.nc.all_engine_barrier()
        self.semaphores = []


class Stage:

    def __init__(self, core, name):
        self.core, self.nc, self.name = core, core.nc, name

    def __enter__(self):
        self.stack = ExitStack()
        self.stack.__enter__()
        self.stats_done = self.sem("stats_done")
        self.aggr_done = self.sem("aggr_done")
        self.root_done = self.sem("root_done")
        self.rstd_done = self.sem("rstd_done")
        self.xn_ready = self.sem("xn_ready")
        self.turned = self.sem("turned")
        self.xnT_ready = self.sem("xnT_ready")
        return self

    def __exit__(self, *e):
        return self.stack.__exit__(*e)

    def sb(self, name, shape, dt=F32):
        return self.stack.enter_context(self.nc.sbuf_tensor(f"{self.name}_{name}", shape, dt))

    def sem(self, name):
        self.core.semaphores.append(self.nc.alloc_semaphore(name=f"{self.name}_{name}"))
        return self.core.semaphores[-1]

    def norm_vector(self, dve):
        c = self.core
        for t in range(NT):
            dve.bn_stats(c.stats[:, t, :], c.X[:, t, :]).then_inc(self.stats_done, 1)
        for t in range(NT):
            dve.wait_ge(self.stats_done, t + 1)
            dve.bn_aggr(c.meanvar[:, t, :], c.stats[:, t, :]).then_inc(self.aggr_done, 1)
        dve.wait_ge(self.root_done, 1)
        dve.reciprocal(c.rstd[:, :], c.rstd[:, :]).then_inc(self.rstd_done, 1)
        dve.wait_ge(self.rstd_done, 1)
        for t in range(NT):
            dve.tensor_scalar(c.xn[:, t, :], c.X[:, t, :], c.meanvar[:, t, 0:1], c.rstd[:, t:t + 1],
                              ALU.subtract, ALU.mult).then_inc(self.xn_ready, 1)

    def norm_tensor(self, pe):
        c = self.core
        for t in range(NT):
            pe.wait_ge(self.xn_ready, t + 1)
            for k in range(DC):
                last = pe.transpose(c.bank[:, 2 * k + t // 4, (t % 4) * P:(t % 4 + 1) * P],
                                    c.xn[:, t, k * P:(k + 1) * P], c.ident[:, :])
            last.then_inc(self.turned, 1)

    def norm_scalar(self, act):
        c = self.core
        act.wait_ge(self.aggr_done, NT)
        act.activation(c.rstd[:, :], c.meanvar[:, :, 1], ACT.Sqrt, bias=c.eps[:, 0:1]).then_inc(self.root_done, 1)
        for h in range(2):
            act.wait_ge(self.turned, 4 * (h + 1))
            for k in range(DC):
                act.copy(c.xnT[:, k, h * HALF:(h + 1) * HALF], c.bank[:, 2 * k + h, :]).then_inc(self.xnT_ready, 1)


def stage_setup(core):
    nc, d = core.nc, core.dram
    with core.stage("setup") as s:
        loaded, ones_set, gate_done = s.sem("loaded"), s.sem("ones_set"), s.sem("gate_done")
        raw = s.sb("raw", [P, 8])
        with nc.Block() as block:
            @block.sync
            def _(sp):
                sp.dma_start(core.X[:, :, :], d["x"].rearrange("(t p) d -> p t d", p=P)).then_inc(loaded, 16)
                sp.dma_start(core.ident[:, :], d["ident"]).then_inc(loaded, 16)
                sp.dma_start(core.identh[:, :], d["identh"]).then_inc(loaded, 16)
                for j, g in enumerate(("g_xattn", "g_ffn")):
                    sp.dma_start(raw[:, 4 * j:4 * j + 4], d[g].partition_broadcast(P)).then_inc(loaded, 16)
                sp.wait_ge(loaded, 5 * 16)

            @block.vector
            def _(dve):
                dve.memset(core.ones[:, :], 1.0).then_inc(ones_set, 1)
                dve.memset(core.eps[:, :], LN_EPS).then_inc(ones_set, 1)

            @block.scalar
            def _(act):
                act.wait_ge(loaded, 5 * 16)
                act.activation(core.gates[:, :], raw[:, :], ACT.Tanh).then_inc(gate_done, 1)


def stage_store(core):
    nc, d = core.nc, core.dram
    with core.stage("store") as s:
        stored = s.sem("stored")
        with nc.Block() as block:
            @block.sync
            def _(sp):
                sp.dma_start(d["out"].rearrange("(t p) d -> p t d", p=P), core.X[:, :, :]).then_inc(stored, 16)
                sp.wait_ge(stored, 16)



def stage_ssm(core):
    nc, d = core.nc, core.dram
    NS, TAPS, DR = 16, 4, 8
    CC = 2
    PAD = TAPS - 1
    with core.stage("ssm") as s:
        w_in, ctxT = s.sb("w_in", [P, CC * P]), s.sb("ctxT", [P, NTOK])
        widths = (TAPS, 1, 1, 1, NS, 2 * NS, DR)
        chan = s.sb("chan", [P, CC, sum(widths)])
        starts = np.cumsum((0,) + widths).tolist()
        conv_w, conv_b, dt_b, skip, a_log, w_bc, w_dt1 = (chan[:, :, a:a + w] for a, w in zip(starts, widths))
        a_neg = s.sb("a_neg", [P, CC, NS])
        w_dt2 = s.sb("w_dt2", [DR, CC * P])
        select3 = s.sb("select3", [96, 2 * NS * P], BF16)
        padded = s.sb("padded", [P, CC, NB, SEQ + PAD])
        conv = s.sb("conv", [P, CC, NTOK])
        u, delta, du = (s.sb(n, [P, CC, NTOK]) for n in ("u", "delta", "du"))
        dt_lo = s.sb("dt_lo", [DR, NTOK])
        rest = s.sb("rest", [2 * NS, NTOK])
        mid = s.sb("mid", [2 * NS, NTOK], BF16)
        parts = s.sb("parts", [96, NTOK], BF16)
        b_row = s.sb("b_row", [P, 2, NTOK])
        decay = s.sb("decay", [P, 2, NB, SEQ])
        drive = s.sb("drive", [P, 2, NTOK])
        state = s.sb("state", [P, 2, NTOK])
        seen = s.sb("seen", [P, 2, NTOK])
        small, is_small = s.sb("small", [P, CC, NTOK]), s.sb("is_small", [P, CC, NTOK], mybir.dt.uint8)
        series = conv
        silu_z = s.sb("silu_z", [P, NT, DM])
        w_s, s_s = s.sem("w_s"), s.sem("s_s")
        names = ("in_done", "pad_ready", "padded_zero", "conv_done", "u_ready", "bc_done", "dt1_done", "dt1_copied",
                 "dt2_done", "pre_ready", "abs_done", "e_ready", "small_known", "delta_ready", "soft", "a_exp", "a_ready", "step", "parts_hi", "parts_mid",
                 "parts_ready", "du_ready", "b_done", "b_copied", "c_done", "decay_ready", "drive_ready", "scanned",
                 "seen_ready", "summed", "silu_z_done", "y_ready", "y_turned", "added")
        S = {n: s.sem(n) for n in names}
        bank = core.bank
        gate = core.gates[:, 0:1]
        two = lambda a: a.rearrange("p (h n) -> p h n", h=2)

        with nc.Block() as block:
            @block.sync
            def _(sp):
                for dst, n in ((ctxT, "ctxT"), (w_in, "l0x_in"), (w_dt2, "l0x_dt2")):
                    sp.dma_start(dst[:, :], d[n]).then_inc(w_s, 16)
                sp.dma_start(chan[:, :, :], d["l0x_chan"].rearrange("(c p) k -> p c k", p=P)).then_inc(w_s, 16)
                sp.dma_start(select3[:, :], d["select3"]).then_inc(s_s, 16)

            @block.tensor
            def _(pe):
                pe.wait_ge(w_s, 4 * 16)
                for k in range(CC):
                    for h in range(2):
                        last = pe.matmul(bank[:, 2 * k + h, :], w_in[:, k * P:(k + 1) * P],
                                         ctxT[:, h * HALF:(h + 1) * HALF], start=True, stop=True)
                    last.then_inc(S["in_done"], 1)
                pe.wait_ge(S["u_ready"], CC)
                for h in range(2):
                    for k in range(CC):
                        last = pe.matmul(bank[0:DR, 6 + h, :], w_dt1[:, k, :], u[:, k, h * HALF:(h + 1) * HALF],
                                         start=k == 0, stop=k == CC - 1)
                last.then_inc(S["dt1_done"], 1)
                for h in range(2):
                    for k in range(CC):
                        last = pe.matmul(bank[0:2 * NS, 4 + h, :], w_bc[:, k, :], u[:, k, h * HALF:(h + 1) * HALF],
                                         start=k == 0, stop=k == CC - 1)
                last.then_inc(S["bc_done"], 1)
                pe.wait_ge(S["dt1_copied"], 1)
                for k in range(CC):
                    for h in range(2):
                        last = pe.matmul(bank[:, 2 * k + h, :], w_dt2[:, k * P:(k + 1) * P],
                                         dt_lo[:, h * HALF:(h + 1) * HALF], start=True, stop=True)
                last.then_inc(S["dt2_done"], 1)
                pe.wait_ge(s_s, 16)
                pe.wait_ge(S["parts_ready"], 1)
                pe.wait_ge(S["pre_ready"], CC)
                pe.wait_ge(S["abs_done"], CC)

                def rows(n, j):
                    if j == 0:
                        await_count(pe, S["b_copied"], n)
                    else:
                        await_count(pe, S["seen_ready"], CC * n)
                    for h in range(2):
                        last = pe.matmul(bank[:, 2 * j + h, :], select3[:, bass.ds((n + NS * j) * P, P)],
                                         parts[:, h * HALF:(h + 1) * HALF], start=True, stop=True)
                    last.then_inc(S["c_done" if j else "b_done"], 1)

                def gather(n, k, first, last_state):
                    pe.wait_ge(S["seen_ready"], CC * n + (k + 1))
                    for h in range(2):
                        last = pe.matmul(bank[:, 4 + 2 * k + h, :], core.ident[:, :], seen[:, k, h * HALF:(h + 1) * HALF],
                                         start=first, stop=last_state, skip_group_check=True)
                    last.then_inc(S["summed"], 1)

                def state_sums(n, first=False, final=False):
                    if not final:
                        rows(n + 2, 0)
                    rows(n, 1)
                    gather(n - 1, 1, first, False)
                    gather(n, 0, False, isinstance(n, int) and n == NS - 1)

                rows(0, 0)
                rows(0, 1)
                rows(1, 0)
                rows(2, 0)
                gather(0, 0, True, False)
                state_sums(1, first=True)
                with pe.Fori(2, NS - 2) as n:
                    state_sums(n)
                state_sums(NS - 2, final=True)
                state_sums(NS - 1, final=True)
                gather(NS - 1, 1, False, True)
                for t in range(NT):
                    b, h = t // 2, t % 2
                    pe.wait_ge(S["y_ready"], CC)
                    if t >= 4:
                        pe.wait_ge(S["added"], t - 3)
                    for k in range(CC):
                        last = pe.transpose(bank[:, t % 4, k * P:(k + 1) * P],
                                            seen[:, k, b * SEQ + h * P:b * SEQ + (h + 1) * P], core.ident[:, :])
                    last.then_inc(S["y_turned"], 1)

            @block.scalar
            def _(act):
                act.wait_ge(S["padded_zero"], 1)
                for k in range(CC):
                    act.wait_ge(S["in_done"], k + 1)
                    for h in range(2):
                        last = act.copy(padded[:, k, 2 * h:2 * h + 2, PAD:PAD + SEQ],
                                        bank[:, 2 * k + h, :].rearrange("p (b n) -> p b n", b=2))
                    last.then_inc(S["pad_ready"], 1)
                for k in range(CC):
                    act.wait_ge(S["conv_done"], k + 1)
                    act.activation(u[:, k, :], conv[:, k, :], ACT.Silu, bias=conv_b[:, k, :]).then_inc(S["u_ready"], 1)
                act.wait_ge(s.aggr_done, NT)
                act.activation(core.rstd[:, :], core.meanvar[:, :, 1], ACT.Sqrt, bias=core.eps[:, 0:1]
                               ).then_inc(s.root_done, 1)
                act.wait_ge(S["dt1_done"], 1)
                act.copy(two(dt_lo[:, :]), bank[0:DR, 6:8, :]).then_inc(S["dt1_copied"], 1)
                act.wait_ge(S["bc_done"], 1)
                act.copy(two(parts[0:2 * NS, :]), bank[0:2 * NS, 4:6, :]).then_inc(S["parts_hi"], 1)
                act.wait_ge(w_s, 4 * 16)
                act.preload_act_table_set("natural_log_exp_and_others")
                act.activation(a_neg[:, :, :], a_log[:, :, :], ACT.Exp).then_inc(S["a_exp"], 1)
                act.wait_ge(S["dt2_done"], 1)
                act.wait_ge(S["pre_ready"], CC)
                for k in range(CC):
                    act.activation(two(delta[:, k, :]), bank[:, 2 * k:2 * k + 2, :], ACT.Abs, bias=dt_b[:, k, :]
                                   ).then_inc(S["abs_done"], 1)
                for k in range(CC):
                    act.wait_ge(S["abs_done"], k + 1)
                    act.activation(small[:, k, :], delta[:, k, :], ACT.Exp, scale=-1.0).then_inc(S["e_ready"], 1)
                for k in range(CC):
                    act.wait_ge(S["e_ready"], k + 1)
                    act.activation(delta[:, k, :], small[:, k, :], ACT.Ln, bias=1.0).then_inc(S["soft"], 1)
                act.wait_ge(S["delta_ready"], CC)
                act.wait_ge(S["a_ready"], 1)

                def copy_b(n, p):
                    act.wait_ge(S["b_done"], n + 1)
                    await_count(act, S["drive_ready"], CC * n - CC)
                    act.copy(two(b_row[:, p, :]), bank[:, 0:2, :]).then_inc(S["b_copied"], 1)

                def decays(n):
                    for k in range(CC):
                        await_count(act, S["scanned"], CC * n + (k - 1))
                        act.activation(decay[:, k, :, 1:SEQ], delta[:, k, :].rearrange("p (b n) -> p b n", b=NB)[:, :, 1:SEQ],
                                       ACT.Exp, scale=a_neg[:, k, bass.ds(n, 1)]).then_inc(S["decay_ready"], 1)

                copy_b(0, 0)
                copy_b(1, 1)
                for p in range(2):
                    decays(p)
                    copy_b(2 + p, p)
                with act.Fori(1, NS // 2 - 1) as i:
                    for p in range(2):
                        decays(2 * i + p)
                        copy_b(2 * i + (p + 2), p)
                decays(NS - 2)
                decays(NS - 1)
                act.wait_ge(s.xn_ready, NT)
                act.activation(silu_z[:, :, :], core.xn[:, :, :], ACT.Silu).then_inc(S["silu_z_done"], 1)

            @block.gpsimd
            def _(pool):
                pool.memset(padded[:, :, :, 0:PAD], 0.0).then_inc(S["padded_zero"], 1)
                pool.memset(decay[:, :, :, 0:1], 0.0).then_inc(S["padded_zero"], 1)
                for k in range(CC):
                    pool.wait_ge(S["delta_ready"], k + 1)
                    pool.tensor_tensor(du[:, k, :], delta[:, k, :], u[:, k, :], ALU.mult).then_inc(S["du_ready"], 1)
                pool.wait_ge(S["du_ready"], CC)

                def drives(n, p):
                    pool.wait_ge(S["b_copied"], n + 1)
                    for k in range(CC):
                        await_count(pool, S["scanned"], CC * n + (k - 1))
                        pool.tensor_tensor(drive[:, k, :], du[:, k, :], b_row[:, p, :], ALU.mult).then_inc(S["drive_ready"], 1)

                for p in range(2):
                    drives(p, p)
                with pool.Fori(1, NS // 2) as i:
                    for p in range(2):
                        drives(2 * i + p, p)

            @block.vector
            def _(dve):
                steps = [0]

                def chain(ins):
                    steps[0] += 1
                    ins.then_inc(S["step"], 1)
                    dve.wait_ge(S["step"], steps[0])

                dve.wait_ge(w_s, 4 * 16)
                dve.wait_ge(S["padded_zero"], 2)
                for k in range(CC):
                    dve.wait_ge(S["pad_ready"], k + 1)
                    out = conv[:, k, :].rearrange("p (b n) -> p b n", b=NB)
                    tap = lambda j: padded[:, k, :, j:j + SEQ]
                    chain(dve.tensor_scalar(out, tap(0), conv_w[:, k, 0:1], None, ALU.mult))
                    for j in range(1, TAPS):
                        ins = dve.scalar_tensor_tensor(out, tap(j), conv_w[:, k, j:j + 1], out, ALU.mult, ALU.add)
                        if j < TAPS - 1:
                            chain(ins)
                    ins.then_inc(S["conv_done"], 1)
                s.norm_vector(dve)
                dve.wait_ge(S["parts_hi"], 1)
                chain(dve.tensor_tensor(two(rest[:, :]), bank[0:2 * NS, 4:6, :], two(parts[0:2 * NS, :]), ALU.subtract))
                chain(dve.tensor_copy(mid[:, :], rest[:, :]))
                dve.tensor_copy(parts[2 * NS:4 * NS, :], mid[:, :])
                dve.tensor_tensor(parts[4 * NS:6 * NS, :], rest[:, :], mid[:, :], ALU.subtract).then_inc(S["parts_ready"], 1)
                dve.wait_ge(S["a_exp"], 1)
                dve.tensor_scalar(a_neg[:, :, :], a_neg[:, :, :], -1.0, None, ALU.mult).then_inc(S["a_ready"], 1)
                dve.wait_ge(S["dt2_done"], 1)
                for k in range(CC):
                    dve.tensor_scalar(two(du[:, k, :]), bank[:, 2 * k:2 * k + 2, :], dt_b[:, k, :], None, ALU.add
                                      ).then_inc(S["pre_ready"], 1)
                for k in range(CC):
                    dve.wait_ge(S["e_ready"], k + 1)
                    chain(dve.tensor_scalar(series[:, k, :], small[:, k, :], -1.0 / 6, None, ALU.mult))
                    for c in (1.0 / 5, -1.0 / 4, 1.0 / 3, -1.0 / 2, 1.0):
                        chain(dve.scalar_tensor_tensor(series[:, k, :], series[:, k, :], c, small[:, k, :], ALU.add, ALU.mult))
                    dve.tensor_scalar(is_small[:, k, :], small[:, k, :], 1.0 / 16, None, ALU.is_lt).then_inc(S["small_known"], 1)
                    dve.wait_ge(S["small_known"], k + 1)
                    dve.wait_ge(S["soft"], k + 1)
                    chain(dve.copy_predicated(delta[:, k, :], is_small[:, k, :], series[:, k, :]))
                    dve.scalar_tensor_tensor(delta[:, k, :], du[:, k, :], 0.0, delta[:, k, :], ALU.max, ALU.add
                                             ).then_inc(S["delta_ready"], 1)

                def scan(n, k):
                    dve.wait_ge(S["decay_ready"], CC * n + (k + 1))
                    dve.wait_ge(S["drive_ready"], CC * n + (k + 1))
                    await_count(dve, S["seen_ready"], CC * n + (k - 1))
                    dve.tensor_tensor_scan(state[:, k, :], decay[:, k, :, :].rearrange("p b n -> p (b n)"), drive[:, k, :], 0.0,
                                           ALU.mult, ALU.add).then_inc(S["scanned"], 1)

                def see(n, k):
                    dve.wait_ge(S["scanned"], CC * n + (k + 1))
                    dve.wait_ge(S["c_done"], n + 1)
                    await_count(dve, S["summed"], CC * n + (k - 1))
                    dve.tensor_tensor(two(seen[:, k, :]), two(state[:, k, :]), bank[:, 2:4, :], ALU.mult
                                      ).then_inc(S["seen_ready"], 1)

                def steps_of(n):
                    scan(n, 1)
                    see(n, 0)
                    scan(n + 1, 0)
                    see(n, 1)

                scan(0, 0)
                steps_of(0)
                with dve.Fori(1, NS - 1) as n:
                    steps_of(n)
                scan(NS - 1, 1)
                see(NS - 1, 0)
                see(NS - 1, 1)
                dve.wait_ge(S["summed"], CC * NS)
                dve.wait_ge(S["silu_z_done"], 1)
                for k in range(CC):
                    chain(dve.scalar_tensor_tensor(two(state[:, k, :]), two(u[:, k, :]), skip[:, k, :],
                                                   bank[:, 4 + 2 * k:6 + 2 * k, :], ALU.mult, ALU.add))
                    z = silu_z[:, :, :].rearrange("p (b c) n -> p c b n", c=CC)[:, k, :, :]
                    dve.tensor_tensor(seen[:, k, :].rearrange("p (b n) -> p b n", b=NB),
                                      state[:, k, :].rearrange("p (b n) -> p b n", b=NB), z, ALU.mult
                                      ).then_inc(S["y_ready"], 1)
                for t in range(NT):
                    dve.wait_ge(S["y_turned"], t + 1)
                    dve.scalar_tensor_tensor(core.X[:, t, :], bank[:, t % 4, 0:DM], gate, core.X[:, t, :],
                                             ALU.mult, ALU.add).then_inc(S["added"], 1)


def one_hot_max(dve, s, chain, e, m, rank8, rank, top, hot):
    wide = lambda a: a.unsqueeze(2).to_broadcast([P, NT, 8])
    chain(dve.tensor_tensor(rank, e, wide(m), ALU.is_equal))
    chain(dve.tensor_tensor(rank, rank, rank8, ALU.mult))
    chain(dve.tensor_reduce(top, rank, AX.X, ALU.max))
    chain(dve.tensor_tensor(hot, rank, wide(top), ALU.is_equal))


def stage_lora_moe(core):
    nc, d = core.nc, core.dram
    NE, RANK = 8, 64
    ER = NE * RANK
    JC = ER // P
    with core.stage("lora") as s:
        wA, wB, wR = s.sb("wA", [P, DC, ER]), s.sb("wB", [P, JC, DM]), s.sb("wR", [P, DC, NE])
        bias, rank8 = s.sb("bias", [P, NE]), s.sb("rank8", [P, NE])
        lg, e8, rank, hot = (s.sb(n, [P, NT, NE]) for n in ("lg", "e8", "rank", "hot"))
        m1, emax, top, total, coef = (s.sb(n, [P, NT]) for n in ("m1", "emax", "top", "total", "coef"))
        hm = s.sb("hm", [P, 2, ER])
        hmT = s.sb("hmT", [P, 2, JC, P])
        loaded, logits, shifted, exps, chained, coefs = (s.sem(n) for n in (
            "loaded", "logits", "shifted", "exps", "chained", "coefs"))
        h_done, masked, h_turned, hT_ready, out_done, added = (s.sem(n) for n in (
            "h_done", "masked", "h_turned", "hT_ready", "out_done", "added"))
        bank = core.bank
        lgp = bank[:, 4, 0:NT * NE].rearrange("p (t e) -> p t e", e=NE)
        gate = core.gates[:, 4:5]

        with nc.Block() as block:
            @block.sync
            def _(sp):
                sp.dma_start(wR[:, :, :], d["l0_Wr"].rearrange("(c p) e -> p c e", p=P)).then_inc(loaded, 16)
                sp.dma_start(bias[:, :], d["l0_br"].partition_broadcast(P)).then_inc(loaded, 16)
                sp.dma_start(rank8[:, :], d["rank8"]).then_inc(loaded, 16)
                sp.dma_start(wA[:, :, :], d["l0_A"].rearrange("(c p) e -> p c e", p=P)).then_inc(loaded, 16)
                sp.dma_start(wB[:, :, :], d["l0_B"].rearrange("(c p) e -> p c e", p=P)).then_inc(loaded, 16)

            @block.tensor
            def _(pe):
                s.norm_tensor(pe)
                pe.wait_ge(loaded, 5 * 16)
                pe.wait_ge(s.xnT_ready, 4)
                for t in range(NT):
                    for c in range(DC):
                        last = pe.matmul(lgp[:, t, :], core.xnT[:, c, t * P:(t + 1) * P], wR[:, c, :],
                                         start=c == 0, stop=c == DC - 1)
                last.then_inc(logits, 1)

                def hidden(t):
                    if t >= 2:
                        pe.wait_ge(masked, t - 1)
                    for c in range(DC):
                        last = pe.matmul(bank[:, t % 2, :], core.xnT[:, c, t * P:(t + 1) * P], wA[:, c, :],
                                         start=c == 0, stop=c == DC - 1)
                    last.then_inc(h_done, 1)

                def turn(t):
                    pe.wait_ge(masked, t + 1)
                    if t >= 2:
                        pe.wait_ge(hT_ready, t - 1)
                    for j in range(JC):
                        last = pe.transpose(bank[:, 2 + t % 2, j * P:(j + 1) * P], hm[:, t % 2, j * P:(j + 1) * P],
                                            core.ident[:, :])
                    last.then_inc(h_turned, 1)

                def out(t):
                    pe.wait_ge(hT_ready, t + 1)
                    if t >= 2:
                        pe.wait_ge(added, t - 1)
                    for j in range(JC):
                        last = pe.matmul(bank[:, 5 + t % 2, 0:DM], hmT[:, t % 2, j, :], wB[:, j, :],
                                         start=j == 0, stop=j == JC - 1)
                    last.then_inc(out_done, 1)

                hidden(0)
                for t in range(NT):
                    if t + 1 < NT:
                        hidden(t + 1)
                    turn(t)
                    if t >= 1:
                        out(t - 1)
                out(NT - 1)

            @block.scalar
            def _(act):
                s.norm_scalar(act)
                act.wait_ge(shifted, 1)
                act.activation(e8[:, :, :], lg[:, :, :], ACT.Exp).then_inc(exps, 1)
                for t in range(NT):
                    act.wait_ge(h_turned, t + 1)
                    if t >= 2:
                        act.wait_ge(out_done, t - 1)
                    act.copy(hmT[:, t % 2, :, :], bank[:, 2 + t % 2, :]).then_inc(hT_ready, 1)

            @block.vector
            def _(dve):
                links = [0]

                def chain(ins):
                    links[0] += 1
                    ins.then_inc(chained, 1)
                    dve.wait_ge(chained, links[0])

                s.norm_vector(dve)
                wide = lambda a: a.unsqueeze(2).to_broadcast([P, NT, NE])
                mid = lambda a: a.unsqueeze(1).to_broadcast([P, NT, NE])
                dve.wait_ge(loaded, 5 * 16)
                dve.wait_ge(logits, 1)
                chain(dve.tensor_tensor(lg[:, :, :], lgp, mid(bias[:, :]), ALU.add))
                chain(dve.tensor_reduce(m1[:, :], lg[:, :, :], AX.X, ALU.max))
                dve.tensor_tensor(lg[:, :, :], lg[:, :, :], wide(m1[:, :]), ALU.subtract).then_inc(shifted, 1)
                dve.wait_ge(exps, 1)
                dve.tensor_reduce(total[:, :], e8[:, :, :], AX.X, ALU.add)
                chain(dve.tensor_reduce(emax[:, :], e8[:, :, :], AX.X, ALU.max))
                one_hot_max(dve, s, chain, e8[:, :, :], emax[:, :], mid(rank8[:, :]), rank[:, :, :], top[:, :], hot[:, :, :])
                chain(dve.reciprocal(total[:, :], total[:, :]))
                chain(dve.scalar_tensor_tensor(coef[:, :], total[:, :], 1.0 / RANK, emax[:, :], ALU.mult, ALU.mult))
                chain(dve.tensor_tensor(hot[:, :, :], hot[:, :, :], wide(coef[:, :]), ALU.mult))

                def add(t):
                    dve.wait_ge(out_done, t + 1)
                    dve.scalar_tensor_tensor(core.X[:, t, :], bank[:, 5 + t % 2, 0:DM], gate, core.X[:, t, :],
                                             ALU.mult, ALU.add).then_inc(added, 1)

                for t in range(NT):
                    dve.wait_ge(h_done, t + 1)
                    if t >= 2:
                        dve.wait_ge(h_turned, t - 1)
                    dve.tensor_tensor(hm[:, t % 2, :].rearrange("p (e r) -> p e r", r=RANK),
                                      bank[:, t % 2, :].rearrange("p (e r) -> p e r", r=RANK),
                                      hot[:, t, :].unsqueeze(2).to_broadcast([P, NE, RANK]), ALU.mult).then_inc(masked, 1)
                    if t >= 2:
                        add(t - 2)
                add(NT - 2)
                add(NT - 1)


def stage_attention_16(core):
    nc, d = core.nc, core.dram
    NH, HD = 16, 128
    LN_SCALE = -0.5 * float(np.log(HD))
    with core.stage("a16") as s:
        ctxT, ctx_nat = s.sb("ctxT", [P, NTOK]), s.sb("ctx_nat", [P, NT, CTX])
        gains, gain = s.sb("gains", [P, 2]), s.sb("gain", [P, 1])
        ln_scale = s.sb("ln_scale", [P, 1])
        wk, wvT = s.sb("wk", [P, 2, HD]), s.sb("wvT", [P, 2, CTX])
        wo, wq = s.sb("wo", [P, 2, DM]), s.sb("wq", [P, DC, HD])
        keys, wvo = s.sb("keys", [P, NH, NTOK]), s.sb("wvo", [P, NH, DM])
        k_sq, k_log, k_row = s.sb("k_sq", [P, 2, NTOK]), s.sb("k_log", [P, NTOK]), s.sb("k_row", [P, NTOK])
        query, q_sq = s.sb("query", [P, 2, HALF]), s.sb("q_sq", [P, HALF])
        q_log, q_factor = s.sb("q_log", [P, 4]), s.sb("q_factor", [P, 2, 4])
        bias = s.sb("bias", [P, 2, 2])
        prob, total, inverse = s.sb("prob", [P, 2, 2, SEQ]), s.sb("total", [P, 2, 2]), s.sb("inverse", [P, 2, 2])
        probT, mixT = s.sb("probT", [P, 2, 2, SEQ]), s.sb("mixT", [P, 2, SEQ])
        in_s, consts = s.sem("in_s"), s.sem("consts")
        kv_in = [s.sem(f"kv_in{k}") for k in range(2)]
        names = ("gain_done", "k_done", "k_squared", "k_sums", "k_logs", "k_rows", "key_ready", "vo_done", "vo_ready",
                 "wq_in", "q_done", "q_squared", "q_ready", "q_sums", "q_logs", "q_factors", "s_done", "top", "bias_ready",
                 "exp_done", "inv_ready", "p_ready", "p_turned", "pT_ready", "mix_done", "mixT_ready", "out_done")
        S = {n: s.sem(n) for n in names}
        bank = core.bank
        gate = core.gates[:, 1:2]
        two = lambda a: a.rearrange("p (h n) -> p h n", h=2)

        with nc.Block() as block:
            @block.sync
            def _(sp):
                sp.dma_start(ctxT[:, :], d["ctxT"]).then_inc(in_s, 16)
                sp.dma_start(ctx_nat[:, :, :], d["ctx"].rearrange("(t p) n -> p t n", p=P)).then_inc(in_s, 16)
                sp.dma_start(gains[:, :], d["l1x_gains"]).then_inc(in_s, 16)

                def load_kv(i, k):
                    h = 2 * i + k
                    for dst, n in ((wk, "l1x_k"), (wvT, "l1x_vT"), (wo, "l1x_o")):
                        sp.dma_start(dst[:, k, :], d[n][bass.ds(h, 1)].rearrange("h p n -> p (h n)")).then_inc(kv_in[k], 16)

                def load_q(h):
                    sp.dma_start(wq[:, :, :], d["l1x_q"][bass.ds(h, 1)].rearrange("h (c p) n -> p (h c) n", p=P)
                                 ).then_inc(S["wq_in"], 16)

                for k in range(2):
                    load_kv(0, k)
                load_q(0)
                with sp.Fori(1, NH // 2) as i:
                    for k in range(2):
                        sp.wait_ge(S["vo_done"], 2 * i + (k - 1))
                        load_kv(i, k)
                with sp.Fori(1, NH) as h:
                    sp.wait_ge(S["q_done"], 2 * h)
                    load_q(h)

            @block.tensor
            def _(pe):
                s.norm_tensor(pe)
                pe.wait_ge(in_s, 3 * 16)
                pe.wait_ge(s.xnT_ready, 4)

                def keys_of(i, k):
                    h = 2 * i + k
                    pe.wait_ge(kv_in[k], 3 * 16 * i + 3 * 16)
                    await_count(pe, S["key_ready"], h - 1)
                    for m in range(2):
                        last = pe.matmul(bank[:, 2 * k + m, :], wk[:, k, :], ctxT[:, m * HALF:(m + 1) * HALF],
                                         start=True, stop=True)
                    last.then_inc(S["k_done"], 1)

                def sums_of(i, k):
                    h = 2 * i + k
                    await_count(pe, S["vo_ready"], h - 1)
                    pe.matmul(bank[:, 6 + k, 0:DM], wvT[:, k, :], wo[:, k, :], start=True, stop=True
                              ).then_inc(S["vo_done"], 1)
                    pe.wait_ge(S["k_squared"], h + 1)
                    await_count(pe, S["k_logs"], h)
                    for m in range(2):
                        last = pe.matmul(bank[:, 4 + m, :], core.ones[:, :], k_sq[:, k, m * HALF:(m + 1) * HALF],
                                         start=True, stop=True)
                    last.then_inc(S["k_sums"], 1)

                for k in range(2):
                    keys_of(0, k)
                    sums_of(0, k)
                with pe.Fori(1, NH // 2) as i:
                    for k in range(2):
                        keys_of(i, k)
                        sums_of(i, k)
                pe.wait_ge(S["key_ready"], NH)
                pe.wait_ge(S["vo_ready"], NH)

                def queries(h, m):
                    n = 2 * h + m
                    if m == 0:
                        pe.wait_ge(S["wq_in"], 16 * h + 16)
                    await_count(pe, S["q_logs"], n)
                    for c in range(DC):
                        last = pe.matmul(bank[:, 4, :], wq[:, c, :], core.xnT[:, c, m * HALF:(m + 1) * HALF],
                                         start=c == 0, stop=c == DC - 1)
                    last.then_inc(S["q_done"], 1)

                def query_sums(h, m):
                    n = 2 * h + m
                    pe.wait_ge(S["q_squared"], n + 1)
                    pe.wait_ge(S["q_ready"], n + 1)
                    for j in range(4):
                        last = pe.matmul(bank[:, 4, j:j + 1], q_sq[:, j * P:(j + 1) * P], core.ones[:, 0:1],
                                         start=True, stop=True)
                    last.then_inc(S["q_sums"], 1)

                def scores(h, b):
                    i = 4 * h + b
                    pe.wait_ge(S["q_ready"], 2 * h + (b // 2 + 1))
                    await_count(pe, S["exp_done"], i)
                    for q in range(2):
                        last = pe.matmul(bank[:, 5, q * SEQ:(q + 1) * SEQ],
                                         query[:, b // 2, (2 * (b % 2) + q) * P:(2 * (b % 2) + q + 1) * P],
                                         keys[:, bass.ds(h, 1), b * SEQ:(b + 1) * SEQ].rearrange("p h n -> p (h n)"),
                                         start=True, stop=True)
                    last.then_inc(S["s_done"], 1)

                def turn(h, b):
                    i = 4 * h + b
                    pe.wait_ge(S["p_ready"], i + 1)
                    await_count(pe, S["pT_ready"], i)
                    for kc in range(2):
                        for q in range(2):
                            last = pe.transpose(bank[:, 6, kc * SEQ + q * P:kc * SEQ + (q + 1) * P],
                                                prob[:, b % 2, q, kc * P:(kc + 1) * P], core.ident[:, :])
                    last.then_inc(S["p_turned"], 1)

                def mix(h, b):
                    i = 4 * h + b
                    pe.wait_ge(S["pT_ready"], i + 1)
                    await_count(pe, S["mixT_ready"], i)
                    for kc in range(2):
                        last = pe.matmul(bank[:, 7, 0:SEQ], ctx_nat[:, 2 * b + kc, :], probT[:, b % 2, kc, :],
                                         start=kc == 0, stop=kc == 1)
                    last.then_inc(S["mix_done"], 1)

                def out(h, b, first, final):
                    pe.wait_ge(S["mixT_ready"], 4 * h + (b + 1))
                    for q in range(2):
                        last = pe.matmul(bank[:, b, q * DM:(q + 1) * DM], mixT[:, b % 2, q * P:(q + 1) * P],
                                         wvo[:, bass.ds(h, 1), :].rearrange("p h n -> p (h n)"),
                                         start=first and q == 0, stop=final, skip_group_check=True)
                    last.then_inc(S["out_done"], 1)

                def head(h, first, final):
                    for b in range(NB):
                        if b == 0:
                            queries(h, 1)
                        scores(h, b)
                        if b == 0:
                            query_sums(h, 1)
                        if not (first == 1 and b == 0):
                            turn(*((h, b - 1) if b else (h - 1, 3)))
                        if not (first == 1 and b < 2):
                            g, e = (h, b - 2) if b >= 2 else (h - 1, b + 2)
                            out(g, e, (first == 1 and b >= 2) or (first == 2 and b < 2), False)
                        if b == 2 and not final:
                            queries(h + 1, 0)
                        if not (first == 1 and b == 0):
                            mix(*((h, b - 1) if b else (h - 1, 3)))
                        if b == 2 and not final:
                            query_sums(h + 1, 0)

                queries(0, 0)
                query_sums(0, 0)
                head(0, 1, False)
                head(1, 2, False)
                with pe.Fori(2, NH - 1) as h:
                    head(h, False, False)
                head(NH - 1, False, True)
                turn(NH - 1, 3)
                mix(NH - 1, 3)
                out(NH - 1, 2, False, True)
                out(NH - 1, 3, False, True)

            @block.scalar
            def _(act):
                s.norm_scalar(act)
                act.preload_act_table_set("natural_log_exp_and_others")

                def keys_of(i, k):
                    h = 2 * i + k
                    act.wait_ge(S["k_done"], h + 1)
                    await_count(act, S["k_sums"], h - 1)
                    act.activation(two(k_sq[:, k, :]), bank[:, 2 * k:2 * k + 2, :], ACT.Square).then_inc(S["k_squared"], 1)
                    act.wait_ge(S["vo_done"], h + 1)
                    act.copy(wvo[:, bass.ds(h, 1), :].rearrange("p h n -> p (h n)"), bank[:, 6 + k, 0:DM]
                             ).then_inc(S["vo_ready"], 1)
                    act.wait_ge(S["k_sums"], h + 1)
                    act.activation(two(k_log[:, :]), bank[:, 4:6, :], ACT.Ln, scale=1.0 / HD, bias=core.eps[:, 0:1]
                                   ).then_inc(S["k_logs"], 1)
                    act.wait_ge(S["k_logs"], h + 1)
                    await_count(act, S["key_ready"], h)
                    act.activation(k_row[:, :], k_log[:, :], ACT.Exp, scale=-0.5).then_inc(S["k_rows"], 1)

                for k in range(2):
                    keys_of(0, k)
                with act.Fori(1, NH // 2) as i:
                    for k in range(2):
                        keys_of(i, k)

                def queries(h, m):
                    n = 2 * h + m
                    act.wait_ge(S["q_done"], n + 1)
                    await_count(act, S["q_sums"], n)
                    act.activation(q_sq[:, :], bank[:, 4, :], ACT.Square).then_inc(S["q_squared"], 1)
                    await_count(act, S["s_done"], 4 * h + (2 * m - 2))
                    act.copy(query[:, m, :], bank[:, 4, :]).then_inc(S["q_ready"], 1)

                def query_factor(h, m):
                    n = 2 * h + m
                    act.wait_ge(S["q_sums"], n + 1)
                    act.activation(q_log[:, :], bank[:, 4, 0:4], ACT.Ln, scale=1.0 / HD, bias=core.eps[:, 0:1]
                                   ).then_inc(S["q_logs"], 1)
                    act.wait_ge(S["q_logs"], n + 1)
                    await_count(act, S["exp_done"], 4 * h + (2 * m - 2))
                    await_count(act, S["bias_ready"], 4 * h + (2 * m - 2))
                    act.activation(q_factor[:, m, :], q_log[:, :], ACT.Exp, scale=-0.5, bias=ln_scale[:, 0:1]
                                   ).then_inc(S["q_factors"], 1)

                def exps(h, b):
                    i = 4 * h + b
                    act.wait_ge(S["q_factors"], 2 * h + (b // 2 + 1))
                    act.wait_ge(S["bias_ready"], i + 1)
                    await_count(act, S["p_turned"], i - 1)
                    await_count(act, S["inv_ready"], i - 1)
                    for q in range(2):
                        last = act.activation(prob[:, b % 2, q, :], bank[:, 5, q * SEQ:(q + 1) * SEQ], ACT.Exp,
                                              scale=q_factor[:, b // 2, 2 * (b % 2) + q:2 * (b % 2) + q + 1],
                                              bias=bias[:, b % 2, q:q + 1], accum_out=total[:, b % 2, q:q + 1])
                    last.then_inc(S["exp_done"], 1)

                def bring_mix(h, b):
                    i = 4 * h + b
                    act.wait_ge(S["mix_done"], i + 1)
                    await_count(act, S["out_done"], i - 1)
                    act.copy(mixT[:, b % 2, :], bank[:, 7, 0:SEQ]).then_inc(S["mixT_ready"], 1)

                def head(h, first, final):
                    for b in range(NB):
                        if b == 0:
                            queries(h, 1)
                        exps(h, b)
                        if b == 0:
                            query_factor(h, 1)
                        if b == 2 and not final:
                            queries(h + 1, 0)
                        if not (first == 1 and b == 0):
                            bring_mix(*((h, b - 1) if b else (h - 1, 3)))
                        if b == 2 and not final:
                            query_factor(h + 1, 0)

                queries(0, 0)
                act.wait_ge(consts, 1)
                query_factor(0, 0)
                head(0, 1, False)
                with act.Fori(1, NH - 1) as h:
                    head(h, False, False)
                head(NH - 1, False, True)
                bring_mix(NH - 1, 3)

            @block.gpsimd
            def _(pool):
                pool.memset(ln_scale[:, :], LN_SCALE).then_inc(consts, 1)

                def normalise(h, b):
                    i = 4 * h + b
                    pool.wait_ge(S["inv_ready"], i + 1)
                    pool.tensor_tensor(prob[:, b % 2, :, :], prob[:, b % 2, :, :],
                                       inverse[:, b % 2, :].unsqueeze(2).to_broadcast([P, 2, SEQ]), ALU.mult
                                       ).then_inc(S["p_ready"], 1)

                with pool.Fori(0, NH) as h:
                    for b in range(NB):
                        normalise(h, b)

            @block.vector
            def _(dve):
                s.norm_vector(dve)
                dve.wait_ge(in_s, 3 * 16)
                dve.tensor_tensor(gain[:, :], gains[:, 0:1], gains[:, 1:2], ALU.mult).then_inc(S["gain_done"], 1)
                dve.wait_ge(S["gain_done"], 1)

                def keys_of(i, k):
                    h = 2 * i + k
                    dve.wait_ge(S["k_rows"], h + 1)
                    dve.scalar_tensor_tensor(keys[:, bass.ds(h, 1), :].rearrange("p h (m n) -> p (h m) n", m=2),
                                             bank[:, 2 * k:2 * k + 2, :], gain[:, 0:1], two(k_row[:, :]),
                                             ALU.mult, ALU.mult).then_inc(S["key_ready"], 1)

                for k in range(2):
                    keys_of(0, k)
                with dve.Fori(1, NH // 2) as i:
                    for k in range(2):
                        keys_of(i, k)

                def top(h, b):
                    i = 4 * h + b
                    dve.wait_ge(S["s_done"], i + 1)
                    await_count(dve, S["exp_done"], i - 1)
                    dve.tensor_reduce(bias[:, b % 2, :], bank[:, 5, :].rearrange("p (q n) -> p q n", q=2), AX.X, ALU.max,
                                      negate=True).then_inc(S["top"], 1)
                    dve.wait_ge(S["top"], i + 1)
                    dve.wait_ge(S["q_factors"], 2 * h + (b // 2 + 1))
                    dve.tensor_tensor(bias[:, b % 2, :], bias[:, b % 2, :],
                                      q_factor[:, b // 2, 2 * (b % 2):2 * (b % 2) + 2], ALU.mult).then_inc(S["bias_ready"], 1)

                def invert(h, b):
                    i = 4 * h + b
                    dve.wait_ge(S["exp_done"], i + 1)
                    await_count(dve, S["p_ready"], i - 1)
                    dve.reciprocal(inverse[:, b % 2, :], total[:, b % 2, :]).then_inc(S["inv_ready"], 1)

                def bring(h, b):
                    i = 4 * h + b
                    dve.wait_ge(S["p_turned"], i + 1)
                    await_count(dve, S["mix_done"], i - 1)
                    dve.tensor_copy(probT[:, b % 2, :, :], bank[:, 6, :].rearrange("p (k n) -> p k n", k=2)
                                    ).then_inc(S["pT_ready"], 1)

                def head(h, first):
                    for b in range(NB):
                        top(h, b)
                        if not (first == 1 and b == 0):
                            bring(*((h, b - 1) if b else (h - 1, 3)))
                        invert(h, b)

                head(0, True)
                with dve.Fori(1, NH) as h:
                    head(h, False)
                bring(NH - 1, 3)
                dve.wait_ge(S["out_done"], 4 * NH)
                for t in range(NT):
                    dve.scalar_tensor_tensor(core.X[:, t, :], bank[:, t // 2, (t % 2) * DM:(t % 2 + 1) * DM], gate,
                                             core.X[:, t, :], ALU.mult, ALU.add)


def stage_bitnet(core):
    nc, d = core.nc, core.dram
    FF = 1024
    FC = FF // P
    QMAX = 128.0
    EPS = 1e-5
    NW = DC * FF
    with core.stage("bit") as s:
        raw = [s.sb(f"raw{i}", [P, NW]) for i in range(3)]
        tern = [s.sb(f"tern{i}", [P, NW], BF16) for i in range(3)]
        w_gate, w_up = (tern[i][:, :].rearrange("p (c f) -> p c f", c=DC) for i in range(2))
        w_down = tern[2][:, :].rearrange("p (c f) -> p c f", c=FC)
        rowsum, wmean, wscale, wback = (s.sb(n, [P, 3]) for n in ("rowsum", "wmean", "wscale", "wback"))
        hadamard = s.sb("hadamard", [P, P])
        amax, qscale, back, gback, uback = (s.sb(n, [P, NT]) for n in ("amax", "qscale", "back", "gback", "uback"))
        shifted = s.sb("shifted", [P, 2, DM])
        xq = s.sb("xq", [P, NT, DM], BF16)
        xqT = s.sb("xqT", [P, DC, NTOK], BF16)
        silu = s.sb("silu", [P, 2, HALF])
        inter = s.sb("inter", [P, 2, HALF])
        interT = s.sb("interT", [P, 2, HALF])
        fly = s.sb("fly", [P, 2, FF])
        fly2 = s.sb("fly2", [P, HALF])
        amax2, qscale2, back2 = (s.sb(n, [P, NT]) for n in ("amax2", "qscale2", "back2"))
        fq = s.sb("fq", [P, 2, FF], BF16)
        fqT = s.sb("fqT", [P, 2, FC, P], BF16)
        loaded = [s.sem(f"loaded{i}") for i in range(3)]
        consts, sums, sums_out, tern_ready, step = (s.sem(n) for n in ("consts", "sums", "sums_out", "tern_ready", "step"))
        xq_scaled = s.sem("xq_scaled")
        xq_ready, xq_turned, xqT_ready = (s.sem(n) for n in ("xq_ready", "xq_turned", "xqT_ready"))
        gate_up, silu_done, inter_ready, inter_turned, interT_ready = (s.sem(n) for n in (
            "gate_up", "silu_done", "inter_ready", "inter_turned", "interT_ready"))
        h_done, h_read, fq_ready, fq_turned, fqT_ready, out_done, added = (s.sem(n) for n in (
            "h_done", "h_read", "fq_ready", "fq_turned", "fqT_ready", "out_done", "added"))
        bank = core.bank
        gate = core.gates[:, 5:6]
        half_bf = lambda b: bank[:, b, :].bitcast(BF16)

        with nc.Block() as block:
            @block.sync
            def _(sp):
                for i, n in enumerate(("l1_gate", "l1_up", "l1_down")):
                    sp.dma_start(raw[i][:, :].rearrange("p (c f) -> p c f", c=DC if i < 2 else FC),
                                 d[n].rearrange("(c p) f -> p c f", p=P)).then_inc(loaded[i], 16)
                sp.dma_start(hadamard[:, :], d["hadamard"]).then_inc(consts, 16)

            @block.tensor
            def _(pe):
                for i in range(3):
                    pe.wait_ge(sums, i + 1)
                    pe.matmul(bank[:, 7, i:i + 1], core.ones[:, :], rowsum[:, i:i + 1], start=True, stop=True
                              ).then_inc(sums_out, 1)
                for t in range(NT):
                    pe.wait_ge(xq_ready, t + 1)
                    if t >= 1:
                        pe.wait_ge(xqT_ready, t)
                    for c in range(DC):
                        last = pe.transpose(half_bf(5)[:, c * P:(c + 1) * P], xq[:, t, c * P:(c + 1) * P],
                                            core.identh[:, :])
                    last.then_inc(xq_turned, 1)
                pe.wait_ge(consts, 16)
                pe.wait_ge(tern_ready, 2)

                def gate_and_up(n):
                    t, h = n // 2, n % 2
                    pe.wait_ge(xqT_ready, t + 1)
                    if n >= 1:
                        pe.wait_ge(inter_ready, n)
                    for k, w in enumerate((w_gate, w_up)):
                        for c in range(DC):
                            last = pe.matmul(bank[:, k, :], xqT[:, c, t * P:(t + 1) * P],
                                             w[:, c, h * HALF:(h + 1) * HALF], start=c == 0, stop=c == DC - 1)
                    last.then_inc(gate_up, 1)

                def turn(n):
                    pe.wait_ge(inter_ready, n + 1)
                    if n >= 1:
                        pe.wait_ge(interT_ready, n)
                    for j in range(4):
                        last = pe.transpose(bank[:, 2, j * P:(j + 1) * P], inter[:, n % 2, j * P:(j + 1) * P],
                                            core.ident[:, :])
                    last.then_inc(inter_turned, 1)

                def transform(n):
                    t, h = n // 2, n % 2
                    pe.wait_ge(interT_ready, n + 1)
                    if t >= 1:
                        pe.wait_ge(h_read, t)
                    for j in range(4):
                        last = pe.matmul(bank[:, 3 + h, j * P:(j + 1) * P], interT[:, n % 2, j * P:(j + 1) * P],
                                         hadamard[:, :], start=True, stop=True)
                    last.then_inc(h_done, 1)

                def turn_fq(t):
                    pe.wait_ge(fq_ready, t + 1)
                    if t >= 1:
                        pe.wait_ge(fqT_ready, t)
                    for j in range(FC):
                        last = pe.transpose(half_bf(5)[:, j * P:(j + 1) * P], fq[:, t % 2, j * P:(j + 1) * P],
                                            core.identh[:, :])
                    last.then_inc(fq_turned, 1)

                def down(t):
                    pe.wait_ge(fqT_ready, t + 1)
                    if t == 0:
                        pe.wait_ge(tern_ready, 3)
                    else:
                        pe.wait_ge(added, t)
                    for j in range(FC):
                        last = pe.matmul(bank[:, 6, 0:DM], fqT[:, t % 2, j, :], w_down[:, j, :],
                                         start=j == 0, stop=j == FC - 1)
                    last.then_inc(out_done, 1)

                pe.wait_ge(xqT_ready, NT)
                gate_and_up(0)
                for n in range(2 * NT):
                    if n + 1 < 2 * NT:
                        gate_and_up(n + 1)
                    turn(n)
                    transform(n)
                    if n % 2 == 1 and n >= 3:
                        turn_fq(n // 2 - 1)
                        down(n // 2 - 1)
                turn_fq(NT - 1)
                down(NT - 1)

            @block.scalar
            def _(act):
                act.wait_ge(s.aggr_done, NT)
                act.activation(core.rstd[:, :], core.meanvar[:, :, 1], ACT.Sqrt, bias=core.eps[:, 0:1]
                               ).then_inc(s.root_done, 1)
                for t in range(NT):
                    act.wait_ge(xq_turned, t + 1)
                    act.copy(xqT[:, :, t * P:(t + 1) * P], half_bf(5)[:, 0:DC * P].rearrange("p (c n) -> p c n", c=DC)
                             ).then_inc(xqT_ready, 1)

                def silu_of(n):
                    act.wait_ge(gate_up, n + 1)
                    if n >= 2:
                        act.wait_ge(inter_ready, n - 1)
                    act.activation(silu[:, n % 2, :], bank[:, 0, :], ACT.Silu, scale=gback[:, n // 2:n // 2 + 1]
                                   ).then_inc(silu_done, 1)

                def bring(n):
                    act.wait_ge(inter_turned, n + 1)
                    if n >= 2:
                        act.wait_ge(h_done, n - 1)
                    act.copy(interT[:, n % 2, :], bank[:, 2, :]).then_inc(interT_ready, 1)

                def bring_fq(t):
                    act.wait_ge(fq_turned, t + 1)
                    if t >= 2:
                        act.wait_ge(out_done, t - 1)
                    act.copy(fqT[:, t % 2, :, :], half_bf(5)).then_inc(fqT_ready, 1)

                act.wait_ge(xq_scaled, 1)
                silu_of(0)
                for n in range(2 * NT):
                    if n + 1 < 2 * NT:
                        silu_of(n + 1)
                    bring(n)
                    if n % 2 == 1 and n >= 3:
                        bring_fq(n // 2 - 1)
                bring_fq(NT - 1)

            @block.gpsimd
            def _(pool):
                pass

            @block.vector
            def _(dve):
                steps = [0]

                def chain(ins):
                    steps[0] += 1
                    ins.then_inc(step, 1)
                    dve.wait_ge(step, steps[0])

                def ternary(i):
                    w = raw[i][:, :]
                    chain(dve.tensor_scalar(w, w, wscale[:, i:i + 1], ROUND, ALU.mult, ALU.add))
                    chain(dve.tensor_scalar(w, w, ROUND, 1.0, ALU.subtract, ALU.min))
                    dve.tensor_scalar(tern[i][:, :], w, -1.0, None, ALU.max).then_inc(tern_ready, 1)

                for i in range(3):
                    dve.wait_ge(loaded[i], 16)
                    dve.tensor_reduce(rowsum[:, i:i + 1], raw[i][:, :], AX.X, ALU.add, apply_absolute_value=True
                                      ).then_inc(sums, 1)
                s.norm_vector(dve)
                dve.wait_ge(sums_out, 3)
                chain(dve.tensor_scalar(wmean[:, :], bank[:, 7, 0:3], 1.0 / (NW * P), EPS, ALU.mult, ALU.max))
                chain(dve.reciprocal(wscale[:, :], wmean[:, :]))
                chain(dve.reciprocal(wback[:, :], wscale[:, :]))
                ternary(0)
                ternary(1)
                dve.wait_ge(s.xn_ready, NT)
                chain(dve.tensor_reduce(amax[:, :], core.xn[:, :, :], AX.X, ALU.max, apply_absolute_value=True))
                chain(dve.tensor_scalar(amax[:, :], amax[:, :], EPS, None, ALU.max))
                chain(dve.reciprocal(qscale[:, :], amax[:, :]))
                chain(dve.tensor_scalar(qscale[:, :], qscale[:, :], QMAX, None, ALU.mult))
                chain(dve.reciprocal(back[:, :], qscale[:, :]))
                for t in range(NT):
                    chain(dve.tensor_scalar(shifted[:, t % 2, :], core.xn[:, t, :], qscale[:, t:t + 1], ROUND,
                                            ALU.mult, ALU.add))
                    dve.tensor_scalar(xq[:, t, :], shifted[:, t % 2, :], ROUND, QMAX - 1, ALU.subtract, ALU.min
                                      ).then_inc(xq_ready, 1)
                chain(dve.tensor_scalar(gback[:, :], back[:, :], wback[:, 0:1], None, ALU.mult))
                dve.tensor_scalar(uback[:, :], back[:, :], wback[:, 1:2], None, ALU.mult).then_inc(xq_scaled, 1)
                dve.wait_ge(xq_scaled, 1)
                ternary(2)

                def inter_of(n):
                    dve.wait_ge(silu_done, n + 1)
                    if n >= 2:
                        dve.wait_ge(inter_turned, n - 1)
                    t = n // 2
                    dve.scalar_tensor_tensor(inter[:, n % 2, :], bank[:, 1, :], uback[:, t:t + 1], silu[:, n % 2, :],
                                             ALU.mult, ALU.mult).then_inc(inter_ready, 1)

                def butterflies(t):
                    dve.wait_ge(h_done, 2 * t + 2)
                    f0, f1 = fly[:, 0, :], fly[:, 1, :]
                    pair = lambda a, m: a.rearrange("p (a two b) -> p a two b", two=2, b=m * P)
                    chain(dve.tensor_copy(fly2[:, :], bank[:, 3, :]))
                    chain(dve.tensor_tensor(fly[:, 0, 0:HALF], fly2[:, :], bank[:, 4, :], ALU.add))
                    dve.tensor_tensor(fly[:, 0, HALF:FF], fly2[:, :], bank[:, 4, :], ALU.subtract).then_inc(h_read, 1)
                    dve.wait_ge(h_read, t + 1)
                    for m, (a, b) in ((2, (f0, f1)), (1, (f1, f0))):
                        pa, pb = pair(a, m), pair(b, m)
                        dve.tensor_tensor(pb[:, :, 0, :], pa[:, :, 0, :], pa[:, :, 1, :], ALU.add)
                        chain(dve.tensor_tensor(pb[:, :, 1, :], pa[:, :, 0, :], pa[:, :, 1, :], ALU.subtract))
                    col = slice(t, t + 1)
                    chain(dve.tensor_reduce(amax2[:, col], f0, AX.X, ALU.max, apply_absolute_value=True))
                    chain(dve.tensor_scalar(amax2[:, col], amax2[:, col], 1.0 / 32, EPS, ALU.mult, ALU.max))
                    chain(dve.reciprocal(qscale2[:, col], amax2[:, col]))
                    chain(dve.tensor_scalar(qscale2[:, col], qscale2[:, col], QMAX, None, ALU.mult))
                    chain(dve.reciprocal(back2[:, col], qscale2[:, col]))
                    chain(dve.tensor_scalar(back2[:, col], back2[:, col], wback[:, 2:3], gate, ALU.mult, ALU.mult))
                    chain(dve.tensor_scalar(qscale2[:, col], qscale2[:, col], 1.0 / 32, None, ALU.mult))
                    chain(dve.tensor_scalar(f1, f0, qscale2[:, col], ROUND, ALU.mult, ALU.add))
                    if t >= 2:
                        dve.wait_ge(fq_turned, t - 1)
                    dve.tensor_scalar(fq[:, t % 2, :], f1, ROUND, QMAX - 1, ALU.subtract, ALU.min).then_inc(fq_ready, 1)

                def add(t):
                    dve.wait_ge(out_done, t + 1)
                    dve.scalar_tensor_tensor(core.X[:, t, :], bank[:, 6, 0:DM], back2[:, t:t + 1], core.X[:, t, :],
                                             ALU.mult, ALU.add).then_inc(added, 1)

                inter_of(0)
                for n in range(2 * NT):
                    if n + 1 < 2 * NT:
                        inter_of(n + 1)
                    if n % 2 == 1:
                        if n >= 5:
                            add(n // 2 - 2)
                        if n >= 3:
                            dve.wait_ge(fq_ready, n // 2)
                        butterflies(n // 2)
                add(NT - 2)
                add(NT - 1)


def stage_attention_32(core):
    nc, d = core.nc, core.dram
    NH, HD = 32, 8
    SCALE = float(HD) ** -0.5
    FREQS = (1.0, 0.01)
    PI = 3.1415925
    TURN_HI, TURN_LO = 6.28125, 2 * float(np.pi) - 6.28125
    Q_PARTS, K_PARTS = (0, 0, 1, 0, 2, 1), (0, 1, 0, 2, 0, 1)
    SHIFT = 64
    NBUF = 3
    VW = HD + 1
    QUAD = 4
    NQ = NH // QUAD
    ANGLE_STEPS = 7
    with core.stage("a32") as s:
        ctxT, wq, wkv, wout = s.sb("ctxT", [P, NTOK]), s.sb("wq", [P, DC, DM]), s.sb("wkv", [P, 2 * DM]), s.sb("wout", [P, DC, DM])
        bout = s.sb("bout", [1, DM])
        pos = s.sb("pos", [P, NT, 2])
        angle, turns, trig = (s.sb(n, [P, NT, 2, 4]) for n in ("angle", "turns", "trig"))
        cos8, sin8 = s.sb("cos8", [P, NT, HD]), s.sb("sin8", [P, NT, HD])
        straight, crossed = s.sb("straight", [P, 2, 2 * DM]), s.sb("crossed", [P, 2, 2 * DM])
        rest = s.sb("rest", [P, 2, 4, P])
        parts = [s.sb(f"part{j}", [P, 4, 2, P], BF16) for j in range(6)]
        values = s.sb("values", [P, NT, NH, VW])
        q_stack = s.sb("q_stack", [P, NBUF, NH, SEQ], BF16)
        k_stack = s.sb("k_stack", [P, NBUF, NH, SEQ], BF16)
        tops, shift = s.sb("tops", [P, 2, 2, NH]), s.sb("shift", [NH, 2, SEQ], BF16)
        prob = s.sb("prob", [P, 2, 4, SEQ])
        outT = s.sb("outT", [P, 2, SEQ])
        inverse, attn = s.sb("inverse", [P, 2, 2, QUAD]), s.sb("attn", [P, NT, DM])
        attnT = s.sb("attnT", [P, 2, DC, P])
        scratch = nc.dram_tensor("a32_scratch", [3, 2, DM, NTOK], BF16).ap()
        scratch_shift = nc.dram_tensor("a32_scratch_shift", [NB, NH, SEQ], BF16).ap()
        names = ("w_in", "pos_in", "step", "trig_done", "qk_done", "values_done", "crossed_r", "roped", "turned32", "v_ready",
                 "ones_set", "q_zero", "k_zero", "row_set", "rows_clear", "banks_clear", "zero_set",  "hi_ready", "rest_ready", "mid_ready", "lo_ready", "s_done", "top_done",
                 "top_turned", "shift_ready", "st_done", "exp_done", "av_done", "outT_ready", "quad_turned", "inv_done", "attn_ready", "attn_turned",
                 "attnT_ready", "out_done", "added")
        S = {n: s.sem(n) for n in names}
        spilled = [s.sem(f"spilled{b}") for b in range(NB)]
        stacked = [s.sem(f"stacked{b}") for b in range(NB)]
        shifted = [s.sem(f"shifted{b}") for b in range(NB)]
        bank = core.bank
        gate = core.gates[:, 2:3]
        NG = NH // 2

        def part(j, b):
            return parts[3 * (b % 2) + j]

        with nc.Block() as block:
            @block.sync
            def _(sp):
                sp.dma_start(ctxT[:, :], d["ctxT"]).then_inc(S["w_in"], 16)
                sp.dma_start(wkv[:, :], d["l2x_kv"]).then_inc(S["w_in"], 16)
                for dst, n in ((wq, "l2x_q"), (wout, "l2x_out")):
                    sp.dma_start(dst[:, :, :], d[n].rearrange("(c p) n -> p c n", p=P)).then_inc(S["w_in"], 16)
                sp.dma_start(bout[:, :], d["l2x_bout"].rearrange("(a n) -> a n", a=1)).then_inc(S["w_in"], 16)
                sp.dma_start(pos[:, :, :], d["pos"].rearrange("(t p) k -> p t k", p=P)).then_inc(S["pos_in"], 16)
                def stack(b):
                    sp.wait_ge(S["lo_ready"], 2 * b + 2)
                    tokens = slice(b * SEQ, (b + 1) * SEQ)
                    for j in range(3):
                        sp.dma_start(scratch[j, :, :, tokens].rearrange("k (c p) n -> p (k c) n", p=P),
                                     part(j, b)[:, :, :, :].rearrange("p k i n -> p k (i n)")).then_inc(spilled[b], 16)
                    sp.wait_ge(spilled[b], 3 * 16)
                    if b == 0:
                        sp.wait_ge(S["q_zero"], NBUF)
                        sp.wait_ge(S["k_zero"], NBUF)
                        for n in range(NBUF):
                            sp.dma_start(k_stack[SHIFT:SHIFT + 1, n, :, :], d["row_of_ones"].rearrange("(a h n) -> a h n", a=1, h=NH)
                                         ).then_inc(S["row_set"], 16)
                    if b >= NBUF:
                        sp.wait_ge(S["st_done"], NG * (b - NBUF + 1))
                        sp.dma_start(q_stack[SHIFT:SHIFT + 1, b % NBUF, :, :], d["row_of_zeros"].rearrange(
                            "(a h n) -> a h n", a=1, h=NH)).then_inc(S["rows_clear"], 16)
                    for kind, stack, which in ((0, q_stack, Q_PARTS), (1, k_stack, K_PARTS)):
                        for slot, j in enumerate(which):
                            sp.dma_start(stack[slot * HD:(slot + 1) * HD, b % NBUF, :, :],
                                         scratch[j, kind, :, tokens].rearrange("(h d) n -> d h n", d=HD)
                                         ).then_inc(stacked[b], 16)

                def place_shift(b):
                    sp.wait_ge(S["shift_ready"], b + 1)
                    sp.dma_start(scratch_shift[b], shift[:, b % 2, :]).then_inc(shifted[b], 16)
                    sp.wait_ge(shifted[b], 16)
                    if b >= NBUF:
                        sp.wait_ge(S["rows_clear"], 16)
                    sp.dma_start(q_stack[SHIFT:SHIFT + 1, b % NBUF, :, :], scratch_shift[b:b + 1]).then_inc(shifted[b], 16)

                for b in range(NBUF):
                    stack(b)
                place_shift(0)
                for b in range(NBUF, NB):
                    stack(b)
                for b in range(1, NB):
                    place_shift(b)

            @block.tensor
            def _(pe):
                s.norm_tensor(pe)
                pe.wait_ge(S["w_in"], 5 * 16)
                pe.wait_ge(s.xnT_ready, 4)

                def project(t):
                    await_count(pe, S["crossed_r"], t - 1)
                    await_count(pe, S["v_ready"], t - 1)
                    for c in range(DC):
                        pe.matmul(bank[:, t % 2, 0:DM], core.xnT[:, c, t * P:(t + 1) * P], wq[:, c, :],
                                         start=c == 0, stop=c == DC - 1)
                    pe.matmul(bank[:, t % 2, DM:2 * DM], ctxT[:, t * P:(t + 1) * P], wkv[:, 0:DM], start=True, stop=True
                              ).then_inc(S["qk_done"], 1)
                    pe.matmul(bank[:, 2 + t % 2, 0:DM], ctxT[:, t * P:(t + 1) * P], wkv[:, DM:2 * DM], start=True, stop=True
                              ).then_inc(S["values_done"], 1)

                def turn(t):
                    pe.wait_ge(S["roped"], t + 1)
                    await_count(pe, S["rest_ready"], t - 1)
                    for k in range(4):
                        last = pe.transpose(bank[:, 4 + t % 2, k * P:(k + 1) * P], straight[:, t % 2, k * P:(k + 1) * P],
                                            core.ident[:, :])
                    last.then_inc(S["turned32"], 1)

                project(0)
                for t in range(NT):
                    if t + 1 < NT:
                        project(t + 1)
                    turn(t)
                pe.wait_ge(S["rest_ready"], NT)
                pe.wait_ge(S["v_ready"], NT)

                def find(b, g, first_bank=0):
                    await_count(pe, S["top_done"], NG * b + g - (b == 0))
                    for k in range(2):
                        for q in range(2):
                            last = pe.matmul(bank[:, first_bank + k, q * SEQ:(q + 1) * SEQ],
                                             q_stack[:, b % NBUF, 2 * g + k, q * P:(q + 1) * P],
                                             k_stack[:, b % NBUF, 2 * g + k, :], start=True, stop=True)
                    last.then_inc(S["s_done"], 1)

                def turn_tops(b):
                    pe.wait_ge(S["top_done"], NG * (b + 1))
                    for q in range(2):
                        last = pe.transpose(bank[0:NH, 0, q * P:(q + 1) * P], tops[:, b % 2, q, :], core.ident[:, :])
                    last.then_inc(S["top_turned"], 1)

                def scores(b, g):
                    await_count(pe, S["exp_done"], NG * b + g - 1)
                    for j in range(2):
                        for kt in range(2):
                            last = pe.matmul(bank[:, 2 + 2 * (g % 2) + j, kt * SEQ:(kt + 1) * SEQ],
                                             k_stack[:, b % NBUF, 2 * g + j, kt * P:(kt + 1) * P],
                                             q_stack[:, b % NBUF, 2 * g + j, :], start=True, stop=True)
                    last.then_inc(S["st_done"], 1)

                def weigh(b, g):
                    u = g // 2
                    pe.wait_ge(S["exp_done"], NG * b + g + 1)
                    if g % 2 == 0:
                        await_count(pe, S["attn_ready"], NQ * b + u - 1)
                    for j in range(2):
                        row = 32 * ((2 * g + j) % QUAD)
                        for kt in range(2):
                            last = pe.matmul(bank[row:row + VW, 6 + u % 2, 0:SEQ], values[:, 2 * b + kt, 2 * g + j, :],
                                             prob[:, g % 2, 2 * j + kt, :], start=kt == 0, stop=kt == 1)
                    last.then_inc(S["av_done"], 1)

                def turn_quad(b, u):
                    pe.wait_ge(S["outT_ready"], NQ * b + u + 1)
                    for q in range(2):
                        last = pe.transpose(bank[:, 6 + u % 2, SEQ + q * P:SEQ + (q + 1) * P],
                                            outT[:, u % 2, q * P:(q + 1) * P], core.ident[:, :])
                    last.then_inc(S["quad_turned"], 1)

                pe.wait_ge(stacked[0], 12 * 16)
                pe.wait_ge(S["row_set"], NBUF * 16)
                for g in range(NG):
                    find(0, g, 2 * (g % 2))
                turn_tops(0)
                pe.wait_ge(S["banks_clear"], 1)
                for b in range(NB):
                    ahead = b + 1 < NB
                    if ahead:
                        pe.wait_ge(stacked[b + 1], 12 * 16)
                        if b + 1 >= NBUF:
                            pe.wait_ge(S["rows_clear"], 16)
                        pe.wait_ge(S["shift_ready"], b + 1)
                    pe.wait_ge(shifted[b], 2 * 16)
                    scores(b, 0)
                    scores(b, 1)
                    for g in range(NG):
                        if ahead:
                            find(b + 1, g)
                        if g >= 2 and g % 2 == 0:
                            turn_quad(b, g // 2 - 1)
                        weigh(b, g)
                        if g + 2 < NG:
                            scores(b, g + 2)
                    if ahead:
                        turn_tops(b + 1)
                    turn_quad(b, NQ - 1)
                for t in range(NT):
                    pe.wait_ge(S["attn_ready"], NQ * (t // 2 + 1))
                    await_count(pe, S["attnT_ready"], t - 1)
                    for c in range(DC):
                        last = pe.transpose(bank[:, t % 2, c * P:(c + 1) * P], attn[:, t, c * P:(c + 1) * P], core.ident[:, :])
                    last.then_inc(S["attn_turned"], 1)
                    pe.wait_ge(S["attnT_ready"], t + 1)
                    await_count(pe, S["added"], t - 1)
                    for c in range(DC):
                        pe.matmul(bank[:, 2 + t % 2, 0:DM], attnT[:, t % 2, c, :], wout[:, c, :], start=c == 0, stop=False)
                    pe.matmul(bank[:, 2 + t % 2, 0:DM], core.ones[0:1, :], bout[:, :], start=False, stop=True
                              ).then_inc(S["out_done"], 1)

            @block.scalar
            def _(act):
                s.norm_scalar(act)
                act.wait_ge(S["step"], ANGLE_STEPS)
                act.activation(trig[:, :, :, :], angle[:, :, :, :], ACT.Sin).then_inc(S["trig_done"], 1)

                def bring(t):
                    act.wait_ge(S["turned32"], t + 1)
                    b, i = t // 2, t % 2
                    if b >= 2:
                        act.wait_ge(spilled[b - 2], 3 * 16)
                    act.copy(part(0, b)[:, :, i, :], bank[:, 4 + t % 2, :].rearrange("p (k n) -> p k n", k=4)
                             ).then_inc(S["hi_ready"], 1)

                def middle(t):
                    act.wait_ge(S["rest_ready"], t + 1)
                    act.copy(part(1, t // 2)[:, :, t % 2, :], rest[:, t % 2, :, :]).then_inc(S["mid_ready"], 1)

                zeros = outT[:, 0, 0:1].to_broadcast([P, NH * SEQ // 2])
                act.wait_ge(S["zero_set"], 1)
                for n in range(NBUF):
                    act.copy(k_stack[:, n, :, :].rearrange("p h n -> p (h n)").bitcast(F32), zeros).then_inc(S["k_zero"], 1)
                act.wait_ge(S["ones_set"], 1)
                for t in range(NT):
                    act.wait_ge(S["values_done"], t + 1)
                    act.copy(values[:, t, :, 0:HD], bank[:, 2 + t % 2, 0:DM].rearrange("p (h d) -> p h d", d=HD)
                             ).then_inc(S["v_ready"], 1)
                    if t >= 1:
                        bring(t - 1)
                    if t >= 2:
                        middle(t - 2)
                bring(NT - 1)
                middle(NT - 2)
                middle(NT - 1)

                def negate(b):
                    act.wait_ge(S["top_turned"], b + 1)
                    if b >= 2:
                        act.wait_ge(shifted[b - 2], 2 * 16)
                    act.activation(shift[:, b % 2, :], bank[0:NH, 0, 0:SEQ], ACT.Copy, scale=-1.0
                                   ).then_inc(S["shift_ready"], 1)

                def exps(b, i, k):
                    n = 4 * i + (NG * b + k)
                    act.wait_ge(S["st_done"], n + 1)
                    await_count(act, S["av_done"], n - 1)
                    act.activation(prob[:, k % 2, :, :], bank[:, 2 + 2 * (k % 2):4 + 2 * (k % 2), :].rearrange(
                        "p j (t n) -> p (j t) n", t=2), ACT.Exp, scale=SCALE).then_inc(S["exp_done"], 1)

                def bring_quad(b, i, k):
                    n = 2 * i + (NQ * b + k)
                    act.wait_ge(S["av_done"], 2 * n + 2)
                    await_count(act, S["quad_turned"], n - 1)
                    act.copy(outT[:, k % 2, :], bank[:, 6 + k % 2, 0:SEQ]).then_inc(S["outT_ready"], 1)

                def four_pairs(b, i, first=False):
                    exps(b, i, 0)
                    if not first:
                        bring_quad(b, i, -1)
                    exps(b, i, 1)
                    exps(b, i, 2)
                    bring_quad(b, i, 0)
                    exps(b, i, 3)

                negate(0)
                for b in range(NB):
                    four_pairs(b, 0, True)
                    with act.Fori(1, NG // 4) as i:
                        four_pairs(b, i)
                    bring_quad(b, NQ // 2, -1)
                    if b + 1 < NB:
                        negate(b + 1)
                for t in range(NT):
                    act.wait_ge(S["attn_turned"], t + 1)
                    if t >= 2:
                        act.wait_ge(S["out_done"], t - 1)
                    act.copy(attnT[:, t % 2, :, :], bank[:, t % 2, 0:DM].rearrange("p (c n) -> p c n", c=DC)
                             ).then_inc(S["attnT_ready"], 1)

            @block.gpsimd
            def _(pool):
                pool.memset(values[:, :, :, HD:VW], 1.0).then_inc(S["ones_set"], 1)
                for n in range(NBUF):
                    pool.memset(q_stack[:, n, :, :].bitcast(mybir.dt.uint32), 0).then_inc(S["q_zero"], 1)

                def split(t):
                    b, i = t // 2, t % 2
                    pool.wait_ge(S["mid_ready"], t + 1)
                    pool.tensor_tensor(part(2, b)[:, :, i, :], rest[:, i, :, :], part(1, b)[:, :, i, :], ALU.subtract
                                       ).then_inc(S["lo_ready"], 1)

                for t in range(NT):
                    pool.wait_ge(S["crossed_r"], t + 1)
                    pool.tensor_tensor(straight[:, t % 2, :], straight[:, t % 2, :], crossed[:, t % 2, :], ALU.add
                                       ).then_inc(S["roped"], 1)
                    if t >= 1:
                        split(t - 1)
                split(NT - 1)

            @block.vector
            def _(dve):
                steps = [0]

                def chain(ins):
                    steps[0] += 1
                    ins.then_inc(S["step"], 1)
                    dve.wait_ge(S["step"], steps[0])

                dve.memset(outT[:, 0, 0:1], 0.0).then_inc(S["zero_set"], 1)
                dve.memset(bank[:, 6:8, 0:SEQ], 0.0).then_inc(S["banks_clear"], 1)
                s.norm_vector(dve)
                dve.wait_ge(S["pos_in"], 16)
                sines = angle[:, :, 0, :].rearrange("p t (k f) -> p t k f", f=2)
                for f in range(2):
                    ins = dve.tensor_scalar(sines[:, :, :, f], pos[:, :, :], FREQS[f], None, ALU.mult)
                chain(ins)
                chain(dve.tensor_scalar(angle[:, :, 1, :], angle[:, :, 0, :], float(np.pi) / 2, None, ALU.add))
                chain(dve.tensor_scalar(turns[:, :, :, :], angle[:, :, :, :], 0.5 / float(np.pi), ROUND, ALU.mult, ALU.add))
                chain(dve.tensor_scalar(turns[:, :, :, :], turns[:, :, :, :], ROUND, None, ALU.subtract))
                for c in (TURN_HI, TURN_LO):
                    chain(dve.scalar_tensor_tensor(angle[:, :, :, :], turns[:, :, :, :], -c, angle[:, :, :, :],
                                                   ALU.mult, ALU.add))
                chain(dve.tensor_scalar(angle[:, :, :, :], angle[:, :, :, :], PI, -PI, ALU.min, ALU.max))
                dve.wait_ge(S["trig_done"], 1)
                pairs = lambda a: a.rearrange("p t (k two) -> p t k two", two=2)
                for e in range(2):
                    dve.tensor_copy(pairs(cos8[:, :, :])[:, :, :, e], trig[:, :, 1, :])
                    ins = dve.tensor_scalar(pairs(sin8[:, :, :])[:, :, :, e], trig[:, :, 0, :], (-1.0, 1.0)[e], None, ALU.mult)
                chain(ins)

                def rotate(t):
                    await_count(dve, S["turned32"], t - 1)
                    await_count(dve, S["roped"], t - 1)
                    dve.wait_ge(S["qk_done"], t + 1)
                    for k in range(2):
                        heads = lambda a: a.rearrange("p (h n) -> p h n", n=HD)
                        src = bank[:, t % 2, k * DM:(k + 1) * DM]
                        wide = lambda a: a.unsqueeze(1).to_broadcast([P, NH, a.shape[-1]])
                        dve.tensor_tensor(heads(straight[:, t % 2, k * DM:(k + 1) * DM]), heads(src),
                                          wide(cos8[:, t, :]), ALU.mult)
                        for e in range(2):
                            at = lambda a, e: a.rearrange("p (h n two) -> p h n two", two=2, n=HD // 2)[:, :, :, e]
                            last = dve.tensor_tensor(at(crossed[:, t % 2, k * DM:(k + 1) * DM], e), at(src, 1 - e),
                                                     wide(sin8[:, t, :].rearrange("p (n two) -> p n two", two=2)[:, :, e]),
                                                     ALU.mult)
                    last.then_inc(S["crossed_r"], 1)

                def remainder(t):
                    dve.wait_ge(S["hi_ready"], t + 1)
                    await_count(dve, S["lo_ready"], t - 1)
                    dve.tensor_tensor(rest[:, t % 2, :, :], bank[:, 4 + t % 2, :].rearrange("p (k n) -> p k n", k=4),
                                      part(0, t // 2)[:, :, t % 2, :], ALU.subtract).then_inc(S["rest_ready"], 1)

                for t in range(NT):
                    rotate(t)
                    if t >= 1:
                        remainder(t - 1)
                remainder(NT - 1)

                def top(b, g, first_bank=0):
                    n = NG * b + g
                    dve.wait_ge(S["s_done"], n + 1)
                    dve.tensor_reduce(tops[:, b % 2, :, bass.ds(2 * g, 2)].rearrange("p q h -> p h q"),
                                      bank[:, first_bank:first_bank + 2, :].rearrange("p h (q n) -> p h q n", q=2), AX.X, ALU.max
                                      ).then_inc(S["top_done"], 1)

                def normalise(b, i, k):
                    n = 2 * i + (NQ * b + k)
                    dve.wait_ge(S["quad_turned"], n + 1)
                    heads = bank[:, 6 + k, SEQ:2 * SEQ].rearrange("p (q h n) -> p q h n", q=2, n=32)
                    dve.reciprocal(inverse[:, k, :, :], heads[:, :, :, HD]).then_inc(S["inv_done"], 1)
                    dve.wait_ge(S["inv_done"], n + 1)
                    dve.tensor_tensor(attn[:, 2 * b:2 * b + 2, bass.ds((2 * i + k) * 32, 32)].rearrange(
                        "p q (h n) -> p q h n", n=HD), heads[:, :, :, 0:HD],
                        inverse[:, k, :, :].unsqueeze(3).to_broadcast([P, 2, QUAD, HD]), ALU.mult
                                      ).then_inc(S["attn_ready"], 1)

                with dve.Fori(0, NG // 2) as i:
                    for k in range(2):
                        top(0, 2 * i + k, 2 * k)
                for b in range(NB):
                    ahead = b + 1 < NB
                    if ahead and b >= 1:
                        dve.wait_ge(S["top_turned"], b)
                    with dve.Fori(0, NG // 4) as i:
                        for k in range(2):
                            if ahead:
                                top(b + 1, 4 * i + 2 * k)
                                top(b + 1, 4 * i + 2 * k + 1)
                            if k == 1:
                                normalise(b, i, 0)
                        normalise(b, i, 1)
                for t in range(NT):
                    dve.wait_ge(S["out_done"], t + 1)
                    dve.scalar_tensor_tensor(core.X[:, t, :], bank[:, 2 + t % 2, 0:DM], gate, core.X[:, t, :],
                                             ALU.mult, ALU.add).then_inc(S["added"], 1)


def stage_moe(core):
    nc, d = core.nc, core.dram
    NE, FF = 8, 512
    JC = FF // P
    with core.stage("moe") as s:
        wR, rank8 = s.sb("wR", [P, DC, NE]), s.sb("rank8", [P, NE])
        lg, e8, rest, rank, hot, hot2, coef = (s.sb(n, [P, NT, NE]) for n in (
            "lg", "e8", "rest", "rank", "hot", "hot2", "coef"))
        m1, emax, esec, top, total = (s.sb(n, [P, NT]) for n in ("m1", "emax", "esec", "top", "total"))
        wup = s.sb("wup", [P, 2, DC, 2 * FF])
        wdn = s.sb("wdn", [P, 2, JC, DM])
        silu = s.sb("silu", [P, 2, HALF])
        act_f = s.sb("act_f", [P, 2, JC, HALF])
        acc = s.sb("acc", [P, NT, DM])
        loaded, logits, shifted, exps, chained = (s.sem(n) for n in ("loaded", "logits", "shifted", "exps", "chained"))
        up_in = [s.sem(f"up_in{k}") for k in range(2)]
        down_in = [s.sem(f"down_in{k}") for k in range(2)]
        gate_up, silu_done, mixed, down_done, added = (s.sem(n) for n in (
            "gate_up", "silu_done", "mixed", "down_done", "added"))
        bank = core.bank
        lgp = bank[:, 4, 0:NT * NE].rearrange("p (t e) -> p t e", e=NE)
        gate = core.gates[:, 6:7]
        STEPS = 2 * JC
        NBK = NT // 2

        with nc.Block() as block:
            @block.sync
            def _(sp):
                sp.dma_start(wR[:, :, :], d["l2_gate"].rearrange("(c p) e -> p c e", p=P)).then_inc(loaded, 16)
                sp.dma_start(rank8[:, :], d["rank8"]).then_inc(loaded, 16)

                def load(e, k):
                    sp.dma_start(wup[:, k, :, :], d["l2_up"][bass.ds(e, 1)].rearrange("e (c p) f -> p (e c) f", p=P)
                                 ).then_inc(up_in[k], 16)
                    sp.dma_start(wdn[:, k, :, :], d["l2_down"][bass.ds(e, 1)].rearrange("e (c p) f -> p (e c) f", p=P)
                                 ).then_inc(down_in[k], 16)
                for k in range(2):
                    load(k, k)
                with sp.Fori(1, NE // 2) as i:
                    for k in range(2):
                        sp.wait_ge(gate_up, 2 * STEPS * i + STEPS * (k - 1))
                        sp.wait_ge(down_done, NT * i + NBK * (k - 1))
                        load(2 * i + k, k)

            @block.tensor
            def _(pe):
                s.norm_tensor(pe)
                pe.wait_ge(loaded, 2 * 16)
                pe.wait_ge(s.xnT_ready, 4)
                for t in range(NT):
                    for c in range(DC):
                        last = pe.matmul(lgp[:, t, :], core.xnT[:, c, t * P:(t + 1) * P], wR[:, c, :],
                                         start=c == 0, stop=c == DC - 1)
                last.then_inc(logits, 1)
                pe.wait_ge(shifted, 1)

                def gate_and_up(e, k, n, first):
                    h, j = n // JC, n % JC
                    if not (first and n < 2):
                        pe.wait_ge(mixed, e * STEPS + (n - 1))
                    for m in range(2):
                        for c in range(DC):
                            last = pe.matmul(bank[:, 4 + 2 * (n % 2) + m, :],
                                             wup[:, k, c, m * FF + j * P:m * FF + (j + 1) * P],
                                             core.xnT[:, c, h * HALF:(h + 1) * HALF], start=c == 0, stop=c == DC - 1)
                    last.then_inc(gate_up, 1)

                def down(e, k, h, first):
                    pe.wait_ge(mixed, e * STEPS + JC * (h + 1))
                    if not first:
                        pe.wait_ge(added, (e - 1) * NT + 4 * (h + 1))
                    for t in range(4 * h, 4 * h + 4):
                        for j in range(JC):
                            last = pe.matmul(bank[:, t // 2, (t % 2) * DM:(t % 2 + 1) * DM],
                                             act_f[:, h, j, (t % 4) * P:(t % 4 + 1) * P], wdn[:, k, j, :],
                                             start=j == 0, stop=j == JC - 1)
                        if t % 2 == 1:
                            last.then_inc(down_done, 1)

                def expert(i, k, first):
                    e = 2 * i + k
                    pe.wait_ge(up_in[k], 16 * i + 16)
                    pe.wait_ge(down_in[k], 16 * i + 16)
                    for n in range(JC + 2):
                        gate_and_up(e, k, n, first and k == 0)
                    down(e, k, 0, first and k == 0)
                    for n in range(JC + 2, STEPS):
                        gate_and_up(e, k, n, False)
                    down(e, k, 1, first and k == 0)

                for k in range(2):
                    expert(0, k, True)
                with pe.Fori(1, NE // 2) as i:
                    for k in range(2):
                        expert(i, k, False)

            @block.scalar
            def _(act):
                s.norm_scalar(act)
                act.wait_ge(shifted, 1)
                act.activation(e8[:, :, :], lg[:, :, :], ACT.Exp).then_inc(exps, 1)

                def silu_of(e, n, first):
                    act.wait_ge(gate_up, e * STEPS + (n + 1))
                    if not (first and n < 2):
                        act.wait_ge(mixed, e * STEPS + (n - 1))
                    act.activation(silu[:, n % 2, :], bank[:, 4 + 2 * (n % 2), :], ACT.Silu).then_inc(silu_done, 1)

                for n in range(STEPS):
                    silu_of(0, n, True)
                with act.Fori(1, NE) as e:
                    for n in range(STEPS):
                        silu_of(e, n, False)

            @block.vector
            def _(dve):
                links = [0]

                def chain(ins):
                    links[0] += 1
                    ins.then_inc(chained, 1)
                    dve.wait_ge(chained, links[0])

                s.norm_vector(dve)
                wide = lambda a: a.unsqueeze(2).to_broadcast([P, NT, NE])
                ranks = rank8[:, :].unsqueeze(1).to_broadcast([P, NT, NE])
                dve.wait_ge(loaded, 2 * 16)
                dve.wait_ge(logits, 1)
                chain(dve.tensor_copy(lg[:, :, :], lgp))
                chain(dve.tensor_reduce(m1[:, :], lg[:, :, :], AX.X, ALU.max))
                dve.tensor_tensor(lg[:, :, :], lg[:, :, :], wide(m1[:, :]), ALU.subtract).then_inc(shifted, 1)
                dve.wait_ge(exps, 1)
                chain(dve.tensor_reduce(emax[:, :], e8[:, :, :], AX.X, ALU.max))
                one_hot_max(dve, s, chain, e8[:, :, :], emax[:, :], ranks, rank[:, :, :], top[:, :], hot[:, :, :])
                chain(dve.scalar_tensor_tensor(rest[:, :, :], hot[:, :, :], -2.0, e8[:, :, :], ALU.mult, ALU.add))
                chain(dve.tensor_reduce(esec[:, :], rest[:, :, :], AX.X, ALU.max))
                one_hot_max(dve, s, chain, rest[:, :, :], esec[:, :], ranks, rank[:, :, :], top[:, :], hot2[:, :, :])
                chain(dve.tensor_tensor(total[:, :], emax[:, :], esec[:, :], ALU.add))
                chain(dve.reciprocal(total[:, :], total[:, :]))
                chain(dve.tensor_tensor(hot[:, :, :], hot[:, :, :], hot2[:, :, :], ALU.add))
                chain(dve.tensor_tensor(hot[:, :, :], hot[:, :, :], e8[:, :, :], ALU.mult))
                chain(dve.tensor_tensor(coef[:, :, :], hot[:, :, :], wide(total[:, :]), ALU.mult))
                chain(dve.memset(acc[:, :, :], 0.0))

                def mix(e, n, first):
                    h, j = n // JC, n % JC
                    dve.wait_ge(silu_done, e * STEPS + (n + 1))
                    if not first and n % JC == 0:
                        dve.wait_ge(down_done, e * NBK + (2 * (h + 1) - NBK))
                    dve.tensor_tensor(act_f[:, h, j, :], bank[:, 5 + 2 * (n % 2), :], silu[:, n % 2, :],
                                      ALU.mult).then_inc(mixed, 1)

                def add(e, t, first):
                    dve.wait_ge(down_done, e * NBK + (t // 2 + 1))
                    if not first:
                        dve.wait_ge(added, e * NT + (t + 1 - NT))
                    dve.scalar_tensor_tensor(acc[:, t, :], bank[:, t // 2, (t % 2) * DM:(t % 2 + 1) * DM],
                                             coef[:, t, bass.ds(e, 1)], acc[:, t, :], ALU.mult, ALU.add).then_inc(added, 1)

                def expert(e, first):
                    for n in range(STEPS):
                        mix(e, n, first)
                    for t in range(NT):
                        add(e, t, first)

                expert(0, True)
                with dve.Fori(1, NE) as e:
                    expert(e, False)
                dve.wait_ge(added, NE * NT)
                for t in range(NT):
                    dve.scalar_tensor_tensor(core.X[:, t, :], acc[:, t, :], gate, core.X[:, t, :], ALU.mult, ALU.add)


def stage_smooth_quant(core):
    nc, d = core.nc, core.dram
    EPS, QMAX = 1e-6, 127.0
    CHUNKS = (DC, 1)
    with core.stage("sq") as s:
        wide = lambda r: CHUNKS[r] * P
        w_nat = [s.sb("w_nat", [P, NT, DM]), s.sb("ctx_nat", [P, NT, CTX])]
        w_turn = [s.sb("w_turn", [P, DC, NTOK]), s.sb("ctx_turn", [P, 1, NTOK])]
        a_nat = s.sb("a_nat", [P, NT, CTX])
        x_nat = [core.xn, a_nat]
        amax_x = [s.sb(f"amax_x{r}", [P, CHUNKS[r] * NB]) for r in range(2)]
        amax_w = [s.sb(f"amax_w{r}", [P, CHUNKS[r] * NB]) for r in range(2)]
        smooth = [s.sb(f"smooth{r}", [P, CHUNKS[r] * NB]) for r in range(2)]
        inverse = [s.sb(f"inverse{r}", [P, CHUNKS[r] * NB]) for r in range(2)]
        diag = s.sb("diag", [P, NT, P])
        diag_inv = s.sb("diag_inv", [P, NT, P])
        inverse_row = [s.sb(f"inverse_row{r}", [P, NB, wide(r)]) for r in range(2)]
        x_mult = [s.sb(f"x_mult{r}", [P, NT]) for r in range(2)]
        w_mult = [s.sb(f"w_mult{r}", [P, NT]) for r in range(2)]
        smooth_row = [s.sb(f"smooth_row{r}", [P, NB, wide(r)]) for r in range(2)]
        x_scale = [s.sb(f"x_scale{r}", [P, NT]) for r in range(2)]
        w_scale = [s.sb(f"w_scale{r}", [P, NT]) for r in range(2)]
        w_scale_row = [s.sb(f"w_scale_row{r}", [P, NTOK]) for r in range(2)]
        xq = [s.sb(f"xq{r}", [P, NT, wide(r)], BF16) for r in range(2)]
        wq = [s.sb(f"wq{r}", [P, NT, wide(r)], BF16) for r in range(2)]
        xqT = [s.sb(f"xqT{r}", [P, CHUNKS[r], NTOK], BF16) for r in range(2)]
        wqT = [s.sb(f"wqT{r}", [P, CHUNKS[r], NTOK], BF16) for r in range(2)]
        hidden = s.sb("hidden", [P, NT, DM])
        silu = s.sb("silu", [P, NT, CTX])
        scaled = s.sb("scaled", [P, 2, DM])
        w_in, c_in, step = s.sem("w_in"), s.sem("c_in"), s.sem("step")
        both = lambda n: [s.sem(f"{n}{r}") for r in range(2)]
        ratio, root, diag_s, row_s, rowcopy_s, diag_w, row_w, rowcopy_w = (both(n) for n in (
            "ratio", "root", "diag_s", "row_s", "rowcopy_s", "diag_w", "row_w", "rowcopy_w"))
        x_int, w_int, x_turned, w_turned, x_back, w_back = (both(n) for n in (
            "x_int", "w_int", "x_turned", "w_turned", "x_back", "w_back"))
        product, used = both("product"), both("used")
        silu_done, a_ready, a_turned, times = (s.sem(n) for n in (
            "silu_done", "a_ready", "a_turned", "times"))
        bank = core.bank
        gate = core.gates[:, 3:4]
        half_bf = lambda b: bank[:, b, :].bitcast(BF16)
        XB, WB = ((4, 5), (6,)), ((6, 7), (7,))

        with nc.Block() as block:
            @block.sync
            def _(sp):
                sp.dma_start(w_turn[0][:, :, :], d["l3x_wT"].rearrange("(c p) n -> p c n", p=P)).then_inc(w_in, 16)
                sp.dma_start(w_nat[0][:, :, :], d["l3x_w"].rearrange("(t p) n -> p t n", p=P)).then_inc(w_in, 16)
                sp.dma_start(w_turn[1][:, :, :], d["ctxT"].rearrange("(c p) n -> p c n", p=P)).then_inc(c_in, 16)
                sp.dma_start(w_nat[1][:, :, :], d["ctx"].rearrange("(t p) n -> p t n", p=P)).then_inc(c_in, 16)

            @block.tensor
            def _(pe):
                s.norm_tensor(pe)
                pe.wait_ge(s.xnT_ready, 4)

                def quantised(r):
                    C = CHUNKS[r]
                    pe.wait_ge(diag_s[r], 1)
                    for h in range(C):
                        pe.matmul(bank[:, h, :], core.ones[:, :], diag[:, 4 * h:4 * h + 4, :], start=True, stop=True)
                        last = pe.matmul(bank[:, 2 + h, :], core.ones[:, :], diag_inv[:, 4 * h:4 * h + 4, :],
                                         start=True, stop=True)
                    last.then_inc(row_s[r], 1)
                    for ints, turned, dst, banks in ((x_int, x_turned, xq, XB), (w_int, w_turned, wq, WB)):
                        pe.wait_ge(ints[r], 1)
                        for c in range(C):
                            for t in range(NT):
                                last = pe.transpose(half_bf(banks[r][c])[:, t * P:(t + 1) * P],
                                                    dst[r][:, t, c * P:(c + 1) * P], core.identh[:, :])
                        last.then_inc(turned[r], 1)
                    pe.wait_ge(diag_w[r], 1)
                    pe.wait_ge(rowcopy_s[r], 2)
                    for h in range(2):
                        last = pe.matmul(bank[:, 2 + h, :], core.ones[:, :], diag[:, 4 * h:4 * h + 4, :], start=True, stop=True)
                    last.then_inc(row_w[r], 1)
                    pe.wait_ge(x_back[r], 1)
                    pe.wait_ge(w_back[r], 1)
                    for t in range(NT):
                        b = t // 2
                        if t >= 2:
                            pe.wait_ge(used[r], t - 1)
                        for c in range(C):
                            last = pe.matmul(bank[:, t % 2, 0:DM], xqT[r][:, c, t * P:(t + 1) * P],
                                             wqT[r][:, c, b * DM:(b + 1) * DM], start=c == 0, stop=c == C - 1)
                        last.then_inc(product[r], 1)

                quantised(0)
                pe.wait_ge(a_ready, 1)
                for t in range(NT):
                    last = pe.transpose(bank[:, 4 + t // 4, (t % 4) * P:(t % 4 + 1) * P], a_nat[:, t, :], core.ident[:, :])
                last.then_inc(a_turned, 1)
                quantised(1)

            @block.scalar
            def _(act):
                s.norm_scalar(act)

                def quantised(r):
                    C = CHUNKS[r]
                    act.wait_ge(ratio[r], 1)
                    act.activation(smooth[r][:, :], amax_x[r][:, :], ACT.Sqrt).then_inc(root[r], 1)
                    act.wait_ge(row_s[r], 1)
                    act.copy(smooth_row[r][:, :, :].rearrange("p b n -> p (b n)").rearrange("p (h n) -> p h n", h=C),
                             bank[:, 0:C, :]).then_inc(rowcopy_s[r], 1)
                    act.copy(inverse_row[r][:, :, :].rearrange("p b n -> p (b n)").rearrange("p (h n) -> p h n", h=C),
                             bank[:, 2:2 + C, :]).then_inc(rowcopy_s[r], 1)
                    act.wait_ge(x_turned[r], 1)
                    act.copy(xqT[r][:, :, :], half_bf_banks(XB[r])).then_inc(x_back[r], 1)
                    act.wait_ge(w_turned[r], 1)
                    act.copy(wqT[r][:, :, :], half_bf_banks(WB[r])).then_inc(w_back[r], 1)
                    act.wait_ge(row_w[r], 1)
                    act.copy(w_scale_row[r][:, :].rearrange("p (h n) -> p h n", h=2), bank[:, 2:4, :]).then_inc(rowcopy_w[r], 1)

                half_bf_banks = lambda bs: bank[:, bs[0]:bs[-1] + 1, :].bitcast(BF16)
                quantised(0)
                act.wait_ge(used[0], NT)
                act.activation(silu[:, :, :], hidden[:, :, 0:CTX], ACT.Silu).then_inc(silu_done, 1)
                quantised(1)

            @block.vector
            def _(dve):
                steps = [0]

                def chain(ins):
                    steps[0] += 1
                    ins.then_inc(step, 1)
                    dve.wait_ge(step, steps[0])

                def diagonals(dst, n, column):
                    for k in range(n):
                        last = dve.tensor_scalar(dst[:, k, :], core.ident[:, :], column(k), None, ALU.mult)
                    return last

                def quantised(r, turned_x):
                    C = CHUNKS[r]
                    chain(dve.tensor_reduce(amax_x[r][:, :], turned_x, AX.X, ALU.max, apply_absolute_value=True))
                    chain(dve.tensor_reduce(amax_w[r][:, :], w_turn[r][:, :, :].rearrange("p c (b n) -> p (c b) n", b=NB),
                                            AX.X, ALU.max, apply_absolute_value=True))
                    chain(dve.tensor_scalar(amax_w[r][:, :], amax_w[r][:, :], EPS, None, ALU.max))
                    chain(dve.tensor_scalar(amax_x[r][:, :], amax_x[r][:, :], EPS, None, ALU.max))
                    chain(dve.reciprocal(amax_w[r][:, :], amax_w[r][:, :]))
                    dve.tensor_tensor(amax_x[r][:, :], amax_x[r][:, :], amax_w[r][:, :], ALU.mult).then_inc(ratio[r], 1)
                    dve.wait_ge(root[r], 1)
                    chain(dve.tensor_scalar(smooth[r][:, :], smooth[r][:, :], EPS, None, ALU.max))
                    chain(dve.reciprocal(inverse[r][:, :], smooth[r][:, :]))
                    at = lambda k: slice((k % C) * NB + k // C, (k % C) * NB + k // C + 1)
                    diagonals(diag, NB * C, lambda k: smooth[r][:, at(k)])
                    diagonals(diag_inv, NB * C, lambda k: inverse[r][:, at(k)]).then_inc(diag_s[r], 1)
                    dve.wait_ge(rowcopy_s[r], 2)
                    shape = lambda a: a.rearrange("p (b i) n -> p b i n", b=NB)
                    for nat, ints, scale, mult, row, done in (
                            (x_nat[r], xq[r], x_scale[r], x_mult[r], inverse_row[r], x_int[r]),
                            (w_nat[r], wq[r], w_scale[r], w_mult[r], smooth_row[r], w_int[r])):
                        rows = row[:, :, :].unsqueeze(2).to_broadcast([P, NB, 2, wide(r)])
                        chain(dve.tensor_tensor(shape(nat[:, :, :]), shape(nat[:, :, :]), rows, ALU.mult))
                        chain(dve.tensor_reduce(scale[:, :], nat[:, :, :], AX.X, ALU.max, apply_absolute_value=True))
                        chain(dve.tensor_scalar(scale[:, :], scale[:, :], EPS, 1.0 / QMAX, ALU.max, ALU.mult))
                        chain(dve.reciprocal(mult[:, :], scale[:, :]))
                        for t in range(NT):
                            last = dve.tensor_scalar(nat[:, t, :], nat[:, t, :], mult[:, t:t + 1], ROUND, ALU.mult, ALU.add)
                        chain(last)
                        dve.tensor_scalar(ints[:, :, :], nat[:, :, :], ROUND, QMAX, ALU.subtract, ALU.min).then_inc(done, 1)
                    dve.wait_ge(row_s[r], 1)
                    diagonals(diag, NT, lambda k: w_scale[r][:, k:k + 1]).then_inc(diag_w[r], 1)
                    dve.wait_ge(rowcopy_w[r], 1)

                def rescale(r, t, dst):
                    dve.wait_ge(product[r], t + 1)
                    b = t // 2
                    return dve.scalar_tensor_tensor(dst, bank[:, t % 2, 0:DM], x_scale[r][:, t:t + 1],
                                                    w_scale_row[r][:, b * DM:(b + 1) * DM], ALU.mult, ALU.mult)

                s.norm_vector(dve)
                dve.wait_ge(s.xnT_ready, 4)
                dve.wait_ge(w_in, 2 * 16)
                quantised(0, core.xnT[:, :, :].rearrange("p c (b n) -> p (c b) n", b=NB))
                for t in range(NT):
                    rescale(0, t, hidden[:, t, :]).then_inc(used[0], 1)
                dve.wait_ge(silu_done, 1)
                dve.tensor_tensor(a_nat[:, :, :], silu[:, :, :], hidden[:, :, CTX:DM], ALU.mult).then_inc(a_ready, 1)
                dve.wait_ge(a_turned, 1)
                dve.wait_ge(c_in, 2 * 16)
                quantised(1, bank[:, 4:6, :].rearrange("p h (b n) -> p (h b) n", b=2))
                for t in range(NT):
                    if t >= 2:
                        dve.wait_ge(times, t - 1)
                    rescale(1, t, scaled[:, t % 2, :]).then_inc(used[1], 1)
                    dve.wait_ge(used[1], t + 1)
                    dve.scalar_tensor_tensor(core.X[:, t, :], scaled[:, t % 2, :], gate, core.X[:, t, :],
                                             ALU.mult, ALU.add).then_inc(times, 1)


def stage_fp8_ffn(core):
    nc, d = core.nc, core.dram
    FF = 768
    JC = FF // P
    F8 = mybir.dt.float8e4
    U8 = mybir.dt.uint8
    with core.stage("fp8") as s:
        wg, wu, wd = s.sb("wg", [P, DC * FF]), s.sb("wu", [P, DC * FF]), s.sb("wd", [P, JC * DM])
        NW = DC * FF
        low8, high8 = s.sb("low8", [P, NW], F8), s.sb("high8", [P, NW], F8)
        large, doubled = s.sb("large", [P, NW], U8), s.sb("doubled", [P, NW])
        gs, us, ds = s.sb("gs", [P, JC]), s.sb("us", [P, JC]), s.sb("ds", [P, DM])
        silu, fuse = s.sb("silu", [P, 2, HALF]), s.sb("fuse", [P, JC, NTOK])
        scaled = s.sb("scaled", [P, 2, DM])
        loaded = [s.sem(f"loaded{i}") for i in range(3)]
        scales, halved, step, rounded = s.sem("scales"), s.sem("halved"), s.sem("step"), s.sem("rounded")
        gate_up, silu_done, fused, out_done, times, added = (s.sem(n) for n in (
            "gate_up", "silu_done", "fused", "out_done", "times", "added"))
        bank = core.bank
        weights = [wg, wu, wd]
        w3 = [wg[:, :].rearrange("p (c f) -> p c f", c=DC), wu[:, :].rearrange("p (c f) -> p c f", c=DC),
              wd[:, :].rearrange("p (c f) -> p c f", c=JC)]
        gate = core.gates[:, 7:8]

        with nc.Block() as block:
            @block.sync
            def _(sp):
                for i, n in enumerate(("l3_gate", "l3_up", "l3_down")):
                    sp.dma_start(w3[i], d[n].rearrange("(c p) f -> p c f", p=P)).then_inc(loaded[i], 16)
                sp.dma_start(gs[:, :], d["l3_gate_scale"]).then_inc(scales, 16)
                sp.dma_start(us[:, :], d["l3_up_scale"]).then_inc(scales, 16)
                sp.dma_start(ds[:, :], d["l3_down_scale"].partition_broadcast(P)).then_inc(scales, 16)

            @block.tensor
            def _(pe):
                s.norm_tensor(pe)
                pe.wait_ge(rounded, 2)
                for h in range(2):
                    pe.wait_ge(s.xnT_ready, 2 * (h + 1))
                    for j in range(JC):
                        n = h * JC + j
                        if n >= 2:
                            pe.wait_ge(fused, n - 1)
                        for k in range(2):
                            for c in range(DC):
                                last = pe.matmul(bank[:, 4 + 2 * (n % 2) + k, :], w3[k][:, c, j * P:(j + 1) * P],
                                                 core.xnT[:, c, h * HALF:(h + 1) * HALF], start=c == 0, stop=c == DC - 1)
                        last.then_inc(gate_up, 1)
                pe.wait_ge(rounded, 3)
                pe.wait_ge(s.xnT_ready, 4)
                for t in range(NT):
                    pe.wait_ge(fused, JC * (t // 4 + 1))
                    for j in range(JC):
                        last = pe.matmul(bank[:, t // 2, (t % 2) * DM:(t % 2 + 1) * DM], fuse[:, j, t * P:(t + 1) * P],
                                         w3[2][:, j, :], start=j == 0, stop=j == JC - 1)
                    if t % 2 == 1:
                        last.then_inc(out_done, 1)

            @block.scalar
            def _(act):
                for i in range(3):
                    act.wait_ge(loaded[i], 16)
                    if i >= 1:
                        act.wait_ge(rounded, i)
                    act.activation(high8[:, :], weights[i][:, :], ACT.Copy, scale=0.5, saturate=False).then_inc(halved, 1)
                    if i == 0:
                        s.norm_scalar(act)
                act.wait_ge(scales, 3 * 16)
                for n in range(2 * JC):
                    act.wait_ge(gate_up, n + 1)
                    if n >= 2:
                        act.wait_ge(fused, n - 1)
                    act.activation(silu[:, n % 2, :], bank[:, 4 + 2 * (n % 2), :], ACT.Silu,
                                   scale=gs[:, n % JC:n % JC + 1]).then_inc(silu_done, 1)

            @block.vector
            def _(dve):
                steps = [0]

                def chain(ins):
                    steps[0] += 1
                    ins.then_inc(step, 1)
                    dve.wait_ge(step, steps[0])

                def round_weight(i):
                    dve.wait_ge(loaded[i], 16)
                    w = weights[i][:, :]
                    if i >= 1:
                        dve.wait_ge(rounded, i)
                    dve.tensor_scalar(low8[:, :], w, 240.0, -240.0, ALU.min, ALU.max, saturate=False)
                    chain(dve.scalar_tensor_tensor(doubled[:, :], w, -1.0, w, ALU.mult, ALU.max))
                    chain(dve.tensor_scalar(large[:, :], doubled[:, :], 128.0, None, ALU.is_ge))
                    dve.wait_ge(halved, i + 1)
                    chain(dve.tensor_scalar(doubled[:, :], high8[:, :], 2.0, None, ALU.mult))
                    chain(dve.tensor_copy(w, low8[:, :]))
                    dve.copy_predicated(w, large[:, :], doubled[:, :]).then_inc(rounded, 1)

                s.norm_vector(dve)
                for i in range(3):
                    round_weight(i)
                dve.wait_ge(scales, 3 * 16)
                for n in range(2 * JC):
                    dve.wait_ge(silu_done, n + 1)
                    j, h = n % JC, n // JC
                    dve.scalar_tensor_tensor(fuse[:, j, h * HALF:(h + 1) * HALF], bank[:, 5 + 2 * (n % 2), :],
                                             us[:, j:j + 1], silu[:, n % 2, :], ALU.mult, ALU.mult).then_inc(fused, 1)
                for t in range(NT):
                    dve.wait_ge(out_done, t // 2 + 1)
                    if t >= 2:
                        dve.wait_ge(added, t - 1)
                    dve.tensor_tensor(scaled[:, t % 2, :], bank[:, t // 2, (t % 2) * DM:(t % 2 + 1) * DM], ds[:, :],
                                      ALU.mult).then_inc(times, 1)
                    dve.wait_ge(times, t + 1)
                    dve.scalar_tensor_tensor(core.X[:, t, :], scaled[:, t % 2, :], gate, core.X[:, t, :],
                                             ALU.mult, ALU.add).then_inc(added, 1)


def build(nc, dram):
    with ExitStack() as ctx:
        core = Core(nc, ctx, dram)
        stage_setup(core)
        steps = (stage_ssm, stage_lora_moe, stage_attention_16, stage_bitnet,
                 stage_attention_32, stage_moe, stage_smooth_quant, stage_fp8_ffn)
        for k in STAGES:
            steps[k](core)
            if k == 3 and len(STAGES) > 6:
                core.clear_semaphores()
        stage_store(core)


def _layouts(np, i):
    flat = lambda a: a.reshape(-1, a.shape[-1])
    T = lambda a: a.T
    return {
        "x": flat(i["x"]),
        "ctx": flat(i["ctx_1024"]),
        "ctxT": T(flat(i["ctx_1024"])),
        "g_xattn": i["g_xattn"],
        "g_ffn": i["g_ffn"],
        "l0_A": T(flat(i["L0_ffn_A"])),
        "l0_B": i["L0_ffn_B"].transpose(0, 2, 1).reshape(-1, DM),
        "l0_Wr": T(i["L0_ffn_Wr"]),
        "l0_br": i["L0_ffn_br"],
        "l0x_in": T(i["L0_xattn_in_proj_w"]),
        "l0x_dt2": T(i["L0_xattn_dt_proj_w"]),
        "l0x_chan": np.concatenate([i["L0_xattn_conv_w"], i["L0_xattn_conv_b"].reshape(-1, 1),
                                    i["L0_xattn_dt_proj_b"].reshape(-1, 1), i["L0_xattn_D"].reshape(-1, 1),
                                    i["L0_xattn_A_log"], T(i["L0_xattn_x_proj_w"][8:40]),
                                    T(i["L0_xattn_x_proj_w"][0:8])], axis=1),
        "l1x_q": i["L1_xattn_Wq"].reshape(DM, 16, -1).transpose(1, 0, 2),
        "l1x_k": i["L1_xattn_Wk"].reshape(CTX, 16, -1).transpose(1, 0, 2),
        "l1x_vT": i["L1_xattn_Wv"].reshape(CTX, 16, -1).transpose(1, 2, 0),
        "l1x_o": i["L1_xattn_Wo"].reshape(16, -1, DM),
        "l1x_gains": T(np.stack([i["L1_xattn_gq"], i["L1_xattn_gk"]])),
        "l1_gate": T(i["L1_ffn_w_gate"]),
        "l1_up": T(i["L1_ffn_w_up"]),
        "l1_down": T(i["L1_ffn_w_down"]),
        "l2x_q": i["L2_xattn_Wq"],
        "l2x_kv": i["L2_xattn_Wkv"],
        "l2x_out": i["L2_xattn_Wout"],
        "l2x_bout": i["L2_xattn_bout"],
        "pos": flat(i["fside_BxSx2_0"]),
        "l2_gate": T(i["L2_ffn_gate_w"]),
        "l2_up": i["L2_ffn_w_up"].transpose(0, 2, 1),
        "l2_down": i["L2_ffn_w_down"].transpose(0, 2, 1),
        "l3x_w": flat(i["fside_BxS2xS2_0"]),
        "l3x_wT": T(flat(i["fside_BxS2xS2_0"])),
        "l3_gate": i["L3_ffn_gate_w"],
        "l3_up": i["L3_ffn_up_w"],
        "l3_down": i["L3_ffn_down_w"],
        "l3_gate_scale": T(i["L3_ffn_gate_scale"].reshape(-1, P)),
        "l3_up_scale": T(i["L3_ffn_up_scale"].reshape(-1, P)),
        "l3_down_scale": i["L3_ffn_down_scale"],
    }


def _constants(np):
    eye = np.eye(P, dtype=np.float32)
    h = np.ones((1, 1), np.float32)
    while h.shape[0] < P:
        h = np.block([[h, h], [h, -h]]).astype(np.float32)
    sel = np.zeros((96, 32, P), np.float32)
    for n in range(32):
        sel[[n, 32 + n, 64 + n], n, :] = 1.0
    return {"row_of_ones": np.ones(32 * SEQ, mybir.dt.np(BF16)), "row_of_zeros": np.zeros(32 * SEQ, mybir.dt.np(BF16)), "ident": eye, "identh": eye.astype(mybir.dt.np(BF16)), "hadamard": h,
            "rank8": np.broadcast_to(np.arange(8, 0, -1, dtype=np.float32), (P, 8)).copy(),
            "select3": sel.reshape(96, 32 * P).astype(mybir.dt.np(BF16))}


def kernel(**inputs):
    import numpy as _np
    import concourse.bacc as _bacc
    from concourse import mybir as _mybir
    from concourse.bass_utils import run_bass_kernel_spmd as _run

    nc = _bacc.Bacc("TRN2", target_bir_lowering=False, num_devices=1)
    arrays, dram = {}, {}
    for group in (_layouts(_np, {k: _np.asarray(v) for k, v in inputs.items()}), _constants(_np)):
        for name, a in group.items():
            a = _np.ascontiguousarray(a)
            arrays[f"in_{name}_dram"] = a
            dram[name] = nc.dram_tensor(f"in_{name}_dram", a.shape, _mybir.dt.from_np(a.dtype), kind="ExternalInput").ap()
    dram["out"] = nc.dram_tensor("out_0_dram", (NTOK, DM), F32, kind="ExternalOutput").ap()
    build(nc, dram)
    r = _run(nc, [arrays], core_ids=[0])
    return r.results[0]["out_0_dram"].reshape(NB, SEQ, DM)
```

```python
from contextlib import ExitStack

import numpy as np
import concourse.bass as bass
from concourse import mybir

ALU = mybir.AluOpType
ACT = mybir.ActivationFunctionType
AX = mybir.AxisListType
F32 = mybir.dt.float32
BF16 = mybir.dt.bfloat16
F16 = mybir.dt.float16

P = 128
NB, SEQ, DM = 4, 256, 256
NT = NB * SEQ // P
NTOK = NB * SEQ
DC = DM // P
CTX = 128
HALF = 512
LN_EPS = 1e-5
ROUND = 1.5 * 2.0 ** 23

STAGES = (0, 1, 2, 3, 4, 5, 6, 7)


def await_count(engine, semaphore, value):
    if isinstance(value, int) and value <= 0:
        return
    engine.wait_ge(semaphore, value)


class Core:

    def __init__(self, nc, ctx, dram):
        self.nc, self.dram = nc, dram
        sb = lambda name, shape, dt=F32: ctx.enter_context(nc.sbuf_tensor(name, shape, dt))
        self.X = sb("X", [P, NT, DM])
        self.xn = sb("xn", [P, NT, DM])
        self.xnT = sb("xnT", [P, DC, NTOK])
        self.stats = sb("stats", [P, NT, 6])
        self.meanvar = sb("meanvar", [P, NT, 2])
        self.rstd = sb("rstd", [P, NT])
        self.ident = sb("ident", [P, P])
        self.identh = sb("identh", [P, P], BF16)
        self.ones = sb("ones", [P, P])
        self.eps = sb("eps", [P, 1])
        self.gates = sb("gates", [P, 8])
        self.bank = ctx.enter_context(nc.psum_tensor("bank", [P, 8, HALF], F32))
        self.semaphores = []

    def stage(self, name):
        return Stage(self, name)

    def clear_semaphores(self):
        self.nc.all_engine_barrier()
        self.nc.clear_and_free_semaphores(self.semaphores)
        self.nc.all_engine_barrier()
        self.semaphores = []


class Stage:

    def __init__(self, core, name):
        self.core, self.nc, self.name = core, core.nc, name

    def __enter__(self):
        self.stack = ExitStack()
        self.stack.__enter__()
        self.stats_done = self.sem("stats_done")
        self.aggr_done = self.sem("aggr_done")
        self.root_done = self.sem("root_done")
        self.rstd_done = self.sem("rstd_done")
        self.xn_ready = self.sem("xn_ready")
        self.turned = self.sem("turned")
        self.xnT_ready = self.sem("xnT_ready")
        return self

    def __exit__(self, *e):
        return self.stack.__exit__(*e)

    def sb(self, name, shape, dt=F32):
        return self.stack.enter_context(self.nc.sbuf_tensor(f"{self.name}_{name}", shape, dt))

    def sem(self, name):
        self.core.semaphores.append(self.nc.alloc_semaphore(name=f"{self.name}_{name}"))
        return self.core.semaphores[-1]

    def norm_vector(self, dve):
        c = self.core
        for t in range(NT):
            dve.bn_stats(c.stats[:, t, :], c.X[:, t, :]).then_inc(self.stats_done, 1)
        for t in range(NT):
            dve.wait_ge(self.stats_done, t + 1)
            dve.bn_aggr(c.meanvar[:, t, :], c.stats[:, t, :]).then_inc(self.aggr_done, 1)
        dve.wait_ge(self.root_done, 1)
        dve.reciprocal(c.rstd[:, :], c.rstd[:, :]).then_inc(self.rstd_done, 1)
        dve.wait_ge(self.rstd_done, 1)
        for t in range(NT):
            dve.tensor_scalar(c.xn[:, t, :], c.X[:, t, :], c.meanvar[:, t, 0:1], c.rstd[:, t:t + 1],
                              ALU.subtract, ALU.mult).then_inc(self.xn_ready, 1)

    def norm_tensor(self, pe):
        c = self.core
        for t in range(NT):
            pe.wait_ge(self.xn_ready, t + 1)
            for k in range(DC):
                last = pe.transpose(c.bank[:, 2 * k + t // 4, (t % 4) * P:(t % 4 + 1) * P],
                                    c.xn[:, t, k * P:(k + 1) * P], c.ident[:, :])
            last.then_inc(self.turned, 1)

    def norm_scalar(self, act):
        c = self.core
        act.wait_ge(self.aggr_done, NT)
        act.activation(c.rstd[:, :], c.meanvar[:, :, 1], ACT.Sqrt, bias=c.eps[:, 0:1]).then_inc(self.root_done, 1)
        for h in range(2):
            act.wait_ge(self.turned, 4 * (h + 1))
            for k in range(DC):
                act.copy(c.xnT[:, k, h * HALF:(h + 1) * HALF], c.bank[:, 2 * k + h, :]).then_inc(self.xnT_ready, 1)


def stage_setup(core):
    nc, d = core.nc, core.dram
    with core.stage("setup") as s:
        loaded, ones_set, gate_done = s.sem("loaded"), s.sem("ones_set"), s.sem("gate_done")
        raw = s.sb("raw", [P, 8])
        with nc.Block() as block:
            @block.sync
            def _(sp):
                sp.dma_start(core.X[:, :, :], d["x"].rearrange("(t p) d -> p t d", p=P)).then_inc(loaded, 16)
                sp.dma_start(core.ident[:, :], d["ident"]).then_inc(loaded, 16)
                sp.dma_start(core.identh[:, :], d["identh"]).then_inc(loaded, 16)
                for j, g in enumerate(("g_xattn", "g_ffn")):
                    sp.dma_start(raw[:, 4 * j:4 * j + 4], d[g].partition_broadcast(P)).then_inc(loaded, 16)
                sp.wait_ge(loaded, 5 * 16)

            @block.vector
            def _(dve):
                dve.memset(core.ones[:, :], 1.0).then_inc(ones_set, 1)
                dve.memset(core.eps[:, :], LN_EPS).then_inc(ones_set, 1)

            @block.scalar
            def _(act):
                act.wait_ge(loaded, 5 * 16)
                act.activation(core.gates[:, :], raw[:, :], ACT.Tanh).then_inc(gate_done, 1)


def stage_store(core):
    nc, d = core.nc, core.dram
    with core.stage("store") as s:
        stored = s.sem("stored")
        with nc.Block() as block:
            @block.sync
            def _(sp):
                sp.dma_start(d["out"].rearrange("(t p) d -> p t d", p=P), core.X[:, :, :]).then_inc(stored, 16)
                sp.wait_ge(stored, 16)



def stage_ssm(core):
    nc, d = core.nc, core.dram
    NS, TAPS, DR = 16, 4, 8
    CC = 2
    PAD = TAPS - 1
    with core.stage("ssm") as s:
        w_in, ctxT = s.sb("w_in", [P, CC * P]), s.sb("ctxT", [P, NTOK])
        widths = (TAPS, 1, 1, 1, NS, 2 * NS, DR)
        chan = s.sb("chan", [P, CC, sum(widths)])
        starts = np.cumsum((0,) + widths).tolist()
        conv_w, conv_b, dt_b, skip, a_log, w_bc, w_dt1 = (chan[:, :, a:a + w] for a, w in zip(starts, widths))
        a_neg = s.sb("a_neg", [P, CC, NS])
        w_dt2 = s.sb("w_dt2", [DR, CC * P])
        select3 = s.sb("select3", [96, 2 * NS * P], BF16)
        padded = s.sb("padded", [P, CC, NB, SEQ + PAD])
        conv = s.sb("conv", [P, CC, NTOK])
        u, delta, du = (s.sb(n, [P, CC, NTOK]) for n in ("u", "delta", "du"))
        dt_lo = s.sb("dt_lo", [DR, NTOK])
        rest = s.sb("rest", [2 * NS, NTOK])
        mid = s.sb("mid", [2 * NS, NTOK], BF16)
        parts = s.sb("parts", [96, NTOK], BF16)
        b_row = s.sb("b_row", [P, 2, NTOK])
        decay = s.sb("decay", [P, 2, NB, SEQ])
        drive = s.sb("drive", [P, 2, NTOK])
        state = s.sb("state", [P, 2, NTOK])
        seen = s.sb("seen", [P, 2, NTOK])
        small, is_small = s.sb("small", [P, CC, NTOK]), s.sb("is_small", [P, CC, NTOK], mybir.dt.uint8)
        series = conv
        silu_z = s.sb("silu_z", [P, NT, DM])
        w_s, s_s = s.sem("w_s"), s.sem("s_s")
        names = ("in_done", "pad_ready", "padded_zero", "conv_done", "u_ready", "bc_done", "dt1_done", "dt1_copied",
                 "dt2_done", "pre_ready", "abs_done", "e_ready", "small_known", "delta_ready", "soft", "a_exp", "a_ready", "step", "parts_hi", "parts_mid",
                 "parts_ready", "du_ready", "b_done", "b_copied", "c_done", "decay_ready", "drive_ready", "scanned",
                 "seen_ready", "summed", "silu_z_done", "y_ready", "y_turned", "added")
        S = {n: s.sem(n) for n in names}
        bank = core.bank
        gate = core.gates[:, 0:1]
        two = lambda a: a.rearrange("p (h n) -> p h n", h=2)

        with nc.Block() as block:
            @block.sync
            def _(sp):
                for dst, n in ((ctxT, "ctxT"), (w_in, "l0x_in"), (w_dt2, "l0x_dt2")):
                    sp.dma_start(dst[:, :], d[n]).then_inc(w_s, 16)
                sp.dma_start(chan[:, :, :], d["l0x_chan"].rearrange("(c p) k -> p c k", p=P)).then_inc(w_s, 16)
                sp.dma_start(select3[:, :], d["select3"]).then_inc(s_s, 16)

            @block.tensor
            def _(pe):
                pe.wait_ge(w_s, 4 * 16)
                for k in range(CC):
                    for h in range(2):
                        last = pe.matmul(bank[:, 2 * k + h, :], w_in[:, k * P:(k + 1) * P],
                                         ctxT[:, h * HALF:(h + 1) * HALF], start=True, stop=True)
                    last.then_inc(S["in_done"], 1)
                pe.wait_ge(S["u_ready"], CC)
                for h in range(2):
                    for k in range(CC):
                        last = pe.matmul(bank[0:DR, 6 + h, :], w_dt1[:, k, :], u[:, k, h * HALF:(h + 1) * HALF],
                                         start=k == 0, stop=k == CC - 1)
                last.then_inc(S["dt1_done"], 1)
                for h in range(2):
                    for k in range(CC):
                        last = pe.matmul(bank[0:2 * NS, 4 + h, :], w_bc[:, k, :], u[:, k, h * HALF:(h + 1) * HALF],
                                         start=k == 0, stop=k == CC - 1)
                last.then_inc(S["bc_done"], 1)
                pe.wait_ge(S["dt1_copied"], 1)
                for k in range(CC):
                    for h in range(2):
                        last = pe.matmul(bank[:, 2 * k + h, :], w_dt2[:, k * P:(k + 1) * P],
                                         dt_lo[:, h * HALF:(h + 1) * HALF], start=True, stop=True)
                last.then_inc(S["dt2_done"], 1)
                pe.wait_ge(s_s, 16)
                pe.wait_ge(S["parts_ready"], 1)
                pe.wait_ge(S["pre_ready"], CC)
                pe.wait_ge(S["abs_done"], CC)

                def rows(n, j):
                    if j == 0:
                        await_count(pe, S["b_copied"], n)
                    else:
                        await_count(pe, S["seen_ready"], CC * n)
                    for h in range(2):
                        last = pe.matmul(bank[:, 2 * j + h, :], select3[:, bass.ds((n + NS * j) * P, P)],
                                         parts[:, h * HALF:(h + 1) * HALF], start=True, stop=True)
                    last.then_inc(S["c_done" if j else "b_done"], 1)

                def gather(n, k, first, last_state):
                    pe.wait_ge(S["seen_ready"], CC * n + (k + 1))
                    for h in range(2):
                        last = pe.matmul(bank[:, 4 + 2 * k + h, :], core.ident[:, :], seen[:, k, h * HALF:(h + 1) * HALF],
                                         start=first, stop=last_state, skip_group_check=True)
                    last.then_inc(S["summed"], 1)

                def state_sums(n, first=False, final=False):
                    if not final:
                        rows(n + 2, 0)
                    rows(n, 1)
                    gather(n - 1, 1, first, False)
                    gather(n, 0, False, isinstance(n, int) and n == NS - 1)

                rows(0, 0)
                rows(0, 1)
                rows(1, 0)
                rows(2, 0)
                gather(0, 0, True, False)
                state_sums(1, first=True)
                with pe.Fori(2, NS - 2) as n:
                    state_sums(n)
                state_sums(NS - 2, final=True)
                state_sums(NS - 1, final=True)
                gather(NS - 1, 1, False, True)
                for t in range(NT):
                    b, h = t // 2, t % 2
                    pe.wait_ge(S["y_ready"], CC)
                    if t >= 4:
                        pe.wait_ge(S["added"], t - 3)
                    for k in range(CC):
                        last = pe.transpose(bank[:, t % 4, k * P:(k + 1) * P],
                                            seen[:, k, b * SEQ + h * P:b * SEQ + (h + 1) * P], core.ident[:, :])
                    last.then_inc(S["y_turned"], 1)

            @block.scalar
            def _(act):
                act.wait_ge(S["padded_zero"], 1)
                for k in range(CC):
                    act.wait_ge(S["in_done"], k + 1)
                    for h in range(2):
                        last = act.copy(padded[:, k, 2 * h:2 * h + 2, PAD:PAD + SEQ],
                                        bank[:, 2 * k + h, :].rearrange("p (b n) -> p b n", b=2))
                    last.then_inc(S["pad_ready"], 1)
                for k in range(CC):
                    act.wait_ge(S["conv_done"], k + 1)
                    act.activation(u[:, k, :], conv[:, k, :], ACT.Silu, bias=conv_b[:, k, :]).then_inc(S["u_ready"], 1)
                act.wait_ge(s.aggr_done, NT)
                act.activation(core.rstd[:, :], core.meanvar[:, :, 1], ACT.Sqrt, bias=core.eps[:, 0:1]
                               ).then_inc(s.root_done, 1)
                act.wait_ge(S["dt1_done"], 1)
                act.copy(two(dt_lo[:, :]), bank[0:DR, 6:8, :]).then_inc(S["dt1_copied"], 1)
                act.wait_ge(S["bc_done"], 1)
                act.copy(two(parts[0:2 * NS, :]), bank[0:2 * NS, 4:6, :]).then_inc(S["parts_hi"], 1)
                act.wait_ge(w_s, 4 * 16)
                act.preload_act_table_set("natural_log_exp_and_others")
                act.activation(a_neg[:, :, :], a_log[:, :, :], ACT.Exp).then_inc(S["a_exp"], 1)
                act.wait_ge(S["dt2_done"], 1)
                act.wait_ge(S["pre_ready"], CC)
                for k in range(CC):
                    act.activation(two(delta[:, k, :]), bank[:, 2 * k:2 * k + 2, :], ACT.Abs, bias=dt_b[:, k, :]
                                   ).then_inc(S["abs_done"], 1)
                for k in range(CC):
                    act.wait_ge(S["abs_done"], k + 1)
                    act.activation(small[:, k, :], delta[:, k, :], ACT.Exp, scale=-1.0).then_inc(S["e_ready"], 1)
                for k in range(CC):
                    act.wait_ge(S["e_ready"], k + 1)
                    act.activation(delta[:, k, :], small[:, k, :], ACT.Ln, bias=1.0).then_inc(S["soft"], 1)
                act.wait_ge(S["delta_ready"], CC)
                act.wait_ge(S["a_ready"], 1)

                def copy_b(n, p):
                    act.wait_ge(S["b_done"], n + 1)
                    await_count(act, S["drive_ready"], CC * n - CC)
                    act.copy(two(b_row[:, p, :]), bank[:, 0:2, :]).then_inc(S["b_copied"], 1)

                def decays(n):
                    for k in range(CC):
                        await_count(act, S["scanned"], CC * n + (k - 1))
                        act.activation(decay[:, k, :, 1:SEQ], delta[:, k, :].rearrange("p (b n) -> p b n", b=NB)[:, :, 1:SEQ],
                                       ACT.Exp, scale=a_neg[:, k, bass.ds(n, 1)]).then_inc(S["decay_ready"], 1)

                copy_b(0, 0)
                copy_b(1, 1)
                for p in range(2):
                    decays(p)
                    copy_b(2 + p, p)
                with act.Fori(1, NS // 2 - 1) as i:
                    for p in range(2):
                        decays(2 * i + p)
                        copy_b(2 * i + (p + 2), p)
                decays(NS - 2)
                decays(NS - 1)
                act.wait_ge(s.xn_ready, NT)
                act.activation(silu_z[:, :, :], core.xn[:, :, :], ACT.Silu).then_inc(S["silu_z_done"], 1)

            @block.gpsimd
            def _(pool):
                pool.memset(padded[:, :, :, 0:PAD], 0.0).then_inc(S["padded_zero"], 1)
                pool.memset(decay[:, :, :, 0:1], 0.0).then_inc(S["padded_zero"], 1)
                for k in range(CC):
                    pool.wait_ge(S["delta_ready"], k + 1)
                    pool.tensor_tensor(du[:, k, :], delta[:, k, :], u[:, k, :], ALU.mult).then_inc(S["du_ready"], 1)
                pool.wait_ge(S["du_ready"], CC)

                def drives(n, p):
                    pool.wait_ge(S["b_copied"], n + 1)
                    for k in range(CC):
                        await_count(pool, S["scanned"], CC * n + (k - 1))
                        pool.tensor_tensor(drive[:, k, :], du[:, k, :], b_row[:, p, :], ALU.mult).then_inc(S["drive_ready"], 1)

                for p in range(2):
                    drives(p, p)
                with pool.Fori(1, NS // 2) as i:
                    for p in range(2):
                        drives(2 * i + p, p)

            @block.vector
            def _(dve):
                steps = [0]

                def chain(ins):
                    steps[0] += 1
                    ins.then_inc(S["step"], 1)
                    dve.wait_ge(S["step"], steps[0])

                dve.wait_ge(w_s, 4 * 16)
                dve.wait_ge(S["padded_zero"], 2)
                for k in range(CC):
                    dve.wait_ge(S["pad_ready"], k + 1)
                    out = conv[:, k, :].rearrange("p (b n) -> p b n", b=NB)
                    tap = lambda j: padded[:, k, :, j:j + SEQ]
                    chain(dve.tensor_scalar(out, tap(0), conv_w[:, k, 0:1], None, ALU.mult))
                    for j in range(1, TAPS):
                        ins = dve.scalar_tensor_tensor(out, tap(j), conv_w[:, k, j:j + 1], out, ALU.mult, ALU.add)
                        if j < TAPS - 1:
                            chain(ins)
                    ins.then_inc(S["conv_done"], 1)
                s.norm_vector(dve)
                dve.wait_ge(S["parts_hi"], 1)
                chain(dve.tensor_tensor(two(rest[:, :]), bank[0:2 * NS, 4:6, :], two(parts[0:2 * NS, :]), ALU.subtract))
                chain(dve.tensor_copy(mid[:, :], rest[:, :]))
                dve.tensor_copy(parts[2 * NS:4 * NS, :], mid[:, :])
                dve.tensor_tensor(parts[4 * NS:6 * NS, :], rest[:, :], mid[:, :], ALU.subtract).then_inc(S["parts_ready"], 1)
                dve.wait_ge(S["a_exp"], 1)
                dve.tensor_scalar(a_neg[:, :, :], a_neg[:, :, :], -1.0, None, ALU.mult).then_inc(S["a_ready"], 1)
                dve.wait_ge(S["dt2_done"], 1)
                for k in range(CC):
                    dve.tensor_scalar(two(du[:, k, :]), bank[:, 2 * k:2 * k + 2, :], dt_b[:, k, :], None, ALU.add
                                      ).then_inc(S["pre_ready"], 1)
                for k in range(CC):
                    dve.wait_ge(S["e_ready"], k + 1)
                    chain(dve.tensor_scalar(series[:, k, :], small[:, k, :], -1.0 / 6, None, ALU.mult))
                    for c in (1.0 / 5, -1.0 / 4, 1.0 / 3, -1.0 / 2, 1.0):
                        chain(dve.scalar_tensor_tensor(series[:, k, :], series[:, k, :], c, small[:, k, :], ALU.add, ALU.mult))
                    dve.tensor_scalar(is_small[:, k, :], small[:, k, :], 1.0 / 16, None, ALU.is_lt).then_inc(S["small_known"], 1)
                    dve.wait_ge(S["small_known"], k + 1)
                    dve.wait_ge(S["soft"], k + 1)
                    chain(dve.copy_predicated(delta[:, k, :], is_small[:, k, :], series[:, k, :]))
                    dve.scalar_tensor_tensor(delta[:, k, :], du[:, k, :], 0.0, delta[:, k, :], ALU.max, ALU.add
                                             ).then_inc(S["delta_ready"], 1)

                def scan(n, k):
                    dve.wait_ge(S["decay_ready"], CC * n + (k + 1))
                    dve.wait_ge(S["drive_ready"], CC * n + (k + 1))
                    await_count(dve, S["seen_ready"], CC * n + (k - 1))
                    dve.tensor_tensor_scan(state[:, k, :], decay[:, k, :, :].rearrange("p b n -> p (b n)"), drive[:, k, :], 0.0,
                                           ALU.mult, ALU.add).then_inc(S["scanned"], 1)

                def see(n, k):
                    dve.wait_ge(S["scanned"], CC * n + (k + 1))
                    dve.wait_ge(S["c_done"], n + 1)
                    await_count(dve, S["summed"], CC * n + (k - 1))
                    dve.tensor_tensor(two(seen[:, k, :]), two(state[:, k, :]), bank[:, 2:4, :], ALU.mult
                                      ).then_inc(S["seen_ready"], 1)

                def steps_of(n):
                    scan(n, 1)
                    see(n, 0)
                    scan(n + 1, 0)
                    see(n, 1)

                scan(0, 0)
                steps_of(0)
                with dve.Fori(1, NS - 1) as n:
                    steps_of(n)
                scan(NS - 1, 1)
                see(NS - 1, 0)
                see(NS - 1, 1)
                dve.wait_ge(S["summed"], CC * NS)
                dve.wait_ge(S["silu_z_done"], 1)
                for k in range(CC):
                    chain(dve.scalar_tensor_tensor(two(state[:, k, :]), two(u[:, k, :]), skip[:, k, :],
                                                   bank[:, 4 + 2 * k:6 + 2 * k, :], ALU.mult, ALU.add))
                    z = silu_z[:, :, :].rearrange("p (b c) n -> p c b n", c=CC)[:, k, :, :]
                    dve.tensor_tensor(seen[:, k, :].rearrange("p (b n) -> p b n", b=NB),
                                      state[:, k, :].rearrange("p (b n) -> p b n", b=NB), z, ALU.mult
                                      ).then_inc(S["y_ready"], 1)
                for t in range(NT):
                    dve.wait_ge(S["y_turned"], t + 1)
                    dve.scalar_tensor_tensor(core.X[:, t, :], bank[:, t % 4, 0:DM], gate, core.X[:, t, :],
                                             ALU.mult, ALU.add).then_inc(S["added"], 1)


def one_hot_max(dve, s, chain, e, m, rank8, rank, top, hot):
    wide = lambda a: a.unsqueeze(2).to_broadcast([P, NT, 8])
    chain(dve.tensor_tensor(rank, e, wide(m), ALU.is_equal))
    chain(dve.tensor_tensor(rank, rank, rank8, ALU.mult))
    chain(dve.tensor_reduce(top, rank, AX.X, ALU.max))
    chain(dve.tensor_tensor(hot, rank, wide(top), ALU.is_equal))


def stage_lora_moe(core):
    nc, d = core.nc, core.dram
    NE, RANK = 8, 64
    ER = NE * RANK
    JC = ER // P
    with core.stage("lora") as s:
        wA, wB, wR = s.sb("wA", [P, DC, ER]), s.sb("wB", [P, JC, DM]), s.sb("wR", [P, DC, NE])
        bias, rank8 = s.sb("bias", [P, NE]), s.sb("rank8", [P, NE])
        lg, e8, rank, hot = (s.sb(n, [P, NT, NE]) for n in ("lg", "e8", "rank", "hot"))
        m1, emax, top, total, coef = (s.sb(n, [P, NT]) for n in ("m1", "emax", "top", "total", "coef"))
        hm = s.sb("hm", [P, 2, ER])
        hmT = s.sb("hmT", [P, 2, JC, P])
        loaded, logits, shifted, exps, chained, coefs = (s.sem(n) for n in (
            "loaded", "logits", "shifted", "exps", "chained", "coefs"))
        h_done, masked, h_turned, hT_ready, out_done, added = (s.sem(n) for n in (
            "h_done", "masked", "h_turned", "hT_ready", "out_done", "added"))
        bank = core.bank
        lgp = bank[:, 4, 0:NT * NE].rearrange("p (t e) -> p t e", e=NE)
        gate = core.gates[:, 4:5]

        with nc.Block() as block:
            @block.sync
            def _(sp):
                sp.dma_start(wR[:, :, :], d["l0_Wr"].rearrange("(c p) e -> p c e", p=P)).then_inc(loaded, 16)
                sp.dma_start(bias[:, :], d["l0_br"].partition_broadcast(P)).then_inc(loaded, 16)
                sp.dma_start(rank8[:, :], d["rank8"]).then_inc(loaded, 16)
                sp.dma_start(wA[:, :, :], d["l0_A"].rearrange("(c p) e -> p c e", p=P)).then_inc(loaded, 16)
                sp.dma_start(wB[:, :, :], d["l0_B"].rearrange("(c p) e -> p c e", p=P)).then_inc(loaded, 16)

            @block.tensor
            def _(pe):
                s.norm_tensor(pe)
                pe.wait_ge(loaded, 5 * 16)
                pe.wait_ge(s.xnT_ready, 4)
                for t in range(NT):
                    for c in range(DC):
                        last = pe.matmul(lgp[:, t, :], core.xnT[:, c, t * P:(t + 1) * P], wR[:, c, :],
                                         start=c == 0, stop=c == DC - 1)
                last.then_inc(logits, 1)

                def hidden(t):
                    if t >= 2:
                        pe.wait_ge(masked, t - 1)
                    for c in range(DC):
                        last = pe.matmul(bank[:, t % 2, :], core.xnT[:, c, t * P:(t + 1) * P], wA[:, c, :],
                                         start=c == 0, stop=c == DC - 1)
                    last.then_inc(h_done, 1)

                def turn(t):
                    pe.wait_ge(masked, t + 1)
                    if t >= 2:
                        pe.wait_ge(hT_ready, t - 1)
                    for j in range(JC):
                        last = pe.transpose(bank[:, 2 + t % 2, j * P:(j + 1) * P], hm[:, t % 2, j * P:(j + 1) * P],
                                            core.ident[:, :])
                    last.then_inc(h_turned, 1)

                def out(t):
                    pe.wait_ge(hT_ready, t + 1)
                    if t >= 2:
                        pe.wait_ge(added, t - 1)
                    for j in range(JC):
                        last = pe.matmul(bank[:, 5 + t % 2, 0:DM], hmT[:, t % 2, j, :], wB[:, j, :],
                                         start=j == 0, stop=j == JC - 1)
                    last.then_inc(out_done, 1)

                hidden(0)
                for t in range(NT):
                    if t + 1 < NT:
                        hidden(t + 1)
                    turn(t)
                    if t >= 1:
                        out(t - 1)
                out(NT - 1)

            @block.scalar
            def _(act):
                s.norm_scalar(act)
                act.wait_ge(shifted, 1)
                act.activation(e8[:, :, :], lg[:, :, :], ACT.Exp).then_inc(exps, 1)
                for t in range(NT):
                    act.wait_ge(h_turned, t + 1)
                    if t >= 2:
                        act.wait_ge(out_done, t - 1)
                    act.copy(hmT[:, t % 2, :, :], bank[:, 2 + t % 2, :]).then_inc(hT_ready, 1)

            @block.vector
            def _(dve):
                links = [0]

                def chain(ins):
                    links[0] += 1
                    ins.then_inc(chained, 1)
                    dve.wait_ge(chained, links[0])

                s.norm_vector(dve)
                wide = lambda a: a.unsqueeze(2).to_broadcast([P, NT, NE])
                mid = lambda a: a.unsqueeze(1).to_broadcast([P, NT, NE])
                dve.wait_ge(loaded, 5 * 16)
                dve.wait_ge(logits, 1)
                chain(dve.tensor_tensor(lg[:, :, :], lgp, mid(bias[:, :]), ALU.add))
                chain(dve.tensor_reduce(m1[:, :], lg[:, :, :], AX.X, ALU.max))
                dve.tensor_tensor(lg[:, :, :], lg[:, :, :], wide(m1[:, :]), ALU.subtract).then_inc(shifted, 1)
                dve.wait_ge(exps, 1)
                dve.tensor_reduce(total[:, :], e8[:, :, :], AX.X, ALU.add)
                chain(dve.tensor_reduce(emax[:, :], e8[:, :, :], AX.X, ALU.max))
                one_hot_max(dve, s, chain, e8[:, :, :], emax[:, :], mid(rank8[:, :]), rank[:, :, :], top[:, :], hot[:, :, :])
                chain(dve.reciprocal(total[:, :], total[:, :]))
                chain(dve.scalar_tensor_tensor(coef[:, :], total[:, :], 1.0 / RANK, emax[:, :], ALU.mult, ALU.mult))
                chain(dve.tensor_tensor(hot[:, :, :], hot[:, :, :], wide(coef[:, :]), ALU.mult))

                def add(t):
                    dve.wait_ge(out_done, t + 1)
                    dve.scalar_tensor_tensor(core.X[:, t, :], bank[:, 5 + t % 2, 0:DM], gate, core.X[:, t, :],
                                             ALU.mult, ALU.add).then_inc(added, 1)

                for t in range(NT):
                    dve.wait_ge(h_done, t + 1)
                    if t >= 2:
                        dve.wait_ge(h_turned, t - 1)
                    dve.tensor_tensor(hm[:, t % 2, :].rearrange("p (e r) -> p e r", r=RANK),
                                      bank[:, t % 2, :].rearrange("p (e r) -> p e r", r=RANK),
                                      hot[:, t, :].unsqueeze(2).to_broadcast([P, NE, RANK]), ALU.mult).then_inc(masked, 1)
                    if t >= 2:
                        add(t - 2)
                add(NT - 2)
                add(NT - 1)


def stage_attention_16(core):
    nc, d = core.nc, core.dram
    NH, HD = 16, 128
    LN_SCALE = -0.5 * float(np.log(HD))
    with core.stage("a16") as s:
        ctxT, ctx_nat = s.sb("ctxT", [P, NTOK]), s.sb("ctx_nat", [P, NT, CTX])
        gains, gain = s.sb("gains", [P, 2]), s.sb("gain", [P, 1])
        ln_scale = s.sb("ln_scale", [P, 1])
        wk, wvT = s.sb("wk", [P, 2, HD]), s.sb("wvT", [P, 2, CTX])
        wo, wq = s.sb("wo", [P, 2, DM]), s.sb("wq", [P, 2, DC, HD])
        keys, wvo = s.sb("keys", [P, NH, NTOK]), s.sb("wvo", [P, NH, DM])
        k_sq, k_log, k_row = (s.sb(n, [P, 2, HALF]) for n in ("k_sq", "k_log", "k_row"))
        query, q_sq = s.sb("query", [P, 2, HALF]), s.sb("q_sq", [P, HALF])
        q_log, q_factor = s.sb("q_log", [P, 4]), s.sb("q_factor", [P, 2, 4])
        bias = s.sb("bias", [P, 2, 2])
        prob, total, inverse = s.sb("prob", [P, 2, 2, SEQ]), s.sb("total", [P, 2, 2]), s.sb("inverse", [P, 2, 2])
        probT, mixT = s.sb("probT", [P, 2, 2, SEQ]), s.sb("mixT", [P, 2, SEQ])
        in_s, consts = s.sem("in_s"), s.sem("consts")
        kv_in = [s.sem(f"kv_in{k}") for k in range(2)]
        wq_in = [s.sem(f"wq_in{k}") for k in range(2)]
        names = ("gain_done", "k_done", "k_squared", "k_sums", "k_logs", "k_rows", "key_ready", "vo_done", "vo_ready",
                 "added", "q_done", "q_squared", "q_ready", "q_sums", "q_logs", "q_factors", "s_done", "top", "bias_ready",
                 "exp_done", "inv_ready", "p_ready", "p_turned", "pT_ready", "mix_done", "mixT_ready", "out_done")
        S = {n: s.sem(n) for n in names}
        bank = core.bank
        gate = core.gates[:, 1:2]

        with nc.Block() as block:
            @block.sync
            def _(sp):
                sp.dma_start(ctxT[:, :], d["ctxT"]).then_inc(in_s, 16)
                sp.dma_start(ctx_nat[:, :, :], d["ctx"].rearrange("(t p) n -> p t n", p=P)).then_inc(in_s, 16)
                sp.dma_start(gains[:, :], d["l1x_gains"]).then_inc(in_s, 16)

                def load_kv(i, k):
                    h = 2 * i + k
                    for dst, n in ((wk, "l1x_k"), (wvT, "l1x_vT"), (wo, "l1x_o")):
                        sp.dma_start(dst[:, k, :], d[n][bass.ds(h, 1)].rearrange("h p n -> p (h n)")).then_inc(kv_in[k], 16)

                def load_q(h, k):
                    sp.dma_start(wq[:, k, :, :], d["l1x_q"][bass.ds(h, 1)].rearrange("h (c p) n -> p (h c) n", p=P)
                                 ).then_inc(wq_in[k], 16)

                for k in range(2):
                    load_kv(0, k)
                for k in range(2):
                    load_q(k, k)
                with sp.Fori(1, NH // 2) as i:
                    for k in range(2):
                        sp.wait_ge(S["k_done"], 4 * i + (2 * k - 2))
                        sp.wait_ge(S["vo_done"], 2 * i + (k - 1))
                        load_kv(i, k)
                for m in range(2):
                    with sp.Fori(1 - m, NH // 2) as i:
                        for k in range(2):
                            sp.wait_ge(S["q_done"], 2 * i + (NH * m + k - 1))
                            load_q(2 * i + k, k)

            @block.tensor
            def _(pe):
                s.norm_tensor(pe)
                pe.wait_ge(in_s, 3 * 16)
                pe.wait_ge(s.xnT_ready, 4)

                def keys_of(i, k, m):
                    n = 4 * i + (2 * k + m)
                    if m == 0:
                        pe.wait_ge(kv_in[k], 3 * 16 * i + 3 * 16)
                    await_count(pe, S["key_ready"], n - 3)
                    pe.matmul(bank[:, 2 * k + m, :], wk[:, k, :], ctxT[:, m * HALF:(m + 1) * HALF], start=True, stop=True
                              ).then_inc(S["k_done"], 1)

                def sums_of(i, k, m):
                    n, h = 4 * i + (2 * k + m), 2 * i + k
                    if m == 0:
                        await_count(pe, S["vo_ready"], h - 1)
                        pe.matmul(bank[:, 6 + k, 0:DM], wvT[:, k, :], wo[:, k, :], start=True, stop=True
                                  ).then_inc(S["vo_done"], 1)
                    pe.wait_ge(S["k_squared"], n + 1)
                    await_count(pe, S["k_logs"], n - 1)
                    pe.matmul(bank[:, 4 + m, :], core.ones[:, :], k_sq[:, m, :], start=True, stop=True
                              ).then_inc(S["k_sums"], 1)

                def two_heads(i, first=False):
                    for k in range(2):
                        for m in range(2):
                            keys_of(i, k, m)
                            if m == 1:
                                sums_of(i, k, 0)
                            elif k == 1:
                                sums_of(i, 0, 1)
                            elif not first:
                                sums_of(i - 1, 1, 1)

                two_heads(0, True)
                with pe.Fori(1, NH // 2) as i:
                    two_heads(i)
                sums_of(NH // 2 - 1, 1, 1)
                pe.wait_ge(S["key_ready"], 2 * NH)
                pe.wait_ge(S["vo_ready"], NH)

                def queries(n, i, m, p):
                    pe.wait_ge(wq_in[p], 16 * i + 16)
                    await_count(pe, S["q_logs"], n - 1)
                    for c in range(DC):
                        last = pe.matmul(bank[:, 6 + p, :], wq[:, p, c, :], core.xnT[:, c, m * HALF:(m + 1) * HALF],
                                         start=c == 0, stop=c == DC - 1)
                    last.then_inc(S["q_done"], 1)

                def query_sums(n, p):
                    pe.wait_ge(S["q_squared"], n + 1)
                    pe.wait_ge(S["q_ready"], n + 1)
                    for j in range(4):
                        last = pe.matmul(bank[:, 6 + p, j:j + 1], q_sq[:, j * P:(j + 1) * P], core.ones[:, 0:1],
                                         start=True, stop=True)
                    last.then_inc(S["q_sums"], 1)

                def scores(n, m, p, j):
                    pe.wait_ge(S["q_ready"], n + 1)
                    await_count(pe, S["exp_done"], 2 * n + (j - 1))
                    b = 2 * m + j
                    for q in range(2):
                        last = pe.matmul(bank[:, 2 + j, q * SEQ:(q + 1) * SEQ],
                                         query[:, p, (2 * j + q) * P:(2 * j + q + 1) * P],
                                         keys[:, bass.ds(n - NH * m, 1), b * SEQ:(b + 1) * SEQ].rearrange("p h n -> p (h n)"),
                                         start=True, stop=True)
                    last.then_inc(S["s_done"], 1)

                def turn(n, j):
                    i = 2 * n + j
                    pe.wait_ge(S["p_ready"], i + 1)
                    await_count(pe, S["pT_ready"], i)
                    for kc in range(2):
                        for q in range(2):
                            last = pe.transpose(bank[:, 4, kc * SEQ + q * P:kc * SEQ + (q + 1) * P],
                                                prob[:, j, q, kc * P:(kc + 1) * P], core.ident[:, :])
                    last.then_inc(S["p_turned"], 1)

                def mix(n, m, j):
                    i = 2 * n + j
                    pe.wait_ge(S["pT_ready"], i + 1)
                    await_count(pe, S["mixT_ready"], i)
                    for kc in range(2):
                        last = pe.matmul(bank[:, 5, 0:SEQ], ctx_nat[:, 2 * (2 * m + j) + kc, :], probT[:, j, kc, :],
                                         start=kc == 0, stop=kc == 1)
                    last.then_inc(S["mix_done"], 1)

                def out(n, m, j):
                    i = 2 * n + j
                    first = isinstance(n, int) and n % NH == 0
                    pe.wait_ge(S["mixT_ready"], i + 1)
                    for q in range(2):
                        last = pe.matmul(bank[:, j, q * DM:(q + 1) * DM], mixT[:, j, q * P:(q + 1) * P],
                                         wvo[:, bass.ds(n - NH * m, 1), :].rearrange("p h n -> p (h n)"),
                                         start=first and q == 0, stop=isinstance(n, int) and n % NH == NH - 1,
                                         skip_group_check=True)
                    last.then_inc(S["out_done"], 1)

                def unit(n, i, m, p, before, after):
                    scores(n, m, p, 0)
                    if before is not None:
                        turn(n - 1, 1)
                    if after is not None:
                        queries(n + 1, i + p, after, 1 - p)
                    if before is not None:
                        mix(n - 1, before, 1)
                        out(n - 1, before, 0)
                    scores(n, m, p, 1)
                    turn(n, 0)
                    if after is not None:
                        query_sums(n + 1, 1 - p)
                    mix(n, m, 0)
                    if before is not None:
                        out(n - 1, before, 1)

                queries(0, 0, 0, 0)
                query_sums(0, 0)
                unit(0, 0, 0, 0, None, 0)
                unit(1, 0, 0, 1, 0, 0)
                with pe.Fori(1, NH // 2 - 1) as i:
                    for p in range(2):
                        unit(2 * i + p, i, 0, p, 0, 0)
                unit(NH - 2, NH // 2 - 1, 0, 0, 0, 0)
                unit(NH - 1, NH // 2 - 1, 0, 1, 0, 1)
                unit(NH, NH // 2, 1, 0, 0, 1)
                pe.wait_ge(S["added"], 1)
                unit(NH + 1, NH // 2, 1, 1, 1, 1)
                with pe.Fori(NH // 2 + 1, NH - 1) as i:
                    for p in range(2):
                        unit(2 * i + p, i, 1, p, 1, 1)
                unit(2 * NH - 2, NH - 1, 1, 0, 1, 1)
                unit(2 * NH - 1, NH - 1, 1, 1, 1, None)
                turn(2 * NH - 1, 1)
                mix(2 * NH - 1, 1, 1)
                out(2 * NH - 1, 1, 0)
                out(2 * NH - 1, 1, 1)

            @block.scalar
            def _(act):
                s.norm_scalar(act)
                act.preload_act_table_set("natural_log_exp_and_others")

                def square(i, k, m):
                    n = 4 * i + (2 * k + m)
                    act.wait_ge(S["k_done"], n + 1)
                    await_count(act, S["k_sums"], n - 1)
                    act.activation(k_sq[:, m, :], bank[:, 2 * k + m, :], ACT.Square).then_inc(S["k_squared"], 1)

                def key_factor(i, k, m):
                    n = 4 * i + (2 * k + m)
                    act.wait_ge(S["k_sums"], n + 1)
                    await_count(act, S["k_rows"], n - 1)
                    act.activation(k_log[:, m, :], bank[:, 4 + m, :], ACT.Ln, scale=1.0 / HD, bias=core.eps[:, 0:1]
                                   ).then_inc(S["k_logs"], 1)
                    act.wait_ge(S["k_logs"], n + 1)
                    await_count(act, S["key_ready"], n - 1)
                    act.activation(k_row[:, m, :], k_log[:, m, :], ACT.Exp, scale=-0.5).then_inc(S["k_rows"], 1)

                def two_heads(i, first=False):
                    for k in range(2):
                        for m in range(2):
                            square(i, k, m)
                            if m == 1:
                                key_factor(i, k, 0)
                            elif k == 1:
                                key_factor(i, 0, 1)
                            elif not first:
                                key_factor(i - 1, 1, 1)

                two_heads(0, True)
                with act.Fori(1, NH // 2) as i:
                    two_heads(i)
                key_factor(NH // 2 - 1, 1, 1)

                def queries(n, p):
                    act.wait_ge(S["q_done"], n + 1)
                    await_count(act, S["q_sums"], n)
                    act.activation(q_sq[:, :], bank[:, 6 + p, :], ACT.Square).then_inc(S["q_squared"], 1)
                    await_count(act, S["s_done"], 2 * n - 2)
                    act.copy(query[:, p, :], bank[:, 6 + p, :]).then_inc(S["q_ready"], 1)

                def query_factor(n, p):
                    act.wait_ge(S["q_sums"], n + 1)
                    await_count(act, S["q_factors"], n)
                    act.activation(q_log[:, :], bank[:, 6 + p, 0:4], ACT.Ln, scale=1.0 / HD, bias=core.eps[:, 0:1]
                                   ).then_inc(S["q_logs"], 1)
                    act.wait_ge(S["q_logs"], n + 1)
                    await_count(act, S["exp_done"], 2 * n - 2)
                    await_count(act, S["bias_ready"], 2 * n - 2)
                    act.activation(q_factor[:, p, :], q_log[:, :], ACT.Exp, scale=-0.5, bias=ln_scale[:, 0:1]
                                   ).then_inc(S["q_factors"], 1)

                def exps(n, p, j):
                    i = 2 * n + j
                    act.wait_ge(S["q_factors"], n + 1)
                    act.wait_ge(S["bias_ready"], i + 1)
                    await_count(act, S["p_turned"], i - 1)
                    await_count(act, S["inv_ready"], i - 1)
                    for q in range(2):
                        last = act.activation(prob[:, j, q, :], bank[:, 2 + j, q * SEQ:(q + 1) * SEQ], ACT.Exp,
                                              scale=q_factor[:, p, 2 * j + q:2 * j + q + 1],
                                              bias=bias[:, j, q:q + 1], accum_out=total[:, j, q:q + 1])
                    last.then_inc(S["exp_done"], 1)

                def bring_mix(n, j):
                    i = 2 * n + j
                    act.wait_ge(S["mix_done"], i + 1)
                    await_count(act, S["out_done"], i - 1)
                    act.copy(mixT[:, j, :], bank[:, 5, 0:SEQ]).then_inc(S["mixT_ready"], 1)

                def unit(n, p, before, after):
                    exps(n, p, 0)
                    if after:
                        queries(n + 1, 1 - p)
                    if before:
                        bring_mix(n - 1, 1)
                    exps(n, p, 1)
                    if after:
                        query_factor(n + 1, 1 - p)
                    bring_mix(n, 0)

                queries(0, 0)
                act.wait_ge(consts, 1)
                query_factor(0, 0)
                unit(0, 0, False, True)
                unit(1, 1, True, True)
                with act.Fori(1, NH - 1) as i:
                    for p in range(2):
                        unit(2 * i + p, p, True, True)
                unit(2 * NH - 2, 0, True, True)
                unit(2 * NH - 1, 1, True, False)
                bring_mix(2 * NH - 1, 1)

            @block.gpsimd
            def _(pool):
                pool.memset(ln_scale[:, :], LN_SCALE).then_inc(consts, 1)

                def normalise(n, j):
                    i = 2 * n + j
                    pool.wait_ge(S["inv_ready"], i + 1)
                    pool.tensor_tensor(prob[:, j, :, :], prob[:, j, :, :],
                                       inverse[:, j, :].unsqueeze(2).to_broadcast([P, 2, SEQ]), ALU.mult
                                       ).then_inc(S["p_ready"], 1)

                with pool.Fori(0, 2 * NH) as n:
                    for j in range(2):
                        normalise(n, j)

            @block.vector
            def _(dve):
                s.norm_vector(dve)
                dve.wait_ge(in_s, 3 * 16)
                dve.tensor_tensor(gain[:, :], gains[:, 0:1], gains[:, 1:2], ALU.mult).then_inc(S["gain_done"], 1)
                dve.wait_ge(S["gain_done"], 1)

                def keys_of(i, k, m):
                    n = 4 * i + (2 * k + m)
                    dve.wait_ge(S["k_rows"], n + 1)
                    dve.scalar_tensor_tensor(keys[:, bass.ds(2 * i + k, 1), m * HALF:(m + 1) * HALF].rearrange("p h n -> p (h n)"),
                                             bank[:, 2 * k + m, :], gain[:, 0:1], k_row[:, m, :],
                                             ALU.mult, ALU.mult).then_inc(S["key_ready"], 1)

                def bring_vo(i, k):
                    dve.wait_ge(S["vo_done"], 2 * i + (k + 1))
                    dve.tensor_copy(wvo[:, bass.ds(2 * i + k, 1), :].rearrange("p h n -> p (h n)"), bank[:, 6 + k, 0:DM]
                                    ).then_inc(S["vo_ready"], 1)

                with dve.Fori(0, NH // 2) as i:
                    for k in range(2):
                        keys_of(i, k, 0)
                        bring_vo(i, k)
                        keys_of(i, k, 1)

                def top(n, j):
                    i = 2 * n + j
                    dve.wait_ge(S["s_done"], i + 1)
                    await_count(dve, S["exp_done"], i - 1)
                    dve.tensor_reduce(bias[:, j, :], bank[:, 2 + j, :].rearrange("p (q n) -> p q n", q=2), AX.X, ALU.max,
                                      negate=True).then_inc(S["top"], 1)

                def scale_top(n, p, j):
                    i = 2 * n + j
                    dve.wait_ge(S["top"], i + 1)
                    dve.wait_ge(S["q_factors"], n + 1)
                    dve.tensor_tensor(bias[:, j, :], bias[:, j, :], q_factor[:, p, 2 * j:2 * j + 2], ALU.mult
                                      ).then_inc(S["bias_ready"], 1)

                def invert(n, j):
                    i = 2 * n + j
                    dve.wait_ge(S["exp_done"], i + 1)
                    await_count(dve, S["p_ready"], i - 1)
                    dve.reciprocal(inverse[:, j, :], total[:, j, :]).then_inc(S["inv_ready"], 1)

                def bring(n, j):
                    i = 2 * n + j
                    dve.wait_ge(S["p_turned"], i + 1)
                    await_count(dve, S["mix_done"], i - 1)
                    dve.tensor_copy(probT[:, j, :, :], bank[:, 4, :].rearrange("p (k n) -> p k n", k=2)
                                    ).then_inc(S["pT_ready"], 1)

                def unit(n, p, before=True):
                    top(n, 0)
                    scale_top(n, p, 0)
                    if before:
                        bring(n - 1, 1)
                    invert(n, 0)
                    top(n, 1)
                    bring(n, 0)
                    scale_top(n, p, 1)
                    invert(n, 1)

                def add(m):
                    dve.wait_ge(S["out_done"], 2 * NH * (m + 1))
                    for j in range(2):
                        for q in range(2):
                            t = 4 * m + 2 * j + q
                            last = dve.scalar_tensor_tensor(core.X[:, t, :], bank[:, j, q * DM:(q + 1) * DM], gate,
                                                            core.X[:, t, :], ALU.mult, ALU.add)
                    last.then_inc(S["added"], 1)

                unit(0, 0, False)
                unit(1, 1)
                with dve.Fori(1, NH // 2) as i:
                    for p in range(2):
                        unit(2 * i + p, p)
                unit(NH, 0)
                add(0)
                unit(NH + 1, 1)
                with dve.Fori(NH // 2 + 1, NH) as i:
                    for p in range(2):
                        unit(2 * i + p, p)
                bring(2 * NH - 1, 1)
                add(1)


def stage_bitnet(core):
    nc, d = core.nc, core.dram
    FF = 1024
    FC = FF // P
    QMAX = 128.0
    EPS = 1e-5
    NW = DC * FF
    with core.stage("bit") as s:
        raw = [s.sb(f"raw{i}", [P, NW]) for i in range(3)]
        tern = [s.sb(f"tern{i}", [P, NW], BF16) for i in range(3)]
        w_gate, w_up = (tern[i][:, :].rearrange("p (c f) -> p c f", c=DC) for i in range(2))
        w_down = tern[2][:, :].rearrange("p (c f) -> p c f", c=FC)
        rowsum, wmean, wscale, wback = (s.sb(n, [P, 3]) for n in ("rowsum", "wmean", "wscale", "wback"))
        hadamard = s.sb("hadamard", [P, P])
        amax, qscale, back, gback, uback = (s.sb(n, [P, NT]) for n in ("amax", "qscale", "back", "gback", "uback"))
        shifted = s.sb("shifted", [P, 2, DM])
        xq = s.sb("xq", [P, NT, DM], BF16)
        xqT = s.sb("xqT", [P, DC, NTOK], BF16)
        silu, up = s.sb("silu", [P, 2, HALF]), s.sb("up", [P, 2, HALF])
        inter = s.sb("inter", [P, 2, HALF])
        interT = s.sb("interT", [P, 2, HALF])
        fly = s.sb("fly", [P, 2, FF])
        fly2 = s.sb("fly2", [P, HALF])
        amax2, qscale2, back2 = (s.sb(n, [P, NT]) for n in ("amax2", "qscale2", "back2"))
        fq = s.sb("fq", [P, 2, FF], BF16)
        fqT = s.sb("fqT", [P, 2, FC, P], BF16)
        loaded = [s.sem(f"loaded{i}") for i in range(3)]
        consts, sums, sums_out, tern_ready, step = (s.sem(n) for n in ("consts", "sums", "sums_out", "tern_ready", "step"))
        xq_scaled = s.sem("xq_scaled")
        xq_ready, xq_turned, xqT_ready = (s.sem(n) for n in ("xq_ready", "xq_turned", "xqT_ready"))
        gate_up, silu_done, inter_ready, inter_turned, interT_ready = (s.sem(n) for n in (
            "gate_up", "silu_done", "inter_ready", "inter_turned", "interT_ready"))
        w_scaled, tern_up = s.sem("w_scaled"), s.sem("tern_up")
        up_done, h_copied, up_step = s.sem("up_done"), s.sem("h_copied"), s.sem("up_step")
        h_done, h_read, fq_ready, fq_turned, fqT_ready, out_done, added = (s.sem(n) for n in (
            "h_done", "h_read", "fq_ready", "fq_turned", "fqT_ready", "out_done", "added"))
        bank = core.bank
        gate = core.gates[:, 5:6]
        half_bf = lambda b: bank[:, b, :].bitcast(BF16)

        with nc.Block() as block:
            @block.sync
            def _(sp):
                for i, n in enumerate(("l1_gate", "l1_up", "l1_down")):
                    sp.dma_start(raw[i][:, :].rearrange("p (c f) -> p c f", c=DC if i < 2 else FC),
                                 d[n].rearrange("(c p) f -> p c f", p=P)).then_inc(loaded[i], 16)
                sp.dma_start(hadamard[:, :], d["hadamard"]).then_inc(consts, 16)

            @block.tensor
            def _(pe):
                for i in range(3):
                    pe.wait_ge(sums, i + 1)
                    pe.matmul(bank[:, 7, i:i + 1], core.ones[:, :], rowsum[:, i:i + 1], start=True, stop=True
                              ).then_inc(sums_out, 1)
                for t in range(NT):
                    pe.wait_ge(xq_ready, t + 1)
                    if t >= 1:
                        pe.wait_ge(xqT_ready, t)
                    for c in range(DC):
                        last = pe.transpose(half_bf(5)[:, c * P:(c + 1) * P], xq[:, t, c * P:(c + 1) * P],
                                            core.identh[:, :])
                    last.then_inc(xq_turned, 1)
                pe.wait_ge(consts, 16)
                pe.wait_ge(tern_ready, 1)
                pe.wait_ge(tern_up, 1)

                def gate_and_up(n):
                    t, h = n // 2, n % 2
                    pe.wait_ge(xqT_ready, t + 1)
                    await_count(pe, silu_done, n)
                    await_count(pe, up_done, n)
                    for k, w in enumerate((w_gate, w_up)):
                        for c in range(DC):
                            last = pe.matmul(bank[:, k, :], xqT[:, c, t * P:(t + 1) * P],
                                             w[:, c, h * HALF:(h + 1) * HALF], start=c == 0, stop=c == DC - 1)
                    last.then_inc(gate_up, 1)

                def turn(n):
                    pe.wait_ge(inter_ready, n + 1)
                    if n >= 1:
                        pe.wait_ge(interT_ready, n)
                    for j in range(4):
                        last = pe.transpose(bank[:, 2, j * P:(j + 1) * P], inter[:, n % 2, j * P:(j + 1) * P],
                                            core.ident[:, :])
                    last.then_inc(inter_turned, 1)

                def transform(n):
                    t, h = n // 2, n % 2
                    pe.wait_ge(interT_ready, n + 1)
                    await_count(pe, h_read if h else h_copied, t)
                    for j in range(4):
                        last = pe.matmul(bank[:, 3 + h, j * P:(j + 1) * P], interT[:, n % 2, j * P:(j + 1) * P],
                                         hadamard[:, :], start=True, stop=True)
                    last.then_inc(h_done, 1)

                def turn_fq(t):
                    pe.wait_ge(fq_ready, t + 1)
                    if t >= 1:
                        pe.wait_ge(fqT_ready, t)
                    for j in range(FC):
                        last = pe.transpose(half_bf(5)[:, j * P:(j + 1) * P], fq[:, t % 2, j * P:(j + 1) * P],
                                            core.identh[:, :])
                    last.then_inc(fq_turned, 1)

                def down(t):
                    pe.wait_ge(fqT_ready, t + 1)
                    if t == 0:
                        pe.wait_ge(tern_ready, 2)
                    else:
                        pe.wait_ge(added, t)
                    for j in range(FC):
                        last = pe.matmul(bank[:, 6, 0:DM], fqT[:, t % 2, j, :], w_down[:, j, :],
                                         start=j == 0, stop=j == FC - 1)
                    last.then_inc(out_done, 1)

                pe.wait_ge(xqT_ready, NT)
                gate_and_up(0)
                gate_and_up(1)
                for n in range(2 * NT):
                    if n + 2 < 2 * NT:
                        gate_and_up(n + 2)
                    turn(n)
                    transform(n)
                    if n % 2 == 1 and n >= 5:
                        turn_fq(n // 2 - 2)
                        down(n // 2 - 2)
                for t in (NT - 2, NT - 1):
                    turn_fq(t)
                    down(t)

            @block.scalar
            def _(act):
                act.wait_ge(s.aggr_done, NT)
                act.activation(core.rstd[:, :], core.meanvar[:, :, 1], ACT.Sqrt, bias=core.eps[:, 0:1]
                               ).then_inc(s.root_done, 1)
                for t in range(NT):
                    act.wait_ge(xq_turned, t + 1)
                    act.copy(xqT[:, :, t * P:(t + 1) * P], half_bf(5)[:, 0:DC * P].rearrange("p (c n) -> p c n", c=DC)
                             ).then_inc(xqT_ready, 1)

                def silu_of(n):
                    act.wait_ge(gate_up, n + 1)
                    if n >= 2:
                        act.wait_ge(inter_ready, n - 1)
                    act.activation(silu[:, n % 2, :], bank[:, 0, :], ACT.Silu, scale=gback[:, n // 2:n // 2 + 1]
                                   ).then_inc(silu_done, 1)
                    act.activation(up[:, n % 2, :], bank[:, 1, :], ACT.Copy, scale=uback[:, n // 2:n // 2 + 1]
                                   ).then_inc(up_done, 1)

                def bring_half(t):
                    act.wait_ge(h_done, 2 * t + 1)
                    await_count(act, h_read, t)
                    act.copy(fly2[:, :], bank[:, 3, :]).then_inc(h_copied, 1)

                def bring(n):
                    act.wait_ge(inter_turned, n + 1)
                    if n >= 2:
                        act.wait_ge(h_done, n - 1)
                    act.copy(interT[:, n % 2, :], bank[:, 2, :]).then_inc(interT_ready, 1)

                def bring_fq(t):
                    act.wait_ge(fq_turned, t + 1)
                    if t >= 2:
                        act.wait_ge(out_done, t - 1)
                    act.copy(fqT[:, t % 2, :, :], half_bf(5)).then_inc(fqT_ready, 1)

                act.wait_ge(xq_scaled, 1)
                silu_of(0)
                silu_of(1)
                for n in range(2 * NT):
                    if n + 2 < 2 * NT:
                        silu_of(n + 2)
                    if n % 2 == 1:
                        bring_half(n // 2)
                    bring(n)
                    if n % 2 == 1 and n >= 5:
                        bring_fq(n // 2 - 2)
                bring_fq(NT - 2)
                bring_fq(NT - 1)

            @block.gpsimd
            def _(pool):
                pool_steps = [0]

                def chain(ins):
                    pool_steps[0] += 1
                    ins.then_inc(up_step, 1)
                    pool.wait_ge(up_step, pool_steps[0])

                def ternary(i, done, count):
                    w = raw[i][:, :]
                    chain(pool.tensor_scalar(w, w, wscale[:, i:i + 1], ROUND, ALU.mult, ALU.add))
                    chain(pool.tensor_scalar(w, w, ROUND, 1.0, ALU.subtract, ALU.min))
                    pool.tensor_scalar(tern[i][:, :], w, -1.0, None, ALU.max).then_inc(done, 1)

                pool.wait_ge(w_scaled, 1)
                ternary(1, tern_up, 1)

                def inter_of(n):
                    pool.wait_ge(silu_done, n + 1)
                    pool.wait_ge(up_done, n + 1)
                    await_count(pool, inter_turned, n - 1)
                    pool.tensor_tensor(inter[:, n % 2, :], up[:, n % 2, :], silu[:, n % 2, :], ALU.mult).then_inc(inter_ready, 1)

                for n in range(2 * NT):
                    inter_of(n)

            @block.vector
            def _(dve):
                steps = [0]

                def chain(ins):
                    steps[0] += 1
                    ins.then_inc(step, 1)
                    dve.wait_ge(step, steps[0])

                def ternary(i):
                    w = raw[i][:, :]
                    chain(dve.tensor_scalar(w, w, wscale[:, i:i + 1], ROUND, ALU.mult, ALU.add))
                    chain(dve.tensor_scalar(w, w, ROUND, 1.0, ALU.subtract, ALU.min))
                    dve.tensor_scalar(tern[i][:, :], w, -1.0, None, ALU.max).then_inc(tern_ready, 1)

                for i in range(3):
                    dve.wait_ge(loaded[i], 16)
                    dve.tensor_reduce(rowsum[:, i:i + 1], raw[i][:, :], AX.X, ALU.add, apply_absolute_value=True
                                      ).then_inc(sums, 1)
                s.norm_vector(dve)
                dve.wait_ge(sums_out, 3)
                chain(dve.tensor_scalar(wmean[:, :], bank[:, 7, 0:3], 1.0 / (NW * P), EPS, ALU.mult, ALU.max))
                dve.reciprocal(wscale[:, :], wmean[:, :]).then_inc(w_scaled, 1)
                dve.wait_ge(w_scaled, 1)
                chain(dve.reciprocal(wback[:, :], wscale[:, :]))
                ternary(0)
                dve.wait_ge(s.xn_ready, NT)
                chain(dve.tensor_reduce(amax[:, :], core.xn[:, :, :], AX.X, ALU.max, apply_absolute_value=True))
                chain(dve.tensor_scalar(amax[:, :], amax[:, :], EPS, None, ALU.max))
                chain(dve.reciprocal(qscale[:, :], amax[:, :]))
                chain(dve.tensor_scalar(qscale[:, :], qscale[:, :], QMAX, None, ALU.mult))
                chain(dve.reciprocal(back[:, :], qscale[:, :]))
                for t in range(NT):
                    chain(dve.tensor_scalar(shifted[:, t % 2, :], core.xn[:, t, :], qscale[:, t:t + 1], ROUND,
                                            ALU.mult, ALU.add))
                    dve.tensor_scalar(xq[:, t, :], shifted[:, t % 2, :], ROUND, QMAX - 1, ALU.subtract, ALU.min
                                      ).then_inc(xq_ready, 1)
                chain(dve.tensor_scalar(gback[:, :], back[:, :], wback[:, 0:1], None, ALU.mult))
                dve.tensor_scalar(uback[:, :], back[:, :], wback[:, 1:2], None, ALU.mult).then_inc(xq_scaled, 1)
                dve.wait_ge(xq_scaled, 1)
                ternary(2)

                def butterflies(t):
                    dve.wait_ge(h_done, 2 * t + 2)
                    f0, f1 = fly[:, 0, :], fly[:, 1, :]
                    pair = lambda a, m: a.rearrange("p (a two b) -> p a two b", two=2, b=m * P)
                    dve.wait_ge(h_copied, t + 1)
                    chain(dve.tensor_tensor(fly[:, 0, 0:HALF], fly2[:, :], bank[:, 4, :], ALU.add))
                    dve.tensor_tensor(fly[:, 0, HALF:FF], fly2[:, :], bank[:, 4, :], ALU.subtract).then_inc(h_read, 1)
                    dve.wait_ge(h_read, t + 1)
                    for m, (a, b) in ((2, (f0, f1)), (1, (f1, f0))):
                        pa, pb = pair(a, m), pair(b, m)
                        dve.tensor_tensor(pb[:, :, 0, :], pa[:, :, 0, :], pa[:, :, 1, :], ALU.add)
                        chain(dve.tensor_tensor(pb[:, :, 1, :], pa[:, :, 0, :], pa[:, :, 1, :], ALU.subtract))
                    col = slice(t, t + 1)
                    chain(dve.tensor_reduce(amax2[:, col], f0, AX.X, ALU.max, apply_absolute_value=True))
                    chain(dve.tensor_scalar(amax2[:, col], amax2[:, col], 1.0 / 32, EPS, ALU.mult, ALU.max))
                    chain(dve.reciprocal(qscale2[:, col], amax2[:, col]))
                    chain(dve.tensor_scalar(qscale2[:, col], qscale2[:, col], QMAX, None, ALU.mult))
                    chain(dve.reciprocal(back2[:, col], qscale2[:, col]))
                    chain(dve.tensor_scalar(back2[:, col], back2[:, col], wback[:, 2:3], gate, ALU.mult, ALU.mult))
                    chain(dve.tensor_scalar(qscale2[:, col], qscale2[:, col], 1.0 / 32, None, ALU.mult))
                    chain(dve.tensor_scalar(f1, f0, qscale2[:, col], ROUND, ALU.mult, ALU.add))
                    if t >= 2:
                        dve.wait_ge(fq_turned, t - 1)
                    dve.tensor_scalar(fq[:, t % 2, :], f1, ROUND, QMAX - 1, ALU.subtract, ALU.min).then_inc(fq_ready, 1)

                def add(t):
                    dve.wait_ge(out_done, t + 1)
                    dve.scalar_tensor_tensor(core.X[:, t, :], bank[:, 6, 0:DM], back2[:, t:t + 1], core.X[:, t, :],
                                             ALU.mult, ALU.add).then_inc(added, 1)

                for t in range(NT):
                    if t >= 3:
                        add(t - 3)
                    await_count(dve, fq_ready, t)
                    butterflies(t)
                for t in range(NT - 3, NT):
                    add(t)


def stage_attention_32(core):
    nc, d = core.nc, core.dram
    NH, HD = 32, 8
    SCALE = float(HD) ** -0.5
    FREQS = (1.0, 0.01)
    PI = 3.1415925
    TURN_HI, TURN_LO = 6.28125, 2 * float(np.pi) - 6.28125
    Q_PARTS, K_PARTS = (0, 0, 1, 0, 2, 1), (0, 1, 0, 2, 0, 1)
    SHIFT = 64
    NBUF = 3
    VW = HD + 1
    QUAD = 4
    NQ = NH // QUAD
    ANGLE_STEPS = 7
    with core.stage("a32") as s:
        ctxT, wq, wkv, wout = s.sb("ctxT", [P, NTOK]), s.sb("wq", [P, DC, DM]), s.sb("wkv", [P, 2 * DM]), s.sb("wout", [P, DC, DM])
        bout = s.sb("bout", [1, DM])
        pos = s.sb("pos", [P, NT, 2])
        angle, turns, trig = (s.sb(n, [P, NT, 2, 4]) for n in ("angle", "turns", "trig"))
        cos8, sin8 = s.sb("cos8", [P, NT, HD]), s.sb("sin8", [P, NT, HD])
        straight, crossed = s.sb("straight", [P, 2, 2 * DM]), s.sb("crossed", [P, 2, 2 * DM])
        rest = s.sb("rest", [P, 2, 4, P])
        parts = [s.sb(f"part{j}", [P, 4, 2, P], BF16) for j in range(6)]
        values = s.sb("values", [P, NT, NH, VW])
        q_stack = s.sb("q_stack", [P, NBUF, NH, SEQ], BF16)
        k_stack = s.sb("k_stack", [P, NBUF, NH, SEQ], BF16)
        tops, shift = s.sb("tops", [P, 2, 2, NH]), s.sb("shift", [NH, 2, SEQ], BF16)
        prob = s.sb("prob", [P, 2, 4, SEQ])
        outT = s.sb("outT", [P, 2, SEQ])
        inverse, attn = s.sb("inverse", [P, 2, 2, QUAD]), s.sb("attn", [P, NT, DM])
        attnT = s.sb("attnT", [P, 2, DC, P])
        scratch = nc.dram_tensor("a32_scratch", [3, 2, DM, NTOK], BF16).ap()
        scratch_shift = nc.dram_tensor("a32_scratch_shift", [NB, NH, SEQ], BF16).ap()
        names = ("w_in", "pos_in", "step", "trig_done", "qk_done", "values_done", "crossed_r", "roped", "turned32", "v_ready",
                 "ones_set", "q_zero", "k_zero", "row_set", "rows_clear", "banks_clear", "zero_set",  "hi_ready", "rest_ready", "mid_ready", "lo_ready", "s_done", "top_done",
                 "top_turned", "shift_ready", "st_done", "exp_done", "av_done", "outT_ready", "quad_turned", "inv_done", "attn_ready", "attn_turned",
                 "attnT_ready", "out_done", "added")
        S = {n: s.sem(n) for n in names}
        spilled = [s.sem(f"spilled{b}") for b in range(NB)]
        stacked = [s.sem(f"stacked{b}") for b in range(NB)]
        shifted = [s.sem(f"shifted{b}") for b in range(NB)]
        bank = core.bank
        gate = core.gates[:, 2:3]
        NG = NH // 2

        def part(j, b):
            return parts[3 * (b % 2) + j]

        with nc.Block() as block:
            @block.sync
            def _(sp):
                sp.dma_start(ctxT[:, :], d["ctxT"]).then_inc(S["w_in"], 16)
                sp.dma_start(wkv[:, :], d["l2x_kv"]).then_inc(S["w_in"], 16)
                for dst, n in ((wq, "l2x_q"), (wout, "l2x_out")):
                    sp.dma_start(dst[:, :, :], d[n].rearrange("(c p) n -> p c n", p=P)).then_inc(S["w_in"], 16)
                sp.dma_start(bout[:, :], d["l2x_bout"].rearrange("(a n) -> a n", a=1)).then_inc(S["w_in"], 16)
                sp.dma_start(pos[:, :, :], d["pos"].rearrange("(t p) k -> p t k", p=P)).then_inc(S["pos_in"], 16)
                def stack(b):
                    sp.wait_ge(S["lo_ready"], 2 * b + 2)
                    tokens = slice(b * SEQ, (b + 1) * SEQ)
                    for j in range(3):
                        sp.dma_start(scratch[j, :, :, tokens].rearrange("k (c p) n -> p (k c) n", p=P),
                                     part(j, b)[:, :, :, :].rearrange("p k i n -> p k (i n)")).then_inc(spilled[b], 16)
                    sp.wait_ge(spilled[b], 3 * 16)
                    if b == 0:
                        sp.wait_ge(S["q_zero"], NBUF)
                        sp.wait_ge(S["k_zero"], NBUF)
                        for n in range(NBUF):
                            sp.dma_start(k_stack[SHIFT:SHIFT + 1, n, :, :], d["row_of_ones"].rearrange("(a h n) -> a h n", a=1, h=NH)
                                         ).then_inc(S["row_set"], 16)
                    if b >= NBUF:
                        sp.wait_ge(S["st_done"], NG * (b - NBUF + 1))
                        sp.dma_start(q_stack[SHIFT:SHIFT + 1, b % NBUF, :, :], d["row_of_zeros"].rearrange(
                            "(a h n) -> a h n", a=1, h=NH)).then_inc(S["rows_clear"], 16)
                    for kind, stack, which in ((0, q_stack, Q_PARTS), (1, k_stack, K_PARTS)):
                        for slot, j in enumerate(which):
                            sp.dma_start(stack[slot * HD:(slot + 1) * HD, b % NBUF, :, :],
                                         scratch[j, kind, :, tokens].rearrange("(h d) n -> d h n", d=HD)
                                         ).then_inc(stacked[b], 16)

                def place_shift(b):
                    sp.wait_ge(S["shift_ready"], b + 1)
                    sp.dma_start(scratch_shift[b], shift[:, b % 2, :]).then_inc(shifted[b], 16)
                    sp.wait_ge(shifted[b], 16)
                    if b >= NBUF:
                        sp.wait_ge(S["rows_clear"], 16)
                    sp.dma_start(q_stack[SHIFT:SHIFT + 1, b % NBUF, :, :], scratch_shift[b:b + 1]).then_inc(shifted[b], 16)

                for b in range(NBUF):
                    stack(b)
                place_shift(0)
                for b in range(NBUF, NB):
                    stack(b)
                for b in range(1, NB):
                    place_shift(b)

            @block.tensor
            def _(pe):
                s.norm_tensor(pe)
                pe.wait_ge(S["w_in"], 5 * 16)
                pe.wait_ge(s.xnT_ready, 4)

                def project(t):
                    await_count(pe, S["crossed_r"], t - 1)
                    await_count(pe, S["v_ready"], t - 1)
                    for c in range(DC):
                        pe.matmul(bank[:, t % 2, 0:DM], core.xnT[:, c, t * P:(t + 1) * P], wq[:, c, :],
                                         start=c == 0, stop=c == DC - 1)
                    pe.matmul(bank[:, t % 2, DM:2 * DM], ctxT[:, t * P:(t + 1) * P], wkv[:, 0:DM], start=True, stop=True
                              ).then_inc(S["qk_done"], 1)
                    pe.matmul(bank[:, 2 + t % 2, 0:DM], ctxT[:, t * P:(t + 1) * P], wkv[:, DM:2 * DM], start=True, stop=True
                              ).then_inc(S["values_done"], 1)

                def turn(t):
                    pe.wait_ge(S["roped"], t + 1)
                    await_count(pe, S["rest_ready"], t - 1)
                    for k in range(4):
                        last = pe.transpose(bank[:, 4 + t % 2, k * P:(k + 1) * P], straight[:, t % 2, k * P:(k + 1) * P],
                                            core.ident[:, :])
                    last.then_inc(S["turned32"], 1)

                project(0)
                for t in range(NT):
                    if t + 1 < NT:
                        project(t + 1)
                    turn(t)
                pe.wait_ge(S["rest_ready"], NT)
                pe.wait_ge(S["v_ready"], NT)

                def find(b, g, first_bank=0):
                    await_count(pe, S["top_done"], NG * b + g - (b == 0))
                    for k in range(2):
                        for q in range(2):
                            last = pe.matmul(bank[:, first_bank + k, q * SEQ:(q + 1) * SEQ],
                                             q_stack[:, b % NBUF, 2 * g + k, q * P:(q + 1) * P],
                                             k_stack[:, b % NBUF, 2 * g + k, :], start=True, stop=True)
                    last.then_inc(S["s_done"], 1)

                def turn_tops(b):
                    pe.wait_ge(S["top_done"], NG * (b + 1))
                    for q in range(2):
                        last = pe.transpose(bank[0:NH, 0, q * P:(q + 1) * P], tops[:, b % 2, q, :], core.ident[:, :])
                    last.then_inc(S["top_turned"], 1)

                def scores(b, g):
                    await_count(pe, S["exp_done"], NG * b + g - 1)
                    for j in range(2):
                        for kt in range(2):
                            last = pe.matmul(bank[:, 2 + 2 * (g % 2) + j, kt * SEQ:(kt + 1) * SEQ],
                                             k_stack[:, b % NBUF, 2 * g + j, kt * P:(kt + 1) * P],
                                             q_stack[:, b % NBUF, 2 * g + j, :], start=True, stop=True)
                    last.then_inc(S["st_done"], 1)

                def weigh(b, g):
                    u = g // 2
                    pe.wait_ge(S["exp_done"], NG * b + g + 1)
                    if g % 2 == 0:
                        await_count(pe, S["attn_ready"], NQ * b + u - 1)
                    for j in range(2):
                        row = 32 * ((2 * g + j) % QUAD)
                        for kt in range(2):
                            last = pe.matmul(bank[row:row + VW, 6 + u % 2, 0:SEQ], values[:, 2 * b + kt, 2 * g + j, :],
                                             prob[:, g % 2, 2 * j + kt, :], start=kt == 0, stop=kt == 1)
                    last.then_inc(S["av_done"], 1)

                def turn_quad(b, u):
                    pe.wait_ge(S["outT_ready"], NQ * b + u + 1)
                    for q in range(2):
                        last = pe.transpose(bank[:, 6 + u % 2, SEQ + q * P:SEQ + (q + 1) * P],
                                            outT[:, u % 2, q * P:(q + 1) * P], core.ident[:, :])
                    last.then_inc(S["quad_turned"], 1)

                pe.wait_ge(stacked[0], 12 * 16)
                pe.wait_ge(S["row_set"], NBUF * 16)
                for g in range(NG):
                    find(0, g, 2 * (g % 2))
                turn_tops(0)
                pe.wait_ge(S["banks_clear"], 1)
                for b in range(NB):
                    ahead = b + 1 < NB
                    if ahead:
                        pe.wait_ge(stacked[b + 1], 12 * 16)
                        if b + 1 >= NBUF:
                            pe.wait_ge(S["rows_clear"], 16)
                        pe.wait_ge(S["shift_ready"], b + 1)
                    pe.wait_ge(shifted[b], 2 * 16)
                    scores(b, 0)
                    scores(b, 1)
                    for g in range(NG):
                        if ahead:
                            find(b + 1, g)
                        if g >= 2 and g % 2 == 0:
                            turn_quad(b, g // 2 - 1)
                        weigh(b, g)
                        if g + 2 < NG:
                            scores(b, g + 2)
                    if ahead:
                        turn_tops(b + 1)
                    turn_quad(b, NQ - 1)
                for t in range(NT):
                    pe.wait_ge(S["attn_ready"], NQ * (t // 2 + 1))
                    await_count(pe, S["attnT_ready"], t - 1)
                    for c in range(DC):
                        last = pe.transpose(bank[:, t % 2, c * P:(c + 1) * P], attn[:, t, c * P:(c + 1) * P], core.ident[:, :])
                    last.then_inc(S["attn_turned"], 1)
                    pe.wait_ge(S["attnT_ready"], t + 1)
                    await_count(pe, S["added"], t - 1)
                    for c in range(DC):
                        pe.matmul(bank[:, 2 + t % 2, 0:DM], attnT[:, t % 2, c, :], wout[:, c, :], start=c == 0, stop=False)
                    pe.matmul(bank[:, 2 + t % 2, 0:DM], core.ones[0:1, :], bout[:, :], start=False, stop=True
                              ).then_inc(S["out_done"], 1)

            @block.scalar
            def _(act):
                s.norm_scalar(act)
                act.wait_ge(S["step"], ANGLE_STEPS)
                act.activation(trig[:, :, :, :], angle[:, :, :, :], ACT.Sin).then_inc(S["trig_done"], 1)

                def bring(t):
                    act.wait_ge(S["turned32"], t + 1)
                    b, i = t // 2, t % 2
                    if b >= 2:
                        act.wait_ge(spilled[b - 2], 3 * 16)
                    act.copy(part(0, b)[:, :, i, :], bank[:, 4 + t % 2, :].rearrange("p (k n) -> p k n", k=4)
                             ).then_inc(S["hi_ready"], 1)

                def middle(t):
                    act.wait_ge(S["rest_ready"], t + 1)
                    act.copy(part(1, t // 2)[:, :, t % 2, :], rest[:, t % 2, :, :]).then_inc(S["mid_ready"], 1)

                zeros = outT[:, 0, 0:1].to_broadcast([P, NH * SEQ // 2])
                act.wait_ge(S["zero_set"], 1)
                for n in range(NBUF):
                    act.copy(k_stack[:, n, :, :].rearrange("p h n -> p (h n)").bitcast(F32), zeros).then_inc(S["k_zero"], 1)
                act.wait_ge(S["ones_set"], 1)
                for t in range(NT):
                    act.wait_ge(S["values_done"], t + 1)
                    act.copy(values[:, t, :, 0:HD], bank[:, 2 + t % 2, 0:DM].rearrange("p (h d) -> p h d", d=HD)
                             ).then_inc(S["v_ready"], 1)
                    if t >= 1:
                        bring(t - 1)
                    if t >= 2:
                        middle(t - 2)
                bring(NT - 1)
                middle(NT - 2)
                middle(NT - 1)

                def negate(b):
                    act.wait_ge(S["top_turned"], b + 1)
                    if b >= 2:
                        act.wait_ge(shifted[b - 2], 2 * 16)
                    act.activation(shift[:, b % 2, :], bank[0:NH, 0, 0:SEQ], ACT.Copy, scale=-1.0
                                   ).then_inc(S["shift_ready"], 1)

                def exps(b, i, k):
                    n = 4 * i + (NG * b + k)
                    act.wait_ge(S["st_done"], n + 1)
                    await_count(act, S["av_done"], n - 1)
                    act.activation(prob[:, k % 2, :, :], bank[:, 2 + 2 * (k % 2):4 + 2 * (k % 2), :].rearrange(
                        "p j (t n) -> p (j t) n", t=2), ACT.Exp, scale=SCALE).then_inc(S["exp_done"], 1)

                def bring_quad(b, i, k):
                    n = 2 * i + (NQ * b + k)
                    act.wait_ge(S["av_done"], 2 * n + 2)
                    await_count(act, S["quad_turned"], n - 1)
                    act.copy(outT[:, k % 2, :], bank[:, 6 + k % 2, 0:SEQ]).then_inc(S["outT_ready"], 1)

                def four_pairs(b, i, first=False):
                    exps(b, i, 0)
                    if not first:
                        bring_quad(b, i, -1)
                    exps(b, i, 1)
                    exps(b, i, 2)
                    bring_quad(b, i, 0)
                    exps(b, i, 3)

                negate(0)
                for b in range(NB):
                    four_pairs(b, 0, True)
                    with act.Fori(1, NG // 4) as i:
                        four_pairs(b, i)
                    bring_quad(b, NQ // 2, -1)
                    if b + 1 < NB:
                        negate(b + 1)
                for t in range(NT):
                    act.wait_ge(S["attn_turned"], t + 1)
                    if t >= 2:
                        act.wait_ge(S["out_done"], t - 1)
                    act.copy(attnT[:, t % 2, :, :], bank[:, t % 2, 0:DM].rearrange("p (c n) -> p c n", c=DC)
                             ).then_inc(S["attnT_ready"], 1)

            @block.gpsimd
            def _(pool):
                pool.memset(values[:, :, :, HD:VW], 1.0).then_inc(S["ones_set"], 1)
                for n in range(NBUF):
                    pool.memset(q_stack[:, n, :, :].bitcast(mybir.dt.uint32), 0).then_inc(S["q_zero"], 1)

                def split(t):
                    b, i = t // 2, t % 2
                    pool.wait_ge(S["mid_ready"], t + 1)
                    pool.tensor_tensor(part(2, b)[:, :, i, :], rest[:, i, :, :], part(1, b)[:, :, i, :], ALU.subtract
                                       ).then_inc(S["lo_ready"], 1)

                for t in range(NT):
                    pool.wait_ge(S["crossed_r"], t + 1)
                    pool.tensor_tensor(straight[:, t % 2, :], straight[:, t % 2, :], crossed[:, t % 2, :], ALU.add
                                       ).then_inc(S["roped"], 1)
                    if t >= 1:
                        split(t - 1)
                split(NT - 1)

            @block.vector
            def _(dve):
                steps = [0]

                def chain(ins):
                    steps[0] += 1
                    ins.then_inc(S["step"], 1)
                    dve.wait_ge(S["step"], steps[0])

                dve.memset(outT[:, 0, 0:1], 0.0).then_inc(S["zero_set"], 1)
                dve.memset(bank[:, 6:8, 0:SEQ], 0.0).then_inc(S["banks_clear"], 1)
                s.norm_vector(dve)
                dve.wait_ge(S["pos_in"], 16)
                sines = angle[:, :, 0, :].rearrange("p t (k f) -> p t k f", f=2)
                for f in range(2):
                    ins = dve.tensor_scalar(sines[:, :, :, f], pos[:, :, :], FREQS[f], None, ALU.mult)
                chain(ins)
                chain(dve.tensor_scalar(angle[:, :, 1, :], angle[:, :, 0, :], float(np.pi) / 2, None, ALU.add))
                chain(dve.tensor_scalar(turns[:, :, :, :], angle[:, :, :, :], 0.5 / float(np.pi), ROUND, ALU.mult, ALU.add))
                chain(dve.tensor_scalar(turns[:, :, :, :], turns[:, :, :, :], ROUND, None, ALU.subtract))
                for c in (TURN_HI, TURN_LO):
                    chain(dve.scalar_tensor_tensor(angle[:, :, :, :], turns[:, :, :, :], -c, angle[:, :, :, :],
                                                   ALU.mult, ALU.add))
                chain(dve.tensor_scalar(angle[:, :, :, :], angle[:, :, :, :], PI, -PI, ALU.min, ALU.max))
                dve.wait_ge(S["trig_done"], 1)
                pairs = lambda a: a.rearrange("p t (k two) -> p t k two", two=2)
                for e in range(2):
                    dve.tensor_copy(pairs(cos8[:, :, :])[:, :, :, e], trig[:, :, 1, :])
                    ins = dve.tensor_scalar(pairs(sin8[:, :, :])[:, :, :, e], trig[:, :, 0, :], (-1.0, 1.0)[e], None, ALU.mult)
                chain(ins)

                def rotate(t):
                    await_count(dve, S["turned32"], t - 1)
                    await_count(dve, S["roped"], t - 1)
                    dve.wait_ge(S["qk_done"], t + 1)
                    for k in range(2):
                        heads = lambda a: a.rearrange("p (h n) -> p h n", n=HD)
                        src = bank[:, t % 2, k * DM:(k + 1) * DM]
                        wide = lambda a: a.unsqueeze(1).to_broadcast([P, NH, a.shape[-1]])
                        dve.tensor_tensor(heads(straight[:, t % 2, k * DM:(k + 1) * DM]), heads(src),
                                          wide(cos8[:, t, :]), ALU.mult)
                        for e in range(2):
                            at = lambda a, e: a.rearrange("p (h n two) -> p h n two", two=2, n=HD // 2)[:, :, :, e]
                            last = dve.tensor_tensor(at(crossed[:, t % 2, k * DM:(k + 1) * DM], e), at(src, 1 - e),
                                                     wide(sin8[:, t, :].rearrange("p (n two) -> p n two", two=2)[:, :, e]),
                                                     ALU.mult)
                    last.then_inc(S["crossed_r"], 1)

                def remainder(t):
                    dve.wait_ge(S["hi_ready"], t + 1)
                    await_count(dve, S["lo_ready"], t - 1)
                    dve.tensor_tensor(rest[:, t % 2, :, :], bank[:, 4 + t % 2, :].rearrange("p (k n) -> p k n", k=4),
                                      part(0, t // 2)[:, :, t % 2, :], ALU.subtract).then_inc(S["rest_ready"], 1)

                for t in range(NT):
                    rotate(t)
                    if t >= 1:
                        remainder(t - 1)
                remainder(NT - 1)

                def top(b, g, first_bank=0):
                    n = NG * b + g
                    dve.wait_ge(S["s_done"], n + 1)
                    dve.tensor_reduce(tops[:, b % 2, :, bass.ds(2 * g, 2)].rearrange("p q h -> p h q"),
                                      bank[:, first_bank:first_bank + 2, :].rearrange("p h (q n) -> p h q n", q=2), AX.X, ALU.max
                                      ).then_inc(S["top_done"], 1)

                def normalise(b, i, k):
                    n = 2 * i + (NQ * b + k)
                    dve.wait_ge(S["quad_turned"], n + 1)
                    heads = bank[:, 6 + k, SEQ:2 * SEQ].rearrange("p (q h n) -> p q h n", q=2, n=32)
                    dve.reciprocal(inverse[:, k, :, :], heads[:, :, :, HD]).then_inc(S["inv_done"], 1)
                    dve.wait_ge(S["inv_done"], n + 1)
                    dve.tensor_tensor(attn[:, 2 * b:2 * b + 2, bass.ds((2 * i + k) * 32, 32)].rearrange(
                        "p q (h n) -> p q h n", n=HD), heads[:, :, :, 0:HD],
                        inverse[:, k, :, :].unsqueeze(3).to_broadcast([P, 2, QUAD, HD]), ALU.mult
                                      ).then_inc(S["attn_ready"], 1)

                with dve.Fori(0, NG // 2) as i:
                    for k in range(2):
                        top(0, 2 * i + k, 2 * k)
                for b in range(NB):
                    ahead = b + 1 < NB
                    if ahead and b >= 1:
                        dve.wait_ge(S["top_turned"], b)
                    with dve.Fori(0, NG // 4) as i:
                        for k in range(2):
                            if ahead:
                                top(b + 1, 4 * i + 2 * k)
                                top(b + 1, 4 * i + 2 * k + 1)
                            if k == 1:
                                normalise(b, i, 0)
                        normalise(b, i, 1)
                for t in range(NT):
                    dve.wait_ge(S["out_done"], t + 1)
                    dve.scalar_tensor_tensor(core.X[:, t, :], bank[:, 2 + t % 2, 0:DM], gate, core.X[:, t, :],
                                             ALU.mult, ALU.add).then_inc(S["added"], 1)


def stage_moe(core):
    nc, d = core.nc, core.dram
    NE, FF = 8, 512
    JC = FF // P
    with core.stage("moe") as s:
        wR, rank8 = s.sb("wR", [P, DC, NE]), s.sb("rank8", [P, NE])
        lg, e8, rest, rank, hot, hot2, coef = (s.sb(n, [P, NT, NE]) for n in (
            "lg", "e8", "rest", "rank", "hot", "hot2", "coef"))
        m1, emax, esec, top, total = (s.sb(n, [P, NT]) for n in ("m1", "emax", "esec", "top", "total"))
        wup = s.sb("wup", [P, 2, DC, 2 * FF])
        wdn = s.sb("wdn", [P, 2, JC, DM])
        silu = s.sb("silu", [P, 2, HALF])
        act_f = s.sb("act_f", [P, 2, JC, HALF])
        acc = s.sb("acc", [P, NT, DM])
        loaded, logits, shifted, exps, chained = (s.sem(n) for n in ("loaded", "logits", "shifted", "exps", "chained"))
        up_in = [s.sem(f"up_in{k}") for k in range(2)]
        down_in = [s.sem(f"down_in{k}") for k in range(2)]
        gate_up, silu_done, mixed, down_done, added = (s.sem(n) for n in (
            "gate_up", "silu_done", "mixed", "down_done", "added"))
        bank = core.bank
        lgp = bank[:, 4, 0:NT * NE].rearrange("p (t e) -> p t e", e=NE)
        gate = core.gates[:, 6:7]
        STEPS = 2 * JC
        NBK = NT // 2

        with nc.Block() as block:
            @block.sync
            def _(sp):
                sp.dma_start(wR[:, :, :], d["l2_gate"].rearrange("(c p) e -> p c e", p=P)).then_inc(loaded, 16)
                sp.dma_start(rank8[:, :], d["rank8"]).then_inc(loaded, 16)

                def load(e, k):
                    sp.dma_start(wup[:, k, :, :], d["l2_up"][bass.ds(e, 1)].rearrange("e (c p) f -> p (e c) f", p=P)
                                 ).then_inc(up_in[k], 16)
                    sp.dma_start(wdn[:, k, :, :], d["l2_down"][bass.ds(e, 1)].rearrange("e (c p) f -> p (e c) f", p=P)
                                 ).then_inc(down_in[k], 16)
                for k in range(2):
                    load(k, k)
                with sp.Fori(1, NE // 2) as i:
                    for k in range(2):
                        sp.wait_ge(gate_up, 2 * STEPS * i + STEPS * (k - 1))
                        sp.wait_ge(down_done, NT * i + NBK * (k - 1))
                        load(2 * i + k, k)

            @block.tensor
            def _(pe):
                s.norm_tensor(pe)
                pe.wait_ge(loaded, 2 * 16)
                pe.wait_ge(s.xnT_ready, 4)
                for t in range(NT):
                    for c in range(DC):
                        last = pe.matmul(lgp[:, t, :], core.xnT[:, c, t * P:(t + 1) * P], wR[:, c, :],
                                         start=c == 0, stop=c == DC - 1)
                last.then_inc(logits, 1)
                pe.wait_ge(shifted, 1)

                def gate_and_up(e, k, n, first):
                    h, j = n // JC, n % JC
                    if not (first and n < 2):
                        pe.wait_ge(mixed, e * STEPS + (n - 1))
                    for m in range(2):
                        for c in range(DC):
                            last = pe.matmul(bank[:, 4 + 2 * (n % 2) + m, :],
                                             wup[:, k, c, m * FF + j * P:m * FF + (j + 1) * P],
                                             core.xnT[:, c, h * HALF:(h + 1) * HALF], start=c == 0, stop=c == DC - 1)
                    last.then_inc(gate_up, 1)

                def down(e, k, h, first):
                    pe.wait_ge(mixed, e * STEPS + JC * (h + 1))
                    if not first:
                        pe.wait_ge(added, (e - 1) * NT + 4 * (h + 1))
                    for t in range(4 * h, 4 * h + 4):
                        for j in range(JC):
                            last = pe.matmul(bank[:, t // 2, (t % 2) * DM:(t % 2 + 1) * DM],
                                             act_f[:, h, j, (t % 4) * P:(t % 4 + 1) * P], wdn[:, k, j, :],
                                             start=j == 0, stop=j == JC - 1)
                        if t % 2 == 1:
                            last.then_inc(down_done, 1)

                def expert(i, k, first):
                    e = 2 * i + k
                    pe.wait_ge(up_in[k], 16 * i + 16)
                    pe.wait_ge(down_in[k], 16 * i + 16)
                    for n in range(JC + 2):
                        gate_and_up(e, k, n, first and k == 0)
                    down(e, k, 0, first and k == 0)
                    for n in range(JC + 2, STEPS):
                        gate_and_up(e, k, n, False)
                    down(e, k, 1, first and k == 0)

                for k in range(2):
                    expert(0, k, True)
                with pe.Fori(1, NE // 2) as i:
                    for k in range(2):
                        expert(i, k, False)

            @block.scalar
            def _(act):
                s.norm_scalar(act)
                act.wait_ge(shifted, 1)
                act.activation(e8[:, :, :], lg[:, :, :], ACT.Exp).then_inc(exps, 1)

                def silu_of(e, n, first):
                    act.wait_ge(gate_up, e * STEPS + (n + 1))
                    if not (first and n < 2):
                        act.wait_ge(mixed, e * STEPS + (n - 1))
                    act.activation(silu[:, n % 2, :], bank[:, 4 + 2 * (n % 2), :], ACT.Silu).then_inc(silu_done, 1)

                for n in range(STEPS):
                    silu_of(0, n, True)
                with act.Fori(1, NE) as e:
                    for n in range(STEPS):
                        silu_of(e, n, False)

            @block.vector
            def _(dve):
                links = [0]

                def chain(ins):
                    links[0] += 1
                    ins.then_inc(chained, 1)
                    dve.wait_ge(chained, links[0])

                s.norm_vector(dve)
                wide = lambda a: a.unsqueeze(2).to_broadcast([P, NT, NE])
                ranks = rank8[:, :].unsqueeze(1).to_broadcast([P, NT, NE])
                dve.wait_ge(loaded, 2 * 16)
                dve.wait_ge(logits, 1)
                chain(dve.tensor_copy(lg[:, :, :], lgp))
                chain(dve.tensor_reduce(m1[:, :], lg[:, :, :], AX.X, ALU.max))
                dve.tensor_tensor(lg[:, :, :], lg[:, :, :], wide(m1[:, :]), ALU.subtract).then_inc(shifted, 1)
                dve.wait_ge(exps, 1)
                chain(dve.tensor_reduce(emax[:, :], e8[:, :, :], AX.X, ALU.max))
                one_hot_max(dve, s, chain, e8[:, :, :], emax[:, :], ranks, rank[:, :, :], top[:, :], hot[:, :, :])
                chain(dve.scalar_tensor_tensor(rest[:, :, :], hot[:, :, :], -2.0, e8[:, :, :], ALU.mult, ALU.add))
                chain(dve.tensor_reduce(esec[:, :], rest[:, :, :], AX.X, ALU.max))
                one_hot_max(dve, s, chain, rest[:, :, :], esec[:, :], ranks, rank[:, :, :], top[:, :], hot2[:, :, :])
                chain(dve.tensor_tensor(total[:, :], emax[:, :], esec[:, :], ALU.add))
                chain(dve.reciprocal(total[:, :], total[:, :]))
                chain(dve.tensor_tensor(hot[:, :, :], hot[:, :, :], hot2[:, :, :], ALU.add))
                chain(dve.tensor_tensor(hot[:, :, :], hot[:, :, :], e8[:, :, :], ALU.mult))
                chain(dve.tensor_tensor(coef[:, :, :], hot[:, :, :], wide(total[:, :]), ALU.mult))
                chain(dve.memset(acc[:, :, :], 0.0))

                def mix(e, n, first):
                    h, j = n // JC, n % JC
                    dve.wait_ge(silu_done, e * STEPS + (n + 1))
                    if not first and n % JC == 0:
                        dve.wait_ge(down_done, e * NBK + (2 * (h + 1) - NBK))
                    dve.tensor_tensor(act_f[:, h, j, :], bank[:, 5 + 2 * (n % 2), :], silu[:, n % 2, :],
                                      ALU.mult).then_inc(mixed, 1)

                def add(e, t, first):
                    dve.wait_ge(down_done, e * NBK + (t // 2 + 1))
                    if not first:
                        dve.wait_ge(added, e * NT + (t + 1 - NT))
                    dve.scalar_tensor_tensor(acc[:, t, :], bank[:, t // 2, (t % 2) * DM:(t % 2 + 1) * DM],
                                             coef[:, t, bass.ds(e, 1)], acc[:, t, :], ALU.mult, ALU.add).then_inc(added, 1)

                def expert(e, first):
                    for n in range(STEPS):
                        mix(e, n, first)
                    for t in range(NT):
                        add(e, t, first)

                expert(0, True)
                with dve.Fori(1, NE) as e:
                    expert(e, False)
                dve.wait_ge(added, NE * NT)
                for t in range(NT):
                    dve.scalar_tensor_tensor(core.X[:, t, :], acc[:, t, :], gate, core.X[:, t, :], ALU.mult, ALU.add)


def stage_smooth_quant(core):
    nc, d = core.nc, core.dram
    EPS, QMAX = 1e-6, 127.0
    CHUNKS = (DC, 1)
    with core.stage("sq") as s:
        wide = lambda r: CHUNKS[r] * P
        w_nat = [s.sb("w_nat", [P, NT, DM]), s.sb("ctx_nat", [P, NT, CTX])]
        w_turn = [s.sb("w_turn", [P, DC, NTOK]), s.sb("ctx_turn", [P, 1, NTOK])]
        a_nat = s.sb("a_nat", [P, NT, CTX])
        x_nat = [core.xn, a_nat]
        amax_x = [s.sb(f"amax_x{r}", [P, CHUNKS[r] * NB]) for r in range(2)]
        amax_w = [s.sb(f"amax_w{r}", [P, CHUNKS[r] * NB]) for r in range(2)]
        smooth = [s.sb(f"smooth{r}", [P, CHUNKS[r] * NB]) for r in range(2)]
        inverse = [s.sb(f"inverse{r}", [P, CHUNKS[r] * NB]) for r in range(2)]
        diag = s.sb("diag", [P, NT, P])
        diag_inv = s.sb("diag_inv", [P, NT, P])
        inverse_row = [s.sb(f"inverse_row{r}", [P, NB, wide(r)]) for r in range(2)]
        x_mult = [s.sb(f"x_mult{r}", [P, NT]) for r in range(2)]
        w_mult = [s.sb(f"w_mult{r}", [P, NT]) for r in range(2)]
        smooth_row = [s.sb(f"smooth_row{r}", [P, NB, wide(r)]) for r in range(2)]
        x_scale = [s.sb(f"x_scale{r}", [P, NT]) for r in range(2)]
        w_scale = [s.sb(f"w_scale{r}", [P, NT]) for r in range(2)]
        w_scale_row = [s.sb(f"w_scale_row{r}", [P, NTOK]) for r in range(2)]
        xq = [s.sb(f"xq{r}", [P, NT, wide(r)], BF16) for r in range(2)]
        wq = [s.sb(f"wq{r}", [P, NT, wide(r)], BF16) for r in range(2)]
        xqT = [s.sb(f"xqT{r}", [P, CHUNKS[r], NTOK], BF16) for r in range(2)]
        wqT = [s.sb(f"wqT{r}", [P, CHUNKS[r], NTOK], BF16) for r in range(2)]
        hidden = s.sb("hidden", [P, NT, DM])
        silu = s.sb("silu", [P, NT, CTX])
        scaled = s.sb("scaled", [P, 2, DM])
        w_in, c_in, step = s.sem("w_in"), s.sem("c_in"), s.sem("step")
        both = lambda n: [s.sem(f"{n}{r}") for r in range(2)]
        ratio, root, diag_s, row_s, rowcopy_s, diag_w, row_w, rowcopy_w = (both(n) for n in (
            "ratio", "root", "diag_s", "row_s", "rowcopy_s", "diag_w", "row_w", "rowcopy_w"))
        x_int, w_int, x_turned, w_turned, x_back, w_back = (both(n) for n in (
            "x_int", "w_int", "x_turned", "w_turned", "x_back", "w_back"))
        product, used = both("product"), both("used")
        silu_done, a_ready, a_turned, times = (s.sem(n) for n in (
            "silu_done", "a_ready", "a_turned", "times"))
        bank = core.bank
        gate = core.gates[:, 3:4]
        half_bf = lambda b: bank[:, b, :].bitcast(BF16)
        XB, WB = ((4, 5), (6,)), ((6, 7), (7,))

        with nc.Block() as block:
            @block.sync
            def _(sp):
                sp.dma_start(w_turn[0][:, :, :], d["l3x_wT"].rearrange("(c p) n -> p c n", p=P)).then_inc(w_in, 16)
                sp.dma_start(w_nat[0][:, :, :], d["l3x_w"].rearrange("(t p) n -> p t n", p=P)).then_inc(w_in, 16)
                sp.dma_start(w_turn[1][:, :, :], d["ctxT"].rearrange("(c p) n -> p c n", p=P)).then_inc(c_in, 16)
                sp.dma_start(w_nat[1][:, :, :], d["ctx"].rearrange("(t p) n -> p t n", p=P)).then_inc(c_in, 16)

            @block.tensor
            def _(pe):
                s.norm_tensor(pe)
                pe.wait_ge(s.xnT_ready, 4)

                def quantised(r):
                    C = CHUNKS[r]
                    pe.wait_ge(diag_s[r], 1)
                    for h in range(C):
                        pe.matmul(bank[:, h, :], core.ones[:, :], diag[:, 4 * h:4 * h + 4, :], start=True, stop=True)
                        last = pe.matmul(bank[:, 2 + h, :], core.ones[:, :], diag_inv[:, 4 * h:4 * h + 4, :],
                                         start=True, stop=True)
                    last.then_inc(row_s[r], 1)
                    for ints, turned, dst, banks in ((x_int, x_turned, xq, XB), (w_int, w_turned, wq, WB)):
                        pe.wait_ge(ints[r], 1)
                        for c in range(C):
                            for t in range(NT):
                                last = pe.transpose(half_bf(banks[r][c])[:, t * P:(t + 1) * P],
                                                    dst[r][:, t, c * P:(c + 1) * P], core.identh[:, :])
                        last.then_inc(turned[r], 1)
                    pe.wait_ge(diag_w[r], 1)
                    pe.wait_ge(rowcopy_s[r], 2)
                    for h in range(2):
                        last = pe.matmul(bank[:, 2 + h, :], core.ones[:, :], diag[:, 4 * h:4 * h + 4, :], start=True, stop=True)
                    last.then_inc(row_w[r], 1)
                    pe.wait_ge(x_back[r], 1)
                    pe.wait_ge(w_back[r], 1)
                    for t in range(NT):
                        b = t // 2
                        if t >= 2:
                            pe.wait_ge(used[r], t - 1)
                        for c in range(C):
                            last = pe.matmul(bank[:, t % 2, 0:DM], xqT[r][:, c, t * P:(t + 1) * P],
                                             wqT[r][:, c, b * DM:(b + 1) * DM], start=c == 0, stop=c == C - 1)
                        last.then_inc(product[r], 1)

                quantised(0)
                pe.wait_ge(a_ready, 1)
                for t in range(NT):
                    last = pe.transpose(bank[:, 4 + t // 4, (t % 4) * P:(t % 4 + 1) * P], a_nat[:, t, :], core.ident[:, :])
                last.then_inc(a_turned, 1)
                quantised(1)

            @block.scalar
            def _(act):
                s.norm_scalar(act)

                def quantised(r):
                    C = CHUNKS[r]
                    act.wait_ge(ratio[r], 1)
                    act.activation(smooth[r][:, :], amax_x[r][:, :], ACT.Sqrt).then_inc(root[r], 1)
                    act.wait_ge(row_s[r], 1)
                    act.copy(smooth_row[r][:, :, :].rearrange("p b n -> p (b n)").rearrange("p (h n) -> p h n", h=C),
                             bank[:, 0:C, :]).then_inc(rowcopy_s[r], 1)
                    act.copy(inverse_row[r][:, :, :].rearrange("p b n -> p (b n)").rearrange("p (h n) -> p h n", h=C),
                             bank[:, 2:2 + C, :]).then_inc(rowcopy_s[r], 1)
                    act.wait_ge(x_turned[r], 1)
                    act.copy(xqT[r][:, :, :], half_bf_banks(XB[r])).then_inc(x_back[r], 1)
                    act.wait_ge(w_turned[r], 1)
                    act.copy(wqT[r][:, :, :], half_bf_banks(WB[r])).then_inc(w_back[r], 1)
                    act.wait_ge(row_w[r], 1)
                    act.copy(w_scale_row[r][:, :].rearrange("p (h n) -> p h n", h=2), bank[:, 2:4, :]).then_inc(rowcopy_w[r], 1)

                half_bf_banks = lambda bs: bank[:, bs[0]:bs[-1] + 1, :].bitcast(BF16)
                quantised(0)
                act.wait_ge(used[0], NT)
                act.activation(silu[:, :, :], hidden[:, :, 0:CTX], ACT.Silu).then_inc(silu_done, 1)
                quantised(1)

            @block.vector
            def _(dve):
                steps = [0]

                def chain(ins):
                    steps[0] += 1
                    ins.then_inc(step, 1)
                    dve.wait_ge(step, steps[0])

                def diagonals(dst, n, column):
                    for k in range(n):
                        last = dve.tensor_scalar(dst[:, k, :], core.ident[:, :], column(k), None, ALU.mult)
                    return last

                def quantised(r, turned_x):
                    C = CHUNKS[r]
                    chain(dve.tensor_reduce(amax_x[r][:, :], turned_x, AX.X, ALU.max, apply_absolute_value=True))
                    chain(dve.tensor_reduce(amax_w[r][:, :], w_turn[r][:, :, :].rearrange("p c (b n) -> p (c b) n", b=NB),
                                            AX.X, ALU.max, apply_absolute_value=True))
                    chain(dve.tensor_scalar(amax_w[r][:, :], amax_w[r][:, :], EPS, None, ALU.max))
                    chain(dve.tensor_scalar(amax_x[r][:, :], amax_x[r][:, :], EPS, None, ALU.max))
                    chain(dve.reciprocal(amax_w[r][:, :], amax_w[r][:, :]))
                    dve.tensor_tensor(amax_x[r][:, :], amax_x[r][:, :], amax_w[r][:, :], ALU.mult).then_inc(ratio[r], 1)
                    dve.wait_ge(root[r], 1)
                    chain(dve.tensor_scalar(smooth[r][:, :], smooth[r][:, :], EPS, None, ALU.max))
                    chain(dve.reciprocal(inverse[r][:, :], smooth[r][:, :]))
                    at = lambda k: slice((k % C) * NB + k // C, (k % C) * NB + k // C + 1)
                    diagonals(diag, NB * C, lambda k: smooth[r][:, at(k)])
                    diagonals(diag_inv, NB * C, lambda k: inverse[r][:, at(k)]).then_inc(diag_s[r], 1)
                    dve.wait_ge(rowcopy_s[r], 2)
                    shape = lambda a: a.rearrange("p (b i) n -> p b i n", b=NB)
                    for nat, ints, scale, mult, row, done in (
                            (x_nat[r], xq[r], x_scale[r], x_mult[r], inverse_row[r], x_int[r]),
                            (w_nat[r], wq[r], w_scale[r], w_mult[r], smooth_row[r], w_int[r])):
                        rows = row[:, :, :].unsqueeze(2).to_broadcast([P, NB, 2, wide(r)])
                        chain(dve.tensor_tensor(shape(nat[:, :, :]), shape(nat[:, :, :]), rows, ALU.mult))
                        chain(dve.tensor_reduce(scale[:, :], nat[:, :, :], AX.X, ALU.max, apply_absolute_value=True))
                        chain(dve.tensor_scalar(scale[:, :], scale[:, :], EPS, 1.0 / QMAX, ALU.max, ALU.mult))
                        chain(dve.reciprocal(mult[:, :], scale[:, :]))
                        for t in range(NT):
                            last = dve.tensor_scalar(nat[:, t, :], nat[:, t, :], mult[:, t:t + 1], ROUND, ALU.mult, ALU.add)
                        chain(last)
                        dve.tensor_scalar(ints[:, :, :], nat[:, :, :], ROUND, QMAX, ALU.subtract, ALU.min).then_inc(done, 1)
                    dve.wait_ge(row_s[r], 1)
                    diagonals(diag, NT, lambda k: w_scale[r][:, k:k + 1]).then_inc(diag_w[r], 1)
                    dve.wait_ge(rowcopy_w[r], 1)

                def rescale(r, t, dst):
                    dve.wait_ge(product[r], t + 1)
                    b = t // 2
                    return dve.scalar_tensor_tensor(dst, bank[:, t % 2, 0:DM], x_scale[r][:, t:t + 1],
                                                    w_scale_row[r][:, b * DM:(b + 1) * DM], ALU.mult, ALU.mult)

                s.norm_vector(dve)
                dve.wait_ge(s.xnT_ready, 4)
                dve.wait_ge(w_in, 2 * 16)
                quantised(0, core.xnT[:, :, :].rearrange("p c (b n) -> p (c b) n", b=NB))
                for t in range(NT):
                    rescale(0, t, hidden[:, t, :]).then_inc(used[0], 1)
                dve.wait_ge(silu_done, 1)
                dve.tensor_tensor(a_nat[:, :, :], silu[:, :, :], hidden[:, :, CTX:DM], ALU.mult).then_inc(a_ready, 1)
                dve.wait_ge(a_turned, 1)
                dve.wait_ge(c_in, 2 * 16)
                quantised(1, bank[:, 4:6, :].rearrange("p h (b n) -> p (h b) n", b=2))
                for t in range(NT):
                    if t >= 2:
                        dve.wait_ge(times, t - 1)
                    rescale(1, t, scaled[:, t % 2, :]).then_inc(used[1], 1)
                    dve.wait_ge(used[1], t + 1)
                    dve.scalar_tensor_tensor(core.X[:, t, :], scaled[:, t % 2, :], gate, core.X[:, t, :],
                                             ALU.mult, ALU.add).then_inc(times, 1)


def stage_fp8_ffn(core):
    nc, d = core.nc, core.dram
    FF = 768
    JC = FF // P
    F8 = mybir.dt.float8e4
    U8 = mybir.dt.uint8
    with core.stage("fp8") as s:
        wg, wu, wd = s.sb("wg", [P, DC * FF]), s.sb("wu", [P, DC * FF]), s.sb("wd", [P, JC * DM])
        NW = DC * FF
        low8, high8 = s.sb("low8", [P, NW], F8), s.sb("high8", [P, NW], F8)
        large, doubled = s.sb("large", [P, NW], U8), s.sb("doubled", [P, NW])
        gs, us, ds = s.sb("gs", [P, JC]), s.sb("us", [P, JC]), s.sb("ds", [P, DM])
        silu, fuse = s.sb("silu", [P, 2, HALF]), s.sb("fuse", [P, JC, NTOK])
        scaled = s.sb("scaled", [P, 2, DM])
        loaded = [s.sem(f"loaded{i}") for i in range(3)]
        scales, halved, step, rounded = s.sem("scales"), s.sem("halved"), s.sem("step"), s.sem("rounded")
        gate_up, silu_done, fused, out_done, times, added = (s.sem(n) for n in (
            "gate_up", "silu_done", "fused", "out_done", "times", "added"))
        bank = core.bank
        weights = [wg, wu, wd]
        w3 = [wg[:, :].rearrange("p (c f) -> p c f", c=DC), wu[:, :].rearrange("p (c f) -> p c f", c=DC),
              wd[:, :].rearrange("p (c f) -> p c f", c=JC)]
        gate = core.gates[:, 7:8]

        with nc.Block() as block:
            @block.sync
            def _(sp):
                for i, n in enumerate(("l3_gate", "l3_up", "l3_down")):
                    sp.dma_start(w3[i], d[n].rearrange("(c p) f -> p c f", p=P)).then_inc(loaded[i], 16)
                sp.dma_start(gs[:, :], d["l3_gate_scale"]).then_inc(scales, 16)
                sp.dma_start(us[:, :], d["l3_up_scale"]).then_inc(scales, 16)
                sp.dma_start(ds[:, :], d["l3_down_scale"].partition_broadcast(P)).then_inc(scales, 16)

            @block.tensor
            def _(pe):
                s.norm_tensor(pe)
                pe.wait_ge(rounded, 2)
                for h in range(2):
                    pe.wait_ge(s.xnT_ready, 2 * (h + 1))
                    for j in range(JC):
                        n = h * JC + j
                        if n >= 2:
                            pe.wait_ge(fused, n - 1)
                        for k in range(2):
                            for c in range(DC):
                                last = pe.matmul(bank[:, 4 + 2 * (n % 2) + k, :], w3[k][:, c, j * P:(j + 1) * P],
                                                 core.xnT[:, c, h * HALF:(h + 1) * HALF], start=c == 0, stop=c == DC - 1)
                        last.then_inc(gate_up, 1)
                pe.wait_ge(rounded, 3)
                pe.wait_ge(s.xnT_ready, 4)
                for t in range(NT):
                    pe.wait_ge(fused, JC * (t // 4 + 1))
                    for j in range(JC):
                        last = pe.matmul(bank[:, t // 2, (t % 2) * DM:(t % 2 + 1) * DM], fuse[:, j, t * P:(t + 1) * P],
                                         w3[2][:, j, :], start=j == 0, stop=j == JC - 1)
                    if t % 2 == 1:
                        last.then_inc(out_done, 1)

            @block.scalar
            def _(act):
                for i in range(3):
                    act.wait_ge(loaded[i], 16)
                    if i >= 1:
                        act.wait_ge(rounded, i)
                    act.activation(high8[:, :], weights[i][:, :], ACT.Copy, scale=0.5, saturate=False).then_inc(halved, 1)
                    if i == 0:
                        s.norm_scalar(act)
                act.wait_ge(scales, 3 * 16)
                for n in range(2 * JC):
                    act.wait_ge(gate_up, n + 1)
                    if n >= 2:
                        act.wait_ge(fused, n - 1)
                    act.activation(silu[:, n % 2, :], bank[:, 4 + 2 * (n % 2), :], ACT.Silu,
                                   scale=gs[:, n % JC:n % JC + 1]).then_inc(silu_done, 1)

            @block.vector
            def _(dve):
                steps = [0]

                def chain(ins):
                    steps[0] += 1
                    ins.then_inc(step, 1)
                    dve.wait_ge(step, steps[0])

                def round_weight(i):
                    dve.wait_ge(loaded[i], 16)
                    w = weights[i][:, :]
                    if i >= 1:
                        dve.wait_ge(rounded, i)
                    dve.tensor_scalar(low8[:, :], w, 240.0, -240.0, ALU.min, ALU.max, saturate=False)
                    chain(dve.scalar_tensor_tensor(doubled[:, :], w, -1.0, w, ALU.mult, ALU.max))
                    chain(dve.tensor_scalar(large[:, :], doubled[:, :], 128.0, None, ALU.is_ge))
                    dve.wait_ge(halved, i + 1)
                    chain(dve.tensor_scalar(doubled[:, :], high8[:, :], 2.0, None, ALU.mult))
                    chain(dve.tensor_copy(w, low8[:, :]))
                    dve.copy_predicated(w, large[:, :], doubled[:, :]).then_inc(rounded, 1)

                s.norm_vector(dve)
                for i in range(3):
                    round_weight(i)
                dve.wait_ge(scales, 3 * 16)
                for n in range(2 * JC):
                    dve.wait_ge(silu_done, n + 1)
                    j, h = n % JC, n // JC
                    dve.scalar_tensor_tensor(fuse[:, j, h * HALF:(h + 1) * HALF], bank[:, 5 + 2 * (n % 2), :],
                                             us[:, j:j + 1], silu[:, n % 2, :], ALU.mult, ALU.mult).then_inc(fused, 1)
                for t in range(NT):
                    dve.wait_ge(out_done, t // 2 + 1)
                    if t >= 2:
                        dve.wait_ge(added, t - 1)
                    dve.tensor_tensor(scaled[:, t % 2, :], bank[:, t // 2, (t % 2) * DM:(t % 2 + 1) * DM], ds[:, :],
                                      ALU.mult).then_inc(times, 1)
                    dve.wait_ge(times, t + 1)
                    dve.scalar_tensor_tensor(core.X[:, t, :], scaled[:, t % 2, :], gate, core.X[:, t, :],
                                             ALU.mult, ALU.add).then_inc(added, 1)


def build(nc, dram):
    with ExitStack() as ctx:
        core = Core(nc, ctx, dram)
        stage_setup(core)
        steps = (stage_ssm, stage_lora_moe, stage_attention_16, stage_bitnet,
                 stage_attention_32, stage_moe, stage_smooth_quant, stage_fp8_ffn)
        for k in STAGES:
            steps[k](core)
            if k == 3 and len(STAGES) > 6:
                core.clear_semaphores()
        stage_store(core)


def _layouts(np, i):
    flat = lambda a: a.reshape(-1, a.shape[-1])
    T = lambda a: a.T
    return {
        "x": flat(i["x"]),
        "ctx": flat(i["ctx_1024"]),
        "ctxT": T(flat(i["ctx_1024"])),
        "g_xattn": i["g_xattn"],
        "g_ffn": i["g_ffn"],
        "l0_A": T(flat(i["L0_ffn_A"])),
        "l0_B": i["L0_ffn_B"].transpose(0, 2, 1).reshape(-1, DM),
        "l0_Wr": T(i["L0_ffn_Wr"]),
        "l0_br": i["L0_ffn_br"],
        "l0x_in": T(i["L0_xattn_in_proj_w"]),
        "l0x_dt2": T(i["L0_xattn_dt_proj_w"]),
        "l0x_chan": np.concatenate([i["L0_xattn_conv_w"], i["L0_xattn_conv_b"].reshape(-1, 1),
                                    i["L0_xattn_dt_proj_b"].reshape(-1, 1), i["L0_xattn_D"].reshape(-1, 1),
                                    i["L0_xattn_A_log"], T(i["L0_xattn_x_proj_w"][8:40]),
                                    T(i["L0_xattn_x_proj_w"][0:8])], axis=1),
        "l1x_q": i["L1_xattn_Wq"].reshape(DM, 16, -1).transpose(1, 0, 2),
        "l1x_k": i["L1_xattn_Wk"].reshape(CTX, 16, -1).transpose(1, 0, 2),
        "l1x_vT": i["L1_xattn_Wv"].reshape(CTX, 16, -1).transpose(1, 2, 0),
        "l1x_o": i["L1_xattn_Wo"].reshape(16, -1, DM),
        "l1x_gains": T(np.stack([i["L1_xattn_gq"], i["L1_xattn_gk"]])),
        "l1_gate": T(i["L1_ffn_w_gate"]),
        "l1_up": T(i["L1_ffn_w_up"]),
        "l1_down": T(i["L1_ffn_w_down"]),
        "l2x_q": i["L2_xattn_Wq"],
        "l2x_kv": i["L2_xattn_Wkv"],
        "l2x_out": i["L2_xattn_Wout"],
        "l2x_bout": i["L2_xattn_bout"],
        "pos": flat(i["fside_BxSx2_0"]),
        "l2_gate": T(i["L2_ffn_gate_w"]),
        "l2_up": i["L2_ffn_w_up"].transpose(0, 2, 1),
        "l2_down": i["L2_ffn_w_down"].transpose(0, 2, 1),
        "l3x_w": flat(i["fside_BxS2xS2_0"]),
        "l3x_wT": T(flat(i["fside_BxS2xS2_0"])),
        "l3_gate": i["L3_ffn_gate_w"],
        "l3_up": i["L3_ffn_up_w"],
        "l3_down": i["L3_ffn_down_w"],
        "l3_gate_scale": T(i["L3_ffn_gate_scale"].reshape(-1, P)),
        "l3_up_scale": T(i["L3_ffn_up_scale"].reshape(-1, P)),
        "l3_down_scale": i["L3_ffn_down_scale"],
    }


def _constants(np):
    eye = np.eye(P, dtype=np.float32)
    h = np.ones((1, 1), np.float32)
    while h.shape[0] < P:
        h = np.block([[h, h], [h, -h]]).astype(np.float32)
    sel = np.zeros((96, 32, P), np.float32)
    for n in range(32):
        sel[[n, 32 + n, 64 + n], n, :] = 1.0
    return {"row_of_ones": np.ones(32 * SEQ, mybir.dt.np(BF16)), "row_of_zeros": np.zeros(32 * SEQ, mybir.dt.np(BF16)), "ident": eye, "identh": eye.astype(mybir.dt.np(BF16)), "hadamard": h,
            "rank8": np.broadcast_to(np.arange(8, 0, -1, dtype=np.float32), (P, 8)).copy(),
            "select3": sel.reshape(96, 32 * P).astype(mybir.dt.np(BF16))}


def kernel(**inputs):
    import numpy as _np
    import concourse.bacc as _bacc
    from concourse import mybir as _mybir
    from concourse.bass_utils import run_bass_kernel_spmd as _run

    nc = _bacc.Bacc("TRN2", target_bir_lowering=False, num_devices=1)
    arrays, dram = {}, {}
    for group in (_layouts(_np, {k: _np.asarray(v) for k, v in inputs.items()}), _constants(_np)):
        for name, a in group.items():
            a = _np.ascontiguousarray(a)
            arrays[f"in_{name}_dram"] = a
            dram[name] = nc.dram_tensor(f"in_{name}_dram", a.shape, _mybir.dt.from_np(a.dtype), kind="ExternalInput").ap()
    dram["out"] = nc.dram_tensor("out_0_dram", (NTOK, DM), F32, kind="ExternalOutput").ap()
    build(nc, dram)
    r = _run(nc, [arrays], core_ids=[0])
    return r.results[0]["out_0_dram"].reshape(NB, SEQ, DM)
```

```python
from contextlib import ExitStack

import numpy as np
import concourse.bass as bass
from concourse import mybir

ALU = mybir.AluOpType
ACT = mybir.ActivationFunctionType
AX = mybir.AxisListType
F32 = mybir.dt.float32
BF16 = mybir.dt.bfloat16
F16 = mybir.dt.float16

P = 128
NB, SEQ, DM = 4, 256, 256
NT = NB * SEQ // P
NTOK = NB * SEQ
DC = DM // P
CTX = 128
HALF = 512
LN_EPS = 1e-5
ROUND = 1.5 * 2.0 ** 23

STAGES = (0, 1, 2, 3, 4, 5, 6, 7)


def await_count(engine, semaphore, value):
    if isinstance(value, int) and value <= 0:
        return
    engine.wait_ge(semaphore, value)


class Core:

    def __init__(self, nc, ctx, dram):
        self.nc, self.dram = nc, dram
        sb = lambda name, shape, dt=F32: ctx.enter_context(nc.sbuf_tensor(name, shape, dt))
        self.X = sb("X", [P, NT, DM])
        self.xn = sb("xn", [P, NT, DM])
        self.xnT = sb("xnT", [P, DC, NTOK])
        self.stats = sb("stats", [P, NT, 6])
        self.meanvar = sb("meanvar", [P, NT, 2])
        self.rstd = sb("rstd", [P, NT])
        self.ident = sb("ident", [P, P])
        self.identh = sb("identh", [P, P], BF16)
        self.ones = sb("ones", [P, P])
        self.eps = sb("eps", [P, 1])
        self.gates = sb("gates", [P, 8])
        self.bank = ctx.enter_context(nc.psum_tensor("bank", [P, 8, HALF], F32))
        self.semaphores = []

    def stage(self, name):
        return Stage(self, name)

    def clear_semaphores(self):
        self.nc.all_engine_barrier()
        self.nc.clear_and_free_semaphores(self.semaphores)
        self.nc.all_engine_barrier()
        self.semaphores = []


class Stage:

    def __init__(self, core, name):
        self.core, self.nc, self.name = core, core.nc, name

    def __enter__(self):
        self.stack = ExitStack()
        self.stack.__enter__()
        self.stats_done = self.sem("stats_done")
        self.aggr_done = self.sem("aggr_done")
        self.root_done = self.sem("root_done")
        self.rstd_done = self.sem("rstd_done")
        self.xn_ready = self.sem("xn_ready")
        self.turned = self.sem("turned")
        self.xnT_ready = self.sem("xnT_ready")
        return self

    def __exit__(self, *e):
        return self.stack.__exit__(*e)

    def sb(self, name, shape, dt=F32):
        return self.stack.enter_context(self.nc.sbuf_tensor(f"{self.name}_{name}", shape, dt))

    def sem(self, name):
        self.core.semaphores.append(self.nc.alloc_semaphore(name=f"{self.name}_{name}"))
        return self.core.semaphores[-1]

    def norm_vector(self, dve):
        c = self.core
        halves = [range(h * NT // 2, (h + 1) * NT // 2) for h in range(2)]
        for tiles in halves:
            for t in tiles:
                dve.bn_stats(c.stats[:, t, :], c.X[:, t, :]).then_inc(self.stats_done, 1)
            for t in tiles:
                dve.wait_ge(self.stats_done, t + 1)
                dve.bn_aggr(c.meanvar[:, t, :], c.stats[:, t, :]).then_inc(self.aggr_done, 1)
        for h, tiles in enumerate(halves):
            cols = slice(tiles[0], tiles[-1] + 1)
            dve.wait_ge(self.root_done, h + 1)
            dve.reciprocal(c.rstd[:, cols], c.rstd[:, cols]).then_inc(self.rstd_done, 1)
            dve.wait_ge(self.rstd_done, h + 1)
            for t in tiles:
                dve.tensor_scalar(c.xn[:, t, :], c.X[:, t, :], c.meanvar[:, t, 0:1], c.rstd[:, t:t + 1],
                                  ALU.subtract, ALU.mult).then_inc(self.xn_ready, 1)

    def norm_tensor(self, pe):
        c = self.core
        for t in range(NT):
            pe.wait_ge(self.xn_ready, t + 1)
            for k in range(DC):
                last = pe.transpose(c.bank[:, 2 * k + t // 4, (t % 4) * P:(t % 4 + 1) * P],
                                    c.xn[:, t, k * P:(k + 1) * P], c.ident[:, :])
            last.then_inc(self.turned, 1)

    def norm_root(self, act):
        c = self.core
        for h in range(2):
            cols = slice(h * NT // 2, (h + 1) * NT // 2)
            act.wait_ge(self.aggr_done, (h + 1) * NT // 2)
            act.activation(c.rstd[:, cols], c.meanvar[:, cols, 1], ACT.Sqrt, bias=c.eps[:, 0:1]).then_inc(self.root_done, 1)

    def norm_bring(self, act):
        c = self.core
        for h in range(2):
            act.wait_ge(self.turned, 4 * (h + 1))
            for k in range(DC):
                act.copy(c.xnT[:, k, h * HALF:(h + 1) * HALF], c.bank[:, 2 * k + h, :]).then_inc(self.xnT_ready, 1)

    def norm_scalar(self, act):
        self.norm_root(act)
        self.norm_bring(act)


def stage_setup(core):
    nc, d = core.nc, core.dram
    with core.stage("setup") as s:
        loaded, ones_set, gate_done = s.sem("loaded"), s.sem("ones_set"), s.sem("gate_done")
        raw = s.sb("raw", [P, 8])
        with nc.Block() as block:
            @block.sync
            def _(sp):
                sp.dma_start(core.X[:, :, :], d["x"].rearrange("(t p) d -> p t d", p=P)).then_inc(loaded, 16)
                sp.dma_start(core.ident[:, :], d["ident"]).then_inc(loaded, 16)
                sp.dma_start(core.identh[:, :], d["identh"]).then_inc(loaded, 16)
                for j, g in enumerate(("g_xattn", "g_ffn")):
                    sp.dma_start(raw[:, 4 * j:4 * j + 4], d[g].partition_broadcast(P)).then_inc(loaded, 16)
                sp.wait_ge(loaded, 5 * 16)

            @block.vector
            def _(dve):
                dve.memset(core.ones[:, :], 1.0).then_inc(ones_set, 1)
                dve.memset(core.eps[:, :], LN_EPS).then_inc(ones_set, 1)

            @block.scalar
            def _(act):
                act.wait_ge(loaded, 5 * 16)
                act.activation(core.gates[:, :], raw[:, :], ACT.Tanh).then_inc(gate_done, 1)


def stage_store(core):
    nc, d = core.nc, core.dram
    with core.stage("store") as s:
        stored = s.sem("stored")
        with nc.Block() as block:
            @block.sync
            def _(sp):
                sp.dma_start(d["out"].rearrange("(t p) d -> p t d", p=P), core.X[:, :, :]).then_inc(stored, 16)
                sp.wait_ge(stored, 16)



def stage_ssm(core):
    nc, d = core.nc, core.dram
    NS, TAPS, DR = 16, 4, 8
    CC = 2
    PAD = TAPS - 1
    with core.stage("ssm") as s:
        w_in, ctxT = s.sb("w_in", [P, CC * P]), s.sb("ctxT", [P, NTOK])
        widths = (TAPS, 1, 1, 1, NS, 2 * NS, DR)
        chan = s.sb("chan", [P, CC, sum(widths)])
        starts = np.cumsum((0,) + widths).tolist()
        conv_w, conv_b, dt_b, skip, a_log, w_bc, w_dt1 = (chan[:, :, a:a + w] for a, w in zip(starts, widths))
        a_neg = s.sb("a_neg", [P, CC, NS])
        w_dt2 = s.sb("w_dt2", [DR, CC * P])
        select3 = s.sb("select3", [96, 2 * NS * P], BF16)
        padded = s.sb("padded", [P, CC, NB, SEQ + PAD])
        conv = s.sb("conv", [P, CC, NTOK])
        u, delta, du = (s.sb(n, [P, CC, NTOK]) for n in ("u", "delta", "du"))
        dt_lo = s.sb("dt_lo", [DR, NTOK])
        rest = s.sb("rest", [2 * NS, NTOK])
        mid = s.sb("mid", [2 * NS, NTOK], BF16)
        parts = s.sb("parts", [96, NTOK], BF16)
        b_row = s.sb("b_row", [P, 2, NTOK])
        decay = s.sb("decay", [P, 2, NB, SEQ])
        drive = s.sb("drive", [P, 2, NTOK])
        state = s.sb("state", [P, 2, NTOK])
        seen = s.sb("seen", [P, 2, NTOK])
        small, is_small = s.sb("small", [P, CC, NTOK]), s.sb("is_small", [P, CC, NTOK], mybir.dt.uint8)
        series = conv
        silu_z = s.sb("silu_z", [P, NT, DM])
        w_s, s_s = s.sem("w_s"), s.sem("s_s")
        names = ("in_done", "pad_ready", "padded_zero", "conv_done", "u_ready", "bc_done", "dt1_done", "dt1_copied",
                 "dt2_done", "pre_ready", "abs_done", "e_ready", "small_known", "delta_ready", "soft", "a_exp",
                 "a_ready", "step", "parts_hi",
                 "parts_ready", "du_ready", "b_done", "b_copied", "c_done", "decay_ready", "drive_ready", "scanned",
                 "seen_ready", "summed", "silu_z_done", "y_ready", "y_turned", "added")
        S = {n: s.sem(n) for n in names}
        bank = core.bank
        gate = core.gates[:, 0:1]
        two = lambda a: a.rearrange("p (h n) -> p h n", h=2)

        with nc.Block() as block:
            @block.sync
            def _(sp):
                for dst, n in ((ctxT, "ctxT"), (w_in, "l0x_in"), (w_dt2, "l0x_dt2")):
                    sp.dma_start(dst[:, :], d[n]).then_inc(w_s, 16)
                sp.dma_start(chan[:, :, :], d["l0x_chan"].rearrange("(c p) k -> p c k", p=P)).then_inc(w_s, 16)
                sp.dma_start(select3[:, :], d["select3"]).then_inc(s_s, 16)

            @block.tensor
            def _(pe):
                pe.wait_ge(w_s, 4 * 16)
                for k in range(CC):
                    for h in range(2):
                        last = pe.matmul(bank[:, 2 * k + h, :], w_in[:, k * P:(k + 1) * P],
                                         ctxT[:, h * HALF:(h + 1) * HALF], start=True, stop=True)
                    last.then_inc(S["in_done"], 1)
                pe.wait_ge(S["u_ready"], CC)
                for h in range(2):
                    for k in range(CC):
                        last = pe.matmul(bank[0:DR, 6 + h, :], w_dt1[:, k, :], u[:, k, h * HALF:(h + 1) * HALF],
                                         start=k == 0, stop=k == CC - 1)
                last.then_inc(S["dt1_done"], 1)
                for h in range(2):
                    for k in range(CC):
                        last = pe.matmul(bank[0:2 * NS, 4 + h, :], w_bc[:, k, :], u[:, k, h * HALF:(h + 1) * HALF],
                                         start=k == 0, stop=k == CC - 1)
                last.then_inc(S["bc_done"], 1)
                pe.wait_ge(S["dt1_copied"], 1)
                for k in range(CC):
                    for h in range(2):
                        last = pe.matmul(bank[:, 2 * k + h, :], w_dt2[:, k * P:(k + 1) * P],
                                         dt_lo[:, h * HALF:(h + 1) * HALF], start=True, stop=True)
                last.then_inc(S["dt2_done"], 1)
                pe.wait_ge(s_s, 16)
                pe.wait_ge(S["parts_ready"], 1)
                pe.wait_ge(S["pre_ready"], CC)
                pe.wait_ge(S["abs_done"], CC)

                def rows(n, j):
                    if j == 0:
                        await_count(pe, S["b_copied"], n)
                    else:
                        await_count(pe, S["seen_ready"], CC * n)
                    for h in range(2):
                        last = pe.matmul(bank[:, 2 * j + h, :], select3[:, bass.ds((n + NS * j) * P, P)],
                                         parts[:, h * HALF:(h + 1) * HALF], start=True, stop=True)
                    last.then_inc(S["c_done" if j else "b_done"], 1)

                def gather(n, k, first, last_state):
                    pe.wait_ge(S["seen_ready"], CC * n + (k + 1))
                    for h in range(2):
                        last = pe.matmul(bank[:, 4 + 2 * k + h, :], core.ident[:, :], seen[:, k, h * HALF:(h + 1) * HALF],
                                         start=first, stop=last_state, skip_group_check=True)
                    last.then_inc(S["summed"], 1)

                def state_sums(n, first=False, final=False):
                    if not final:
                        rows(n + 2, 0)
                    rows(n, 1)
                    gather(n - 1, 1, first, False)
                    gather(n, 0, False, isinstance(n, int) and n == NS - 1)

                rows(0, 0)
                rows(0, 1)
                rows(1, 0)
                rows(2, 0)
                gather(0, 0, True, False)
                state_sums(1, first=True)
                with pe.Fori(2, NS - 2) as n:
                    state_sums(n)
                state_sums(NS - 2, final=True)
                state_sums(NS - 1, final=True)
                gather(NS - 1, 1, False, True)
                for t in range(NT):
                    b, h = t // 2, t % 2
                    pe.wait_ge(S["y_ready"], CC)
                    if t >= 4:
                        pe.wait_ge(S["added"], t - 3)
                    for k in range(CC):
                        last = pe.transpose(bank[:, t % 4, k * P:(k + 1) * P],
                                            seen[:, k, b * SEQ + h * P:b * SEQ + (h + 1) * P], core.ident[:, :])
                    last.then_inc(S["y_turned"], 1)

            @block.scalar
            def _(act):
                act.wait_ge(S["padded_zero"], 1)
                for k in range(CC):
                    act.wait_ge(S["in_done"], k + 1)
                    for h in range(2):
                        last = act.copy(padded[:, k, 2 * h:2 * h + 2, PAD:PAD + SEQ],
                                        bank[:, 2 * k + h, :].rearrange("p (b n) -> p b n", b=2))
                    last.then_inc(S["pad_ready"], 1)
                for k in range(CC):
                    act.wait_ge(S["conv_done"], k + 1)
                    act.activation(u[:, k, :], conv[:, k, :], ACT.Silu, bias=conv_b[:, k, :]).then_inc(S["u_ready"], 1)
                s.norm_root(act)
                act.wait_ge(S["dt1_done"], 1)
                act.copy(two(dt_lo[:, :]), bank[0:DR, 6:8, :]).then_inc(S["dt1_copied"], 1)
                act.wait_ge(S["bc_done"], 1)
                act.copy(two(parts[0:2 * NS, :]), bank[0:2 * NS, 4:6, :]).then_inc(S["parts_hi"], 1)
                act.wait_ge(w_s, 4 * 16)
                act.preload_act_table_set("natural_log_exp_and_others")
                act.activation(a_neg[:, :, :], a_log[:, :, :], ACT.Exp).then_inc(S["a_exp"], 1)
                act.wait_ge(S["dt2_done"], 1)
                act.wait_ge(S["pre_ready"], CC)
                for k in range(CC):
                    act.activation(two(delta[:, k, :]), bank[:, 2 * k:2 * k + 2, :], ACT.Abs, bias=dt_b[:, k, :]
                                   ).then_inc(S["abs_done"], 1)
                for k in range(CC):
                    act.wait_ge(S["abs_done"], k + 1)
                    act.activation(small[:, k, :], delta[:, k, :], ACT.Exp, scale=-1.0).then_inc(S["e_ready"], 1)
                for k in range(CC):
                    act.wait_ge(S["e_ready"], k + 1)
                    act.activation(delta[:, k, :], small[:, k, :], ACT.Ln, bias=1.0).then_inc(S["soft"], 1)
                act.wait_ge(S["delta_ready"], CC)
                act.wait_ge(S["a_ready"], 1)

                def copy_b(n, p):
                    act.wait_ge(S["b_done"], n + 1)
                    await_count(act, S["drive_ready"], CC * n - CC)
                    act.copy(two(b_row[:, p, :]), bank[:, 0:2, :]).then_inc(S["b_copied"], 1)

                def decays(n):
                    for k in range(CC):
                        await_count(act, S["scanned"], CC * n + (k - 1))
                        act.activation(decay[:, k, :, 1:SEQ], delta[:, k, :].rearrange("p (b n) -> p b n", b=NB)[:, :, 1:SEQ],
                                       ACT.Exp, scale=a_neg[:, k, bass.ds(n, 1)]).then_inc(S["decay_ready"], 1)

                copy_b(0, 0)
                copy_b(1, 1)
                for p in range(2):
                    decays(p)
                    copy_b(2 + p, p)
                with act.Fori(1, NS // 2 - 1) as i:
                    for p in range(2):
                        decays(2 * i + p)
                        copy_b(2 * i + (p + 2), p)
                decays(NS - 2)
                decays(NS - 1)
                act.wait_ge(s.xn_ready, NT)
                act.activation(silu_z[:, :, :], core.xn[:, :, :], ACT.Silu).then_inc(S["silu_z_done"], 1)

            @block.gpsimd
            def _(pool):
                pool.memset(padded[:, :, :, 0:PAD], 0.0).then_inc(S["padded_zero"], 1)
                pool.memset(decay[:, :, :, 0:1], 0.0).then_inc(S["padded_zero"], 1)
                for k in range(CC):
                    pool.wait_ge(S["delta_ready"], k + 1)
                    pool.tensor_tensor(du[:, k, :], delta[:, k, :], u[:, k, :], ALU.mult).then_inc(S["du_ready"], 1)
                pool.wait_ge(S["du_ready"], CC)

                def drives(n, p):
                    pool.wait_ge(S["b_copied"], n + 1)
                    for k in range(CC):
                        await_count(pool, S["scanned"], CC * n + (k - 1))
                        pool.tensor_tensor(drive[:, k, :], du[:, k, :], b_row[:, p, :], ALU.mult).then_inc(S["drive_ready"], 1)

                for p in range(2):
                    drives(p, p)
                with pool.Fori(1, NS // 2) as i:
                    for p in range(2):
                        drives(2 * i + p, p)

            @block.vector
            def _(dve):
                steps = [0]

                def chain(ins):
                    steps[0] += 1
                    ins.then_inc(S["step"], 1)
                    dve.wait_ge(S["step"], steps[0])

                dve.wait_ge(w_s, 4 * 16)
                dve.wait_ge(S["padded_zero"], 2)
                for k in range(CC):
                    dve.wait_ge(S["pad_ready"], k + 1)
                    out = conv[:, k, :].rearrange("p (b n) -> p b n", b=NB)
                    tap = lambda j: padded[:, k, :, j:j + SEQ]
                    chain(dve.tensor_scalar(out, tap(0), conv_w[:, k, 0:1], None, ALU.mult))
                    for j in range(1, TAPS):
                        ins = dve.scalar_tensor_tensor(out, tap(j), conv_w[:, k, j:j + 1], out, ALU.mult, ALU.add)
                        if j < TAPS - 1:
                            chain(ins)
                    ins.then_inc(S["conv_done"], 1)
                s.norm_vector(dve)
                dve.wait_ge(S["parts_hi"], 1)
                chain(dve.tensor_tensor(two(rest[:, :]), bank[0:2 * NS, 4:6, :], two(parts[0:2 * NS, :]), ALU.subtract))
                chain(dve.tensor_copy(mid[:, :], rest[:, :]))
                dve.tensor_copy(parts[2 * NS:4 * NS, :], mid[:, :])
                dve.tensor_tensor(parts[4 * NS:6 * NS, :], rest[:, :], mid[:, :], ALU.subtract).then_inc(S["parts_ready"], 1)
                dve.wait_ge(S["a_exp"], 1)
                dve.tensor_scalar(a_neg[:, :, :], a_neg[:, :, :], -1.0, None, ALU.mult).then_inc(S["a_ready"], 1)
                dve.wait_ge(S["dt2_done"], 1)
                for k in range(CC):
                    dve.tensor_scalar(two(du[:, k, :]), bank[:, 2 * k:2 * k + 2, :], dt_b[:, k, :], None, ALU.add
                                      ).then_inc(S["pre_ready"], 1)
                for k in range(CC):
                    dve.wait_ge(S["e_ready"], k + 1)
                    chain(dve.tensor_scalar(series[:, k, :], small[:, k, :], -1.0 / 6, None, ALU.mult))
                    for c in (1.0 / 5, -1.0 / 4, 1.0 / 3, -1.0 / 2, 1.0):
                        chain(dve.scalar_tensor_tensor(series[:, k, :], series[:, k, :], c, small[:, k, :], ALU.add, ALU.mult))
                    dve.tensor_scalar(is_small[:, k, :], small[:, k, :], 1.0 / 16, None, ALU.is_lt).then_inc(S["small_known"], 1)
                    dve.wait_ge(S["small_known"], k + 1)
                    dve.wait_ge(S["soft"], k + 1)
                    chain(dve.copy_predicated(delta[:, k, :], is_small[:, k, :], series[:, k, :]))
                    dve.scalar_tensor_tensor(delta[:, k, :], du[:, k, :], 0.0, delta[:, k, :], ALU.max, ALU.add
                                             ).then_inc(S["delta_ready"], 1)

                def scan(n, k):
                    dve.wait_ge(S["decay_ready"], CC * n + (k + 1))
                    dve.wait_ge(S["drive_ready"], CC * n + (k + 1))
                    await_count(dve, S["seen_ready"], CC * n + (k - 1))
                    dve.tensor_tensor_scan(state[:, k, :], decay[:, k, :, :].rearrange("p b n -> p (b n)"), drive[:, k, :], 0.0,
                                           ALU.mult, ALU.add).then_inc(S["scanned"], 1)

                def see(n, k):
                    dve.wait_ge(S["scanned"], CC * n + (k + 1))
                    dve.wait_ge(S["c_done"], n + 1)
                    await_count(dve, S["summed"], CC * n + (k - 1))
                    dve.tensor_tensor(two(seen[:, k, :]), two(state[:, k, :]), bank[:, 2:4, :], ALU.mult
                                      ).then_inc(S["seen_ready"], 1)

                def steps_of(n):
                    scan(n, 1)
                    see(n, 0)
                    scan(n + 1, 0)
                    see(n, 1)

                scan(0, 0)
                steps_of(0)
                with dve.Fori(1, NS - 1) as n:
                    steps_of(n)
                scan(NS - 1, 1)
                see(NS - 1, 0)
                see(NS - 1, 1)
                dve.wait_ge(S["summed"], CC * NS)
                dve.wait_ge(S["silu_z_done"], 1)
                for k in range(CC):
                    chain(dve.scalar_tensor_tensor(two(state[:, k, :]), two(u[:, k, :]), skip[:, k, :],
                                                   bank[:, 4 + 2 * k:6 + 2 * k, :], ALU.mult, ALU.add))
                    z = silu_z[:, :, :].rearrange("p (b c) n -> p c b n", c=CC)[:, k, :, :]
                    dve.tensor_tensor(seen[:, k, :].rearrange("p (b n) -> p b n", b=NB),
                                      state[:, k, :].rearrange("p (b n) -> p b n", b=NB), z, ALU.mult
                                      ).then_inc(S["y_ready"], 1)
                for t in range(NT):
                    dve.wait_ge(S["y_turned"], t + 1)
                    dve.scalar_tensor_tensor(core.X[:, t, :], bank[:, t % 4, 0:DM], gate, core.X[:, t, :],
                                             ALU.mult, ALU.add).then_inc(S["added"], 1)


def one_hot_max(dve, s, chain, e, m, rank8, rank, top, hot):
    wide = lambda a: a.unsqueeze(2).to_broadcast([P, NT, 8])
    chain(dve.tensor_tensor(rank, e, wide(m), ALU.is_equal))
    chain(dve.tensor_tensor(rank, rank, rank8, ALU.mult))
    chain(dve.tensor_reduce(top, rank, AX.X, ALU.max))
    chain(dve.tensor_tensor(hot, rank, wide(top), ALU.is_equal))


def stage_lora_moe(core):
    nc, d = core.nc, core.dram
    NE, RANK = 8, 64
    ER = NE * RANK
    JC = ER // P
    with core.stage("lora") as s:
        wA, wB, wR = s.sb("wA", [P, DC, ER]), s.sb("wB", [P, JC, DM]), s.sb("wR", [P, DC, NE])
        bias, rank8 = s.sb("bias", [P, NE]), s.sb("rank8", [P, NE])
        lg, e8, rank, hot = (s.sb(n, [P, NT, NE]) for n in ("lg", "e8", "rank", "hot"))
        m1, emax, top, total, coef = (s.sb(n, [P, NT]) for n in ("m1", "emax", "top", "total", "coef"))
        hm = s.sb("hm", [P, 2, ER])
        hmT = s.sb("hmT", [P, 2, JC, P])
        loaded, logits, shifted, exps, chained, coefs = (s.sem(n) for n in (
            "loaded", "logits", "shifted", "exps", "chained", "coefs"))
        h_done, masked, h_turned, hT_ready, out_done, added = (s.sem(n) for n in (
            "h_done", "masked", "h_turned", "hT_ready", "out_done", "added"))
        bank = core.bank
        lgp = bank[:, 4, 0:NT * NE].rearrange("p (t e) -> p t e", e=NE)
        gate = core.gates[:, 4:5]

        with nc.Block() as block:
            @block.sync
            def _(sp):
                sp.dma_start(wR[:, :, :], d["l0_Wr"].rearrange("(c p) e -> p c e", p=P)).then_inc(loaded, 16)
                sp.dma_start(bias[:, :], d["l0_br"].partition_broadcast(P)).then_inc(loaded, 16)
                sp.dma_start(rank8[:, :], d["rank8"]).then_inc(loaded, 16)
                sp.dma_start(wA[:, :, :], d["l0_A"].rearrange("(c p) e -> p c e", p=P)).then_inc(loaded, 16)
                sp.dma_start(wB[:, :, :], d["l0_B"].rearrange("(c p) e -> p c e", p=P)).then_inc(loaded, 16)

            @block.tensor
            def _(pe):
                s.norm_tensor(pe)
                pe.wait_ge(loaded, 5 * 16)
                pe.wait_ge(s.xnT_ready, 4)
                for t in range(NT):
                    for c in range(DC):
                        last = pe.matmul(lgp[:, t, :], core.xnT[:, c, t * P:(t + 1) * P], wR[:, c, :],
                                         start=c == 0, stop=c == DC - 1)
                last.then_inc(logits, 1)

                def hidden(t):
                    if t >= 2:
                        pe.wait_ge(masked, t - 1)
                    for c in range(DC):
                        last = pe.matmul(bank[:, t % 2, :], core.xnT[:, c, t * P:(t + 1) * P], wA[:, c, :],
                                         start=c == 0, stop=c == DC - 1)
                    last.then_inc(h_done, 1)

                def turn(t):
                    pe.wait_ge(masked, t + 1)
                    if t >= 2:
                        pe.wait_ge(hT_ready, t - 1)
                    for j in range(JC):
                        last = pe.transpose(bank[:, 2 + t % 2, j * P:(j + 1) * P], hm[:, t % 2, j * P:(j + 1) * P],
                                            core.ident[:, :])
                    last.then_inc(h_turned, 1)

                def out(t):
                    pe.wait_ge(hT_ready, t + 1)
                    if t >= 2:
                        pe.wait_ge(added, t - 1)
                    for j in range(JC):
                        last = pe.matmul(bank[:, 5 + t % 2, 0:DM], hmT[:, t % 2, j, :], wB[:, j, :],
                                         start=j == 0, stop=j == JC - 1)
                    last.then_inc(out_done, 1)

                hidden(0)
                for t in range(NT):
                    if t + 1 < NT:
                        hidden(t + 1)
                    turn(t)
                    if t >= 1:
                        out(t - 1)
                out(NT - 1)

            @block.scalar
            def _(act):
                s.norm_scalar(act)
                act.wait_ge(shifted, 1)
                act.activation(e8[:, :, :], lg[:, :, :], ACT.Exp).then_inc(exps, 1)
                for t in range(NT):
                    act.wait_ge(h_turned, t + 1)
                    if t >= 2:
                        act.wait_ge(out_done, t - 1)
                    act.copy(hmT[:, t % 2, :, :], bank[:, 2 + t % 2, :]).then_inc(hT_ready, 1)

            @block.vector
            def _(dve):
                links = [0]

                def chain(ins):
                    links[0] += 1
                    ins.then_inc(chained, 1)
                    dve.wait_ge(chained, links[0])

                s.norm_vector(dve)
                wide = lambda a: a.unsqueeze(2).to_broadcast([P, NT, NE])
                mid = lambda a: a.unsqueeze(1).to_broadcast([P, NT, NE])
                dve.wait_ge(loaded, 5 * 16)
                dve.wait_ge(logits, 1)
                chain(dve.tensor_tensor(lg[:, :, :], lgp, mid(bias[:, :]), ALU.add))
                chain(dve.tensor_reduce(m1[:, :], lg[:, :, :], AX.X, ALU.max))
                dve.tensor_tensor(lg[:, :, :], lg[:, :, :], wide(m1[:, :]), ALU.subtract).then_inc(shifted, 1)
                dve.wait_ge(exps, 1)
                dve.tensor_reduce(total[:, :], e8[:, :, :], AX.X, ALU.add)
                chain(dve.tensor_reduce(emax[:, :], e8[:, :, :], AX.X, ALU.max))
                one_hot_max(dve, s, chain, e8[:, :, :], emax[:, :], mid(rank8[:, :]), rank[:, :, :], top[:, :], hot[:, :, :])
                chain(dve.reciprocal(total[:, :], total[:, :]))
                chain(dve.scalar_tensor_tensor(coef[:, :], total[:, :], 1.0 / RANK, emax[:, :], ALU.mult, ALU.mult))
                chain(dve.tensor_tensor(hot[:, :, :], hot[:, :, :], wide(coef[:, :]), ALU.mult))

                def add(t):
                    dve.wait_ge(out_done, t + 1)
                    dve.scalar_tensor_tensor(core.X[:, t, :], bank[:, 5 + t % 2, 0:DM], gate, core.X[:, t, :],
                                             ALU.mult, ALU.add).then_inc(added, 1)

                for t in range(NT):
                    dve.wait_ge(h_done, t + 1)
                    if t >= 2:
                        dve.wait_ge(h_turned, t - 1)
                    dve.tensor_tensor(hm[:, t % 2, :].rearrange("p (e r) -> p e r", r=RANK),
                                      bank[:, t % 2, :].rearrange("p (e r) -> p e r", r=RANK),
                                      hot[:, t, :].unsqueeze(2).to_broadcast([P, NE, RANK]), ALU.mult).then_inc(masked, 1)
                    if t >= 2:
                        add(t - 2)
                add(NT - 2)
                add(NT - 1)


def stage_attention_16(core):
    nc, d = core.nc, core.dram
    NH, HD = 16, 128
    LN_SCALE = -0.5 * float(np.log(HD))
    P_SCALE = 2.0 ** 12
    C_TOP = 2.0 ** 13
    TINY = 2.0 ** -100
    EXPONENT = 0x7F800000
    with core.stage("a16") as s:
        ctxT, ctx_nat = s.sb("ctxT", [P, NTOK]), s.sb("ctx_nat", [P, NT, CTX])
        gains, gain = s.sb("gains", [P, 2]), s.sb("gain", [P, 1])
        ln_scale = s.sb("ln_scale", [P, 1])
        wk, wvT = s.sb("wk", [P, 2, HD]), s.sb("wvT", [P, 2, CTX])
        wo, wq = s.sb("wo", [P, 2, DM]), s.sb("wq", [P, 2, DC, HD])
        keys, wvo = s.sb("keys", [P, NH, NTOK]), s.sb("wvo", [P, NH, DM])
        k_sq, k_log, k_row = (s.sb(n, [P, 2, HALF]) for n in ("k_sq", "k_log", "k_row"))
        query, q_sq = s.sb("query", [P, 2, HALF]), s.sb("q_sq", [P, HALF])
        q_log, q_factor = s.sb("q_log", [P, 4]), s.sb("q_factor", [P, 2, 4])
        bias = s.sb("bias", [P, 2, 2])
        prob, total, inverse = s.sb("prob", [P, 2, 2, SEQ]), s.sb("total", [P, 2, 2]), s.sb("inverse", [P, 2, 2])
        p_hi, p_lo = s.sb("p_hi", [P, 2, 2, SEQ], F16), s.sb("p_lo", [P, 2, 2, SEQ], F16)
        mixT = s.sb("mixT", [P, 2, SEQ])
        c_hi, c_lo = s.sb("c_hi", [P, NT, CTX], F16), s.sb("c_lo", [P, NT, CTX], F16)
        row_top, power, c_scale, c_back = (s.sb(n, [P, 1]) for n in ("row_top", "power", "c_scale", "c_back"))
        in_s, consts = s.sem("in_s"), s.sem("consts")
        kv_in = [s.sem(f"kv_in{k}") for k in range(2)]
        wq_in = [s.sem(f"wq_in{k}") for k in range(2)]
        names = ("gain_done", "k_done", "k_squared", "k_sums", "k_logs", "k_rows", "key_ready", "vo_done", "vo_ready",
                 "added", "q_done", "q_squared", "q_ready", "q_sums", "q_logs", "q_factors", "s_done", "top", "bias_ready",
                 "exp_done", "inv_ready", "p_ready", "p_turned", "hi_ready", "pT_ready", "row_topped", "sum_done",
                 "scale_step", "c_scaled", "c_hi_ready", "c_split", "mix_done", "mixT_ready", "out_done")
        S = {n: s.sem(n) for n in names}
        bank = core.bank
        gate = core.gates[:, 1:2]

        with nc.Block() as block:
            @block.sync
            def _(sp):
                sp.dma_start(ctxT[:, :], d["ctxT"]).then_inc(in_s, 16)
                sp.dma_start(ctx_nat[:, :, :], d["ctx"].rearrange("(t p) n -> p t n", p=P)).then_inc(in_s, 16)
                sp.dma_start(gains[:, :], d["l1x_gains"]).then_inc(in_s, 16)

                def load_kv(i, k):
                    h = 2 * i + k
                    for dst, n in ((wk, "l1x_k"), (wvT, "l1x_vT"), (wo, "l1x_o")):
                        sp.dma_start(dst[:, k, :], d[n][bass.ds(h, 1)].rearrange("h p n -> p (h n)")).then_inc(kv_in[k], 16)

                def load_q(h, k):
                    sp.dma_start(wq[:, k, :, :], d["l1x_q"][bass.ds(h, 1)].rearrange("h (c p) n -> p (h c) n", p=P)
                                 ).then_inc(wq_in[k], 16)

                for k in range(2):
                    load_kv(0, k)
                for k in range(2):
                    load_q(k, k)
                with sp.Fori(1, NH // 2) as i:
                    for k in range(2):
                        sp.wait_ge(S["k_done"], 4 * i + (2 * k - 2))
                        sp.wait_ge(S["vo_done"], 2 * i + (k - 1))
                        load_kv(i, k)
                for m in range(2):
                    with sp.Fori(1 - m, NH // 2) as i:
                        for k in range(2):
                            sp.wait_ge(S["q_done"], 2 * i + (NH * m + k - 1))
                            load_q(2 * i + k, k)

            @block.tensor
            def _(pe):
                s.norm_tensor(pe)
                pe.wait_ge(in_s, 3 * 16)
                pe.wait_ge(s.xnT_ready, 4)

                def keys_of(i, k, m):
                    n = 4 * i + (2 * k + m)
                    if m == 0:
                        pe.wait_ge(kv_in[k], 3 * 16 * i + 3 * 16)
                    await_count(pe, S["key_ready"], n - 3)
                    pe.matmul(bank[:, 2 * k + m, :], wk[:, k, :], ctxT[:, m * HALF:(m + 1) * HALF], start=True, stop=True
                              ).then_inc(S["k_done"], 1)

                def sums_of(i, k, m):
                    n, h = 4 * i + (2 * k + m), 2 * i + k
                    if m == 0:
                        await_count(pe, S["vo_ready"], h - 1)
                        pe.matmul(bank[:, 6 + k, 0:DM], wvT[:, k, :], wo[:, k, :], start=True, stop=True
                                  ).then_inc(S["vo_done"], 1)
                    pe.wait_ge(S["k_squared"], n + 1)
                    await_count(pe, S["k_logs"], n - 1)
                    pe.matmul(bank[:, 4 + m, :], core.ones[:, :], k_sq[:, m, :], start=True, stop=True
                              ).then_inc(S["k_sums"], 1)

                def two_heads(i, first=False):
                    for k in range(2):
                        for m in range(2):
                            keys_of(i, k, m)
                            if m == 1:
                                sums_of(i, k, 0)
                            elif k == 1:
                                sums_of(i, 0, 1)
                            elif not first:
                                sums_of(i - 1, 1, 1)

                pe.wait_ge(S["row_topped"], 1)
                pe.matmul(bank[:, 7, 0:1], core.ones[:, :], row_top[:, :], start=True, stop=True).then_inc(S["sum_done"], 1)
                pe.wait_ge(S["c_scaled"], 1)
                two_heads(0, True)
                with pe.Fori(1, NH // 2) as i:
                    two_heads(i)
                sums_of(NH // 2 - 1, 1, 1)
                pe.wait_ge(S["key_ready"], 2 * NH)
                pe.wait_ge(S["vo_ready"], NH)

                def queries(n, i, m, p):
                    pe.wait_ge(wq_in[p], 16 * i + 16)
                    await_count(pe, S["q_logs"], n - 1)
                    for c in range(DC):
                        last = pe.matmul(bank[:, 6 + p, :], wq[:, p, c, :], core.xnT[:, c, m * HALF:(m + 1) * HALF],
                                         start=c == 0, stop=c == DC - 1)
                    last.then_inc(S["q_done"], 1)

                def query_sums(n, p):
                    pe.wait_ge(S["q_squared"], n + 1)
                    pe.wait_ge(S["q_ready"], n + 1)
                    for j in range(4):
                        last = pe.matmul(bank[:, 6 + p, j:j + 1], q_sq[:, j * P:(j + 1) * P], core.ones[:, 0:1],
                                         start=True, stop=True)
                    last.then_inc(S["q_sums"], 1)

                def scores(n, m, p, j):
                    pe.wait_ge(S["q_ready"], n + 1)
                    await_count(pe, S["exp_done"], 2 * n + (j - 1))
                    b = 2 * m + j
                    for q in range(2):
                        last = pe.matmul(bank[:, 2 + j, q * SEQ:(q + 1) * SEQ],
                                         query[:, p, (2 * j + q) * P:(2 * j + q + 1) * P],
                                         keys[:, bass.ds(n - NH * m, 1), b * SEQ:(b + 1) * SEQ].rearrange("p h n -> p (h n)"),
                                         start=True, stop=True)
                    last.then_inc(S["s_done"], 1)

                def turn(n, j):
                    i = 2 * n + j
                    pe.wait_ge(S["p_ready"], i + 1)
                    await_count(pe, S["pT_ready"], i)
                    for kc in range(2):
                        for q in range(2):
                            last = pe.transpose(bank[:, 4, kc * SEQ + q * P:kc * SEQ + (q + 1) * P],
                                                prob[:, j, q, kc * P:(kc + 1) * P], core.ident[:, :])
                    last.then_inc(S["p_turned"], 1)

                def mix(n, m, j):
                    i = 2 * n + j
                    pe.wait_ge(S["pT_ready"], i + 1)
                    await_count(pe, S["mixT_ready"], i)
                    products = [(c, p, kc) for kc in range(2) for c, p in ((c_hi, p_hi), (c_hi, p_lo), (c_lo, p_hi))]
                    for c, p, kc in products:
                        last = pe.matmul(bank[:, 5, 0:SEQ], c[:, 2 * (2 * m + j) + kc, :], p[:, j, kc, :],
                                         start=(c, p, kc) == products[0], stop=(c, p, kc) == products[-1])
                    last.then_inc(S["mix_done"], 1)

                def out(n, m, j):
                    i = 2 * n + j
                    first = isinstance(n, int) and n % NH == 0
                    pe.wait_ge(S["mixT_ready"], i + 1)
                    for q in range(2):
                        last = pe.matmul(bank[:, j, q * DM:(q + 1) * DM], mixT[:, j, q * P:(q + 1) * P],
                                         wvo[:, bass.ds(n - NH * m, 1), :].rearrange("p h n -> p (h n)"),
                                         start=first and q == 0, stop=isinstance(n, int) and n % NH == NH - 1,
                                         skip_group_check=True)
                    last.then_inc(S["out_done"], 1)

                def unit(n, i, m, p, before, after):
                    scores(n, m, p, 0)
                    if before is not None:
                        turn(n - 1, 1)
                    if after is not None:
                        queries(n + 1, i + p, after, 1 - p)
                    if before is not None:
                        out(n - 1, before, 0)
                        mix(n - 1, before, 1)
                    scores(n, m, p, 1)
                    turn(n, 0)
                    if after is not None:
                        query_sums(n + 1, 1 - p)
                    if before is not None:
                        out(n - 1, before, 1)
                    mix(n, m, 0)

                pe.wait_ge(S["c_split"], 1)
                queries(0, 0, 0, 0)
                query_sums(0, 0)
                unit(0, 0, 0, 0, None, 0)
                unit(1, 0, 0, 1, 0, 0)
                with pe.Fori(1, NH // 2 - 1) as i:
                    for p in range(2):
                        unit(2 * i + p, i, 0, p, 0, 0)
                unit(NH - 2, NH // 2 - 1, 0, 0, 0, 0)
                unit(NH - 1, NH // 2 - 1, 0, 1, 0, 1)
                unit(NH, NH // 2, 1, 0, 0, 1)
                pe.wait_ge(S["added"], 1)
                unit(NH + 1, NH // 2, 1, 1, 1, 1)
                with pe.Fori(NH // 2 + 1, NH - 1) as i:
                    for p in range(2):
                        unit(2 * i + p, i, 1, p, 1, 1)
                unit(2 * NH - 2, NH - 1, 1, 0, 1, 1)
                unit(2 * NH - 1, NH - 1, 1, 1, 1, None)
                turn(2 * NH - 1, 1)
                mix(2 * NH - 1, 1, 1)
                out(2 * NH - 1, 1, 0)
                out(2 * NH - 1, 1, 1)

            @block.scalar
            def _(act):
                s.norm_scalar(act)
                act.preload_act_table_set("natural_log_exp_and_others")

                def square(i, k, m):
                    n = 4 * i + (2 * k + m)
                    act.wait_ge(S["k_done"], n + 1)
                    await_count(act, S["k_sums"], n - 1)
                    act.activation(k_sq[:, m, :], bank[:, 2 * k + m, :], ACT.Square).then_inc(S["k_squared"], 1)

                def key_factor(i, k, m):
                    n = 4 * i + (2 * k + m)
                    act.wait_ge(S["k_sums"], n + 1)
                    await_count(act, S["k_rows"], n - 1)
                    act.activation(k_log[:, m, :], bank[:, 4 + m, :], ACT.Ln, scale=1.0 / HD, bias=core.eps[:, 0:1]
                                   ).then_inc(S["k_logs"], 1)
                    act.wait_ge(S["k_logs"], n + 1)
                    await_count(act, S["key_ready"], n - 1)
                    act.activation(k_row[:, m, :], k_log[:, m, :], ACT.Exp, scale=-0.5).then_inc(S["k_rows"], 1)

                def two_heads(i, first=False):
                    for k in range(2):
                        for m in range(2):
                            square(i, k, m)
                            if m == 1:
                                key_factor(i, k, 0)
                            elif k == 1:
                                key_factor(i, 0, 1)
                            elif not first:
                                key_factor(i - 1, 1, 1)

                act.wait_ge(S["c_scaled"], 1)
                act.activation(c_hi[:, :, :], ctx_nat[:, :, :], ACT.Copy, scale=c_scale[:, 0:1]).then_inc(S["c_hi_ready"], 1)
                two_heads(0, True)
                with act.Fori(1, NH // 2) as i:
                    two_heads(i)
                key_factor(NH // 2 - 1, 1, 1)

                def queries(n, p):
                    act.wait_ge(S["q_done"], n + 1)
                    await_count(act, S["q_sums"], n)
                    act.activation(q_sq[:, :], bank[:, 6 + p, :], ACT.Square).then_inc(S["q_squared"], 1)
                    await_count(act, S["s_done"], 2 * n - 2)
                    act.copy(query[:, p, :], bank[:, 6 + p, :]).then_inc(S["q_ready"], 1)

                def query_factor(n, p):
                    act.wait_ge(S["q_sums"], n + 1)
                    await_count(act, S["q_factors"], n)
                    act.activation(q_log[:, :], bank[:, 6 + p, 0:4], ACT.Ln, scale=1.0 / HD, bias=core.eps[:, 0:1]
                                   ).then_inc(S["q_logs"], 1)
                    act.wait_ge(S["q_logs"], n + 1)
                    await_count(act, S["exp_done"], 2 * n - 2)
                    await_count(act, S["bias_ready"], 2 * n - 2)
                    act.activation(q_factor[:, p, :], q_log[:, :], ACT.Exp, scale=-0.5, bias=ln_scale[:, 0:1]
                                   ).then_inc(S["q_factors"], 1)

                def exps(n, p, j):
                    i = 2 * n + j
                    act.wait_ge(S["q_factors"], n + 1)
                    act.wait_ge(S["bias_ready"], i + 1)
                    await_count(act, S["p_turned"], i - 1)
                    await_count(act, S["inv_ready"], i - 1)
                    for q in range(2):
                        last = act.activation(prob[:, j, q, :], bank[:, 2 + j, q * SEQ:(q + 1) * SEQ], ACT.Exp,
                                              scale=q_factor[:, p, 2 * j + q:2 * j + q + 1],
                                              bias=bias[:, j, q:q + 1], accum_out=total[:, j, q:q + 1])
                    last.then_inc(S["exp_done"], 1)

                def bring_mix(n, j):
                    i = 2 * n + j
                    act.wait_ge(S["mix_done"], i + 1)
                    await_count(act, S["out_done"], i - 1)
                    act.activation(mixT[:, j, :], bank[:, 5, 0:SEQ], ACT.Copy, scale=c_back[:, 0:1]).then_inc(S["mixT_ready"], 1)

                def high_part(n, j):
                    i = 2 * n + j
                    act.wait_ge(S["p_turned"], i + 1)
                    await_count(act, S["mix_done"], i - 1)
                    act.activation(p_hi[:, j, :, :], bank[:, 4, :].rearrange("p (k n) -> p k n", k=2), ACT.Copy, scale=P_SCALE
                                   ).then_inc(S["hi_ready"], 1)

                def unit(n, p, before, after):
                    if before:
                        high_part(n - 1, 1)
                    exps(n, p, 0)
                    if after:
                        queries(n + 1, 1 - p)
                    if before:
                        bring_mix(n - 1, 1)
                    high_part(n, 0)
                    exps(n, p, 1)
                    if after:
                        query_factor(n + 1, 1 - p)
                    bring_mix(n, 0)

                queries(0, 0)
                act.wait_ge(consts, 1)
                query_factor(0, 0)
                unit(0, 0, False, True)
                unit(1, 1, True, True)
                with act.Fori(1, NH - 1) as i:
                    for p in range(2):
                        unit(2 * i + p, p, True, True)
                unit(2 * NH - 2, 0, True, True)
                unit(2 * NH - 1, 1, True, False)
                high_part(2 * NH - 1, 1)
                bring_mix(2 * NH - 1, 1)

            @block.gpsimd
            def _(pool):
                pool.memset(ln_scale[:, :], LN_SCALE).then_inc(consts, 1)

                def normalise(n, j):
                    i = 2 * n + j
                    pool.wait_ge(S["inv_ready"], i + 1)
                    pool.tensor_tensor(prob[:, j, :, :], prob[:, j, :, :],
                                       inverse[:, j, :].unsqueeze(2).to_broadcast([P, 2, SEQ]), ALU.mult
                                       ).then_inc(S["p_ready"], 1)

                with pool.Fori(0, 2 * NH) as n:
                    for j in range(2):
                        normalise(n, j)

            @block.vector
            def _(dve):
                s.norm_vector(dve)
                dve.wait_ge(in_s, 3 * 16)
                dve.tensor_tensor(gain[:, :], gains[:, 0:1], gains[:, 1:2], ALU.mult).then_inc(S["gain_done"], 1)
                dve.wait_ge(S["gain_done"], 1)

                def keys_of(i, k, m):
                    n = 4 * i + (2 * k + m)
                    dve.wait_ge(S["k_rows"], n + 1)
                    dve.scalar_tensor_tensor(keys[:, bass.ds(2 * i + k, 1), m * HALF:(m + 1) * HALF].rearrange("p h n -> p (h n)"),
                                             bank[:, 2 * k + m, :], gain[:, 0:1], k_row[:, m, :],
                                             ALU.mult, ALU.mult).then_inc(S["key_ready"], 1)

                def bring_vo(i, k):
                    dve.wait_ge(S["vo_done"], 2 * i + (k + 1))
                    dve.tensor_copy(wvo[:, bass.ds(2 * i + k, 1), :].rearrange("p h n -> p (h n)"), bank[:, 6 + k, 0:DM]
                                    ).then_inc(S["vo_ready"], 1)

                dve.tensor_reduce(row_top[:, :], ctx_nat[:, :, :].rearrange("p t n -> p (t n)"), AX.X, ALU.max,
                                  apply_absolute_value=True).then_inc(S["row_topped"], 1)
                dve.wait_ge(S["sum_done"], 1)
                dve.tensor_scalar(power[:, :], bank[:, 7, 0:1], TINY, None, ALU.max).then_inc(S["scale_step"], 1)
                dve.wait_ge(S["scale_step"], 1)
                bits = power[:, :].bitcast(mybir.dt.uint32)
                dve.tensor_scalar(bits, bits, EXPONENT, None, ALU.bitwise_and).then_inc(S["scale_step"], 1)
                dve.wait_ge(S["scale_step"], 2)
                dve.reciprocal(c_scale[:, :], power[:, :]).then_inc(S["scale_step"], 1)
                dve.wait_ge(S["scale_step"], 3)
                dve.tensor_scalar(c_back[:, :], power[:, :], 1.0 / (C_TOP * P_SCALE), None, ALU.mult)
                dve.tensor_scalar(c_scale[:, :], c_scale[:, :], C_TOP, None, ALU.mult).then_inc(S["c_scaled"], 1)
                dve.wait_ge(S["c_hi_ready"], 1)
                dve.scalar_tensor_tensor(c_lo[:, :, :], ctx_nat[:, :, :], c_scale[:, 0:1], c_hi[:, :, :], ALU.mult, ALU.subtract
                                         ).then_inc(S["c_split"], 1)
                with dve.Fori(0, NH // 2) as i:
                    for k in range(2):
                        keys_of(i, k, 0)
                        bring_vo(i, k)
                        keys_of(i, k, 1)

                def top(n, j):
                    i = 2 * n + j
                    dve.wait_ge(S["s_done"], i + 1)
                    await_count(dve, S["exp_done"], i - 1)
                    dve.tensor_reduce(bias[:, j, :], bank[:, 2 + j, :].rearrange("p (q n) -> p q n", q=2), AX.X, ALU.max,
                                      negate=True).then_inc(S["top"], 1)

                def scale_top(n, p, j):
                    i = 2 * n + j
                    dve.wait_ge(S["top"], i + 1)
                    dve.wait_ge(S["q_factors"], n + 1)
                    dve.tensor_tensor(bias[:, j, :], bias[:, j, :], q_factor[:, p, 2 * j:2 * j + 2], ALU.mult
                                      ).then_inc(S["bias_ready"], 1)

                def invert(n, j):
                    i = 2 * n + j
                    dve.wait_ge(S["exp_done"], i + 1)
                    await_count(dve, S["p_ready"], i - 1)
                    dve.reciprocal(inverse[:, j, :], total[:, j, :]).then_inc(S["inv_ready"], 1)

                def bring(n, j):
                    i = 2 * n + j
                    dve.wait_ge(S["hi_ready"], i + 1)
                    await_count(dve, S["mix_done"], i - 1)
                    dve.scalar_tensor_tensor(p_lo[:, j, :, :], bank[:, 4, :].rearrange("p (k n) -> p k n", k=2), P_SCALE,
                                             p_hi[:, j, :, :], ALU.mult, ALU.subtract).then_inc(S["pT_ready"], 1)

                def unit(n, p, before=True):
                    top(n, 0)
                    scale_top(n, p, 0)
                    if before:
                        bring(n - 1, 1)
                    invert(n, 0)
                    top(n, 1)
                    scale_top(n, p, 1)
                    bring(n, 0)
                    invert(n, 1)

                def add(m):
                    dve.wait_ge(S["out_done"], 2 * NH * (m + 1))
                    for j in range(2):
                        for q in range(2):
                            t = 4 * m + 2 * j + q
                            last = dve.scalar_tensor_tensor(core.X[:, t, :], bank[:, j, q * DM:(q + 1) * DM], gate,
                                                            core.X[:, t, :], ALU.mult, ALU.add)
                    last.then_inc(S["added"], 1)

                unit(0, 0, False)
                unit(1, 1)
                with dve.Fori(1, NH // 2) as i:
                    for p in range(2):
                        unit(2 * i + p, p)
                unit(NH, 0)
                add(0)
                unit(NH + 1, 1)
                with dve.Fori(NH // 2 + 1, NH) as i:
                    for p in range(2):
                        unit(2 * i + p, p)
                bring(2 * NH - 1, 1)
                add(1)


def stage_bitnet(core):
    nc, d = core.nc, core.dram
    FF = 1024
    FC = FF // P
    QMAX = 128.0
    EPS = 1e-5
    NW = DC * FF
    with core.stage("bit") as s:
        raw = [s.sb(f"raw{i}", [P, NW]) for i in range(3)]
        tern = [s.sb(f"tern{i}", [P, NW], BF16) for i in range(3)]
        w_gate, w_up = (tern[i][:, :].rearrange("p (c f) -> p c f", c=DC) for i in range(2))
        w_down = tern[2][:, :].rearrange("p (c f) -> p c f", c=FC)
        rowsum, wmean, wscale, wback = (s.sb(n, [P, 3]) for n in ("rowsum", "wmean", "wscale", "wback"))
        hadamard = s.sb("hadamard", [P, P])
        amax, qscale, back, gback, uback = (s.sb(n, [P, NT]) for n in ("amax", "qscale", "back", "gback", "uback"))
        shifted = s.sb("shifted", [P, 2, DM])
        xq = s.sb("xq", [P, NT, DM], BF16)
        xqT = s.sb("xqT", [P, DC, NTOK], BF16)
        silu, up = s.sb("silu", [P, 2, HALF]), s.sb("up", [P, 2, HALF])
        inter = s.sb("inter", [P, 2, HALF])
        interT = s.sb("interT", [P, 2, HALF])
        fly = s.sb("fly", [P, 2, FF])
        fly2 = s.sb("fly2", [P, HALF])
        amax2, qscale2, back2 = (s.sb(n, [P, NT]) for n in ("amax2", "qscale2", "back2"))
        fq = s.sb("fq", [P, 2, FF], BF16)
        fqT = s.sb("fqT", [P, 2, FC, P], BF16)
        loaded = [s.sem(f"loaded{i}") for i in range(3)]
        consts, sums, sums_out, tern_ready, step = (s.sem(n) for n in ("consts", "sums", "sums_out", "tern_ready", "step"))
        xq_scaled = s.sem("xq_scaled")
        xq_ready, xq_turned, xqT_ready = (s.sem(n) for n in ("xq_ready", "xq_turned", "xqT_ready"))
        gate_up, silu_done, inter_ready, inter_turned, interT_ready = (s.sem(n) for n in (
            "gate_up", "silu_done", "inter_ready", "inter_turned", "interT_ready"))
        w_scaled, tern_up = s.sem("w_scaled"), s.sem("tern_up")
        up_done, h_copied, up_step = s.sem("up_done"), s.sem("h_copied"), s.sem("up_step")
        h_done, h_read, fq_ready, fq_turned, fqT_ready, out_done, added = (s.sem(n) for n in (
            "h_done", "h_read", "fq_ready", "fq_turned", "fqT_ready", "out_done", "added"))
        bank = core.bank
        gate = core.gates[:, 5:6]
        half_bf = lambda b: bank[:, b, :].bitcast(BF16)

        with nc.Block() as block:
            @block.sync
            def _(sp):
                for i, n in enumerate(("l1_gate", "l1_up", "l1_down")):
                    sp.dma_start(raw[i][:, :].rearrange("p (c f) -> p c f", c=DC if i < 2 else FC),
                                 d[n].rearrange("(c p) f -> p c f", p=P)).then_inc(loaded[i], 16)
                sp.dma_start(hadamard[:, :], d["hadamard"]).then_inc(consts, 16)

            @block.tensor
            def _(pe):
                def sum_of(i):
                    pe.wait_ge(sums, i + 1)
                    pe.matmul(bank[:, 7, i:i + 1], core.ones[:, :], rowsum[:, i:i + 1], start=True, stop=True
                              ).then_inc(sums_out, 1)

                for i in range(2):
                    sum_of(i)
                for t in range(NT):
                    pe.wait_ge(xq_ready, t + 1)
                    if t >= 1:
                        pe.wait_ge(xqT_ready, t)
                    for c in range(DC):
                        last = pe.transpose(half_bf(5)[:, c * P:(c + 1) * P], xq[:, t, c * P:(c + 1) * P],
                                            core.identh[:, :])
                    last.then_inc(xq_turned, 1)
                sum_of(2)
                pe.wait_ge(consts, 16)
                pe.wait_ge(tern_ready, 1)
                pe.wait_ge(tern_up, 1)

                def gate_and_up(n):
                    t, h = n // 2, n % 2
                    pe.wait_ge(xqT_ready, t + 1)
                    await_count(pe, silu_done, n)
                    await_count(pe, up_done, n)
                    for k, w in enumerate((w_gate, w_up)):
                        for c in range(DC):
                            last = pe.matmul(bank[:, k, :], xqT[:, c, t * P:(t + 1) * P],
                                             w[:, c, h * HALF:(h + 1) * HALF], start=c == 0, stop=c == DC - 1)
                    last.then_inc(gate_up, 1)

                def turn(n):
                    pe.wait_ge(inter_ready, n + 1)
                    if n >= 1:
                        pe.wait_ge(interT_ready, n)
                    for j in range(4):
                        last = pe.transpose(bank[:, 2, j * P:(j + 1) * P], inter[:, n % 2, j * P:(j + 1) * P],
                                            core.ident[:, :])
                    last.then_inc(inter_turned, 1)

                def transform(n):
                    t, h = n // 2, n % 2
                    pe.wait_ge(interT_ready, n + 1)
                    await_count(pe, h_read if h else h_copied, t)
                    for j in range(4):
                        last = pe.matmul(bank[:, 3 + h, j * P:(j + 1) * P], interT[:, n % 2, j * P:(j + 1) * P],
                                         hadamard[:, :], start=True, stop=True)
                    last.then_inc(h_done, 1)

                def turn_fq(t):
                    pe.wait_ge(fq_ready, t + 1)
                    if t >= 1:
                        pe.wait_ge(fqT_ready, t)
                    for j in range(FC):
                        last = pe.transpose(half_bf(5)[:, j * P:(j + 1) * P], fq[:, t % 2, j * P:(j + 1) * P],
                                            core.identh[:, :])
                    last.then_inc(fq_turned, 1)

                def down(t):
                    pe.wait_ge(fqT_ready, t + 1)
                    if t == 0:
                        pe.wait_ge(tern_ready, 2)
                    else:
                        pe.wait_ge(added, t)
                    for j in range(FC):
                        last = pe.matmul(bank[:, 6, 0:DM], fqT[:, t % 2, j, :], w_down[:, j, :],
                                         start=j == 0, stop=j == FC - 1)
                    last.then_inc(out_done, 1)

                pe.wait_ge(xqT_ready, NT)
                gate_and_up(0)
                gate_and_up(1)
                for n in range(2 * NT):
                    turn(n)
                    if n + 2 < 2 * NT:
                        gate_and_up(n + 2)
                    transform(n)
                    if n % 2 == 1 and n >= 5:
                        turn_fq(n // 2 - 2)
                        down(n // 2 - 2)
                for t in (NT - 2, NT - 1):
                    turn_fq(t)
                    down(t)

            @block.scalar
            def _(act):
                s.norm_root(act)
                for t in range(NT):
                    act.wait_ge(xq_turned, t + 1)
                    act.copy(xqT[:, :, t * P:(t + 1) * P], half_bf(5)[:, 0:DC * P].rearrange("p (c n) -> p c n", c=DC)
                             ).then_inc(xqT_ready, 1)

                def silu_of(n):
                    act.wait_ge(gate_up, n + 1)
                    if n >= 2:
                        act.wait_ge(inter_ready, n - 1)
                    act.activation(silu[:, n % 2, :], bank[:, 0, :], ACT.Silu, scale=gback[:, n // 2:n // 2 + 1]
                                   ).then_inc(silu_done, 1)
                    act.activation(up[:, n % 2, :], bank[:, 1, :], ACT.Copy, scale=uback[:, n // 2:n // 2 + 1]
                                   ).then_inc(up_done, 1)

                def bring_half(t):
                    act.wait_ge(h_done, 2 * t + 1)
                    await_count(act, h_read, t)
                    act.copy(fly2[:, :], bank[:, 3, :]).then_inc(h_copied, 1)

                def bring(n):
                    act.wait_ge(inter_turned, n + 1)
                    if n >= 2:
                        act.wait_ge(h_done, n - 1)
                    act.copy(interT[:, n % 2, :], bank[:, 2, :]).then_inc(interT_ready, 1)

                def bring_fq(t):
                    act.wait_ge(fq_turned, t + 1)
                    if t >= 2:
                        act.wait_ge(out_done, t - 1)
                    act.copy(fqT[:, t % 2, :, :], half_bf(5)).then_inc(fqT_ready, 1)

                act.wait_ge(xq_scaled, 1)
                silu_of(0)
                silu_of(1)
                for n in range(2 * NT):
                    if n % 2 == 1:
                        bring_half(n // 2)
                    bring(n)
                    if n + 2 < 2 * NT:
                        silu_of(n + 2)
                    if n % 2 == 1 and n >= 5:
                        bring_fq(n // 2 - 2)
                bring_fq(NT - 2)
                bring_fq(NT - 1)

            @block.gpsimd
            def _(pool):
                pool_steps = [0]

                def chain(ins):
                    pool_steps[0] += 1
                    ins.then_inc(up_step, 1)
                    pool.wait_ge(up_step, pool_steps[0])

                def ternary(i, done, count):
                    w = raw[i][:, :]
                    chain(pool.tensor_scalar(w, w, wscale[:, i:i + 1], ROUND, ALU.mult, ALU.add))
                    chain(pool.tensor_scalar(w, w, ROUND, 1.0, ALU.subtract, ALU.min))
                    pool.tensor_scalar(tern[i][:, :], w, -1.0, None, ALU.max).then_inc(done, 1)

                pool.wait_ge(w_scaled, 1)
                ternary(1, tern_up, 1)

                def inter_of(n):
                    pool.wait_ge(silu_done, n + 1)
                    pool.wait_ge(up_done, n + 1)
                    await_count(pool, inter_turned, n - 1)
                    pool.tensor_tensor(inter[:, n % 2, :], up[:, n % 2, :], silu[:, n % 2, :], ALU.mult).then_inc(inter_ready, 1)

                for n in range(2 * NT):
                    inter_of(n)

            @block.vector
            def _(dve):
                steps = [0]

                def chain(ins):
                    steps[0] += 1
                    ins.then_inc(step, 1)
                    dve.wait_ge(step, steps[0])

                def ternary(i):
                    w = raw[i][:, :]
                    chain(dve.tensor_scalar(w, w, wscale[:, i:i + 1], ROUND, ALU.mult, ALU.add))
                    chain(dve.tensor_scalar(w, w, ROUND, 1.0, ALU.subtract, ALU.min))
                    dve.tensor_scalar(tern[i][:, :], w, -1.0, None, ALU.max).then_inc(tern_ready, 1)

                def sum_sizes(i):
                    dve.wait_ge(loaded[i], 16)
                    dve.tensor_reduce(rowsum[:, i:i + 1], raw[i][:, :], AX.X, ALU.add, apply_absolute_value=True
                                      ).then_inc(sums, 1)

                def scales_of(a, b):
                    dve.wait_ge(sums_out, b)
                    chain(dve.tensor_scalar(wmean[:, a:b], bank[:, 7, a:b], 1.0 / (NW * P), EPS, ALU.mult, ALU.max))
                    chain(dve.reciprocal(wscale[:, a:b], wmean[:, a:b]))
                    dve.reciprocal(wback[:, a:b], wscale[:, a:b]).then_inc(w_scaled, 1)

                s.norm_vector(dve)
                sum_sizes(0)
                sum_sizes(1)
                scales_of(0, 2)
                ternary(0)
                dve.wait_ge(s.xn_ready, NT)
                chain(dve.tensor_reduce(amax[:, :], core.xn[:, :, :], AX.X, ALU.max, apply_absolute_value=True))
                chain(dve.tensor_scalar(amax[:, :], amax[:, :], EPS, None, ALU.max))
                chain(dve.reciprocal(qscale[:, :], amax[:, :]))
                chain(dve.tensor_scalar(qscale[:, :], qscale[:, :], QMAX, None, ALU.mult))
                chain(dve.reciprocal(back[:, :], qscale[:, :]))
                for t in range(NT):
                    chain(dve.tensor_scalar(shifted[:, t % 2, :], core.xn[:, t, :], qscale[:, t:t + 1], ROUND,
                                            ALU.mult, ALU.add))
                    dve.tensor_scalar(xq[:, t, :], shifted[:, t % 2, :], ROUND, QMAX - 1, ALU.subtract, ALU.min
                                      ).then_inc(xq_ready, 1)
                chain(dve.tensor_scalar(gback[:, :], back[:, :], wback[:, 0:1], None, ALU.mult))
                dve.tensor_scalar(uback[:, :], back[:, :], wback[:, 1:2], None, ALU.mult).then_inc(xq_scaled, 1)
                dve.wait_ge(xq_scaled, 1)
                sum_sizes(2)
                scales_of(2, 3)
                dve.wait_ge(w_scaled, 2)
                ternary(2)

                def butterflies(t):
                    dve.wait_ge(h_done, 2 * t + 2)
                    f0, f1 = fly[:, 0, :], fly[:, 1, :]
                    pair = lambda a, m: a.rearrange("p (a two b) -> p a two b", two=2, b=m * P)
                    dve.wait_ge(h_copied, t + 1)
                    chain(dve.tensor_tensor(fly[:, 0, 0:HALF], fly2[:, :], bank[:, 4, :], ALU.add))
                    dve.tensor_tensor(fly[:, 0, HALF:FF], fly2[:, :], bank[:, 4, :], ALU.subtract).then_inc(h_read, 1)
                    dve.wait_ge(h_read, t + 1)
                    for m, (a, b) in ((2, (f0, f1)), (1, (f1, f0))):
                        pa, pb = pair(a, m), pair(b, m)
                        dve.tensor_tensor(pb[:, :, 0, :], pa[:, :, 0, :], pa[:, :, 1, :], ALU.add)
                        chain(dve.tensor_tensor(pb[:, :, 1, :], pa[:, :, 0, :], pa[:, :, 1, :], ALU.subtract))
                    col = slice(t, t + 1)
                    chain(dve.tensor_reduce(amax2[:, col], f0, AX.X, ALU.max, apply_absolute_value=True))
                    chain(dve.tensor_scalar(amax2[:, col], amax2[:, col], 1.0 / 32, EPS, ALU.mult, ALU.max))
                    chain(dve.reciprocal(qscale2[:, col], amax2[:, col]))
                    chain(dve.tensor_scalar(qscale2[:, col], qscale2[:, col], QMAX, None, ALU.mult))
                    chain(dve.reciprocal(back2[:, col], qscale2[:, col]))
                    chain(dve.tensor_scalar(back2[:, col], back2[:, col], wback[:, 2:3], gate, ALU.mult, ALU.mult))
                    chain(dve.tensor_scalar(qscale2[:, col], qscale2[:, col], 1.0 / 32, None, ALU.mult))
                    chain(dve.tensor_scalar(f1, f0, qscale2[:, col], ROUND, ALU.mult, ALU.add))
                    if t >= 2:
                        dve.wait_ge(fq_turned, t - 1)
                    dve.tensor_scalar(fq[:, t % 2, :], f1, ROUND, QMAX - 1, ALU.subtract, ALU.min).then_inc(fq_ready, 1)

                def add(t):
                    dve.wait_ge(out_done, t + 1)
                    dve.scalar_tensor_tensor(core.X[:, t, :], bank[:, 6, 0:DM], back2[:, t:t + 1], core.X[:, t, :],
                                             ALU.mult, ALU.add).then_inc(added, 1)

                for t in range(NT):
                    if t >= 3:
                        add(t - 3)
                    await_count(dve, fq_ready, t)
                    butterflies(t)
                for t in range(NT - 3, NT):
                    add(t)


def stage_attention_32(core):
    nc, d = core.nc, core.dram
    NH, HD = 32, 8
    SCALE = float(HD) ** -0.5
    FREQS = (1.0, 0.01)
    PI = 3.1415925
    TURN_HI, TURN_LO = 6.28125, 2 * float(np.pi) - 6.28125
    Q_PARTS, K_PARTS = (0, 0, 1, 0, 2, 1), (0, 1, 0, 2, 0, 1)
    SHIFT = 64
    NBUF = 3
    VW = HD + 1
    QUAD = 4
    NQ = NH // QUAD
    ANGLE_STEPS = 7
    with core.stage("a32") as s:
        ctxT, wq, wkv, wout = s.sb("ctxT", [P, NTOK]), s.sb("wq", [P, DC, DM]), s.sb("wkv", [P, 2 * DM]), s.sb("wout", [P, DC, DM])
        bout = s.sb("bout", [1, DM])
        pos = s.sb("pos", [P, NT, 2])
        angle, turns, trig = (s.sb(n, [P, NT, 2, 4]) for n in ("angle", "turns", "trig"))
        cos8, sin8 = s.sb("cos8", [P, NT, HD]), s.sb("sin8", [P, NT, HD])
        straight, crossed = s.sb("straight", [P, 2, 2 * DM]), s.sb("crossed", [P, 2, 2 * DM])
        rest = s.sb("rest", [P, 2, 4, P])
        parts = [s.sb(f"part{j}", [P, 4, 2, P], BF16) for j in range(6)]
        values = s.sb("values", [P, NT, NH, VW])
        q_stack = s.sb("q_stack", [P, NBUF, NH, SEQ], BF16)
        k_stack = s.sb("k_stack", [P, NBUF, NH, SEQ], BF16)
        tops, shift = s.sb("tops", [P, 2, 2, NH]), s.sb("shift", [NH, 2, SEQ], BF16)
        prob = s.sb("prob", [P, 2, 4, SEQ])
        outT = s.sb("outT", [P, 2, SEQ])
        inverse, attn = s.sb("inverse", [P, 2, 2, QUAD]), s.sb("attn", [P, NT, DM])
        attnT = s.sb("attnT", [P, 2, DC, P])
        scratch = nc.dram_tensor("a32_scratch", [3, 2, DM, NTOK], BF16).ap()
        scratch_shift = nc.dram_tensor("a32_scratch_shift", [NB, NH, SEQ], BF16).ap()
        names = ("w_in", "pos_in", "step", "trig_done", "qk_done", "values_done", "crossed_r", "roped", "turned32", "v_ready",
                 "ones_set", "q_zero", "k_zero", "rows_clear", "banks_clear", "zero_set",  "hi_ready", "rest_ready", "mid_ready", "lo_ready", "s_done", "top_done",
                 "top_turned", "shift_ready", "st_done", "exp_done", "av_done", "outT_ready", "quad_turned",
                 "inv_done", "attn_ready", "attn_turned",
                 "attnT_ready", "out_done", "added")
        S = {n: s.sem(n) for n in names}
        spilled = [s.sem(f"spilled{b}") for b in range(NB)]
        stacked = [s.sem(f"stacked{b}") for b in range(NB)]
        shifted = [s.sem(f"shifted{b}") for b in range(NB)]
        bank = core.bank
        gate = core.gates[:, 2:3]
        NG = NH // 2

        LAST_FIND = 3 * NG // 4

        def found_at(g, place, ahead):
            first = 4 * (g // 3)
            if not ahead or g >= LAST_FIND:
                return []
            return [first + j for j, at in enumerate(((0, 0), (0, 2), (1, 2), (2, 1))) if at == (g % 3, place)]

        def part(j, b):
            return parts[3 * (b % 2) + j]

        with nc.Block() as block:
            @block.sync
            def _(sp):
                sp.dma_start(ctxT[:, :], d["ctxT"]).then_inc(S["w_in"], 16)
                sp.dma_start(wkv[:, :], d["l2x_kv"]).then_inc(S["w_in"], 16)
                for dst, n in ((wq, "l2x_q"), (wout, "l2x_out")):
                    sp.dma_start(dst[:, :, :], d[n].rearrange("(c p) n -> p c n", p=P)).then_inc(S["w_in"], 16)
                sp.dma_start(bout[:, :], d["l2x_bout"].rearrange("(a n) -> a n", a=1)).then_inc(S["w_in"], 16)
                sp.dma_start(pos[:, :, :], d["pos"].rearrange("(t p) k -> p t k", p=P)).then_inc(S["pos_in"], 16)
                def stack(b):
                    sp.wait_ge(S["lo_ready"], 2 * b + 2)
                    tokens = slice(b * SEQ, (b + 1) * SEQ)
                    for j in range(3):
                        sp.dma_start(scratch[j, :, :, tokens].rearrange("k (c p) n -> p (k c) n", p=P),
                                     part(j, b)[:, :, :, :].rearrange("p k i n -> p k (i n)")).then_inc(spilled[b], 16)
                    sp.wait_ge(spilled[b], 3 * 16)
                    if b < NBUF:
                        sp.wait_ge(S["q_zero"], b + 1)
                        sp.wait_ge(S["k_zero"], b + 1)
                        sp.dma_start(k_stack[SHIFT:SHIFT + 1, b, :, :], d["row_of_ones"].rearrange("(a h n) -> a h n", a=1, h=NH)
                                     ).then_inc(stacked[b], 16)
                    if b >= NBUF:
                        sp.wait_ge(S["st_done"], NG * (b - NBUF + 1))
                        sp.dma_start(q_stack[SHIFT:SHIFT + 1, b % NBUF, :, :], d["row_of_zeros"].rearrange(
                            "(a h n) -> a h n", a=1, h=NH)).then_inc(S["rows_clear"], 16)
                    for kind, stack, which in ((0, q_stack, Q_PARTS), (1, k_stack, K_PARTS)):
                        for slot, j in enumerate(which):
                            sp.dma_start(stack[slot * HD:(slot + 1) * HD, b % NBUF, :, :],
                                         scratch[j, kind, :, tokens].rearrange("(h d) n -> d h n", d=HD)
                                         ).then_inc(stacked[b], 16)

                def place_shift(b):
                    sp.wait_ge(S["shift_ready"], b + 1)
                    sp.dma_start(scratch_shift[b], shift[:, b % 2, :]).then_inc(shifted[b], 16)
                    sp.wait_ge(shifted[b], 16)
                    if b >= NBUF:
                        sp.wait_ge(S["rows_clear"], 16)
                    sp.dma_start(q_stack[SHIFT:SHIFT + 1, b % NBUF, :, :], scratch_shift[b:b + 1]).then_inc(shifted[b], 16)

                for b in range(NBUF):
                    stack(b)
                for b in range(NB):
                    place_shift(b)
                    if 1 <= b <= NB - NBUF:
                        stack(b + NBUF - 1)

            @block.tensor
            def _(pe):
                s.norm_tensor(pe)
                pe.wait_ge(S["w_in"], 5 * 16)
                pe.wait_ge(s.xnT_ready, 4)

                def project(t):
                    await_count(pe, S["crossed_r"], t - 1)
                    await_count(pe, S["v_ready"], t - 1)
                    for c in range(DC):
                        pe.matmul(bank[:, t % 2, 0:DM], core.xnT[:, c, t * P:(t + 1) * P], wq[:, c, :],
                                         start=c == 0, stop=c == DC - 1)
                    pe.matmul(bank[:, t % 2, DM:2 * DM], ctxT[:, t * P:(t + 1) * P], wkv[:, 0:DM], start=True, stop=True
                              ).then_inc(S["qk_done"], 1)
                    pe.matmul(bank[:, 2 + t % 2, 0:DM], ctxT[:, t * P:(t + 1) * P], wkv[:, DM:2 * DM], start=True, stop=True
                              ).then_inc(S["values_done"], 1)

                def turn(t):
                    pe.wait_ge(S["roped"], t + 1)
                    await_count(pe, S["rest_ready"], t - 1)
                    for k in range(4):
                        last = pe.transpose(bank[:, 4 + t % 2, k * P:(k + 1) * P], straight[:, t % 2, k * P:(k + 1) * P],
                                            core.ident[:, :])
                    last.then_inc(S["turned32"], 1)

                project(0)
                for t in range(NT):
                    if t + 1 < NT:
                        project(t + 1)
                    turn(t)
                pe.wait_ge(S["rest_ready"], NT)
                pe.wait_ge(S["v_ready"], NT)

                def find(b, g, first_bank=0):
                    await_count(pe, S["top_done"], NG * b + g - (b == 0))
                    for k in range(2):
                        for q in range(2):
                            last = pe.matmul(bank[:, first_bank + k, q * SEQ:(q + 1) * SEQ],
                                             q_stack[:, b % NBUF, 2 * g + k, q * P:(q + 1) * P],
                                             k_stack[:, b % NBUF, 2 * g + k, :], start=True, stop=True)
                    last.then_inc(S["s_done"], 1)

                def turn_tops(b):
                    pe.wait_ge(S["top_done"], NG * (b + 1))
                    for q in range(2):
                        last = pe.transpose(bank[0:NH, 0, q * P:(q + 1) * P], tops[:, b % 2, q, :], core.ident[:, :])
                    last.then_inc(S["top_turned"], 1)

                def scores(b, g):
                    await_count(pe, S["exp_done"], NG * b + g - 1)
                    for j in range(2):
                        for kt in range(2):
                            last = pe.matmul(bank[:, 2 + 2 * (g % 2) + j, kt * SEQ:(kt + 1) * SEQ],
                                             k_stack[:, b % NBUF, 2 * g + j, kt * P:(kt + 1) * P],
                                             q_stack[:, b % NBUF, 2 * g + j, :], start=True, stop=True)
                    last.then_inc(S["st_done"], 1)

                def weigh(b, g, j):
                    u = g // 2
                    pe.wait_ge(S["exp_done"], NG * b + g + 1)
                    if g % 2 == 0:
                        await_count(pe, S["attn_ready"], NQ * b + u - 1)
                    row = 32 * ((2 * g + j) % QUAD)
                    for kt in range(2):
                        last = pe.matmul(bank[row:row + VW, 6 + u % 2, 0:SEQ], values[:, 2 * b + kt, 2 * g + j, :],
                                         prob[:, g % 2, 2 * j + kt, :], start=kt == 0, stop=kt == 1)
                    last.then_inc(S["av_done"], 1)

                def turn_quad(b, u):
                    pe.wait_ge(S["outT_ready"], NQ * b + u + 1)
                    for q in range(2):
                        last = pe.transpose(bank[:, 6 + u % 2, SEQ + q * P:SEQ + (q + 1) * P],
                                            outT[:, u % 2, q * P:(q + 1) * P], core.ident[:, :])
                    last.then_inc(S["quad_turned"], 1)

                pe.wait_ge(stacked[0], 13 * 16)
                for g in range(NG):
                    find(0, g, 2 * (g % 2))
                turn_tops(0)
                pe.wait_ge(S["banks_clear"], 1)
                for b in range(NB):
                    ahead = b + 1 < NB
                    if ahead:
                        pe.wait_ge(stacked[b + 1], (13 if b + 1 < NBUF else 12) * 16)
                        if b + 1 >= NBUF:
                            pe.wait_ge(S["rows_clear"], 16)
                        pe.wait_ge(S["shift_ready"], b + 1)
                    pe.wait_ge(shifted[b], 2 * 16)
                    scores(b, 0)
                    scores(b, 1)
                    for g in range(NG):
                        if ahead and g == LAST_FIND:
                            turn_tops(b + 1)
                        for f in found_at(g, 0, ahead):
                            find(b + 1, f)
                        if g >= 2 and g % 2 == 0:
                            turn_quad(b, g // 2 - 1)
                        for j in range(2):
                            weigh(b, g, j)
                            for f in found_at(g, 1 + j, ahead):
                                find(b + 1, f)
                        if g + 2 < NG:
                            scores(b, g + 2)
                    turn_quad(b, NQ - 1)
                for t in range(NT):
                    pe.wait_ge(S["attn_ready"], NQ * (t // 2 + 1))
                    await_count(pe, S["attnT_ready"], t - 1)
                    for c in range(DC):
                        last = pe.transpose(bank[:, t % 2, c * P:(c + 1) * P], attn[:, t, c * P:(c + 1) * P], core.ident[:, :])
                    last.then_inc(S["attn_turned"], 1)
                    pe.wait_ge(S["attnT_ready"], t + 1)
                    await_count(pe, S["added"], t - 1)
                    for c in range(DC):
                        pe.matmul(bank[:, 2 + t % 2, 0:DM], attnT[:, t % 2, c, :], wout[:, c, :], start=c == 0, stop=False)
                    pe.matmul(bank[:, 2 + t % 2, 0:DM], core.ones[0:1, :], bout[:, :], start=False, stop=True
                              ).then_inc(S["out_done"], 1)

            @block.scalar
            def _(act):
                s.norm_scalar(act)
                act.wait_ge(S["step"], ANGLE_STEPS)
                act.activation(trig[:, :, :, :], angle[:, :, :, :], ACT.Sin).then_inc(S["trig_done"], 1)

                def bring(t):
                    act.wait_ge(S["turned32"], t + 1)
                    b, i = t // 2, t % 2
                    if b >= 2:
                        act.wait_ge(spilled[b - 2], 3 * 16)
                    act.copy(part(0, b)[:, :, i, :], bank[:, 4 + t % 2, :].rearrange("p (k n) -> p k n", k=4)
                             ).then_inc(S["hi_ready"], 1)

                def middle(t):
                    act.wait_ge(S["rest_ready"], t + 1)
                    act.copy(part(1, t // 2)[:, :, t % 2, :], rest[:, t % 2, :, :]).then_inc(S["mid_ready"], 1)

                zeros = outT[:, 0, 0:1].to_broadcast([P, NH * SEQ // 2])
                act.wait_ge(S["zero_set"], 1)

                def zero(n):
                    act.copy(k_stack[:, n, :, :].rearrange("p h n -> p (h n)").bitcast(F32), zeros).then_inc(S["k_zero"], 1)
                zero(0)
                act.wait_ge(S["ones_set"], 1)
                for t in range(NT):
                    act.wait_ge(S["values_done"], t + 1)
                    act.copy(values[:, t, :, 0:HD], bank[:, 2 + t % 2, 0:DM].rearrange("p (h d) -> p h d", d=HD)
                             ).then_inc(S["v_ready"], 1)
                    if t >= 1:
                        bring(t - 1)
                    if t >= 2:
                        middle(t - 2)
                    if t in (3, 5):
                        zero(t // 2)
                bring(NT - 1)
                middle(NT - 2)
                middle(NT - 1)

                def negate(b):
                    act.wait_ge(S["top_turned"], b + 1)
                    if b >= 2:
                        act.wait_ge(shifted[b - 2], 2 * 16)
                    act.activation(shift[:, b % 2, :], bank[0:NH, 0, 0:SEQ], ACT.Copy, scale=-1.0
                                   ).then_inc(S["shift_ready"], 1)

                def exps(b, i, k):
                    n = 4 * i + (NG * b + k)
                    act.wait_ge(S["st_done"], n + 1)
                    await_count(act, S["av_done"], 2 * n - 2)
                    act.activation(prob[:, k % 2, :, :], bank[:, 2 + 2 * (k % 2):4 + 2 * (k % 2), :].rearrange(
                        "p j (t n) -> p (j t) n", t=2), ACT.Exp, scale=SCALE).then_inc(S["exp_done"], 1)

                def bring_quad(b, i, k):
                    n = 2 * i + (NQ * b + k)
                    act.wait_ge(S["av_done"], 4 * n + 4)
                    await_count(act, S["quad_turned"], n - 1)
                    act.copy(outT[:, k % 2, :], bank[:, 6 + k % 2, 0:SEQ]).then_inc(S["outT_ready"], 1)

                def four_pairs(b, i):
                    exps(b, i, 0)
                    if i >= 1:
                        bring_quad(b, i, -1)
                    exps(b, i, 1)
                    if 4 * i == LAST_FIND and b + 1 < NB:
                        negate(b + 1)
                    exps(b, i, 2)
                    bring_quad(b, i, 0)
                    exps(b, i, 3)

                negate(0)
                for b in range(NB):
                    for i in range(NG // 4):
                        four_pairs(b, i)
                    bring_quad(b, NQ // 2, -1)
                for t in range(NT):
                    act.wait_ge(S["attn_turned"], t + 1)
                    if t >= 2:
                        act.wait_ge(S["out_done"], t - 1)
                    act.copy(attnT[:, t % 2, :, :], bank[:, t % 2, 0:DM].rearrange("p (c n) -> p c n", c=DC)
                             ).then_inc(S["attnT_ready"], 1)

            @block.gpsimd
            def _(pool):
                pool.memset(values[:, :, :, HD:VW], 1.0).then_inc(S["ones_set"], 1)
                for n in range(NBUF):
                    pool.memset(q_stack[:, n, :, :].bitcast(mybir.dt.uint32), 0).then_inc(S["q_zero"], 1)

                def split(t):
                    b, i = t // 2, t % 2
                    pool.wait_ge(S["mid_ready"], t + 1)
                    pool.tensor_tensor(part(2, b)[:, :, i, :], rest[:, i, :, :], part(1, b)[:, :, i, :], ALU.subtract
                                       ).then_inc(S["lo_ready"], 1)

                for t in range(NT):
                    pool.wait_ge(S["crossed_r"], t + 1)
                    pool.tensor_tensor(straight[:, t % 2, :], straight[:, t % 2, :], crossed[:, t % 2, :], ALU.add
                                       ).then_inc(S["roped"], 1)
                    if t >= 2:
                        split(t - 2)
                split(NT - 2)
                split(NT - 1)

            @block.vector
            def _(dve):
                steps = [0]

                def chain(ins):
                    steps[0] += 1
                    ins.then_inc(S["step"], 1)
                    dve.wait_ge(S["step"], steps[0])

                dve.memset(outT[:, 0, 0:1], 0.0).then_inc(S["zero_set"], 1)
                dve.memset(bank[:, 6:8, 0:SEQ], 0.0).then_inc(S["banks_clear"], 1)
                s.norm_vector(dve)
                dve.wait_ge(S["pos_in"], 16)
                sines = angle[:, :, 0, :].rearrange("p t (k f) -> p t k f", f=2)
                for f in range(2):
                    ins = dve.tensor_scalar(sines[:, :, :, f], pos[:, :, :], FREQS[f], None, ALU.mult)
                chain(ins)
                chain(dve.tensor_scalar(angle[:, :, 1, :], angle[:, :, 0, :], float(np.pi) / 2, None, ALU.add))
                chain(dve.tensor_scalar(turns[:, :, :, :], angle[:, :, :, :], 0.5 / float(np.pi), ROUND, ALU.mult, ALU.add))
                chain(dve.tensor_scalar(turns[:, :, :, :], turns[:, :, :, :], ROUND, None, ALU.subtract))
                for c in (TURN_HI, TURN_LO):
                    chain(dve.scalar_tensor_tensor(angle[:, :, :, :], turns[:, :, :, :], -c, angle[:, :, :, :],
                                                   ALU.mult, ALU.add))
                chain(dve.tensor_scalar(angle[:, :, :, :], angle[:, :, :, :], PI, -PI, ALU.min, ALU.max))
                dve.wait_ge(S["trig_done"], 1)
                pairs = lambda a: a.rearrange("p t (k two) -> p t k two", two=2)
                for e in range(2):
                    dve.tensor_copy(pairs(cos8[:, :, :])[:, :, :, e], trig[:, :, 1, :])
                    ins = dve.tensor_scalar(pairs(sin8[:, :, :])[:, :, :, e], trig[:, :, 0, :], (-1.0, 1.0)[e], None, ALU.mult)
                chain(ins)

                def rotate(t):
                    await_count(dve, S["turned32"], t - 1)
                    await_count(dve, S["roped"], t - 1)
                    dve.wait_ge(S["qk_done"], t + 1)
                    for k in range(2):
                        heads = lambda a: a.rearrange("p (h n) -> p h n", n=HD)
                        src = bank[:, t % 2, k * DM:(k + 1) * DM]
                        wide = lambda a: a.unsqueeze(1).to_broadcast([P, NH, a.shape[-1]])
                        dve.tensor_tensor(heads(straight[:, t % 2, k * DM:(k + 1) * DM]), heads(src),
                                          wide(cos8[:, t, :]), ALU.mult)
                        for e in range(2):
                            at = lambda a, e: a.rearrange("p (h n two) -> p h n two", two=2, n=HD // 2)[:, :, :, e]
                            last = dve.tensor_tensor(at(crossed[:, t % 2, k * DM:(k + 1) * DM], e), at(src, 1 - e),
                                                     wide(sin8[:, t, :].rearrange("p (n two) -> p n two", two=2)[:, :, e]),
                                                     ALU.mult)
                    last.then_inc(S["crossed_r"], 1)

                def remainder(t):
                    dve.wait_ge(S["hi_ready"], t + 1)
                    await_count(dve, S["lo_ready"], t - 1)
                    dve.tensor_tensor(rest[:, t % 2, :, :], bank[:, 4 + t % 2, :].rearrange("p (k n) -> p k n", k=4),
                                      part(0, t // 2)[:, :, t % 2, :], ALU.subtract).then_inc(S["rest_ready"], 1)

                for t in range(NT):
                    rotate(t)
                    if t >= 2:
                        remainder(t - 2)
                remainder(NT - 2)
                remainder(NT - 1)

                def top(b, g, first_bank=0):
                    n = NG * b + g
                    dve.wait_ge(S["s_done"], n + 1)
                    dve.tensor_reduce(tops[:, b % 2, :, bass.ds(2 * g, 2)].rearrange("p q h -> p h q"),
                                      bank[:, first_bank:first_bank + 2, :].rearrange("p h (q n) -> p h q n", q=2), AX.X, ALU.max
                                      ).then_inc(S["top_done"], 1)

                def normalise(b, i, k):
                    n = 2 * i + (NQ * b + k)
                    dve.wait_ge(S["quad_turned"], n + 1)
                    heads = bank[:, 6 + k, SEQ:2 * SEQ].rearrange("p (q h n) -> p q h n", q=2, n=32)
                    dve.reciprocal(inverse[:, k, :, :], heads[:, :, :, HD]).then_inc(S["inv_done"], 1)
                    dve.wait_ge(S["inv_done"], n + 1)
                    dve.tensor_tensor(attn[:, 2 * b:2 * b + 2, bass.ds((2 * i + k) * 32, 32)].rearrange(
                        "p q (h n) -> p q h n", n=HD), heads[:, :, :, 0:HD],
                        inverse[:, k, :, :].unsqueeze(3).to_broadcast([P, 2, QUAD, HD]), ALU.mult
                                      ).then_inc(S["attn_ready"], 1)

                with dve.Fori(0, NG // 2) as i:
                    for k in range(2):
                        top(0, 2 * i + k, 2 * k)
                for b in range(NB):
                    ahead = b + 1 < NB
                    if ahead and b >= 1:
                        dve.wait_ge(S["top_turned"], b)
                    for g in range(NG):
                        for f in found_at(g, 0, ahead):
                            top(b + 1, f)
                        if g >= 2 and g % 2 == 0:
                            normalise(b, (g // 2 - 1) // 2, (g // 2 - 1) % 2)
                        for j in range(2):
                            for f in found_at(g, 1 + j, ahead):
                                top(b + 1, f)
                    normalise(b, NQ // 2 - 1, 1)
                for t in range(NT):
                    dve.wait_ge(S["out_done"], t + 1)
                    dve.scalar_tensor_tensor(core.X[:, t, :], bank[:, 2 + t % 2, 0:DM], gate, core.X[:, t, :],
                                             ALU.mult, ALU.add).then_inc(S["added"], 1)


def stage_moe(core):
    nc, d = core.nc, core.dram
    NE, FF = 8, 512
    JC = FF // P
    NW = DC * 2 * FF
    X_SCALE = 2.0 ** 8
    W_TOP = 2.0 ** 13
    TINY = 2.0 ** -100
    EXPONENT = 0x7F800000
    with core.stage("moe") as s:
        wR, rank8 = s.sb("wR", [P, DC, NE]), s.sb("rank8", [P, NE])
        lg, e8, rest, rank, hot, hot2, coef = (s.sb(n, [P, NT, NE]) for n in (
            "lg", "e8", "rest", "rank", "hot", "hot2", "coef"))
        m1, emax, esec, top, total = (s.sb(n, [P, NT]) for n in ("m1", "emax", "esec", "top", "total"))
        wup = s.sb("wup", [P, 2, NW])
        w_hi, w_lo = s.sb("w_hi", [P, 2, DC, 2 * FF], F16), s.sb("w_lo", [P, 2, DC, 2 * FF], F16)
        x_hi, x_lo = s.sb("x_hi", [P, DC, NTOK], F16), s.sb("x_lo", [P, DC, NTOK], F16)
        row_top, power, w_scale, w_back = (s.sb(n, [P, 2]) for n in ("row_top", "power", "w_scale", "w_back"))
        wdn = s.sb("wdn", [P, 2, JC, DM])
        silu = s.sb("silu", [P, 2, HALF])
        act_f = s.sb("act_f", [P, 2, JC, HALF])
        acc = s.sb("acc", [P, NT, DM])
        loaded, logits, shifted, exps, chained = (s.sem(n) for n in ("loaded", "logits", "shifted", "exps", "chained"))
        up_in = [s.sem(f"up_in{k}") for k in range(2)]
        down_in = [s.sem(f"down_in{k}") for k in range(2)]
        gate_up, silu_done, mixed, down_done, added = (s.sem(n) for n in (
            "gate_up", "silu_done", "mixed", "down_done", "added"))
        acc_zero = s.sem("acc_zero")
        lg_read, row_topped, sum_done, scale_step, scale_ready, hi_ready, lo_ready, x_hi_ready, x_lo_ready = (
            s.sem(n) for n in ("lg_read", "row_topped", "sum_done", "scale_step", "scale_ready", "hi_ready", "lo_ready",
                               "x_hi_ready", "x_lo_ready"))
        bank = core.bank
        flat = lambda a: a.rearrange("p c n -> p (c n)")
        lgp = bank[:, 4, 0:NT * NE].rearrange("p (t e) -> p t e", e=NE)
        gate = core.gates[:, 6:7]
        STEPS = 2 * JC
        NBK = NT // 2

        with nc.Block() as block:
            @block.sync
            def _(sp):
                sp.dma_start(wR[:, :, :], d["l2_gate"].rearrange("(c p) e -> p c e", p=P)).then_inc(loaded, 16)
                sp.dma_start(rank8[:, :], d["rank8"]).then_inc(loaded, 16)

                def load(e, k):
                    sp.dma_start(wup[:, k, :].rearrange("p (c f) -> p c f", c=DC),
                                 d["l2_up"][bass.ds(e, 1)].rearrange("e (c p) f -> p (e c) f", p=P)).then_inc(up_in[k], 16)
                    sp.dma_start(wdn[:, k, :, :], d["l2_down"][bass.ds(e, 1)].rearrange("e (c p) f -> p (e c) f", p=P)
                                 ).then_inc(down_in[k], 16)
                for k in range(2):
                    load(k, k)
                with sp.Fori(1, NE // 2) as i:
                    for k in range(2):
                        sp.wait_ge(hi_ready, 2 * i + (k - 1))
                        sp.wait_ge(lo_ready, 2 * i + (k - 1))
                        sp.wait_ge(down_done, NT * i + NBK * (k - 1))
                        load(2 * i + k, k)

            @block.tensor
            def _(pe):
                s.norm_tensor(pe)
                pe.wait_ge(s.xnT_ready, 4)

                def gate_and_up(e, k, n, first):
                    h, j = n // JC, n % JC
                    if not (first and n < 2):
                        pe.wait_ge(mixed, e * STEPS + (n - 1))
                    products = [(w, x, c) for c in range(DC) for w, x in ((w_hi, x_hi), (w_hi, x_lo), (w_lo, x_hi))]
                    for m in range(2):
                        for w, x, c in products:
                            last = pe.matmul(bank[:, 4 + 2 * (n % 2) + m, :],
                                             w[:, k, c, m * FF + j * P:m * FF + (j + 1) * P],
                                             x[:, c, h * HALF:(h + 1) * HALF], start=(w, x, c) == products[0],
                                             stop=(w, x, c) == products[-1])
                    last.then_inc(gate_up, 1)

                def sum_tops(e, k, first):
                    pe.wait_ge(row_topped, e + 1)
                    if not first:
                        pe.wait_ge(added, (e - 2) * NT + 2)
                    pe.matmul(bank[:, 0, 0:1], core.ones[:, :], row_top[:, k:k + 1], start=True, stop=True
                              ).then_inc(sum_done, 1)

                def down(e, k, h, first):
                    pe.wait_ge(mixed, e * STEPS + JC * (h + 1))
                    if not first:
                        pe.wait_ge(added, (e - 1) * NT + 4 * (h + 1))
                    for t in range(4 * h, 4 * h + 4):
                        for j in range(JC):
                            last = pe.matmul(bank[:, t // 2, (t % 2) * DM:(t % 2 + 1) * DM],
                                             act_f[:, h, j, (t % 4) * P:(t % 4 + 1) * P], wdn[:, k, j, :],
                                             start=j == 0, stop=j == JC - 1)
                        if t % 2 == 1:
                            last.then_inc(down_done, 1)

                def expert(i, k, first, final=False):
                    e = 2 * i + k
                    pe.wait_ge(hi_ready, e + 1)
                    pe.wait_ge(lo_ready, e + 1)
                    pe.wait_ge(down_in[k], 16 * i + 16)
                    for n in range(JC + 2):
                        gate_and_up(e, k, n, first and k == 0)
                        if n == 3 and not final:
                            sum_tops(e + 1, 1 - k, first and k == 0)
                    if not final:
                        pe.wait_ge(scale_ready, e + 2)
                    down(e, k, 0, first and k == 0)
                    for n in range(JC + 2, STEPS):
                        gate_and_up(e, k, n, False)
                    down(e, k, 1, first and k == 0)

                sum_tops(0, 0, True)
                pe.wait_ge(loaded, 2 * 16)
                for t in range(NT):
                    for c in range(DC):
                        last = pe.matmul(lgp[:, t, :], core.xnT[:, c, t * P:(t + 1) * P], wR[:, c, :],
                                         start=c == 0, stop=c == DC - 1)
                last.then_inc(logits, 1)
                pe.wait_ge(x_hi_ready, 1)
                pe.wait_ge(x_lo_ready, 1)
                pe.wait_ge(scale_ready, 1)
                pe.wait_ge(lg_read, 1)
                for k in range(2):
                    expert(0, k, True)
                with pe.Fori(1, NE // 2 - 1) as i:
                    for k in range(2):
                        expert(i, k, False)
                for k in range(2):
                    expert(NE // 2 - 1, k, False, k == 1)

            @block.scalar
            def _(act):
                s.norm_scalar(act)
                act.wait_ge(s.xnT_ready, 4)
                act.activation(flat(x_hi[:, :, :]), flat(core.xnT[:, :, :]), ACT.Copy, scale=X_SCALE).then_inc(x_hi_ready, 1)

                def high_part(e, k):
                    act.wait_ge(scale_ready, e + 1)
                    act.activation(flat(w_hi[:, k, :, :]), wup[:, k, :], ACT.Copy, scale=w_scale[:, k:k + 1]
                                   ).then_inc(hi_ready, 1)

                high_part(0, 0)
                act.wait_ge(shifted, 1)
                act.activation(e8[:, :, :], lg[:, :, :], ACT.Exp).then_inc(exps, 1)

                def silu_of(e, k, n, first):
                    act.wait_ge(gate_up, e * STEPS + (n + 1))
                    if not (first and n < 2):
                        act.wait_ge(mixed, e * STEPS + (n - 1))
                    act.activation(silu[:, n % 2, :], bank[:, 4 + 2 * (n % 2), :], ACT.Silu, scale=w_back[:, k:k + 1]
                                   ).then_inc(silu_done, 1)

                def expert(i, k, first=False, final=False):
                    for n in range(STEPS):
                        silu_of(2 * i + k, k, n, first)
                        if n == JC and not final:
                            high_part(2 * i + (k + 1), 1 - k)

                expert(0, 0, True)
                expert(0, 1)
                with act.Fori(1, NE // 2 - 1) as i:
                    for k in range(2):
                        expert(i, k)
                expert(NE // 2 - 1, 0)
                expert(NE // 2 - 1, 1, final=True)

            @block.gpsimd
            def _(pool):
                pool.memset(acc[:, :, :], 0.0).then_inc(acc_zero, 1)

            @block.vector
            def _(dve):
                links = [0]

                def chain(ins):
                    links[0] += 1
                    ins.then_inc(chained, 1)
                    dve.wait_ge(chained, links[0])

                def top_rows(e, i, k):
                    dve.wait_ge(up_in[k], 16 * i + 16)
                    dve.tensor_reduce(row_top[:, k:k + 1], wup[:, k, :], AX.X, ALU.max, apply_absolute_value=True
                                      ).then_inc(row_topped, 1)

                def scale_of(e, k):
                    dve.wait_ge(sum_done, e + 1)
                    dve.tensor_scalar(power[:, k:k + 1], bank[:, 0, 0:1], TINY, None, ALU.max).then_inc(scale_step, 1)
                    dve.wait_ge(scale_step, 3 * e + 1)
                    bits = power[:, k:k + 1].bitcast(mybir.dt.uint32)
                    dve.tensor_scalar(bits, bits, EXPONENT, None, ALU.bitwise_and).then_inc(scale_step, 1)
                    dve.wait_ge(scale_step, 3 * e + 2)
                    dve.reciprocal(w_scale[:, k:k + 1], power[:, k:k + 1]).then_inc(scale_step, 1)
                    dve.wait_ge(scale_step, 3 * e + 3)
                    dve.tensor_scalar(w_back[:, k:k + 1], power[:, k:k + 1], 1.0 / (W_TOP * X_SCALE), None, ALU.mult)
                    dve.tensor_scalar(w_scale[:, k:k + 1], w_scale[:, k:k + 1], W_TOP, None, ALU.mult).then_inc(scale_ready, 1)

                def low_part(e, k):
                    dve.wait_ge(hi_ready, e + 1)
                    dve.scalar_tensor_tensor(flat(w_lo[:, k, :, :]), wup[:, k, :], w_scale[:, k:k + 1], flat(w_hi[:, k, :, :]),
                                             ALU.mult, ALU.subtract).then_inc(lo_ready, 1)

                s.norm_vector(dve)
                top_rows(0, 0, 0)
                scale_of(0, 0)
                dve.wait_ge(x_hi_ready, 1)
                dve.scalar_tensor_tensor(flat(x_lo[:, :, :]), flat(core.xnT[:, :, :]), X_SCALE, flat(x_hi[:, :, :]),
                                         ALU.mult, ALU.subtract).then_inc(x_lo_ready, 1)
                low_part(0, 0)
                wide = lambda a: a.unsqueeze(2).to_broadcast([P, NT, NE])
                ranks = rank8[:, :].unsqueeze(1).to_broadcast([P, NT, NE])
                dve.wait_ge(loaded, 2 * 16)
                dve.wait_ge(logits, 1)
                dve.tensor_copy(lg[:, :, :], lgp).then_inc(lg_read, 1)
                dve.wait_ge(lg_read, 1)
                chain(dve.tensor_reduce(m1[:, :], lg[:, :, :], AX.X, ALU.max))
                dve.tensor_tensor(lg[:, :, :], lg[:, :, :], wide(m1[:, :]), ALU.subtract).then_inc(shifted, 1)
                dve.wait_ge(exps, 1)
                chain(dve.tensor_reduce(emax[:, :], e8[:, :, :], AX.X, ALU.max))
                one_hot_max(dve, s, chain, e8[:, :, :], emax[:, :], ranks, rank[:, :, :], top[:, :], hot[:, :, :])
                chain(dve.scalar_tensor_tensor(rest[:, :, :], hot[:, :, :], -2.0, e8[:, :, :], ALU.mult, ALU.add))
                chain(dve.tensor_reduce(esec[:, :], rest[:, :, :], AX.X, ALU.max))
                one_hot_max(dve, s, chain, rest[:, :, :], esec[:, :], ranks, rank[:, :, :], top[:, :], hot2[:, :, :])
                chain(dve.tensor_tensor(total[:, :], emax[:, :], esec[:, :], ALU.add))
                chain(dve.reciprocal(total[:, :], total[:, :]))
                chain(dve.tensor_tensor(hot[:, :, :], hot[:, :, :], hot2[:, :, :], ALU.add))
                chain(dve.tensor_tensor(hot[:, :, :], hot[:, :, :], e8[:, :, :], ALU.mult))
                chain(dve.tensor_tensor(coef[:, :, :], hot[:, :, :], wide(total[:, :]), ALU.mult))
                dve.wait_ge(acc_zero, 1)

                def mix(e, k, n, first):
                    h, j = n // JC, n % JC
                    dve.wait_ge(silu_done, e * STEPS + (n + 1))
                    if not first and n % JC == 0:
                        dve.wait_ge(down_done, e * NBK + (2 * (h + 1) - NBK))
                    dve.scalar_tensor_tensor(act_f[:, h, j, :], bank[:, 5 + 2 * (n % 2), :], w_back[:, k:k + 1],
                                             silu[:, n % 2, :], ALU.mult, ALU.mult).then_inc(mixed, 1)

                def add(e, t, first):
                    dve.wait_ge(down_done, e * NBK + (t // 2 + 1))
                    if not first:
                        dve.wait_ge(added, e * NT + (t + 1 - NT))
                    dve.scalar_tensor_tensor(acc[:, t, :], bank[:, t // 2, (t % 2) * DM:(t % 2 + 1) * DM],
                                             coef[:, t, bass.ds(e, 1)], acc[:, t, :], ALU.mult, ALU.add).then_inc(added, 1)

                def expert(i, k, first=False, final=False):
                    e = 2 * i + k
                    for n in range(STEPS):
                        mix(e, k, n, first)
                        if not final and n == 1:
                            top_rows(e + 1, i + k, 1 - k)
                        if not final and n == 3:
                            scale_of(e + 1, 1 - k)
                        if not final and n == 5:
                            low_part(e + 1, 1 - k)
                    for t in range(NT):
                        add(e, t, first)

                expert(0, 0, True)
                expert(0, 1)
                with dve.Fori(1, NE // 2 - 1) as i:
                    for k in range(2):
                        expert(i, k)
                expert(NE // 2 - 1, 0)
                expert(NE // 2 - 1, 1, final=True)
                dve.wait_ge(added, NE * NT)
                for t in range(NT):
                    dve.scalar_tensor_tensor(core.X[:, t, :], acc[:, t, :], gate, core.X[:, t, :], ALU.mult, ALU.add)


def stage_smooth_quant(core):
    nc, d = core.nc, core.dram
    EPS, QMAX = 1e-6, 127.0
    CHUNKS = (DC, 1)
    with core.stage("sq") as s:
        wide = lambda r: CHUNKS[r] * P
        w_nat = [s.sb("w_nat", [P, NT, DM]), s.sb("ctx_nat", [P, NT, CTX])]
        w_turn = [s.sb("w_turn", [P, DC, NTOK]), s.sb("ctx_turn", [P, 1, NTOK])]
        a_nat = s.sb("a_nat", [P, NT, CTX])
        x_nat = [core.xn, a_nat]
        amax_x = [s.sb(f"amax_x{r}", [P, CHUNKS[r] * NB]) for r in range(2)]
        amax_w = [s.sb(f"amax_w{r}", [P, CHUNKS[r] * NB]) for r in range(2)]
        smooth = [s.sb(f"smooth{r}", [P, CHUNKS[r] * NB]) for r in range(2)]
        inverse = [s.sb(f"inverse{r}", [P, CHUNKS[r] * NB]) for r in range(2)]
        diag = s.sb("diag", [P, NT, P])
        diag_inv = s.sb("diag_inv", [P, NT, P])
        inverse_row = [s.sb(f"inverse_row{r}", [P, NB, wide(r)]) for r in range(2)]
        x_mult = [s.sb(f"x_mult{r}", [P, NT]) for r in range(2)]
        w_mult = [s.sb(f"w_mult{r}", [P, NT]) for r in range(2)]
        smooth_row = [s.sb(f"smooth_row{r}", [P, NB, wide(r)]) for r in range(2)]
        x_scale = [s.sb(f"x_scale{r}", [P, NT]) for r in range(2)]
        w_scale = [s.sb(f"w_scale{r}", [P, NT]) for r in range(2)]
        w_scale_row = [s.sb(f"w_scale_row{r}", [P, NTOK]) for r in range(2)]
        xq = [s.sb(f"xq{r}", [P, NT, wide(r)], BF16) for r in range(2)]
        wq = [s.sb(f"wq{r}", [P, NT, wide(r)], BF16) for r in range(2)]
        xqT = [s.sb(f"xqT{r}", [P, CHUNKS[r], NTOK], BF16) for r in range(2)]
        wqT = [s.sb(f"wqT{r}", [P, CHUNKS[r], NTOK], BF16) for r in range(2)]
        hidden = s.sb("hidden", [P, NT, DM])
        silu = s.sb("silu", [P, NT, CTX])
        scaled = s.sb("scaled", [P, 2, DM])
        w_in, c_in, step = s.sem("w_in"), s.sem("c_in"), s.sem("step")
        both = lambda n: [s.sem(f"{n}{r}") for r in range(2)]
        ratio, root, diag_s, row_s, rowcopy_s, diag_w, row_w, rowcopy_w = (both(n) for n in (
            "ratio", "root", "diag_s", "row_s", "rowcopy_s", "diag_w", "row_w", "rowcopy_w"))
        x_int, w_int, x_turned, w_turned, x_back, w_back = (both(n) for n in (
            "x_int", "w_int", "x_turned", "w_turned", "x_back", "w_back"))
        w_smoothed, x_shifted = both("w_smoothed"), both("x_shifted")
        product, used = both("product"), both("used")
        silu_done, a_ready, a_turned, times = (s.sem(n) for n in (
            "silu_done", "a_ready", "a_turned", "times"))
        bank = core.bank
        gate = core.gates[:, 3:4]
        shape = lambda a: a.rearrange("p (b i) n -> p b i n", b=NB)
        rows = lambda r, row: row[:, :, :].unsqueeze(2).to_broadcast([P, NB, 2, wide(r)])
        half_bf = lambda b: bank[:, b, :].bitcast(BF16)
        XB, WB = ((4, 5), (6,)), ((6, 7), (7,))

        with nc.Block() as block:
            @block.sync
            def _(sp):
                sp.dma_start(w_turn[0][:, :, :], d["l3x_wT"].rearrange("(c p) n -> p c n", p=P)).then_inc(w_in, 16)
                sp.dma_start(w_nat[0][:, :, :], d["l3x_w"].rearrange("(t p) n -> p t n", p=P)).then_inc(w_in, 16)
                sp.dma_start(w_turn[1][:, :, :], d["ctxT"].rearrange("(c p) n -> p c n", p=P)).then_inc(c_in, 16)
                sp.dma_start(w_nat[1][:, :, :], d["ctx"].rearrange("(t p) n -> p t n", p=P)).then_inc(c_in, 16)

            @block.tensor
            def _(pe):
                s.norm_tensor(pe)
                pe.wait_ge(s.xnT_ready, 4)

                def quantised(r):
                    C = CHUNKS[r]
                    for k, (first, factors) in enumerate(((2, diag_inv), (0, diag))):
                        pe.wait_ge(diag_s[r], k + 1)
                        for h in range(C):
                            last = pe.matmul(bank[:, first + h, :], core.ones[:, :], factors[:, 4 * h:4 * h + 4, :],
                                             start=True, stop=True)
                        last.then_inc(row_s[r], 1)
                    for ints, count, turned, dst, banks in ((x_int, 2, x_turned, xq, XB), (w_int, 1, w_turned, wq, WB)):
                        pe.wait_ge(ints[r], count)
                        for c in range(C):
                            for t in range(NT):
                                last = pe.transpose(half_bf(banks[r][c])[:, t * P:(t + 1) * P],
                                                    dst[r][:, t, c * P:(c + 1) * P], core.identh[:, :])
                        last.then_inc(turned[r], 1)
                    pe.wait_ge(diag_w[r], 1)
                    pe.wait_ge(rowcopy_s[r], 2)
                    for h in range(2):
                        last = pe.matmul(bank[:, 2 + h, :], core.ones[:, :], diag[:, 4 * h:4 * h + 4, :], start=True, stop=True)
                    last.then_inc(row_w[r], 1)
                    pe.wait_ge(x_back[r], 1)
                    pe.wait_ge(w_back[r], 1)
                    for t in range(NT):
                        b = t // 2
                        if t >= 2:
                            pe.wait_ge(used[r], t - 1)
                        for c in range(C):
                            last = pe.matmul(bank[:, t % 2, 0:DM], xqT[r][:, c, t * P:(t + 1) * P],
                                             wqT[r][:, c, b * DM:(b + 1) * DM], start=c == 0, stop=c == C - 1)
                        last.then_inc(product[r], 1)

                quantised(0)
                pe.wait_ge(a_ready, 1)
                for t in range(NT):
                    last = pe.transpose(bank[:, 4 + t // 4, (t % 4) * P:(t % 4 + 1) * P], a_nat[:, t, :], core.ident[:, :])
                last.then_inc(a_turned, 1)
                quantised(1)

            @block.scalar
            def _(act):
                s.norm_scalar(act)

                def quantised(r):
                    C = CHUNKS[r]
                    act.wait_ge(ratio[r], 1)
                    act.activation(smooth[r][:, :], amax_x[r][:, :], ACT.Sqrt).then_inc(root[r], 1)
                    act.wait_ge(row_s[r], 1)
                    act.copy(inverse_row[r][:, :, :].rearrange("p b n -> p (b n)").rearrange("p (h n) -> p h n", h=C),
                             bank[:, 2:2 + C, :]).then_inc(rowcopy_s[r], 1)
                    act.wait_ge(row_s[r], 2)
                    act.copy(smooth_row[r][:, :, :].rearrange("p b n -> p (b n)").rearrange("p (h n) -> p h n", h=C),
                             bank[:, 0:C, :]).then_inc(rowcopy_s[r], 1)
                    act.wait_ge(x_turned[r], 1)
                    act.copy(xqT[r][:, :, :], half_bf_banks(XB[r])).then_inc(x_back[r], 1)
                    act.wait_ge(w_turned[r], 1)
                    act.copy(wqT[r][:, :, :], half_bf_banks(WB[r])).then_inc(w_back[r], 1)
                    act.wait_ge(row_w[r], 1)
                    act.copy(w_scale_row[r][:, :].rearrange("p (h n) -> p h n", h=2), bank[:, 2:4, :]).then_inc(rowcopy_w[r], 1)

                half_bf_banks = lambda bs: bank[:, bs[0]:bs[-1] + 1, :].bitcast(BF16)
                quantised(0)
                act.wait_ge(used[0], NT)
                act.activation(silu[:, :, :], hidden[:, :, 0:CTX], ACT.Silu).then_inc(silu_done, 1)
                quantised(1)

            @block.gpsimd
            def _(pool):
                for r in range(2):
                    pool.wait_ge((w_in, c_in)[r], 2 * 16)
                    pool.wait_ge(rowcopy_s[r], 2)
                    pool.tensor_tensor(shape(w_nat[r][:, :, :]), shape(w_nat[r][:, :, :]), rows(r, smooth_row[r]), ALU.mult
                                       ).then_inc(w_smoothed[r], 1)
                    pool.wait_ge(x_shifted[r], 1)
                    pool.tensor_scalar(xq[r][:, 0:NT // 2, :], x_nat[r][:, 0:NT // 2, :], ROUND, QMAX,
                                       ALU.subtract, ALU.min).then_inc(x_int[r], 1)

            @block.vector
            def _(dve):
                steps = [0]

                def chain(ins):
                    steps[0] += 1
                    ins.then_inc(step, 1)
                    dve.wait_ge(step, steps[0])

                def diagonals(dst, n, column):
                    for k in range(n):
                        last = dve.tensor_scalar(dst[:, k, :], core.ident[:, :], column(k), None, ALU.mult)
                    return last

                def quantised(r, turned_x):
                    C = CHUNKS[r]
                    chain(dve.tensor_reduce(amax_x[r][:, :], turned_x, AX.X, ALU.max, apply_absolute_value=True))
                    chain(dve.tensor_scalar(amax_x[r][:, :], amax_x[r][:, :], EPS, None, ALU.max))
                    dve.tensor_tensor(amax_x[r][:, :], amax_x[r][:, :], amax_w[r][:, :], ALU.mult).then_inc(ratio[r], 1)
                    dve.wait_ge(root[r], 1)
                    chain(dve.tensor_scalar(smooth[r][:, :], smooth[r][:, :], EPS, None, ALU.max))
                    chain(dve.reciprocal(inverse[r][:, :], smooth[r][:, :]))
                    at = lambda k: slice((k % C) * NB + k // C, (k % C) * NB + k // C + 1)
                    diagonals(diag_inv, NB * C, lambda k: inverse[r][:, at(k)]).then_inc(diag_s[r], 1)
                    diagonals(diag, NB * C, lambda k: smooth[r][:, at(k)]).then_inc(diag_s[r], 1)
                    if r == 0:
                        dve.wait_ge(c_in, 2 * 16)
                        weight_tops(1)
                    dve.wait_ge(rowcopy_s[r], 1)
                    chain(dve.tensor_tensor(shape(x_nat[r][:, :, :]), shape(x_nat[r][:, :, :]), rows(r, inverse_row[r]), ALU.mult))
                    for nat, scale, mult in ((x_nat[r], x_scale[r], x_mult[r]), (w_nat[r], w_scale[r], w_mult[r])):
                        if nat is w_nat[r]:
                            dve.wait_ge(w_smoothed[r], 1)
                        chain(dve.tensor_reduce(scale[:, :], nat[:, :, :], AX.X, ALU.max, apply_absolute_value=True))
                        chain(dve.tensor_scalar(scale[:, :], scale[:, :], EPS, 1.0 / QMAX, ALU.max, ALU.mult))
                        chain(dve.reciprocal(mult[:, :], scale[:, :]))
                        for t in range(NT):
                            last = dve.tensor_scalar(nat[:, t, :], nat[:, t, :], mult[:, t:t + 1], ROUND, ALU.mult, ALU.add)
                        if nat is x_nat[r]:
                            last.then_inc(x_shifted[r], 1)
                            dve.wait_ge(x_shifted[r], 1)
                            dve.tensor_scalar(xq[r][:, NT // 2:NT, :], x_nat[r][:, NT // 2:NT, :], ROUND, QMAX,
                                              ALU.subtract, ALU.min).then_inc(x_int[r], 1)
                        else:
                            chain(last)
                    dve.tensor_scalar(wq[r][:, :, :], w_nat[r][:, :, :], ROUND, QMAX, ALU.subtract, ALU.min).then_inc(w_int[r], 1)
                    dve.wait_ge(row_s[r], 2)
                    diagonals(diag, NT, lambda k: w_scale[r][:, k:k + 1]).then_inc(diag_w[r], 1)
                    dve.wait_ge(rowcopy_w[r], 1)

                def rescale(r, t, dst):
                    dve.wait_ge(product[r], t + 1)
                    b = t // 2
                    return dve.scalar_tensor_tensor(dst, bank[:, t % 2, 0:DM], x_scale[r][:, t:t + 1],
                                                    w_scale_row[r][:, b * DM:(b + 1) * DM], ALU.mult, ALU.mult)

                def weight_tops(r):
                    chain(dve.tensor_reduce(amax_w[r][:, :], w_turn[r][:, :, :].rearrange("p c (b n) -> p (c b) n", b=NB),
                                            AX.X, ALU.max, apply_absolute_value=True))
                    chain(dve.tensor_scalar(amax_w[r][:, :], amax_w[r][:, :], EPS, None, ALU.max))
                    chain(dve.reciprocal(amax_w[r][:, :], amax_w[r][:, :]))

                s.norm_vector(dve)
                dve.wait_ge(w_in, 2 * 16)
                weight_tops(0)
                dve.wait_ge(s.xnT_ready, 4)
                quantised(0, core.xnT[:, :, :].rearrange("p c (b n) -> p (c b) n", b=NB))
                for t in range(NT):
                    rescale(0, t, hidden[:, t, :]).then_inc(used[0], 1)
                dve.wait_ge(silu_done, 1)
                dve.tensor_tensor(a_nat[:, :, :], silu[:, :, :], hidden[:, :, CTX:DM], ALU.mult).then_inc(a_ready, 1)
                dve.wait_ge(a_turned, 1)
                quantised(1, bank[:, 4:6, :].rearrange("p h (b n) -> p (h b) n", b=2))
                for t in range(NT):
                    if t >= 2:
                        dve.wait_ge(times, t - 1)
                    rescale(1, t, scaled[:, t % 2, :]).then_inc(used[1], 1)
                    dve.wait_ge(used[1], t + 1)
                    dve.scalar_tensor_tensor(core.X[:, t, :], scaled[:, t % 2, :], gate, core.X[:, t, :],
                                             ALU.mult, ALU.add).then_inc(times, 1)


def stage_fp8_ffn(core):
    nc, d = core.nc, core.dram
    FF = 768
    JC = FF // P
    F8 = mybir.dt.float8e4
    U8 = mybir.dt.uint8
    X_SCALE = 2.0 ** 8
    with core.stage("fp8") as s:
        wg, wu, wd = s.sb("wg", [P, DC * FF]), s.sb("wu", [P, DC * FF]), s.sb("wd", [P, JC * DM])
        NW = DC * FF
        low8, high8 = s.sb("low8", [P, NW], F8), s.sb("high8", [P, NW], F8)
        large, size = s.sb("large", [P, NW], U8), s.sb("size", [P, NW])
        doubled = [s.sb(f"doubled{i}", [P, NW], dt) for i, dt in enumerate((F16, F16, BF16))]
        rounded_w = [s.sb(f"rounded_w{i}", [P, NW], dt) for i, dt in enumerate((F16, F16, BF16))]
        x_hi, x_lo = s.sb("x_hi", [P, DC, NTOK], F16), s.sb("x_lo", [P, DC, NTOK], F16)
        gs, us, ds = s.sb("gs", [P, JC]), s.sb("us", [P, JC]), s.sb("ds", [P, DM])
        silu, fuse = s.sb("silu", [P, 2, HALF]), s.sb("fuse", [P, 2, HALF])
        f_rest = s.sb("f_rest", [P, 2, HALF])
        f_parts = [s.sb(f"f_part{i}", [P, JC, NTOK], BF16) for i in range(3)]
        scaled = s.sb("scaled", [P, 2, DM])
        loaded = [s.sem(f"loaded{i}") for i in range(3)]
        scales, halved, step, rounded = s.sem("scales"), s.sem("halved"), s.sem("step"), s.sem("rounded")
        x_hi_ready, x_ready, f_hi, f_rested, f_mid, f_lo, shrunk = (s.sem(n) for n in (
            "x_hi_ready", "x_ready", "f_hi", "f_rested", "f_mid", "f_lo", "shrunk"))
        sized, large_known, doubled_done = s.sem("sized"), s.sem("large_known"), s.sem("doubled_done")
        gate_up, silu_done, fused, out_done, times, added = (s.sem(n) for n in (
            "gate_up", "silu_done", "fused", "out_done", "times", "added"))
        bank = core.bank
        weights = [wg, wu, wd]
        split = lambda i, a: a[:, :].rearrange("p (c f) -> p c f", c=(DC, DC, JC)[i])
        w3 = [split(i, w) for i, w in enumerate(rounded_w)]
        gate = core.gates[:, 7:8]

        def part_of(i, n):
            return f_parts[i][:, n % JC, n // JC * HALF:(n // JC + 1) * HALF]

        with nc.Block() as block:
            @block.sync
            def _(sp):
                for i, n in enumerate(("l3_gate", "l3_up", "l3_down")):
                    sp.dma_start(split(i, weights[i]), d[n].rearrange("(c p) f -> p c f", p=P)).then_inc(loaded[i], 16)
                sp.dma_start(gs[:, :], d["l3_gate_scale"]).then_inc(scales, 16)
                sp.dma_start(us[:, :], d["l3_up_scale"]).then_inc(scales, 16)
                sp.dma_start(ds[:, :], d["l3_down_scale"].partition_broadcast(P)).then_inc(scales, 16)

            @block.tensor
            def _(pe):
                s.norm_tensor(pe)
                pe.wait_ge(rounded, 2)
                for h in range(2):
                    pe.wait_ge(x_ready, h + 1)
                    for j in range(JC):
                        n = h * JC + j
                        if n >= 2:
                            pe.wait_ge(fused, n - 1)
                        for k in range(2):
                            for c in range(DC):
                                for x in (x_hi, x_lo):
                                    last = pe.matmul(bank[:, 4 + 2 * (n % 2) + k, :], w3[k][:, c, j * P:(j + 1) * P],
                                                     x[:, c, h * HALF:(h + 1) * HALF], start=c == 0 and x is x_hi,
                                                     stop=c == DC - 1 and x is x_lo)
                        last.then_inc(gate_up, 1)
                pe.wait_ge(rounded, 3)
                pe.wait_ge(s.xnT_ready, 4)
                for t in range(NT):
                    pe.wait_ge(f_lo, JC * (t // 4 + 1))
                    for j in range(JC):
                        for i in range(3):
                            last = pe.matmul(bank[:, t // 2, (t % 2) * DM:(t % 2 + 1) * DM],
                                             f_parts[i][:, j, t * P:(t + 1) * P], w3[2][:, j, :],
                                             start=j == 0 and i == 0, stop=j == JC - 1 and i == 2)
                    if t % 2 == 1:
                        last.then_inc(out_done, 1)

            @block.scalar
            def _(act):
                s.norm_root(act)
                for i in range(3):
                    act.wait_ge(loaded[i], 16)
                    if i >= 1:
                        act.wait_ge(large_known, i)
                    act.activation(size[:, :], weights[i][:, :], ACT.Abs).then_inc(sized, 1)
                    if i >= 1:
                        act.wait_ge(doubled_done, i)
                    act.activation(high8[:, :], weights[i][:, :], ACT.Copy, scale=0.5, saturate=False).then_inc(halved, 1)
                    act.wait_ge(halved, i + 1)
                    act.activation(doubled[i][:, :], high8[:, :], ACT.Copy, scale=2.0).then_inc(doubled_done, 1)
                    if i == 0:
                        s.norm_bring(act)
                        for h in range(2):
                            half = slice(h * HALF, (h + 1) * HALF)
                            act.wait_ge(s.xnT_ready, 2 * (h + 1))
                            act.activation(x_hi[:, :, half], core.xnT[:, :, half], ACT.Copy, scale=X_SCALE
                                           ).then_inc(x_hi_ready, 1)
                act.wait_ge(shrunk, 1)

                def silu_of(n):
                    act.wait_ge(gate_up, n + 1)
                    if n >= 2:
                        act.wait_ge(fused, n - 1)
                    act.activation(silu[:, n % 2, :], bank[:, 4 + 2 * (n % 2), :], ACT.Silu,
                                   scale=gs[:, n % JC:n % JC + 1]).then_inc(silu_done, 1)

                def high_part(n):
                    act.wait_ge(fused, n + 1)
                    act.copy(part_of(0, n), fuse[:, n % 2, :]).then_inc(f_hi, 1)

                silu_of(0)
                for n in range(2 * JC):
                    if n + 1 < 2 * JC:
                        silu_of(n + 1)
                    high_part(n)
                    if n >= 1:
                        act.wait_ge(f_rested, n)
                        act.copy(part_of(1, n - 1), f_rest[:, (n - 1) % 2, :]).then_inc(f_mid, 1)
                act.wait_ge(f_rested, 2 * JC)
                act.copy(part_of(1, 2 * JC - 1), f_rest[:, 1, :]).then_inc(f_mid, 1)

            @block.gpsimd
            def _(pool):
                for i in range(3):
                    pool.wait_ge(sized, i + 1)
                    if i >= 1:
                        pool.wait_ge(rounded, i)
                    pool.tensor_scalar(large[:, :], size[:, :], 128.0, None, ALU.is_ge).then_inc(large_known, 1)
                for n in range(2 * JC):
                    pool.wait_ge(f_hi, n + 1)
                    await_count(pool, f_lo, n - 1)
                    await_count(pool, f_mid, n - 1)
                    pool.tensor_tensor(f_rest[:, n % 2, :], fuse[:, n % 2, :], part_of(0, n), ALU.subtract
                                       ).then_inc(f_rested, 1)

            @block.vector
            def _(dve):
                steps = [0]

                def chain(ins):
                    steps[0] += 1
                    ins.then_inc(step, 1)
                    dve.wait_ge(step, steps[0])

                def round_weight(i):
                    dve.wait_ge(loaded[i], 16)
                    w = weights[i][:, :]
                    chain(dve.tensor_scalar(low8[:, :], w, 240.0, -240.0, ALU.min, ALU.max, saturate=False))
                    dve.wait_ge(doubled_done, i + 1)
                    dve.wait_ge(large_known, i + 1)
                    chain(dve.tensor_copy(rounded_w[i][:, :], low8[:, :]))
                    dve.copy_predicated(rounded_w[i][:, :], large[:, :], doubled[i][:, :]).then_inc(rounded, 1)

                s.norm_vector(dve)
                dve.wait_ge(scales, 3 * 16)
                for k in (gs, us):
                    last = dve.tensor_scalar(k[:, :], k[:, :], 1.0 / X_SCALE, None, ALU.mult)
                last.then_inc(shrunk, 1)
                for i in range(3):
                    round_weight(i)
                    for h in range(2 if i == 0 else 0):
                        half = slice(h * HALF, (h + 1) * HALF)
                        dve.wait_ge(x_hi_ready, h + 1)
                        dve.scalar_tensor_tensor(x_lo[:, :, half], core.xnT[:, :, half], X_SCALE, x_hi[:, :, half],
                                                 ALU.mult, ALU.subtract).then_inc(x_ready, 1)
                dve.wait_ge(shrunk, 1)

                def low_part(n):
                    dve.wait_ge(f_mid, n + 1)
                    dve.tensor_tensor(part_of(2, n), f_rest[:, n % 2, :], part_of(1, n), ALU.subtract).then_inc(f_lo, 1)

                for n in range(2 * JC):
                    dve.wait_ge(silu_done, n + 1)
                    j = n % JC
                    await_count(dve, f_hi, n - 1)
                    await_count(dve, f_rested, n - 1)
                    dve.scalar_tensor_tensor(fuse[:, n % 2, :], bank[:, 5 + 2 * (n % 2), :],
                                             us[:, j:j + 1], silu[:, n % 2, :], ALU.mult, ALU.mult).then_inc(fused, 1)
                    if n >= 2:
                        low_part(n - 2)
                low_part(2 * JC - 2)
                low_part(2 * JC - 1)
                for t in range(NT):
                    dve.wait_ge(out_done, t // 2 + 1)
                    if t >= 2:
                        dve.wait_ge(added, t - 1)
                    dve.tensor_tensor(scaled[:, t % 2, :], bank[:, t // 2, (t % 2) * DM:(t % 2 + 1) * DM], ds[:, :],
                                      ALU.mult).then_inc(times, 1)
                    dve.wait_ge(times, t + 1)
                    dve.scalar_tensor_tensor(core.X[:, t, :], scaled[:, t % 2, :], gate, core.X[:, t, :],
                                             ALU.mult, ALU.add).then_inc(added, 1)


def build(nc, dram):
    with ExitStack() as ctx:
        core = Core(nc, ctx, dram)
        stage_setup(core)
        steps = (stage_ssm, stage_lora_moe, stage_attention_16, stage_bitnet,
                 stage_attention_32, stage_moe, stage_smooth_quant, stage_fp8_ffn)
        for k in STAGES:
            steps[k](core)
            if k in (2, 4):
                core.clear_semaphores()
        stage_store(core)


def _layouts(np, i):
    flat = lambda a: a.reshape(-1, a.shape[-1])
    T = lambda a: a.T
    return {
        "x": flat(i["x"]),
        "ctx": flat(i["ctx_1024"]),
        "ctxT": T(flat(i["ctx_1024"])),
        "g_xattn": i["g_xattn"],
        "g_ffn": i["g_ffn"],
        "l0_A": T(flat(i["L0_ffn_A"])),
        "l0_B": i["L0_ffn_B"].transpose(0, 2, 1).reshape(-1, DM),
        "l0_Wr": T(i["L0_ffn_Wr"]),
        "l0_br": i["L0_ffn_br"],
        "l0x_in": T(i["L0_xattn_in_proj_w"]),
        "l0x_dt2": T(i["L0_xattn_dt_proj_w"]),
        "l0x_chan": np.concatenate([i["L0_xattn_conv_w"], i["L0_xattn_conv_b"].reshape(-1, 1),
                                    i["L0_xattn_dt_proj_b"].reshape(-1, 1), i["L0_xattn_D"].reshape(-1, 1),
                                    i["L0_xattn_A_log"], T(i["L0_xattn_x_proj_w"][8:40]),
                                    T(i["L0_xattn_x_proj_w"][0:8])], axis=1),
        "l1x_q": i["L1_xattn_Wq"].reshape(DM, 16, -1).transpose(1, 0, 2),
        "l1x_k": i["L1_xattn_Wk"].reshape(CTX, 16, -1).transpose(1, 0, 2),
        "l1x_vT": i["L1_xattn_Wv"].reshape(CTX, 16, -1).transpose(1, 2, 0),
        "l1x_o": i["L1_xattn_Wo"].reshape(16, -1, DM),
        "l1x_gains": T(np.stack([i["L1_xattn_gq"], i["L1_xattn_gk"]])),
        "l1_gate": T(i["L1_ffn_w_gate"]),
        "l1_up": T(i["L1_ffn_w_up"]),
        "l1_down": T(i["L1_ffn_w_down"]),
        "l2x_q": i["L2_xattn_Wq"],
        "l2x_kv": i["L2_xattn_Wkv"],
        "l2x_out": i["L2_xattn_Wout"],
        "l2x_bout": i["L2_xattn_bout"],
        "pos": flat(i["fside_BxSx2_0"]),
        "l2_gate": T(i["L2_ffn_gate_w"]),
        "l2_up": i["L2_ffn_w_up"].transpose(0, 2, 1),
        "l2_down": i["L2_ffn_w_down"].transpose(0, 2, 1),
        "l3x_w": flat(i["fside_BxS2xS2_0"]),
        "l3x_wT": T(flat(i["fside_BxS2xS2_0"])),
        "l3_gate": i["L3_ffn_gate_w"],
        "l3_up": i["L3_ffn_up_w"],
        "l3_down": i["L3_ffn_down_w"],
        "l3_gate_scale": T(i["L3_ffn_gate_scale"].reshape(-1, P)),
        "l3_up_scale": T(i["L3_ffn_up_scale"].reshape(-1, P)),
        "l3_down_scale": i["L3_ffn_down_scale"],
    }


def _constants(np):
    eye = np.eye(P, dtype=np.float32)
    h = np.ones((1, 1), np.float32)
    while h.shape[0] < P:
        h = np.block([[h, h], [h, -h]]).astype(np.float32)
    sel = np.zeros((96, 32, P), np.float32)
    for n in range(32):
        sel[[n, 32 + n, 64 + n], n, :] = 1.0
    bf16 = mybir.dt.np(BF16)
    return {"row_of_ones": np.ones(32 * SEQ, bf16), "row_of_zeros": np.zeros(32 * SEQ, bf16),
            "ident": eye, "identh": eye.astype(bf16), "hadamard": h,
            "rank8": np.broadcast_to(np.arange(8, 0, -1, dtype=np.float32), (P, 8)).copy(),
            "select3": sel.reshape(96, 32 * P).astype(bf16)}


def kernel(**inputs):
    import numpy as _np
    import concourse.bacc as _bacc
    from concourse import mybir as _mybir
    from concourse.bass_utils import run_bass_kernel_spmd as _run

    nc = _bacc.Bacc("TRN2", target_bir_lowering=False, num_devices=1)
    arrays, dram = {}, {}
    for group in (_layouts(_np, {k: _np.asarray(v) for k, v in inputs.items()}), _constants(_np)):
        for name, a in group.items():
            a = _np.ascontiguousarray(a)
            arrays[f"in_{name}_dram"] = a
            dram[name] = nc.dram_tensor(f"in_{name}_dram", a.shape, _mybir.dt.from_np(a.dtype), kind="ExternalInput").ap()
    dram["out"] = nc.dram_tensor("out_0_dram", (NTOK, DM), F32, kind="ExternalOutput").ap()
    build(nc, dram)
    r = _run(nc, [arrays], core_ids=[0])
    return r.results[0]["out_0_dram"].reshape(NB, SEQ, DM)
```
